# Optimizing a Trainium2 kernel written in Bass

```python
import numpy as np
import jax
import jax.numpy as jnp

def _softmax(x, axis=-1):
    return jax.nn.softmax(x, axis=axis)

def _gelu(x):
    return jax.nn.gelu(x, approximate=True)

def _silu(x):
    return jax.nn.silu(x)

def _sigmoid(x):
    return jax.nn.sigmoid(x)

def _layernorm(x, axis=-1, eps=1e-05):
    m = jnp.mean(x, axis=axis, keepdims=True)
    v = jnp.var(x, axis=axis, keepdims=True)
    return (x - m) / jnp.sqrt(v + eps)

def _scatter_add(tgt, idx, src, axis=0):
    return tgt.at[idx].add(src)

def _segment_sum(src, seg, n):
    return jax.ops.segment_sum(src, seg, n)
kernel_name = 'mk_adaln_d4_jaxref_r8_938f84'

def setup_inputs(seed: int=0):
    np.random.seed(seed)
    _w = jnp.asarray

    def _L0_attn_setup():
        import jax, jax.numpy as jnp
        import numpy as np
        D_MODEL = 128
        D_STATE = 128
        HEADDIM = 64
        EXPAND = 2
        CHUNK = 64
        D_CONV = 4
        D_INNER = EXPAND * D_MODEL
        NHEADS = D_INNER // HEADDIM
        D_IN_PROJ = 2 * D_INNER + 2 * D_STATE + NHEADS
        CONV_CH = D_INNER + 2 * D_STATE
        EPS = 1e-05

        def segsum(x):
            T = x.shape[-1]
            m1 = jnp.tril(jnp.ones((T, T), bool), -1)
            xr = jnp.where(m1, x[..., :, None], 0.0)
            s = jnp.cumsum(xr, axis=-2)
            m0 = jnp.tril(jnp.ones((T, T), bool), 0)
            return jnp.where(m0, s, -jnp.inf)

        def ssd(x, A, B, C, chunk):
            b, L, h, p = x.shape
            c = L // chunk
            x = x.reshape(b, c, chunk, h, p)
            A = A.reshape(b, c, chunk, h).transpose(0, 3, 1, 2)
            B = B.reshape(b, c, chunk, -1)
            C = C.reshape(b, c, chunk, -1)
            A_cum = jnp.cumsum(A, axis=-1)
            Lm = jnp.exp(segsum(A))
            Y_diag = jnp.einsum('bcln,bcsn,bhcls,bcshp->bclhp', C, B, Lm, x)
            decay_states = jnp.exp(A_cum[:, :, :, -1:] - A_cum)
            states = jnp.einsum('bcln,bhcl,bclhp->bchpn', B, decay_states, x)
            init = jnp.zeros_like(states[:, :1])
            states = jnp.concatenate([init, states], axis=1)
            Ac_last = jnp.pad(A_cum[:, :, :, -1], ((0, 0), (0, 0), (1, 0)))
            decay_chunk = jnp.exp(segsum(Ac_last))
            new_states = jnp.einsum('bhzc,bchpn->bzhpn', decay_chunk, states)
            states = new_states[:, :-1]
            sdo = jnp.exp(A_cum)
            Y_off = jnp.einsum('bcln,bchpn,bhcl->bclhp', C, states, sdo)
            return (Y_diag + Y_off).reshape(b, L, h, p)
        key = jax.random.key(seed)
        ks = jax.random.split(key, 8)
        return {'u': jax.random.normal(ks[0], (2, 512, D_MODEL), jnp.float32), 'W_in': jax.random.normal(ks[1], (D_MODEL, D_IN_PROJ), jnp.float32) * 0.02, 'conv_w': jax.random.normal(ks[2], (CONV_CH, D_CONV), jnp.float32) * 0.3, 'conv_b': jax.random.normal(ks[3], (CONV_CH,), jnp.float32) * 0.1, 'dt_bias': jax.random.normal(ks[4], (NHEADS,), jnp.float32), 'A_log': jax.random.normal(ks[5], (NHEADS,), jnp.float32) * 0.5, 'D': jax.random.normal(ks[6], (NHEADS,), jnp.float32), 'norm_w': jnp.ones((D_INNER,), jnp.float32), 'W_out': jax.random.normal(ks[7], (D_INNER, D_MODEL), jnp.float32) * 0.02}
    _L0_attn_in = _L0_attn_setup()

    def _L0_ffn_setup():
        import jax, jax.numpy as jnp
        import numpy as np
        B, S, D = (2, 256, 128)
        M = 256
        E = 8
        TOP_K = 2
        key = jax.random.key(seed)
        ks = jax.random.split(key, 5)
        std = 0.02
        return {'residual': jax.random.normal(ks[0], (B, S, D), jnp.float32), 'W_router': jax.random.normal(ks[1], (D, E), jnp.float32) * std, 'W_gate': jax.random.normal(ks[2], (E, D, M), jnp.float32) * std, 'b_gate': jnp.zeros((E, M), jnp.float32), 'W_up': jax.random.normal(ks[3], (E, D, M), jnp.float32) * std, 'b_up': jnp.zeros((E, M), jnp.float32), 'W_out': jax.random.normal(ks[4], (E, M, D), jnp.float32) * std, 'b_out': jnp.zeros((E, D), jnp.float32)}
    _L0_ffn_in = _L0_ffn_setup()
    _L0_c = _w((lambda *s: np.random.randn(*s).astype(np.float32) * 0.05)(2, 128))
    _L0_wmod = _w((lambda *s: np.random.randn(*s).astype(np.float32) * 0.05)(128, 6 * 128) * 128 ** (-0.5))

    def _L1_attn_setup():
        import jax, jax.numpy as jnp
        import numpy as np
        N_HEAD = 16
        D_HEAD = 64
        D_MODEL = 128
        SEQ = 256
        BATCH = 2
        key = jax.random.key(seed)
        k1, k2, k3, k4 = jax.random.split(key, 4)
        s = 1.0 / np.sqrt(D_MODEL)
        return {'h': jax.random.normal(k1, (SEQ, BATCH, D_MODEL), dtype=jnp.float32), 'Wq': jax.random.normal(k2, (D_MODEL, N_HEAD * D_HEAD), dtype=jnp.float32) * s, 'Wkv': jax.random.normal(k3, (D_MODEL, 2 * N_HEAD * D_HEAD), dtype=jnp.float32) * s, 'Wo': jax.random.normal(k4, (N_HEAD * D_HEAD, D_MODEL), dtype=jnp.float32) * s}
    _L1_attn_in = _L1_attn_setup()

    def _L1_ffn_setup():
        import jax, jax.numpy as jnp
        import numpy as np
        DIM = 128
        DEPTH = 2
        HEADS = 8
        DIM_HEAD = 64
        WINDOW = 64
        INNER = HEADS * DIM_HEAD
        HID = int(DIM * 4 * 2 / 3)
        B, N = (2, 1024)
        QK_SCALE = 8.0

        def shift_token(t):
            t1, t2 = jnp.split(t, 2, axis=-1)
            t2 = jnp.pad(t2, ((0, 0), (1, 0), (0, 0)))[:, :-1]
            return jnp.concatenate([t1, t2], axis=-1)

        def l2norm(t):
            return t / jnp.clip(jnp.linalg.norm(t, axis=-1, keepdims=True), 1e-12)

        def rotate_half(x):
            x1, x2 = jnp.split(x, 2, axis=-1)
            return jnp.concatenate([-x2, x1], axis=-1)

        def rotary_xpos(q, k):
            n = q.shape[-2]
            half_idx = jnp.arange(0, DIM_HEAD, 2, dtype=jnp.float32)
            inv_freq = 1.0 / 10000.0 ** (half_idx / DIM_HEAD)
            t = jnp.arange(n, dtype=jnp.float32)
            freqs = t[:, None] * inv_freq[None, :]
            freqs = jnp.concatenate([freqs, freqs], axis=-1)
            base = (half_idx + 0.4 * DIM_HEAD) / (1.4 * DIM_HEAD)
            power = (t - n // 2) / float(WINDOW // 2)
            scale = base[None, :] ** power[:, None]
            scale = jnp.concatenate([scale, scale], axis=-1)
            cos, sin = (jnp.cos(freqs), jnp.sin(freqs))
            q = q * cos * scale + rotate_half(q) * sin * scale
            k = k * cos / scale + rotate_half(k) * sin / scale
            return (q, k)

        def local_attention(q, k, v):
            b, h, n, d = q.shape
            w = n // WINDOW
            bq = q.reshape(b, h, w, WINDOW, d) * QK_SCALE
            bk = k.reshape(b, h, w, WINDOW, d)
            bv = v.reshape(b, h, w, WINDOW, d)

            def look_around(t):
                p = jnp.pad(t, ((0, 0), (0, 0), (1, 0), (0, 0), (0, 0)))
                return jnp.concatenate([p[:, :, :w], p[:, :, 1:]], axis=3)
            bk, bv = (look_around(bk), look_around(bv))
            bt = jnp.arange(n).reshape(w, WINDOW)
            btp = jnp.pad(bt, ((1, 0), (0, 0)), constant_values=-1)
            btk = jnp.concatenate([btp[:w], btp[1:]], axis=1)
            sim = jnp.einsum('bhwid,bhwjd->bhwij', bq, bk)
            i = bt[:, :, None]
            j = btk[:, None, :]
            mask = (i < j) | (i > j + WINDOW) | (j == -1)
            sim = jnp.where(mask, -jnp.finfo(sim.dtype).max, sim)
            attn = jax.nn.softmax(sim, axis=-1)
            out = jnp.einsum('bhwij,bhwjd->bhwid', attn, bv)
            return out.reshape(b, h, n, d)

        def _layer(x, wqkv, qs, ksc, wo, lg, lb, w1, b1, w2, b2):
            b, n, _ = x.shape
            h = shift_token(x)
            qkv = h @ wqkv
            q, k, v = jnp.split(qkv, 3, axis=-1)
            to_heads = lambda t: t.reshape(b, n, HEADS, DIM_HEAD).transpose(0, 2, 1, 3)
            q, k, v = (to_heads(q), to_heads(k), to_heads(v))
            q = l2norm(q) * qs
            k = l2norm(k) * ksc
            q, k = rotary_xpos(q, k)
            o = local_attention(q, k, v)
            o = o.transpose(0, 2, 1, 3).reshape(b, n, INNER)
            x = x + o @ wo
            h = shift_token(x)
            mu = h.mean(-1, keepdims=True)
            var = h.var(-1, keepdims=True)
            h = (h - mu) / jnp.sqrt(var + 1e-05) * lg + lb
            h = h @ w1 + b1
            a, g = jnp.split(h, 2, axis=-1)
            h = a * jax.nn.gelu(g, approximate=False)
            x = x + h @ w2 + b2
            return x
        key = jax.random.key(seed)
        ks = jax.random.split(key, 6)
        return {'x': jax.random.normal(ks[0], (B, N, DIM), jnp.float32), 'wqkv': jax.random.normal(ks[1], (DEPTH, DIM, 3 * INNER), jnp.float32) * 0.02, 'q_scale': jnp.ones((DEPTH, DIM_HEAD), jnp.float32), 'k_scale': jnp.ones((DEPTH, DIM_HEAD), jnp.float32), 'wo': jax.random.normal(ks[2], (DEPTH, INNER, DIM), jnp.float32) * 0.02, 'ln_g': jnp.ones((DEPTH, DIM), jnp.float32), 'ln_b': jnp.zeros((DEPTH, DIM), jnp.float32), 'w1': jax.random.normal(ks[3], (DEPTH, DIM, 2 * HID), jnp.float32) * 0.02, 'b1': jnp.zeros((DEPTH, 2 * HID), jnp.float32), 'w2': jax.random.normal(ks[4], (DEPTH, HID, DIM), jnp.float32) * 0.02, 'b2': jnp.zeros((DEPTH, DIM), jnp.float32)}
    _L1_ffn_in = _L1_ffn_setup()
    _L1_c = _w((lambda *s: np.random.randn(*s).astype(np.float32) * 0.05)(2, 128))
    _L1_wmod = _w((lambda *s: np.random.randn(*s).astype(np.float32) * 0.05)(128, 6 * 128) * 128 ** (-0.5))

    def _L2_attn_setup():
        import jax, jax.numpy as jnp
        import numpy as np
        D_MODEL = 128
        NUM_HEADS = 16
        B, S = (1, 512)
        key = jax.random.key(seed)
        kx, kq, kk, kv, ko = jax.random.split(key, 5)
        std = (1.0 / D_MODEL) ** 0.5

        def trunc(k):
            return std * jax.random.truncated_normal(k, -3.0, 3.0, (D_MODEL, D_MODEL), dtype=jnp.float32)
        return {'x': jax.random.normal(kx, (B, S, D_MODEL), dtype=jnp.float32), 'W_Q': trunc(kq), 'W_K': trunc(kk), 'W_V': trunc(kv), 'W_O': trunc(ko)}
    _L2_attn_in = _L2_attn_setup()

    def _L2_ffn_setup():
        import jax, jax.numpy as jnp
        import numpy as np
        NUM_EXPERTS = 8
        HIDDEN = 128
        FFN = 512
        BATCH = 2
        SEQ = 256
        key = jax.random.key(seed)
        k_x, k_g, k_u, k_d = jax.random.split(key, 4)
        scale_in = 1.0 / np.sqrt(HIDDEN)
        scale_mid = 1.0 / np.sqrt(FFN)
        return {'hidden_states': jax.random.normal(k_x, (BATCH, SEQ, HIDDEN), dtype=jnp.float32), 'Wg': jax.random.normal(k_g, (NUM_EXPERTS, HIDDEN, FFN), dtype=jnp.float32) * scale_in, 'Wu': jax.random.normal(k_u, (NUM_EXPERTS, HIDDEN, FFN), dtype=jnp.float32) * scale_in, 'Wd': jax.random.normal(k_d, (NUM_EXPERTS, FFN, HIDDEN), dtype=jnp.float32) * scale_mid}
    _L2_ffn_in = _L2_ffn_setup()
    _L2_c = _w((lambda *s: np.random.randn(*s).astype(np.float32) * 0.05)(2, 128))
    _L2_wmod = _w((lambda *s: np.random.randn(*s).astype(np.float32) * 0.05)(128, 6 * 128) * 128 ** (-0.5))

    def _L3_attn_setup():
        import math
        import jax, jax.numpy as jnp
        import numpy as np
        EPS_SUM = 1e-07
        EPS_NORM = 1e-12

        def _l2norm(x, axis):
            n = jnp.sqrt(jnp.sum(x * x, axis=axis, keepdims=True))
            return x / jnp.maximum(n, EPS_NORM)
        key = jax.random.key(seed)
        ks = jax.random.split(key, 5)
        b, N, C = (4, 512, 128)
        x = jax.random.normal(ks[0], (b, N, C), dtype=jnp.float32)
        Wqkv = jax.random.normal(ks[1], (C, 3 * C), dtype=jnp.float32) / math.sqrt(C)
        bqkv = jax.random.normal(ks[2], (3 * C,), dtype=jnp.float32) * 0.01
        Wln = jax.random.normal(ks[3], (C, C), dtype=jnp.float32) / math.sqrt(C)
        bln = jax.random.normal(ks[4], (C,), dtype=jnp.float32) * 0.01
        return {'x': x, 'Wqkv': Wqkv, 'bqkv': bqkv, 'Wln': Wln, 'bln': bln}
    _L3_attn_in = _L3_attn_setup()

    def _L3_ffn_setup():
        import jax, jax.numpy as jnp
        import numpy as np
        TOP_K = 2
        key = jax.random.key(seed)
        ks = jax.random.split(key, 6)
        B, T, H, E, F = (2, 256, 128, 8, 512)
        s = 0.02
        return {'hidden_states': jax.random.normal(ks[0], (B, T, H), dtype=jnp.float32), 'router_w': jax.random.normal(ks[1], (E, H), dtype=jnp.float32) * s, 'w1': jax.random.normal(ks[2], (E, F, H), dtype=jnp.float32) * s, 'b1': jax.random.normal(ks[3], (E, F), dtype=jnp.float32) * s, 'w2': jax.random.normal(ks[4], (E, H, F), dtype=jnp.float32) * s, 'b2': jax.random.normal(ks[5], (E, H), dtype=jnp.float32) * s}
    _L3_ffn_in = _L3_ffn_setup()
    _L3_c = _w((lambda *s: np.random.randn(*s).astype(np.float32) * 0.05)(2, 128))
    _L3_wmod = _w((lambda *s: np.random.randn(*s).astype(np.float32) * 0.05)(128, 6 * 128) * 128 ** (-0.5))
    _d = {'L0_attn_u': _L0_attn_in['u'], 'L0_attn_W_in': _L0_attn_in['W_in'], 'L0_attn_conv_w': _L0_attn_in['conv_w'], 'L0_attn_conv_b': _L0_attn_in['conv_b'], 'L0_attn_dt_bias': _L0_attn_in['dt_bias'], 'L0_attn_A_log': _L0_attn_in['A_log'], 'L0_attn_D': _L0_attn_in['D'], 'L0_attn_norm_w': _L0_attn_in['norm_w'], 'L0_attn_W_out': _L0_attn_in['W_out'], 'L0_ffn_W_router': _L0_ffn_in['W_router'], 'L0_ffn_W_gate': _L0_ffn_in['W_gate'], 'L0_ffn_b_gate': _L0_ffn_in['b_gate'], 'L0_ffn_W_up': _L0_ffn_in['W_up'], 'L0_ffn_b_up': _L0_ffn_in['b_up'], 'L0_ffn_W_out': _L0_ffn_in['W_out'], 'L0_ffn_b_out': _L0_ffn_in['b_out'], 'L0_c': _L0_c, 'L0_wmod': _L0_wmod, 'L1_attn_Wq': _L1_attn_in['Wq'], 'L1_attn_Wkv': _L1_attn_in['Wkv'], 'L1_attn_Wo': _L1_attn_in['Wo'], 'L1_ffn_wqkv': _L1_ffn_in['wqkv'], 'L1_ffn_q_scale': _L1_ffn_in['q_scale'], 'L1_ffn_k_scale': _L1_ffn_in['k_scale'], 'L1_ffn_wo': _L1_ffn_in['wo'], 'L1_ffn_ln_g': _L1_ffn_in['ln_g'], 'L1_ffn_ln_b': _L1_ffn_in['ln_b'], 'L1_ffn_w1': _L1_ffn_in['w1'], 'L1_ffn_b1': _L1_ffn_in['b1'], 'L1_ffn_w2': _L1_ffn_in['w2'], 'L1_ffn_b2': _L1_ffn_in['b2'], 'L1_c': _L1_c, 'L1_wmod': _L1_wmod, 'L2_attn_W_Q': _L2_attn_in['W_Q'], 'L2_attn_W_K': _L2_attn_in['W_K'], 'L2_attn_W_V': _L2_attn_in['W_V'], 'L2_attn_W_O': _L2_attn_in['W_O'], 'L2_ffn_Wg': _L2_ffn_in['Wg'], 'L2_ffn_Wu': _L2_ffn_in['Wu'], 'L2_ffn_Wd': _L2_ffn_in['Wd'], 'L2_c': _L2_c, 'L2_wmod': _L2_wmod, 'L3_attn_Wqkv': _L3_attn_in['Wqkv'], 'L3_attn_bqkv': _L3_attn_in['bqkv'], 'L3_attn_Wln': _L3_attn_in['Wln'], 'L3_attn_bln': _L3_attn_in['bln'], 'L3_ffn_router_w': _L3_ffn_in['router_w'], 'L3_ffn_w1': _L3_ffn_in['w1'], 'L3_ffn_b1': _L3_ffn_in['b1'], 'L3_ffn_w2': _L3_ffn_in['w2'], 'L3_ffn_b2': _L3_ffn_in['b2'], 'L3_c': _L3_c, 'L3_wmod': _L3_wmod}
    _x0 = _d['L0_attn_u']
    _d['L0_attn_u'] = jax.random.normal(jax.random.fold_in(jax.random.key(seed), 1), (2, 1024, 128), dtype=_x0.dtype)
    del _x0
    return _d

def reference(L0_attn_u, L0_attn_W_in, L0_attn_conv_w, L0_attn_conv_b, L0_attn_dt_bias, L0_attn_A_log, L0_attn_D, L0_attn_norm_w, L0_attn_W_out, L0_ffn_W_router, L0_ffn_W_gate, L0_ffn_b_gate, L0_ffn_W_up, L0_ffn_b_up, L0_ffn_W_out, L0_ffn_b_out, L0_c, L0_wmod, L1_attn_Wq, L1_attn_Wkv, L1_attn_Wo, L1_ffn_wqkv, L1_ffn_q_scale, L1_ffn_k_scale, L1_ffn_wo, L1_ffn_ln_g, L1_ffn_ln_b, L1_ffn_w1, L1_ffn_b1, L1_ffn_w2, L1_ffn_b2, L1_c, L1_wmod, L2_attn_W_Q, L2_attn_W_K, L2_attn_W_V, L2_attn_W_O, L2_ffn_Wg, L2_ffn_Wu, L2_ffn_Wd, L2_c, L2_wmod, L3_attn_Wqkv, L3_attn_bqkv, L3_attn_Wln, L3_attn_bln, L3_ffn_router_w, L3_ffn_w1, L3_ffn_b1, L3_ffn_w2, L3_ffn_b2, L3_c, L3_wmod):

    def _L0_attn_ref(u, W_in, conv_w, conv_b, dt_bias, A_log, D, norm_w, W_out):
        import jax, jax.numpy as jnp
        import numpy as np
        D_MODEL = 128
        D_STATE = 128
        HEADDIM = 64
        EXPAND = 2
        CHUNK = 64
        D_CONV = 4
        D_INNER = EXPAND * D_MODEL
        NHEADS = D_INNER // HEADDIM
        D_IN_PROJ = 2 * D_INNER + 2 * D_STATE + NHEADS
        CONV_CH = D_INNER + 2 * D_STATE
        EPS = 1e-05

        def segsum(x):
            T = x.shape[-1]
            m1 = jnp.tril(jnp.ones((T, T), bool), -1)
            xr = jnp.where(m1, x[..., :, None], 0.0)
            s = jnp.cumsum(xr, axis=-2)
            m0 = jnp.tril(jnp.ones((T, T), bool), 0)
            return jnp.where(m0, s, -jnp.inf)

        def ssd(x, A, B, C, chunk):
            b, L, h, p = x.shape
            c = L // chunk
            x = x.reshape(b, c, chunk, h, p)
            A = A.reshape(b, c, chunk, h).transpose(0, 3, 1, 2)
            B = B.reshape(b, c, chunk, -1)
            C = C.reshape(b, c, chunk, -1)
            A_cum = jnp.cumsum(A, axis=-1)
            Lm = jnp.exp(segsum(A))
            Y_diag = jnp.einsum('bcln,bcsn,bhcls,bcshp->bclhp', C, B, Lm, x)
            decay_states = jnp.exp(A_cum[:, :, :, -1:] - A_cum)
            states = jnp.einsum('bcln,bhcl,bclhp->bchpn', B, decay_states, x)
            init = jnp.zeros_like(states[:, :1])
            states = jnp.concatenate([init, states], axis=1)
            Ac_last = jnp.pad(A_cum[:, :, :, -1], ((0, 0), (0, 0), (1, 0)))
            decay_chunk = jnp.exp(segsum(Ac_last))
            new_states = jnp.einsum('bhzc,bchpn->bzhpn', decay_chunk, states)
            states = new_states[:, :-1]
            sdo = jnp.exp(A_cum)
            Y_off = jnp.einsum('bcln,bchpn,bhcl->bclhp', C, states, sdo)
            return (Y_diag + Y_off).reshape(b, L, h, p)
        b, L, _ = u.shape
        zxbcdt = u @ W_in
        z = zxbcdt[..., :D_INNER]
        xBC = zxbcdt[..., D_INNER:D_INNER + CONV_CH]
        dt = jax.nn.softplus(zxbcdt[..., -NHEADS:] + dt_bias)
        xc = jnp.pad(xBC.transpose(0, 2, 1), ((0, 0), (0, 0), (D_CONV - 1, 0)))
        xc = jax.lax.conv_general_dilated(xc, conv_w[:, None, :], (1,), 'VALID', feature_group_count=CONV_CH, dimension_numbers=('NCH', 'OIH', 'NCH')) + conv_b[None, :, None]
        xBC = jax.nn.silu(xc.transpose(0, 2, 1))
        x = xBC[..., :D_INNER].reshape(b, L, NHEADS, HEADDIM)
        B = xBC[..., D_INNER:D_INNER + D_STATE]
        C = xBC[..., D_INNER + D_STATE:]
        A = -jnp.exp(A_log)
        y = ssd(x * dt[..., None], A * dt, B, C, CHUNK)
        y = y + x * D[:, None]
        y = y.reshape(b, L, D_INNER)
        y = y * jax.nn.silu(z)
        y = y * jax.lax.rsqrt(jnp.mean(y * y, axis=-1, keepdims=True) + EPS) * norm_w
        return y @ W_out

    def _L0_ffn_ref(residual, W_router, W_gate, b_gate, W_up, b_up, W_out, b_out):
        import jax, jax.numpy as jnp
        import numpy as np
        B, S, D = (2, 256, 128)
        M = 256
        E = 8
        TOP_K = 2
        router_logits = jnp.einsum('bsd,de->bse', residual, W_router)
        router_probs = jax.nn.softmax(router_logits, axis=-1)
        top_k_probs, top_k_idx = jax.lax.top_k(router_probs, TOP_K)
        top_k_probs = top_k_probs / (jnp.sum(top_k_probs, -1, keepdims=True) + 1e-08)
        one_hot = jax.nn.one_hot(top_k_idx, E, dtype=residual.dtype)
        expert_weights = jnp.einsum('bsk,bske->bse', top_k_probs, one_hot)
        gate = jax.nn.silu(jnp.einsum('bsd,edm->ebsm', residual, W_gate) + b_gate[:, None, None, :])
        up = jnp.einsum('bsd,edm->ebsm', residual, W_up) + b_up[:, None, None, :]
        hidden = gate * up
        expert_out = jnp.einsum('ebsm,emd->ebsd', hidden, W_out) + b_out[:, None, None, :]
        output = jnp.einsum('bse,ebsd->bsd', expert_weights, expert_out)
        return output

    def _L1_attn_ref(h, Wq, Wkv, Wo):
        import jax, jax.numpy as jnp
        import numpy as np
        N_HEAD = 16
        D_HEAD = 64
        D_MODEL = 128
        SEQ = 256
        BATCH = 2
        L, B, _ = h.shape
        scale = 1.0 / np.sqrt(D_HEAD).astype(np.float32)
        q = (h @ Wq).reshape(L, B, N_HEAD, D_HEAD)
        k, v = jnp.split(h @ Wkv, 2, axis=-1)
        k = k.reshape(L, B, N_HEAD, D_HEAD)
        v = v.reshape(L, B, N_HEAD, D_HEAD)
        score = jnp.einsum('ibnd,jbnd->ijbn', q, k) * scale
        prob = jax.nn.softmax(score, axis=1)
        vec = jnp.einsum('ijbn,jbnd->ibnd', prob, v).reshape(L, B, N_HEAD * D_HEAD)
        return vec @ Wo

    def _L1_ffn_ref(x, wqkv, q_scale, k_scale, wo, ln_g, ln_b, w1, b1, w2, b2):
        import jax, jax.numpy as jnp
        import numpy as np
        DIM = 128
        DEPTH = 2
        HEADS = 8
        DIM_HEAD = 64
        WINDOW = 64
        INNER = HEADS * DIM_HEAD
        HID = int(DIM * 4 * 2 / 3)
        B, N = (2, 1024)
        QK_SCALE = 8.0

        def shift_token(t):
            t1, t2 = jnp.split(t, 2, axis=-1)
            t2 = jnp.pad(t2, ((0, 0), (1, 0), (0, 0)))[:, :-1]
            return jnp.concatenate([t1, t2], axis=-1)

        def l2norm(t):
            return t / jnp.clip(jnp.linalg.norm(t, axis=-1, keepdims=True), 1e-12)

        def rotate_half(x):
            x1, x2 = jnp.split(x, 2, axis=-1)
            return jnp.concatenate([-x2, x1], axis=-1)

        def rotary_xpos(q, k):
            n = q.shape[-2]
            half_idx = jnp.arange(0, DIM_HEAD, 2, dtype=jnp.float32)
            inv_freq = 1.0 / 10000.0 ** (half_idx / DIM_HEAD)
            t = jnp.arange(n, dtype=jnp.float32)
            freqs = t[:, None] * inv_freq[None, :]
            freqs = jnp.concatenate([freqs, freqs], axis=-1)
            base = (half_idx + 0.4 * DIM_HEAD) / (1.4 * DIM_HEAD)
            power = (t - n // 2) / float(WINDOW // 2)
            scale = base[None, :] ** power[:, None]
            scale = jnp.concatenate([scale, scale], axis=-1)
            cos, sin = (jnp.cos(freqs), jnp.sin(freqs))
            q = q * cos * scale + rotate_half(q) * sin * scale
            k = k * cos / scale + rotate_half(k) * sin / scale
            return (q, k)

        def local_attention(q, k, v):
            b, h, n, d = q.shape
            w = n // WINDOW
            bq = q.reshape(b, h, w, WINDOW, d) * QK_SCALE
            bk = k.reshape(b, h, w, WINDOW, d)
            bv = v.reshape(b, h, w, WINDOW, d)

            def look_around(t):
                p = jnp.pad(t, ((0, 0), (0, 0), (1, 0), (0, 0), (0, 0)))
                return jnp.concatenate([p[:, :, :w], p[:, :, 1:]], axis=3)
            bk, bv = (look_around(bk), look_around(bv))
            bt = jnp.arange(n).reshape(w, WINDOW)
            btp = jnp.pad(bt, ((1, 0), (0, 0)), constant_values=-1)
            btk = jnp.concatenate([btp[:w], btp[1:]], axis=1)
            sim = jnp.einsum('bhwid,bhwjd->bhwij', bq, bk)
            i = bt[:, :, None]
            j = btk[:, None, :]
            mask = (i < j) | (i > j + WINDOW) | (j == -1)
            sim = jnp.where(mask, -jnp.finfo(sim.dtype).max, sim)
            attn = jax.nn.softmax(sim, axis=-1)
            out = jnp.einsum('bhwij,bhwjd->bhwid', attn, bv)
            return out.reshape(b, h, n, d)

        def _layer(x, wqkv, qs, ksc, wo, lg, lb, w1, b1, w2, b2):
            b, n, _ = x.shape
            h = shift_token(x)
            qkv = h @ wqkv
            q, k, v = jnp.split(qkv, 3, axis=-1)
            to_heads = lambda t: t.reshape(b, n, HEADS, DIM_HEAD).transpose(0, 2, 1, 3)
            q, k, v = (to_heads(q), to_heads(k), to_heads(v))
            q = l2norm(q) * qs
            k = l2norm(k) * ksc
            q, k = rotary_xpos(q, k)
            o = local_attention(q, k, v)
            o = o.transpose(0, 2, 1, 3).reshape(b, n, INNER)
            x = x + o @ wo
            h = shift_token(x)
            mu = h.mean(-1, keepdims=True)
            var = h.var(-1, keepdims=True)
            h = (h - mu) / jnp.sqrt(var + 1e-05) * lg + lb
            h = h @ w1 + b1
            a, g = jnp.split(h, 2, axis=-1)
            h = a * jax.nn.gelu(g, approximate=False)
            x = x + h @ w2 + b2
            return x
        for l in range(DEPTH):
            x = _layer(x, wqkv[l], q_scale[l], k_scale[l], wo[l], ln_g[l], ln_b[l], w1[l], b1[l], w2[l], b2[l])
        return x

    def _L2_attn_ref(x, W_Q, W_K, W_V, W_O):
        import jax, jax.numpy as jnp
        import numpy as np
        D_MODEL = 128
        NUM_HEADS = 16
        B, S = (1, 512)
        Bx, Sx, Dm = x.shape
        H = NUM_HEADS
        d_attn = Dm // H
        Q = x @ W_Q.T
        K = x @ W_K.T
        V = x @ W_V.T
        Q = Q.reshape(Bx, Sx, H, d_attn).transpose(0, 2, 1, 3)
        K = K.reshape(Bx, Sx, H, d_attn).transpose(0, 2, 1, 3)
        V = V.reshape(Bx, Sx, H, d_attn).transpose(0, 2, 1, 3)
        scale = 1.0 / jnp.sqrt(jnp.asarray(d_attn, dtype=x.dtype))
        attn = jnp.einsum('bhqd,bhkd->bhqk', Q, K) * scale
        causal = jnp.tril(jnp.ones((Sx, Sx), dtype=bool))
        attn = jnp.where(causal, attn, jnp.asarray(-jnp.inf, dtype=attn.dtype))
        probs = jax.nn.softmax(attn, axis=-1)
        y = jnp.einsum('bhqk,bhkd->bhqd', probs, V)
        y = y.transpose(0, 2, 1, 3).reshape(Bx, Sx, Dm)
        return y @ W_O.T

    def _L2_ffn_ref(hidden_states, Wg, Wu, Wd):
        import jax, jax.numpy as jnp
        import numpy as np
        NUM_EXPERTS = 8
        HIDDEN = 128
        FFN = 512
        BATCH = 2
        SEQ = 256
        B, S, H = hidden_states.shape
        x = hidden_states.reshape(-1, H)

        def expert_step(acc, w):
            wg, wu, wd = w
            h = jax.nn.silu(x @ wg) * (x @ wu)
            return (acc + h @ wd, None)
        acc, _ = jax.lax.scan(expert_step, jnp.zeros_like(x), (Wg, Wu, Wd))
        return acc.reshape(B, S, H)

    def _L3_attn_ref(x, Wqkv, bqkv, Wln, bln):
        import math
        import jax, jax.numpy as jnp
        import numpy as np
        EPS_SUM = 1e-07
        EPS_NORM = 1e-12

        def _l2norm(x, axis):
            n = jnp.sqrt(jnp.sum(x * x, axis=axis, keepdims=True))
            return x / jnp.maximum(n, EPS_NORM)
        b, N, C = x.shape
        qkv = x @ Wqkv + bqkv
        q, k, v = jnp.split(qkv, 3, axis=2)
        q = q - q.mean(axis=2, keepdims=True)
        k = k - k.mean(axis=2, keepdims=True)
        q2 = q * q
        k2 = k * k
        q2 = q2 / (q2.sum(axis=2, keepdims=True) + EPS_SUM)
        q2 = _l2norm(q2, axis=-1)
        k2 = k2 / (k2.sum(axis=2, keepdims=True) + EPS_SUM)
        k2 = _l2norm(k2, axis=-2)
        kv = jnp.einsum('bnc,bnd->bcd', k2, v)
        t2 = jnp.einsum('bnc,bcd->bnd', q2, kv) / math.sqrt(N)
        return (v + t2) @ Wln + bln

    def _L3_ffn_ref(hidden_states, router_w, w1, b1, w2, b2):
        import jax, jax.numpy as jnp
        import numpy as np
        TOP_K = 2
        x = hidden_states
        router_logits = jnp.einsum('bth,eh->bte', x, router_w)
        topk_values, topk_indices = jax.lax.top_k(router_logits, TOP_K)
        topk_weights = jax.nn.softmax(topk_values.astype(jnp.float32), axis=-1).astype(x.dtype)
        h1 = jnp.einsum('bth,efh->btef', x, w1) + b1
        h1 = jax.nn.gelu(h1, approximate=False)
        expert_outputs = jnp.einsum('btef,ehf->bteh', h1, w2) + b2
        gather_idx = topk_indices[..., None]
        topk_expert_outputs = jnp.take_along_axis(expert_outputs, gather_idx, axis=2)
        mixed_output = jnp.sum(topk_expert_outputs * topk_weights[..., None], axis=2)
        return mixed_output
    x = L0_attn_u
    mod = (_silu(L0_c) @ L0_wmod).reshape(L0_c.shape[0], 6, 1, -1)
    sa, ca, ga, sb, cb, gb = (mod[:, 0], mod[:, 1], mod[:, 2], mod[:, 3], mod[:, 4], mod[:, 5])
    ga = (2 * (ga >= 0) - 1) * jnp.maximum(jnp.abs(ga), 0.25)
    gb = (2 * (gb >= 0) - 1) * jnp.maximum(jnp.abs(gb), 0.25)
    h = _layernorm(x, axis=-1) * (1 + ca) + sa
    x = x + ga * _L0_attn_ref(h, L0_attn_W_in, L0_attn_conv_w, L0_attn_conv_b, L0_attn_dt_bias, L0_attn_A_log, L0_attn_D, L0_attn_norm_w, L0_attn_W_out)
    h = _layernorm(x, axis=-1) * (1 + cb) + sb
    x = x + gb * _L0_ffn_ref(h, L0_ffn_W_router, L0_ffn_W_gate, L0_ffn_b_gate, L0_ffn_W_up, L0_ffn_b_up, L0_ffn_W_out, L0_ffn_b_out)
    mod = (_silu(L1_c) @ L1_wmod).reshape(L1_c.shape[0], 6, 1, -1)
    sa, ca, ga, sb, cb, gb = (mod[:, 0], mod[:, 1], mod[:, 2], mod[:, 3], mod[:, 4], mod[:, 5])
    ga = (2 * (ga >= 0) - 1) * jnp.maximum(jnp.abs(ga), 0.25)
    gb = (2 * (gb >= 0) - 1) * jnp.maximum(jnp.abs(gb), 0.25)
    h = _layernorm(x, axis=-1) * (1 + ca) + sa
    x = x + ga * _L1_attn_ref(h, L1_attn_Wq, L1_attn_Wkv, L1_attn_Wo)
    h = _layernorm(x, axis=-1) * (1 + cb) + sb
    x = x + gb * _L1_ffn_ref(h, L1_ffn_wqkv, L1_ffn_q_scale, L1_ffn_k_scale, L1_ffn_wo, L1_ffn_ln_g, L1_ffn_ln_b, L1_ffn_w1, L1_ffn_b1, L1_ffn_w2, L1_ffn_b2)
    mod = (_silu(L2_c) @ L2_wmod).reshape(L2_c.shape[0], 6, 1, -1)
    sa, ca, ga, sb, cb, gb = (mod[:, 0], mod[:, 1], mod[:, 2], mod[:, 3], mod[:, 4], mod[:, 5])
    ga = (2 * (ga >= 0) - 1) * jnp.maximum(jnp.abs(ga), 0.25)
    gb = (2 * (gb >= 0) - 1) * jnp.maximum(jnp.abs(gb), 0.25)
    h = _layernorm(x, axis=-1) * (1 + ca) + sa
    x = x + ga * _L2_attn_ref(h, L2_attn_W_Q, L2_attn_W_K, L2_attn_W_V, L2_attn_W_O)
    h = _layernorm(x, axis=-1) * (1 + cb) + sb
    x = x + gb * _L2_ffn_ref(h, L2_ffn_Wg, L2_ffn_Wu, L2_ffn_Wd)
    mod = (_silu(L3_c) @ L3_wmod).reshape(L3_c.shape[0], 6, 1, -1)
    sa, ca, ga, sb, cb, gb = (mod[:, 0], mod[:, 1], mod[:, 2], mod[:, 3], mod[:, 4], mod[:, 5])
    ga = (2 * (ga >= 0) - 1) * jnp.maximum(jnp.abs(ga), 0.25)
    gb = (2 * (gb >= 0) - 1) * jnp.maximum(jnp.abs(gb), 0.25)
    h = _layernorm(x, axis=-1) * (1 + ca) + sa
    x = x + ga * _L3_attn_ref(h, L3_attn_Wqkv, L3_attn_bqkv, L3_attn_Wln, L3_attn_bln)
    h = _layernorm(x, axis=-1) * (1 + cb) + sb
    x = x + gb * _L3_ffn_ref(h, L3_ffn_router_w, L3_ffn_w1, L3_ffn_b1, L3_ffn_w2, L3_ffn_b2)
    return x

_drawn_inputs = setup_inputs


def setup_inputs(seed=0):
    import zlib

    import numpy as np

    out = dict(_drawn_inputs(seed))
    spreads = {'L0_attn_norm_w': (1.0, 0.6),
     'L0_ffn_b_gate': (0.0, 0.8),
     'L0_ffn_b_up': (0.0, 0.8),
     'L0_ffn_b_out': (0.0, 0.368),
     'L1_ffn_q_scale': (1.0, 0.6),
     'L1_ffn_k_scale': (1.0, 0.6),
     'L1_ffn_ln_g': (1.0, 0.6),
     'L1_ffn_ln_b': (0.0, 0.8),
     'L1_ffn_b1': (0.0, 0.8),
     'L1_ffn_b2': (0.0, 0.8)}
    factors = {'L0_attn_dt_bias': 8.0,
     'L0_attn_A_log': 23.211,
     'L0_ffn_W_router': 3.193,
     'L0_ffn_W_gate': 8.0,
     'L0_ffn_W_up': 8.0,
     'L0_ffn_W_out': 8.0,
     'L1_ffn_wqkv': 8.0,
     'L1_ffn_wo': 7.992,
     'L1_ffn_w1': 8.0,
     'L1_ffn_w2': 8.0,
     'L3_attn_bqkv': 44.368,
     'L3_attn_bln': 64.0,
     'L3_ffn_router_w': 8.0,
     'L3_ffn_w1': 7.734,
     'L3_ffn_b1': 64.0,
     'L3_ffn_w2': 7.578,
     'L3_ffn_b2': 64.0,
     'L2_attn_W_Q': 8.0,
     'L2_attn_W_K': 8.0,
     'L2_attn_W_V': 6.359,
     'L2_attn_W_O': 6.073,
     'L2_ffn_Wg': 3.015,
     'L2_ffn_Wu': 2.892,
     'L2_ffn_Wd': 2.741}
    for name, (base, spread) in spreads.items():
        noise = np.random.default_rng([zlib.crc32(name.encode()), seed]).standard_normal(out[name].shape)
        drawn = base * np.exp(spread * noise) if base else spread * noise
        out[name] = jnp.asarray(drawn.astype(out[name].dtype))
    for name, factor in factors.items():
        out[name] = (out[name] * factor).astype(out[name].dtype)
    return out
```

```python
from contextlib import ExitStack

import numpy as np

import concourse.bass as bass
from concourse import mybir

ALU = mybir.AluOpType
ACT = mybir.ActivationFunctionType
F32 = mybir.dt.float32
BF16 = mybir.dt.bfloat16
U32 = mybir.dt.uint32
HOST16 = mybir.dt.np(BF16)
AX = mybir.AxisListType.X

P = 128
NB = 2
SEQ = 1024
T = NB * SEQ
CH = 512
NCH = T // CH
NT = T // P
EPS = 1e-5
NEG = -1e30

SHIFT_A, SCALE_A, GATE_A, SHIFT_B, SCALE_B, GATE_B = range(6)



class Kit:
    pass


def chunk(c):
    return slice(c * CH, (c + 1) * CH)


def tile(t):
    return slice(t * P, (t + 1) * P)


def batch_of(c):
    return c * CH // SEQ


def modulation_stage(nc, k):
    with ExitStack() as ctx:
        c_sb = ctx.enter_context(nc.sbuf_tensor("c_sb", [P, 4 * NB], F32))
        w_sb = ctx.enter_context(nc.sbuf_tensor("wmod_sb", [P, 4, 6 * P], F32))
        sign = ctx.enter_context(nc.sbuf_tensor("gate_sign", [P, 4, 6, NB], F32))
        size = ctx.enter_context(nc.sbuf_tensor("gate_size", [P, 4, 6, NB], F32))
        ps = ctx.enter_context(nc.psum_tensor("mod_ps", [P, 4, 6, NB], F32))
        c_loaded = nc.alloc_semaphore("c_loaded")
        wmod_loaded = nc.alloc_semaphore("wmod_loaded")
        silu_ready = nc.alloc_semaphore("silu_c_ready")
        mod_ps_ready = nc.alloc_semaphore("mod_ps_ready")
        mod_steps = nc.alloc_semaphore("mod_steps")
        block = ctx.enter_context(nc.Block())

        @block.sync
        def _(sp):
            sp.dma_start(c_sb[:], k.dram["cT"]).then_inc(c_loaded, 16)
            sp.dma_start(w_sb[:], k.dram["wmod"]).then_inc(wmod_loaded, 16)
            sp.dma_start(k.x[:], k.dram["xT"]).then_inc(k.first_loaded, 16)
            for name in FIRST:
                sp.dma_start(k.w[name][:], k.dram[name]).then_inc(k.first_loaded, 16)
            sp.wait_ge(k.first_loaded, 16 * (1 + len(FIRST)))

        @block.scalar
        def _(act):
            act.wait_ge(c_loaded, 16)
            nc.scalar.activation(c_sb[:], c_sb[:], ACT.Silu).then_inc(silu_ready, 1)

        @block.tensor
        def _(pe):
            pe.wait_ge(wmod_loaded, 16)
            pe.wait_ge(silu_ready, 1)
            for layer in range(4):
                for j in range(6):
                    last = nc.tensor.matmul(ps[:, layer, j, :], w_sb[:, layer, tile(j)],
                                            c_sb[:, NB * layer:NB * layer + NB], start=True, stop=True)
            last.then_inc(mod_ps_ready, 1)

        @block.vector
        def _(dve):
            dve.wait_ge(mod_ps_ready, 1)
            nc.vector.tensor_copy(k.mod[:], ps[:]).then_inc(mod_steps, 1)
            dve.wait_ge(mod_steps, 1)
            nc.vector.tensor_scalar(sign[:], k.mod[:], 0.0, 2.0, ALU.is_ge, ALU.mult).then_inc(mod_steps, 1)
            nc.vector.scalar_tensor_tensor(out=size[:], in0=k.mod[:], scalar=-1.0, in1=k.mod[:], op0=ALU.mult,
                                           op1=ALU.max).then_inc(mod_steps, 1)
            dve.wait_ge(mod_steps, 3)
            nc.vector.tensor_scalar(size[:], size[:], 0.25, None, ALU.max).then_inc(mod_steps, 1)
            for j in (SCALE_A, SCALE_B):
                nc.vector.tensor_scalar(k.mod[:, :, j], k.mod[:, :, j], 1.0, None, ALU.add).then_inc(mod_steps, 1)
            dve.wait_ge(mod_steps, 6)
            for j in (GATE_A, GATE_B):
                nc.vector.scalar_tensor_tensor(out=k.mod[:, :, j], in0=sign[:, :, j], scalar=-1.0,
                                               in1=size[:, :, j], op0=ALU.add, op1=ALU.mult).then_inc(mod_steps, 1)
            dve.wait_ge(mod_steps, 8)


def adaln_stage(nc, k, layer, scale_at, shift_at, weights):
    layernorm_stage(nc, k, f"{layer}{scale_at}", k.x, k.h,
                    lambda b: (k.mod[:, layer, scale_at, b:b + 1], k.mod[:, layer, shift_at, b:b + 1]), weights)


def layernorm_stage(nc, k, name, src, dst, affine, weights=()):
    tag = f"_ln{name}"
    with ExitStack() as ctx:
        xc = ctx.enter_context(nc.sbuf_tensor("xc" + tag, [P, T], F32))
        sq = ctx.enter_context(nc.sbuf_tensor("sq" + tag, [P, 2, CH], F32))
        std = ctx.enter_context(nc.sbuf_tensor("std" + tag, [P, 2, CH], F32))
        rstd = ctx.enter_context(nc.sbuf_tensor("rstd" + tag, [P, 2, CH], F32))
        mean_ps = ctx.enter_context(nc.psum_tensor("mean_ps" + tag, [P, 2, CH], F32))
        var_ps = ctx.enter_context(nc.psum_tensor("var_ps" + tag, [P, 2, CH], F32))
        sem = lambda name: nc.alloc_semaphore(name + tag)
        mean_ready, centered, squared, var_ready = sem("mean"), sem("centered"), sem("squared"), sem("var")
        std_ready, rstd_ready, normed, h_ready, loaded = sem("std"), sem("rstd"), sem("normed"), sem("h"), sem("loaded")
        block = ctx.enter_context(nc.Block())

        @block.sync
        def _(sp):
            for w in weights:
                sp.dma_start(k.w[w][:], k.dram[w]).then_inc(loaded, 16)
            if weights:
                sp.wait_ge(loaded, 16 * len(weights))

        @block.tensor
        def _(pe):
            for c in range(NCH + 1):
                if c < NCH:
                    if c >= 2:
                        pe.wait_ge(centered, c - 1)
                    nc.tensor.matmul(mean_ps[:, c % 2], k.w["mean_w"][:], src[:, chunk(c)],
                                     start=True, stop=True).then_inc(mean_ready, 1)
                if c >= 1:
                    pe.wait_ge(squared, c)
                    if c >= 3:
                        pe.wait_ge(std_ready, c - 2)
                    nc.tensor.matmul(var_ps[:, (c - 1) % 2], k.w["mean_w"][:], sq[:, (c - 1) % 2],
                                     start=True, stop=True).then_inc(var_ready, 1)

        @block.scalar
        def _(act):
            for c in range(NCH + 1):
                if c < NCH:
                    act.wait_ge(centered, c + 1)
                    if c >= 2:
                        act.wait_ge(var_ready, c - 1)
                    nc.scalar.activation(sq[:, c % 2], xc[:, chunk(c)], ACT.Square).then_inc(squared, 1)
                if c >= 1:
                    act.wait_ge(var_ready, c)
                    if c >= 3:
                        act.wait_ge(rstd_ready, c - 2)
                    nc.scalar.activation(std[:, (c - 1) % 2], var_ps[:, (c - 1) % 2], ACT.Sqrt,
                                         bias=k.w["eps"][:, 0:1]).then_inc(std_ready, 1)

        @block.vector
        def _(dve):
            for c in range(NCH + 1):
                if c < NCH:
                    dve.wait_ge(mean_ready, c + 1)
                    nc.vector.tensor_tensor(xc[:, chunk(c)], src[:, chunk(c)], mean_ps[:, c % 2],
                                            ALU.subtract).then_inc(centered, 1)
                if c >= 1:
                    e, b = c - 1, batch_of(c - 1)
                    dve.wait_ge(std_ready, e + 1)
                    if e >= 2:
                        dve.wait_ge(normed, e - 1)
                    nc.vector.reciprocal(rstd[:, e % 2], std[:, e % 2]).then_inc(rstd_ready, 1)
                    dve.wait_ge(rstd_ready, e + 1)
                    nc.vector.tensor_tensor(dst[:, chunk(e)], xc[:, chunk(e)], rstd[:, e % 2],
                                            ALU.mult).then_inc(normed, 1)
                    dve.wait_ge(normed, e + 1)
                    nc.vector.tensor_scalar(dst[:, chunk(e)], dst[:, chunk(e)], *affine(b), ALU.mult, ALU.add).then_inc(h_ready, 1)


def half_layer(layer, half, weights, body):
    def stages(nc, k):
        with nc.cleanup_on_exit(), ExitStack() as ctx:
            for name in weights:
                d = k.dram[name]
                k.w[name] = ctx.enter_context(nc.sbuf_tensor(f"{name}_{layer}{half}", list(d.shape), d.dtype))
            at = (SCALE_A, SHIFT_A) if half == 0 else (SCALE_B, SHIFT_B)
            adaln_stage(nc, k, layer, *at, weights)
            body(nc, k)
    return stages


D_CONV = 4
HEADS0 = 4
HD0 = 64
NG = SEQ // P


def mamba_project_stage(nc, k, s):
    with ExitStack() as ctx:
        raw = ctx.enter_context(nc.sbuf_tensor("raw_xbc", [P, 2, NB, SEQ + D_CONV - 1], F32))
        conv = ctx.enter_context(nc.sbuf_tensor("conv_acc", [P, 2, NB, SEQ], F32))
        ps = ctx.enter_context(nc.psum_tensor("proj_ps", [P, 4, CH], F32))
        dt_ps = ctx.enter_context(nc.psum_tensor("dt_ps", [P, NT, HEADS0], F32))
        tmp = ctx.enter_context(nc.sbuf_tensor("dt_tmp", [P, 8, NT * HEADS0], F32))
        sem = lambda name: nc.alloc_semaphore(name + "_mp")
        proj_ready, evacuated, dt_ready, pads_ready = sem("proj"), sem("evacuated"), sem("dt_ps"), sem("pads")
        conv_step, conv_ready, silu_ready, dt_step, dt_act = (
            sem("conv_step"), sem("conv"), sem("silu"), sem("dt_step"), sem("dt_act"))
        win, cw = k.w["L0_W_in"], k.w["L0_conv"]
        block = ctx.enter_context(nc.Block())
        bank = lambda m, c: (m * NCH + c) % 4

        @block.tensor
        def _(pe):
            for t in range(NT):
                last = nc.tensor.matmul(dt_ps[:, t], k.h[:, tile(t)], win[:, 6 * P:6 * P + HEADS0],
                                        start=True, stop=True)
            last.then_inc(dt_ready, 1)
            for i, m in enumerate((2, 3, 4, 5, 0, 1)):
                for c in range(NCH):
                    n = i * NCH + c
                    if n >= 4:
                        pe.wait_ge(evacuated, n - 3)
                    nc.tensor.matmul(ps[:, n % 4], win[:, tile(m)], k.h[:, chunk(c)],
                                     start=True, stop=True).then_inc(proj_ready, 1)

        @block.scalar
        def _(act):
            act.wait_ge(pads_ready, 1)
            for i in range(6):
                if 2 <= i < 4:
                    act.wait_ge(conv_ready, i - 1)
                for c in range(NCH):
                    n = i * NCH + c
                    act.wait_ge(proj_ready, n + 1)
                    if i < 4:
                        b, at = batch_of(c), c * CH % SEQ
                        out, func = raw[:, i % 2, b, D_CONV - 1 + at:D_CONV - 1 + at + CH], ACT.Copy
                    else:
                        out, func = s.zg[:, i - 4, chunk(c)], ACT.Silu
                    nc.scalar.activation(out, ps[:, n % 4], func).then_inc(evacuated, 1)
            for i in range(4):
                act.wait_ge(conv_ready, i + 1)
                nc.scalar.activation(s.xbc[:, i].rearrange("p (b n) -> p b n", b=NB), s.conv_out[:, i],
                                     ACT.Silu).then_inc(silu_ready, 1)
            act.wait_ge(dt_step, 3)
            nc.scalar.activation(tmp[:, 2], tmp[:, 1], ACT.Exp, scale=-1.0).then_inc(dt_act, 1)
            nc.scalar.activation(s.decay_rate[:], k.w["L0_heads"][:, HEADS0:2 * HEADS0], ACT.Exp).then_inc(dt_act, 1)
            act.wait_ge(dt_act, 1)
            nc.scalar.activation(tmp[:, 3], tmp[:, 2], ACT.Ln, bias=1.0).then_inc(dt_act, 1)

        @block.vector
        def _(dve):
            nc.vector.memset(raw[:, :, :, 0:D_CONV - 1], 0.0).then_inc(pads_ready, 1)
            dve.wait_ge(dt_ready, 1)
            steps = [0]
            flat = dt_ps[:].rearrange("p t h -> p (t h)")
            bias = k.w["L0_heads"][:, 0:HEADS0].unsqueeze(1).to_broadcast([P, NT, HEADS0])
            nc.vector.tensor_tensor(tmp[:, 0].rearrange("p (t h) -> p t h", h=HEADS0), dt_ps[:], bias,
                                    ALU.add).then_inc(dt_step, 1)
            dve.wait_ge(dt_step, 1)
            nc.vector.scalar_tensor_tensor(out=tmp[:, 1], in0=tmp[:, 0], scalar=-1.0, in1=tmp[:, 0], op0=ALU.mult,
                                           op1=ALU.max).then_inc(dt_step, 1)
            dve.wait_ge(dt_step, 2)
            nc.vector.tensor_scalar(tmp[:, 0], tmp[:, 0], 0.0, None, ALU.max).then_inc(dt_step, 1)
            for i in range(4):
                if i >= 1:
                    dve.wait_ge(conv_ready, i)
                dve.wait_ge(evacuated, NCH * (i + 1))
                tap = lambda j: raw[:, i % 2, :, j:j + SEQ]
                nc.vector.tensor_scalar(conv[:, 0], tap(0), cw[:, i, 0:1], cw[:, i, D_CONV:D_CONV + 1],
                                        ALU.mult, ALU.add).then_inc(conv_step, 1)
                for j in range(1, D_CONV):
                    dve.wait_ge(conv_step, (D_CONV - 1) * i + j)
                    out = conv[:, j % 2] if j < D_CONV - 1 else s.conv_out[:, i]
                    nc.vector.scalar_tensor_tensor(out=out, in0=tap(j), scalar=cw[:, i, j:j + 1],
                                                   in1=conv[:, (j - 1) % 2], op0=ALU.mult,
                                                   op1=ALU.add).then_inc(
                                                       conv_ready if j == D_CONV - 1 else conv_step, 1)
            e, poly, small = tmp[:, 2], tmp[:, 4], tmp[:, 5]
            dve.wait_ge(dt_act, 1)
            n = 3
            nc.vector.tensor_scalar(poly, e, 1.0 / 7, -1.0 / 6, ALU.mult, ALU.add).then_inc(dt_step, 1)
            for coefficient in (1.0 / 5, -1.0 / 4, 1.0 / 3, -1.0 / 2, 1.0):
                n += 1
                dve.wait_ge(dt_step, n)
                nc.vector.tensor_tensor(poly, poly, e, ALU.mult).then_inc(dt_step, 1)
                n += 1
                dve.wait_ge(dt_step, n)
                nc.vector.tensor_scalar(poly, poly, coefficient, None, ALU.add).then_inc(dt_step, 1)
            n += 1
            dve.wait_ge(dt_step, n)
            nc.vector.tensor_tensor(poly, poly, e, ALU.mult).then_inc(dt_step, 1)
            nc.vector.tensor_scalar(small, e, 1.0 / 16, None, ALU.is_lt).then_inc(dt_step, 1)
            dve.wait_ge(dt_act, 3)
            n += 2
            dve.wait_ge(dt_step, n)
            nc.vector.tensor_tensor(poly, poly, tmp[:, 3], ALU.subtract).then_inc(dt_step, 1)
            dve.wait_ge(dt_step, n + 1)
            nc.vector.tensor_tensor(poly, poly, small, ALU.mult).then_inc(dt_step, 1)
            dve.wait_ge(dt_step, n + 2)
            nc.vector.tensor_tensor(poly, poly, tmp[:, 3], ALU.add).then_inc(dt_step, 1)
            dve.wait_ge(dt_step, n + 3)
            nc.vector.tensor_tensor(s.dt[:].rearrange("p t h -> p (t h)"), tmp[:, 0], poly,
                                    ALU.add).then_inc(dt_step, 1)
            dve.wait_ge(dt_step, n + 4)
            rate = s.decay_rate[:].unsqueeze(1).to_broadcast([P, NT, HEADS0])
            nc.vector.scalar_tensor_tensor(out=s.a[:], in0=s.dt[:], scalar=-1.0, in1=rate,
                                           op0=ALU.mult, op1=ALU.mult).then_inc(dt_step, 1)


def mamba_scan_stage(nc, k, s):
    HP = HEADS0 * HD0
    with ExitStack() as ctx:
        sb = lambda name, shape: ctx.enter_context(nc.sbuf_tensor(name, shape, F32))
        x_tok, b_tok = sb("x_dt_tok", [P, 2, HEADS0, HD0]), sb("b_tok", [P, 2, P])
        al, e1, e2 = sb("a_upto_l", [P, 2, HEADS0, P]), sb("e_between", [P, 2, HEADS0, P]), sb("e_upto", [P, 2, HEADS0, P])
        g, m = sb("cb_masked", [P, 2, P]), sb("m_masked", [P, 2, HEADS0, P])
        ce, xd = sb("c_decayed", [P, 2, HEADS0, P]), sb("x_decayed", [P, 2, HEADS0, HD0])
        state, kept = sb("state", [P, 2, HEADS0, HD0]), sb("state_kept", [P, HEADS0, HD0])
        t_ps = ctx.enter_context(nc.psum_tensor("turn_ps", [P, 2, 4, P], F32))
        seg_ps = ctx.enter_context(nc.psum_tensor("seg_ps", [P, 2, CH], F32))
        cum_ps = ctx.enter_context(nc.psum_tensor("cum_ps", [P, CH], F32))
        y_ps = ctx.enter_context(nc.psum_tensor("y_ps", [P, 2, CH], F32))
        ds_ps = ctx.enter_context(nc.psum_tensor("ds_ps", [P, HEADS0, HD0], F32))
        sem = lambda name: nc.alloc_semaphore(name + "_ms")
        turned, x_tok_ready, b_tok_ready, al_ready = sem("turned"), sem("x_tok"), sem("b_tok"), sem("al")
        seg_ready, cum_ready, e1_ready, e2_ready = sem("seg"), sem("cum"), sem("e1"), sem("e2")
        g_ready, m_ready, ce_ready, xd_ready = sem("g"), sem("m"), sem("ce"), sem("xd")
        y_ready, ds_ready, state_ready, kept_ready, y_taken = sem("y"), sem("ds"), sem("state"), sem("kept"), sem("y_taken")
        B, C = s.xbc[:, 2], s.xbc[:, 3]
        upto, after = k.w["upto"], k.w["after"]
        N = NT
        block = ctx.enter_context(nc.Block())

        @block.gpsimd
        def _(pool):
            def decays_in(n):
                if n >= 2:
                    pool.wait_ge(cum_ready, n - 1)
                nc.gpsimd.tensor_tensor(
                    al[:, n % 2], upto[:].unsqueeze(1).to_broadcast([P, HEADS0, P]),
                    s.a[:, n].unsqueeze(2).to_broadcast([P, HEADS0, P]), ALU.mult).then_inc(al_ready, 1)

            decays_in(0)
            for n in range(N):
                if n + 1 < N:
                    decays_in(n + 1)
                pool.wait_ge(e1_ready, n + 1)
                pool.wait_ge(x_tok_ready, n + 1)
                if n >= 2:
                    pool.wait_ge(ds_ready, n - 1)
                nc.gpsimd.tensor_tensor(xd[:, n % 2], x_tok[:, n % 2],
                                        e1[:, n % 2, :, P - 1:P].to_broadcast([P, HEADS0, HD0]),
                                        ALU.mult).then_inc(xd_ready, 1)
                if n % NG:
                    pool.wait_ge(e2_ready, n + 1)
                    if n >= 2:
                        pool.wait_ge(y_ready, n - 1)
                    nc.gpsimd.tensor_tensor(ce[:, n % 2], e2[:, n % 2],
                                            C[:, tile(n)].unsqueeze(1).to_broadcast([P, HEADS0, P]),
                                            ALU.mult).then_inc(ce_ready, 1)

        @block.tensor
        def _(pe):
            def turn(n):
                if n >= 2:
                    pe.wait_ge(g_ready, n - 1)
                for j in range(3):
                    nc.tensor.transpose(t_ps[:, n % 2, j], s.xbc[:, j, tile(n)], k.w["ident"][:])
                nc.tensor.matmul(t_ps[:, n % 2, 3], B[:, tile(n)], C[:, tile(n)],
                                 start=True, stop=True).then_inc(turned, 1)

            def decays(n):
                pe.wait_ge(al_ready, n + 1)
                if n >= 2:
                    pe.wait_ge(e1_ready, n - 1)
                nc.tensor.matmul(seg_ps[:, n % 2], after[:], al[:, n % 2].rearrange("p h l -> p (h l)"),
                                 start=True, stop=True).then_inc(seg_ready, 1)
                if n >= 1:
                    pe.wait_ge(e2_ready, n)
                nc.tensor.matmul(cum_ps[:], k.w["ones"][:], al[:, n % 2].rearrange("p h l -> p (h l)"),
                                 start=True, stop=True).then_inc(cum_ready, 1)

            turn(0)
            decays(0)
            for n in range(N):
                if n + 1 < N:
                    turn(n + 1)
                    decays(n + 1)
                pe.wait_ge(xd_ready, n + 1)
                pe.wait_ge(b_tok_ready, n + 1)
                if n >= 1:
                    pe.wait_ge(state_ready, n)
                nc.tensor.matmul(ds_ps[:].rearrange("p h d -> p (h d)"), b_tok[:, n % 2],
                                 xd[:, n % 2].rearrange("p h d -> p (h d)"), start=True, stop=True).then_inc(ds_ready, 1)
                pe.wait_ge(m_ready, n + 1)
                first = n % NG == 0
                if not first:
                    pe.wait_ge(ce_ready, n - n // NG)
                if n >= 2:
                    pe.wait_ge(y_taken, n - 1)
                for h in range(HEADS0):
                    out = y_ps[HD0 * (h % 2):HD0 * (h % 2) + HD0, n % 2, (h // 2) * P:(h // 2) * P + P]
                    last = nc.tensor.matmul(out, x_tok[:, n % 2, h], m[:, n % 2, h], start=True, stop=first)
                    if not first:
                        last = nc.tensor.matmul(out, state[:, (n - 1) % 2, h], ce[:, n % 2, h],
                                                start=False, stop=True)
                last.then_inc(y_ready, 1)

        @block.scalar
        def _(act):
            for n in range(N):
                act.wait_ge(seg_ready, n + 1)
                if n >= 2:
                    act.wait_ge(m_ready, n - 1)
                    act.wait_ge(xd_ready, n - 1)
                nc.scalar.activation(e1[:, n % 2].rearrange("p h l -> p (h l)"), seg_ps[:, n % 2],
                                     ACT.Exp).then_inc(e1_ready, 1)
                act.wait_ge(cum_ready, n + 1)
                if n >= 2:
                    act.wait_ge(kept_ready, n - 1)
                    if n >= 3:
                        act.wait_ge(ce_ready, (n - 1) - (n - 2) // NG - 1)
                nc.scalar.activation(e2[:, n % 2].rearrange("p h l -> p (h l)"), cum_ps[:],
                                     ACT.Exp).then_inc(e2_ready, 1)

        @block.vector
        def _(dve):
            for n in range(N):
                dve.wait_ge(turned, n + 1)
                if n >= 2:
                    dve.wait_ge(y_ready, n - 1)
                    dve.wait_ge(xd_ready, n - 1)
                nc.vector.tensor_tensor(x_tok[:, n % 2], t_ps[:, n % 2, 0:2].rearrange("p j (h d) -> p (j h) d", d=HD0),
                                        s.dt[:, n].unsqueeze(2).to_broadcast([P, HEADS0, HD0]),
                                        ALU.mult).then_inc(x_tok_ready, 1)
                if n >= 2:
                    dve.wait_ge(ds_ready, n - 1)
                nc.vector.tensor_copy(b_tok[:, n % 2], t_ps[:, n % 2, 2]).then_inc(b_tok_ready, 1)
                if n >= 2:
                    dve.wait_ge(m_ready, n - 1)
                nc.vector.tensor_tensor(g[:, n % 2], t_ps[:, n % 2, 3], upto[:], ALU.mult).then_inc(g_ready, 1)
                dve.wait_ge(g_ready, n + 1)
                dve.wait_ge(e1_ready, n + 1)
                nc.vector.tensor_tensor(m[:, n % 2], e1[:, n % 2],
                                        g[:, n % 2].unsqueeze(1).to_broadcast([P, HEADS0, P]),
                                        ALU.mult).then_inc(m_ready, 1)
                dve.wait_ge(e2_ready, n + 1)
                if n % NG == 0:
                    if n >= 1:
                        dve.wait_ge(state_ready, n)
                    nc.vector.memset(kept[:], 0.0).then_inc(kept_ready, 1)
                else:
                    dve.wait_ge(state_ready, n)
                    nc.vector.tensor_tensor(kept[:], state[:, (n - 1) % 2],
                                            e2[:, n % 2, :, P - 1:P].to_broadcast([P, HEADS0, HD0]),
                                            ALU.mult).then_inc(kept_ready, 1)
                dve.wait_ge(kept_ready, n + 1)
                dve.wait_ge(ds_ready, n + 1)
                if n >= 1:
                    dve.wait_ge(y_ready, n)
                nc.vector.tensor_tensor(state[:, n % 2], kept[:], ds_ps[:], ALU.add).then_inc(state_ready, 1)
                dve.wait_ge(y_ready, n + 1)
                for j in range(2):
                    last = nc.vector.scalar_tensor_tensor(
                        out=s.y[:, j, tile(n)], in0=s.xbc[:, j, tile(n)], scalar=k.w["L0_D"][:, j:j + 1],
                        in1=y_ps[:, n % 2, j * P:(j + 1) * P], op0=ALU.mult, op1=ALU.add)
                last.then_inc(y_taken, 1)


def mamba_out_stage(nc, k, s):
    with ExitStack() as ctx:
        sb = lambda name, shape: ctx.enter_context(nc.sbuf_tensor(name, shape, F32))
        yz, sq = sb("y_gated", [P, 2, 2, CH]), sb("y_squared", [P, 2, 2, CH])
        rms, rinv, w, tmp = sb("rms", [P, 2, CH]), sb("rms_inv", [P, 2, CH]), sb("w_out_n", [P, 2, P]), sb("out_n", [P, 2, CH])
        o_ps = ctx.enter_context(nc.psum_tensor("o_ps", [P, 2, CH], F32))
        s_ps = ctx.enter_context(nc.psum_tensor("s_ps", [P, 2, CH], F32))
        sem = lambda name: nc.alloc_semaphore(name + "_mo")
        w_ready, gated, squared, sum_ready, out_ready = sem("w"), sem("gated"), sem("squared"), sem("sum"), sem("out")
        rms_ready, rinv_ready, scaled, added = sem("rms"), sem("rinv"), sem("scaled"), sem("added")
        block = ctx.enter_context(nc.Block())

        @block.tensor
        def _(pe):
            pe.wait_ge(w_ready, 2)
            for c in range(NCH):
                pe.wait_ge(gated, c + 1)
                if c >= 2:
                    pe.wait_ge(scaled, c - 1)
                for j in range(2):
                    last = nc.tensor.matmul(o_ps[:, c % 2], w[:, j], yz[:, c % 2, j], start=j == 0, stop=j == 1)
                last.then_inc(out_ready, 1)
                pe.wait_ge(squared, c + 1)
                if c >= 2:
                    pe.wait_ge(rms_ready, c - 1)
                for j in range(2):
                    last = nc.tensor.matmul(s_ps[:, c % 2], k.w["mean_w"][:], sq[:, c % 2, j], start=j == 0, stop=j == 1)
                last.then_inc(sum_ready, 1)

        @block.scalar
        def _(act):
            for c in range(NCH):
                act.wait_ge(gated, c + 1)
                if c >= 2:
                    act.wait_ge(sum_ready, c - 1)
                nc.scalar.activation(sq[:, c % 2], yz[:, c % 2], ACT.Square).then_inc(squared, 1)
                act.wait_ge(sum_ready, c + 1)
                if c >= 2:
                    act.wait_ge(rinv_ready, c - 1)
                nc.scalar.activation(rms[:, c % 2], s_ps[:, c % 2], ACT.Sqrt, bias=k.w["eps"][:, 0:1],
                                     scale=0.5).then_inc(rms_ready, 1)

        @block.vector
        def _(dve):
            for j in range(2):
                nc.vector.tensor_scalar(w[:, j], k.w["L0_W_out"][:, j], k.w["L0_norm_w"][:, j:j + 1], None,
                                        ALU.mult).then_inc(w_ready, 1)

            def gate(c):
                if c >= 2:
                    dve.wait_ge(out_ready, c - 1)
                    dve.wait_ge(squared, c - 1)
                nc.vector.tensor_tensor(yz[:, c % 2], s.y[:, :, chunk(c)], s.zg[:, :, chunk(c)],
                                        ALU.mult).then_inc(gated, 1)

            gate(0)
            for c in range(NCH):
                if c + 1 < NCH:
                    gate(c + 1)
                b = batch_of(c)
                dve.wait_ge(rms_ready, c + 1)
                if c >= 2:
                    dve.wait_ge(scaled, c - 1)
                nc.vector.reciprocal(rinv[:, c % 2], rms[:, c % 2]).then_inc(rinv_ready, 1)
                dve.wait_ge(rinv_ready, c + 1)
                dve.wait_ge(out_ready, c + 1)
                if c >= 2:
                    dve.wait_ge(added, c - 1)
                nc.vector.tensor_tensor(tmp[:, c % 2], o_ps[:, c % 2], rinv[:, c % 2], ALU.mult).then_inc(scaled, 1)
                dve.wait_ge(scaled, c + 1)
                nc.vector.scalar_tensor_tensor(out=k.x[:, chunk(c)], in0=tmp[:, c % 2],
                                               scalar=k.mod[:, 0, GATE_A, b:b + 1], in1=k.x[:, chunk(c)],
                                               op0=ALU.mult, op1=ALU.add).then_inc(added, 1)


def mamba_block(nc, k):
    with ExitStack() as ctx:
        sb = lambda name, shape: ctx.enter_context(nc.sbuf_tensor(name, shape, F32))
        s = Kit()
        s.zg, s.xbc, s.y = sb("z_gate", [P, 2, T]), sb("xbc", [P, 4, T]), sb("y0", [P, 2, T])
        s.dt, s.a, s.decay_rate = sb("dt", [P, NT, HEADS0]), sb("a_dt", [P, NT, HEADS0]), sb("decay_rate", [P, HEADS0])
        with nc.sbuf_tensor("conv_out", [P, 4, NB, SEQ], F32) as s.conv_out:
            mamba_project_stage(nc, k, s)
        mamba_scan_stage(nc, k, s)
        mamba_out_stage(nc, k, s)

E = 8
PARTS = 3
PART = 32
TOP_EPS = 1e-8


def routing_stage(nc, k, r, router, top_sum_eps):
    tag = "_rt" + router
    TE = NT * E
    steps = 2 + 2 * NT + 3 + 2 + 3 + (1 if top_sum_eps else 0) + 2 + 3 * PARTS - 1
    with ExitStack() as ctx:
        sb = lambda name, shape, dt=F32: ctx.enter_context(nc.sbuf_tensor(name + tag, shape, dt))
        lg, top, top_at, at = sb("lg", [P, NT, E]), sb("top", [P, NT, E]), sb("top_at", [P, NT, E], U32), sb("at", [P, NT, E])
        ex, total, den = sb("ex", [P, NT, E]), sb("total", [P, NT, 1]), sb("den", [P, NT, 1])
        hit, rest = sb("hit", [P, 2, NT, E]), sb("rest", [P, 2, NT, E])
        part = sb("part", [P, PARTS, NT, E], BF16)
        spread = sb("spread", [P, NT, PARTS, PART])
        parts16 = sb("parts16", [PARTS * PART, T], BF16)
        lg_ps = ctx.enter_context(nc.psum_tensor("lg_ps" + tag, [P, CH], F32))
        t_ps = ctx.enter_context(nc.psum_tensor("t_ps" + tag, [P, 2, CH], F32))
        w_ps = ctx.enter_context(nc.psum_tensor("w_ps" + tag, [P, 4, CH], F32))
        sem = lambda name: nc.alloc_semaphore(name + tag)
        logits_ready, dve_step, act_step, turned = sem("logits"), sem("dve_step"), sem("act_step"), sem("turned")
        parts_ready, parts16_ready, wide_ready, wide_read_a, wide_read_v = (
            sem("parts"), sem("parts16"), sem("wide"), sem("wide_read_a"), sem("wide_read_v"))
        block = ctx.enter_context(nc.Block())

        @block.sync
        def _(sp):
            for s in range(2):
                sp.dma_start(r.slot[:, s], r.weights[s]).then_inc(r.slot_loaded[s], 16)

        @block.tensor
        def _(pe):
            for t in range(NT):
                last = nc.tensor.matmul(lg_ps[:, t * E:(t + 1) * E], k.h[:, tile(t)], k.w[router][:],
                                        start=True, stop=True)
            last.then_inc(logits_ready, 1)
            pe.wait_ge(dve_step, steps)
            for c in range(NCH):
                if c >= 2:
                    pe.wait_ge(parts_ready, c - 1)
                for j in range(CH // P):
                    last = nc.tensor.transpose(t_ps[0:PARTS * PART, c % 2, tile(j)],
                                               spread[:, c * CH // P + j].rearrange("p i e -> p (i e)"),
                                               k.w["ident"][:])
                last.then_inc(turned, 1)
            for e in range(E):
                for c in range(NCH):
                    n = e * NCH + c
                    if e == 0:
                        pe.wait_ge(parts16_ready, c + 1)
                    if n >= 4:
                        pe.wait_ge(wide_read_v if n % 2 else wide_read_a, n // 2 - 1)
                    nc.tensor.matmul(w_ps[:, n % 4], k.w["pick"][:, e], parts16[:, chunk(c)],
                                     start=True, stop=True).then_inc(wide_ready, 1)

        @block.scalar
        def _(act):
            act.wait_ge(dve_step, 2 + 2 * NT + 1)
            nc.scalar.activation(ex[:], ex[:], ACT.Exp).then_inc(act_step, 1)
            for c in range(NCH):
                act.wait_ge(turned, c + 1)
                nc.scalar.activation(r.parts[:, chunk(c)], t_ps[0:PARTS * PART, c % 2], ACT.Copy).then_inc(parts_ready, 1)
            for n in range(0, E * NCH, 2):
                act.wait_ge(wide_ready, n + 1)
                nc.scalar.activation(r.wide[:, n // NCH, chunk(n % NCH)], w_ps[:, n % 4],
                                     ACT.Copy).then_inc(wide_read_a, 1)

        count = [0]

        @block.vector
        def _(dve):
            def step(instruction):
                count[0] += 1
                instruction.then_inc(dve_step, 1)
                dve.wait_ge(dve_step, count[0])

            dve.wait_ge(logits_ready, 1)
            step(nc.vector.memset(spread[:], 0.0))
            step(nc.vector.tensor_copy(lg[:].rearrange("p t e -> p (t e)"), lg_ps[:, 0:TE]))
            for t in range(NT):
                nc.vector.max(top[:, t], lg[:, t]).then_inc(dve_step, 1)
            count[0] += NT
            dve.wait_ge(dve_step, count[0])
            for t in range(NT):
                nc.vector.max_index(top_at[:, t], top[:, t], lg[:, t]).then_inc(dve_step, 1)
            count[0] += NT
            dve.wait_ge(dve_step, count[0])
            greatest = top[:, :, 0:1].to_broadcast([P, NT, E])
            step(nc.vector.tensor_tensor(ex[:], lg[:], greatest, ALU.subtract))
            dve.wait_ge(act_step, 1)
            step(nc.vector.tensor_reduce(total[:, :, 0], ex[:], AX, ALU.add))
            step(nc.vector.tensor_copy(at[:], top_at[:]))
            for i in range(2):
                step(nc.vector.tensor_tensor(hit[:, i], k.w["iota8"][:].unsqueeze(1).to_broadcast([P, NT, E]),
                                             at[:, :, i:i + 1].to_broadcast([P, NT, E]), ALU.is_equal))
            step(nc.vector.tensor_tensor(hit[:, 0], hit[:, 0], hit[:, 1], ALU.add))
            step(nc.vector.tensor_tensor(hit[:, 0], hit[:, 0], ex[:], ALU.mult))
            step(nc.vector.tensor_reduce(den[:, :, 0], hit[:, 0], AX, ALU.add))
            if top_sum_eps:
                step(nc.vector.scalar_tensor_tensor(out=den[:], in0=total[:], scalar=top_sum_eps, in1=den[:],
                                                    op0=ALU.mult, op1=ALU.add))
            step(nc.vector.reciprocal(den[:], den[:]))
            step(nc.vector.tensor_tensor(rest[:, 0], hit[:, 0], den[:].to_broadcast([P, NT, E]), ALU.mult))
            for i in range(PARTS):
                step(nc.vector.tensor_copy(part[:, i], rest[:, i % 2]))
                step(nc.vector.tensor_copy(spread[:, :, i, 0:E], part[:, i]))
                if i + 1 < PARTS:
                    step(nc.vector.tensor_tensor(rest[:, (i + 1) % 2], rest[:, i % 2], part[:, i], ALU.subtract))
            for c in range(NCH):
                dve.wait_ge(parts_ready, c + 1)
                nc.vector.tensor_copy(parts16[:, chunk(c)], r.parts[:, chunk(c)]).then_inc(parts16_ready, 1)
            for n in range(1, E * NCH, 2):
                dve.wait_ge(wide_ready, n + 1)
                nc.vector.tensor_copy(r.wide[:, n // NCH, chunk(n % NCH)], w_ps[:, n % 4]).then_inc(wide_read_v, 1)

        assert count[0] == steps


CREDIT = 2


def experts_stage(nc, k, r, layer, tiles, func, gated, routed):
    tag = f"_ex{layer}"
    M, LAG, HB = tiles, 2, 4
    wide_cols = M * P
    UNITS = NCH * M
    PAIR = 2 * UNITS
    G0, U0 = 0, wide_cols
    D0 = (2 if gated else 1) * wide_cols
    BG, BU = D0 + M * P, D0 + M * P + M
    with ExitStack() as ctx:
        sb = lambda name, shape: ctx.enter_context(nc.sbuf_tensor(name + tag, shape, F32))
        act_out, mid, hid = sb("act_out", [P, 2, CH]), sb("mid", [P, 2, CH]), sb("hid", [P, HB, CH])
        zero = sb("zero", [P, P])
        acc = ctx.enter_context(nc.psum_tensor("acc" + tag, [P, NCH, CH], F32))
        g_ps = ctx.enter_context(nc.psum_tensor("g_ps" + tag, [P, 2, CH], F32))
        u_ps = ctx.enter_context(nc.psum_tensor("u_ps" + tag, [P, 2, CH], F32))
        sem = lambda name: nc.alloc_semaphore(name + tag)
        zero_ready, g_ready, u_ready, act_ready, mid_ready, hid_ready, down_done, added = (
            sem("zero"), sem("g"), sem("u"), sem("act"), sem("mid"), sem("hid"), sem("down"), sem("added"))
        block = ctx.enter_context(nc.Block())
        units = [(s, c, m) for s in range(2) for c in range(NCH) for m in range(M)]

        @block.sync
        def _(sp):
            with sp.Fori(0, E // 2 - 1, 1) as it:
                for s in range(2):
                    sp.wait_ge(down_done, it * PAIR + (s + 1) * UNITS + CREDIT)
                    sp.dma_start(r.slot[:, s], r.weights[bass.ds(it * 2 + (2 + s), 1)].rearrange("o p n -> p (o n)")
                                 ).then_inc(r.slot_loaded[s], 16)

        @block.tensor
        def _(pe):
            def up(it, u):
                s, c, m = units[u]
                if u % UNITS == 0:
                    pe.wait_ge(r.slot_loaded[s], it * 16 + 16)
                pe.wait_ge(act_ready, it * PAIR + (u + 1))
                nc.tensor.matmul(g_ps[:, u % 2], r.slot[:, s, G0 + m * P:G0 + (m + 1) * P], k.h[:, chunk(c)],
                                 start=True, stop=True).then_inc(g_ready, 1)
                if gated:
                    pe.wait_ge(mid_ready if routed else hid_ready, it * PAIR + (u + 1))
                    nc.tensor.matmul(u_ps[:, u % 2], r.slot[:, s, U0 + m * P:U0 + (m + 1) * P], k.h[:, chunk(c)],
                                     start=True, stop=True).then_inc(u_ready, 1)

            def down(it, u):
                s, c, m = units[u]
                pe.wait_ge(hid_ready, it * PAIR + (u + 1 + CREDIT))
                nc.tensor.matmul(acc[:, c], r.slot[:, s, D0 + m * P:D0 + (m + 1) * P], hid[:, u % HB],
                                 start=False, stop=True, skip_group_check=True).then_inc(down_done, 1)

            pe.sem_inc(down_done, CREDIT)
            if not routed:
                pe.wait_ge(zero_ready, 1)
            for c in range(NCH):
                if routed:
                    nc.tensor.matmul(acc[:, c], k.w[r.out_bias][:], r.parts[:, chunk(c)], start=True, stop=True)
                else:
                    nc.tensor.matmul(acc[:, c], zero[:], k.h[:, chunk(c)], start=True, stop=True)
            with pe.Fori(0, E // 2, 1) as it:
                for u in range(PAIR + LAG):
                    if u < PAIR:
                        up(it, u)
                    if u >= LAG:
                        down(it, u - LAG)

        @block.scalar
        def _(act):
            act.sem_inc(act_ready, CREDIT)
            with act.Fori(0, E // 2, 1) as it:
                for u, (s, c, m) in enumerate(units):
                    act.wait_ge(g_ready, it * PAIR + (u + 1))
                    act.wait_ge(mid_ready if gated and routed else hid_ready, it * PAIR + (u + 1))
                    bias = r.slot[:, s, BG + m:BG + m + 1] if routed else 0.0
                    nc.scalar.activation(act_out[:, u % 2], g_ps[:, u % 2], func, bias=bias).then_inc(act_ready, 1)

        @block.vector
        def _(dve):
            if not routed:
                nc.vector.memset(zero[:], 0.0).then_inc(zero_ready, 1)
            dve.sem_inc(hid_ready, CREDIT)
            dve.sem_inc(mid_ready, CREDIT)
            with dve.Fori(0, E // 2, 1) as it:
                for u, (s, c, m) in enumerate(units):
                    if gated:
                        dve.wait_ge(u_ready, it * PAIR + (u + 1))
                    if gated and routed:
                        dve.wait_ge(act_ready, it * PAIR + (u + 1 + CREDIT))
                        dve.wait_ge(hid_ready, it * PAIR + (u + 1))
                        nc.vector.scalar_tensor_tensor(
                            out=mid[:, u % 2], in0=u_ps[:, u % 2], scalar=r.slot[:, s, BU + m:BU + m + 1],
                            in1=act_out[:, u % 2], op0=ALU.add, op1=ALU.mult).then_inc(mid_ready, 1)
                        dve.wait_ge(mid_ready, it * PAIR + (u + 1 + CREDIT))
                    else:
                        dve.wait_ge(act_ready, it * PAIR + (u + 1 + CREDIT))
                    if u >= HB:
                        dve.wait_ge(down_done, it * PAIR + (u - HB + 1 + CREDIT))
                    else:
                        dve.wait_ge(down_done, it * PAIR + CREDIT)
                    if routed:
                        nc.vector.tensor_tensor(
                            hid[:, u % HB], (mid if gated else act_out)[:, u % 2],
                            r.wide[:, bass.ds(it * 2 + s, 1), chunk(c)].rearrange("p o n -> p (o n)"),
                            ALU.mult).then_inc(hid_ready, 1)
                    else:
                        nc.vector.tensor_tensor(hid[:, u % HB], u_ps[:, u % 2], act_out[:, u % 2],
                                                ALU.mult).then_inc(hid_ready, 1)
            dve.wait_ge(down_done, E * UNITS + CREDIT)
            for c in range(NCH):
                b = batch_of(c)
                last = nc.vector.scalar_tensor_tensor(
                    out=k.x[:, chunk(c)], in0=acc[:, c], scalar=k.mod[:, layer, GATE_B, b:b + 1],
                    in1=k.x[:, chunk(c)], op0=ALU.mult, op1=ALU.add)
            last.then_inc(added, 1)


def experts_block(nc, k, layer, tiles, func, gated, routed, top_sum_eps=None):
    cols = tiles * P * (3 if gated else 2) + (tiles * (2 if gated else 1) if routed else 0)
    with ExitStack() as ctx:
        r = Kit()
        r.weights = k.dram[f"L{layer}_experts"]
        r.slot = ctx.enter_context(nc.sbuf_tensor(f"slot{layer}", [P, 2, cols], F32))
        r.slot_loaded = [nc.alloc_semaphore(f"slot{layer}_{s}") for s in range(2)]
        r.out_bias = f"L{layer}_out_bias"
        if routed:
            r.parts = ctx.enter_context(nc.sbuf_tensor(f"parts{layer}", [PARTS * PART, T], F32))
            r.wide = ctx.enter_context(nc.sbuf_tensor(f"wide{layer}", [P, E, T], F32))
            routing_stage(nc, k, r, f"L{layer}_router", top_sum_eps)
        else:
            with nc.Block() as block:
                @block.sync
                def _(sp):
                    for s in range(2):
                        sp.dma_start(r.slot[:, s], r.weights[s]).then_inc(r.slot_loaded[s], 16)
        experts_stage(nc, k, r, layer, tiles, func, gated, routed)

HEADS1 = 16
HD1 = 64
LANE = 32


def pair_attention_stage(nc, k):
    NJ = SEQ // CH
    M = HEADS1 * HD1 // P
    units = [(j, t) for j in range(NJ) for t in range(M)]
    U = len(units)
    scale = 1.0 / HD1 ** 0.5
    wq, wkv, wo = k.w["L1_Wq"], k.w["L1_Wkv"], k.w["L1_Wo"]
    row = lambda i, j: slice(i * SEQ + j * CH, i * SEQ + (j + 1) * CH)
    lanes = lambda i, j: slice(LANE * (2 * i + j), LANE * (2 * i + j) + LANE)
    with ExitStack() as ctx:
        sb = lambda name, shape: ctx.enter_context(nc.sbuf_tensor(name + "_pa", shape, F32))
        hd = sb("h_diff", [P, SEQ])
        kd, prod = sb("k_diff", [P, 2, CH]), sb("qk_prod", [P, 2, 2, CH])
        mx, e0, e1, w0 = sb("mx", [P, CH]), sb("e0", [P, CH]), sb("e1", [P, CH]), sb("w0", [P, CH])
        vd, wv, vec = sb("v_diff", [P, 2, CH]), sb("w_v", [P, 2, 2, CH]), sb("vec", [P, 2, 2, CH])
        sem = lambda name: nc.alloc_semaphore(name + "_pa")
        hd_ready, kd_ps_ready, q_ready, kd_ready, prod_ready, dots_done = (
            sem("hd"), sem("kd_ps"), sem("q"), sem("kd"), sem("prod"), sem("dots"))
        soft_step, e_ready = sem("soft_step"), sem("e")
        vd_ps_ready, v1_ready, wide_ready, vd_ready, wv_ready, vec_ready, out_ready, added = (
            sem("vd_ps"), sem("v1"), sem("wide"), sem("vd"), sem("wv"), sem("vec"), sem("out"), sem("added"))

        with ExitStack() as first:
            q_ps = first.enter_context(nc.psum_tensor("q_ps_pa", [P, 2, 2, CH], F32))
            kd_ps = first.enter_context(nc.psum_tensor("kd_ps_pa", [P, 2, CH], F32))
            d_ps = first.enter_context(nc.psum_tensor("d_ps_pa", [P, CH], F32))
            block = first.enter_context(nc.Block())

            @block.tensor
            def _(pe):
                def project(u):
                    j, t = units[u]
                    if u >= 2:
                        pe.wait_ge(kd_ready, u - 1)
                    nc.tensor.matmul(kd_ps[:, u % 2], wkv[:, tile(t)], hd[:, j * CH:(j + 1) * CH],
                                     start=True, stop=True).then_inc(kd_ps_ready, 1)
                    if u >= 2:
                        pe.wait_ge(prod_ready, 2 * (u - 1))
                    for i in range(NB):
                        nc.tensor.matmul(q_ps[:, u % 2, i], wq[:, tile(t)], k.h[:, row(i, j)],
                                         start=True, stop=True).then_inc(q_ready, 1)

                def dots(u):
                    j, t = units[u]
                    for i in range(NB):
                        pe.wait_ge(prod_ready, 2 * u + i + 1)
                        nc.tensor.matmul(d_ps[lanes(i, j)], k.w["head_sum"][:, t], prod[:, u % 2, i],
                                         start=t == 0, stop=t == M - 1,
                                         tile_position=(0, lanes(i, j).start)).then_inc(dots_done, 1)

                pe.wait_ge(hd_ready, 1)
                for u in range(U + 1):
                    if u < U:
                        project(u)
                    if u >= 1:
                        dots(u - 1)

            @block.scalar
            def _(act):
                for u in range(U):
                    act.wait_ge(kd_ps_ready, u + 1)
                    if u >= 2:
                        act.wait_ge(prod_ready, 2 * (u - 1))
                    nc.scalar.activation(kd[:, u % 2], kd_ps[:, u % 2], ACT.Copy).then_inc(kd_ready, 1)
                act.wait_ge(soft_step, 2)
                nc.scalar.activation(e0[:], e0[:], ACT.Exp, scale=scale).then_inc(e_ready, 1)
                nc.scalar.activation(e1[:], mx[:], ACT.Exp, scale=-scale).then_inc(e_ready, 1)

            @block.vector
            def _(dve):
                nc.vector.tensor_tensor(hd[:], k.h[:, 0:SEQ], k.h[:, SEQ:T], ALU.subtract).then_inc(hd_ready, 1)
                for u in range(U):
                    dve.wait_ge(kd_ready, u + 1)
                    for i in range(NB):
                        dve.wait_ge(q_ready, 2 * u + i + 1)
                        if u >= 2:
                            dve.wait_ge(dots_done, 2 * (u - 2) + i + 1)
                        nc.vector.tensor_tensor(prod[:, u % 2, i], q_ps[:, u % 2, i], kd[:, u % 2],
                                                ALU.mult).then_inc(prod_ready, 1)
                dve.wait_ge(dots_done, 2 * U)
                nc.vector.tensor_scalar(mx[:], d_ps[:], 0.0, None, ALU.max).then_inc(soft_step, 1)
                dve.wait_ge(soft_step, 1)
                nc.vector.tensor_tensor(e0[:], d_ps[:], mx[:], ALU.subtract).then_inc(soft_step, 1)
                dve.wait_ge(e_ready, 2)
                nc.vector.tensor_tensor(e1[:], e0[:], e1[:], ALU.add).then_inc(soft_step, 1)
                dve.wait_ge(soft_step, 3)
                nc.vector.reciprocal(e1[:], e1[:]).then_inc(soft_step, 1)
                dve.wait_ge(soft_step, 4)
                nc.vector.tensor_tensor(w0[:], e0[:], e1[:], ALU.mult).then_inc(soft_step, 1)

        vd_ps = ctx.enter_context(nc.psum_tensor("vd_ps_pa", [P, CH], F32))
        v1_ps = ctx.enter_context(nc.psum_tensor("v1_ps_pa", [P, 2, CH], F32))
        wide_ps = ctx.enter_context(nc.psum_tensor("wide_ps_pa", [P, 2, CH], F32))
        o_ps = ctx.enter_context(nc.psum_tensor("o_ps_pa", [P, 2, CH], F32))
        block = ctx.enter_context(nc.Block())
        VK = M * P

        @block.tensor
        def _(pe):
            def project(u):
                j, t = units[u]
                w = wkv[:, VK + t * P:VK + (t + 1) * P]
                if u >= 1:
                    pe.wait_ge(vd_ready, u)
                nc.tensor.matmul(vd_ps[:], w, hd[:, j * CH:(j + 1) * CH],
                                 start=True, stop=True).then_inc(vd_ps_ready, 1)
                for i in range(NB):
                    if u >= 1:
                        pe.wait_ge(wv_ready, 2 * (u - 1) + i + 1)
                    q = lanes(i, j)
                    nc.tensor.matmul(wide_ps[:, i], k.w["head_pick"][q, t], w0[q], start=True, stop=True,
                                     tile_position=(q.start, 0)).then_inc(wide_ready, 1)
                if u >= 2:
                    pe.wait_ge(vec_ready, 2 * (u - 1))
                nc.tensor.matmul(v1_ps[:, u % 2], w, k.h[:, row(1, j)],
                                 start=True, stop=True).then_inc(v1_ready, 1)

            def out(u):
                j, t = units[u]
                for i in range(NB):
                    pe.wait_ge(vec_ready, 2 * u + i + 1)
                    if j and t == 0:
                        pe.wait_ge(added, 2 * (j - 1) + i + 1)
                    nc.tensor.matmul(o_ps[:, i], wo[:, t], vec[:, u % 2, i],
                                     start=t == 0, stop=t == M - 1).then_inc(out_ready, 1)

            for u in range(U + 1):
                if u < U:
                    project(u)
                if u >= 1:
                    out(u - 1)

        @block.scalar
        def _(act):
            for u in range(U):
                act.wait_ge(vd_ps_ready, u + 1)
                if u >= 2:
                    act.wait_ge(wv_ready, 2 * (u - 1))
                nc.scalar.activation(vd[:, u % 2], vd_ps[:], ACT.Copy).then_inc(vd_ready, 1)

        @block.vector
        def _(dve):
            def add(j):
                for i in range(NB):
                    dve.wait_ge(out_ready, 2 * (j + 1) * M - 1 + i)
                    nc.vector.scalar_tensor_tensor(out=k.x[:, row(i, j)], in0=o_ps[:, i],
                                                   scalar=k.mod[:, 1, GATE_A, i:i + 1], in1=k.x[:, row(i, j)],
                                                   op0=ALU.mult, op1=ALU.add).then_inc(added, 1)

            for u in range(U):
                dve.wait_ge(vd_ready, u + 1)
                for i in range(NB):
                    dve.wait_ge(wide_ready, 2 * u + i + 1)
                    if u >= 2:
                        dve.wait_ge(vec_ready, 2 * (u - 2) + i + 1)
                    nc.vector.tensor_tensor(wv[:, u % 2, i], wide_ps[:, i], vd[:, u % 2],
                                            ALU.mult).then_inc(wv_ready, 1)
                dve.wait_ge(v1_ready, u + 1)
                for i in range(NB):
                    dve.wait_ge(wv_ready, 2 * u + i + 1)
                    if u >= 2:
                        dve.wait_ge(out_ready, 2 * (u - 2) + i + 1)
                    nc.vector.tensor_tensor(vec[:, u % 2, i], wv[:, u % 2, i], v1_ps[:, u % 2],
                                            ALU.add).then_inc(vec_ready, 1)
                if u == M:
                    add(0)
            add(1)


DEPTH = 2
HEADS2 = 8
HD2 = 64
HALF = HD2 // 2
INNER = HEADS2 * HD2
WINDOW = 64
HID = P * 4 * 2 // 3
QK_SCALE = 8.0
NORM_EPS = 1e-12
QT = INNER // P


def shift_stage(nc, k, depth, half, dst):
    with ExitStack() as ctx:
        shifted = nc.alloc_semaphore(f"shifted{depth}{half}")
        block = ctx.enter_context(nc.Block())
        late = slice(P // 2, P)

        @block.scalar
        def _(act):
            nc.scalar.activation(dst[0:P // 2], k.h[0:P // 2], ACT.Copy).then_inc(shifted, 1)

        @block.vector
        def _(dve):
            for b in range(NB):
                nc.vector.memset(dst[late, b * SEQ:b * SEQ + 1], 0.0).then_inc(shifted, 1)
                nc.vector.tensor_copy(dst[late, b * SEQ + 1:(b + 1) * SEQ],
                                      k.h[late, b * SEQ:(b + 1) * SEQ - 1]).then_inc(shifted, 1)


def local_qkv_stage(nc, k, s, depth):
    tag = f"_lq{depth}"
    w = k.w["L1_wqkv"]
    heads = lambda ap: ap.rearrange("p (h d) -> p h d", d=HD2)
    with ExitStack() as ctx:
        sb = lambda name, shape: ctx.enter_context(nc.sbuf_tensor(name + tag, shape, F32))
        table = sb("table", [P, 4, SEQ // P, HD2])
        sq, ss, norm, rk = sb("sq", [P, 2 * INNER]), sb("ss", [P, 2, 2 * HEADS2]), sb("norm", [P, 2, 2 * HEADS2]), sb("rk", [P, 2, 2 * HEADS2])
        straight, crossed = sb("straight", [P, 2, 2, INNER]), sb("crossed", [P, 2, 2, INNER])
        turned = straight
        qkv_ps = ctx.enter_context(nc.psum_tensor("qkv_ps" + tag, [P, 2, 3, CH], F32))
        t_ps = ctx.enter_context(nc.psum_tensor("t_ps" + tag, [P, 2, QT, P], F32))
        sem = lambda name: nc.alloc_semaphore(name + tag)
        tables_ready, qkv_ready, v_read, squared, summed, normed, clipped, rk_ready = (
            sem("tables"), sem("qkv"), sem("v_read"), sem("squared"), sem("summed"), sem("normed"), sem("clipped"), sem("rk"))
        mults, sums_q, sums_k, k_scaled, t_ready, t_read = (
            sem("mults"), sem("sums_q"), sem("sums_k"), sem("k_scaled"), sem("t"), sem("t_read"))
        block = ctx.enter_context(nc.Block())

        @block.tensor
        def _(pe):
            def project(t):
                if t >= 2:
                    pe.wait_ge(v_read, t - 1)
                    pe.wait_ge(squared, t - 1)
                    pe.wait_ge(mults, 4 * (t - 1))
                for j in range(3):
                    last = nc.tensor.matmul(qkv_ps[:, t % 2, j], s.shifted[:, tile(t)],
                                            w[:, depth, j * INNER:(j + 1) * INNER], start=True, stop=True)
                last.then_inc(qkv_ready, 1)

            def turn(t):
                for i in range(2):
                    pe.wait_ge(k_scaled if i else sums_q, t + 1)
                    if t:
                        pe.wait_ge(t_read, 2 * (t - 1) + i + 1)
                    for j in range(QT):
                        last = nc.tensor.transpose(t_ps[:, i, j], turned[:, t % 2, i, tile(j)], k.w["ident"][:])
                    last.then_inc(t_ready, 1)

            for t in range(NT + 1):
                if t < NT:
                    project(t)
                if t >= 1:
                    turn(t - 1)

        @block.scalar
        def _(act):
            def store(t):
                for i, dst in enumerate((s.qT, s.kT)):
                    act.wait_ge(t_ready, 2 * t + i + 1)
                    nc.scalar.activation(dst[:, :, tile(t)], t_ps[:, i], ACT.Copy).then_inc(t_read, 1)

            for t in range(NT + 1):
                if t < NT:
                    act.wait_ge(qkv_ready, t + 1)
                    if t >= 1:
                        act.wait_ge(summed, t)
                    nc.scalar.activation(sq[:].rearrange("p (j n) -> p j n", j=2), qkv_ps[:, t % 2, 0:2],
                                         ACT.Square).then_inc(squared, 1)
                    nc.scalar.activation(s.v[:, t], qkv_ps[:, t % 2, 2], ACT.Copy).then_inc(v_read, 1)
                    act.wait_ge(summed, t + 1)
                    if t >= 2:
                        act.wait_ge(clipped, t - 1)
                    nc.scalar.activation(norm[:, t % 2], ss[:, t % 2], ACT.Sqrt).then_inc(normed, 1)
                if t >= 1:
                    store(t - 1)

        @block.vector
        def _(dve):
            for j in range(4):
                nc.vector.tensor_tensor(table[:, j], k.w["rotary"][:, j],
                                        k.w["L1_qk_scale"][:, depth, j].unsqueeze(1).to_broadcast([P, SEQ // P, HD2]),
                                        ALU.mult).then_inc(tables_ready, 1)
            dve.wait_ge(tables_ready, 4)
            for t in range(NT):
                dve.wait_ge(squared, t + 1)
                if t >= 2:
                    dve.wait_ge(normed, t - 1)
                nc.vector.tensor_reduce(ss[:, t % 2], heads(sq[:]), AX, ALU.add).then_inc(summed, 1)
                if t >= 2:
                    dve.wait_ge(t_ready, 2 * (t - 1))
                dve.wait_ge(qkv_ready, t + 1)
                dve.wait_ge(v_read, t + 1)
                for i in range(2):
                    ps = heads(qkv_ps[:, t % 2, i])
                    cos = table[:, 2 * i, t % (SEQ // P)].unsqueeze(1).to_broadcast([P, HEADS2, HD2])
                    sin = table[:, 2 * i + 1, t % (SEQ // P)]
                    nc.vector.tensor_tensor(heads(straight[:, t % 2, i]), ps, cos, ALU.mult).then_inc(mults, 1)
                    for half in range(2):
                        here, there = slice(half * HALF, (half + 1) * HALF), slice((1 - half) * HALF, (2 - half) * HALF)
                        last = nc.vector.tensor_tensor(
                            heads(crossed[:, t % 2, i])[:, :, here], ps[:, :, there],
                            sin[:, here].unsqueeze(1).to_broadcast([P, HEADS2, HALF]), ALU.mult)
                    last.then_inc(mults, 1)
                dve.wait_ge(normed, t + 1)
                nc.vector.tensor_scalar(norm[:, t % 2], norm[:, t % 2], NORM_EPS, None, ALU.max).then_inc(clipped, 1)
                dve.wait_ge(clipped, t + 1)
                if t >= 2:
                    dve.wait_ge(k_scaled, t - 1)
                nc.vector.reciprocal(rk[:, t % 2], norm[:, t % 2]).then_inc(rk_ready, 1)
                dve.wait_ge(rk_ready, t + 1)
                nc.vector.tensor_scalar(s.rq[:, t], rk[:, t % 2, 0:HEADS2], QK_SCALE, None, ALU.mult)

        @block.gpsimd
        def _(pool):
            for t in range(NT):
                for i, done in enumerate((sums_q, sums_k)):
                    pool.wait_ge(mults, 4 * t + 2 * i + 2)
                    nc.gpsimd.tensor_tensor(turned[:, t % 2, i], straight[:, t % 2, i], crossed[:, t % 2, i],
                                            ALU.add).then_inc(done, 1)
                pool.wait_ge(rk_ready, t + 1)
                pool.wait_ge(sums_k, t + 1)
                nc.gpsimd.tensor_tensor(heads(turned[:, t % 2, 1]), heads(turned[:, t % 2, 1]),
                                        rk[:, t % 2, HEADS2:].unsqueeze(2).to_broadcast([P, HEADS2, HD2]),
                                        ALU.mult).then_inc(k_scaled, 1)


def local_attention_stage(nc, k, s, depth):
    tag = f"_la{depth}"
    PAIRS = HEADS2 // 2
    units = [(t, p) for t in range(NT) for p in range(PAIRS)]
    U = len(units)
    first_tile = lambda t: t % (SEQ // P) == 0
    KW = 2 * P
    with ExitStack() as ctx:
        sb = lambda name, shape, dt=F32: ctx.enter_context(nc.sbuf_tensor(name + tag, shape, dt))
        mx, bias, total = sb("mx", [P, 4, 2]), sb("bias", [P, 4, 2]), sb("total", [P, 2, HEADS2])
        prob, probT = sb("prob", [P, 2, 2, KW]), sb("probT", [P, 2, 2, KW])
        inv, o = sb("inv", [P, 2, HEADS2]), sb("o", [P, 2, INNER])
        s_ps = ctx.enter_context(nc.psum_tensor("s_ps" + tag, [P, 2, 2, CH], F32))
        p_ps = ctx.enter_context(nc.psum_tensor("p_ps" + tag, [P, 2, 2, KW], F32))
        o_ps = ctx.enter_context(nc.psum_tensor("o_ps" + tag, [P, HEADS2, HD2], F32))
        t_ps = ctx.enter_context(nc.psum_tensor("ot_ps" + tag, [P, QT, P], F32))
        sem = lambda name: nc.alloc_semaphore(name + tag)
        s_ready, mx_ready, bias_ready, prob_ready, p_turned, probT_ready, o_ready = (
            sem("s"), sem("mx"), sem("bias"), sem("prob"), sem("p_turned"), sem("probT"), sem("o"))
        inv_ready, o_scaled, o_turned, oT_ready = sem("inv"), sem("o_scaled"), sem("o_turned"), sem("oT")
        block = ctx.enter_context(nc.Block())

        def blocks(t):
            return ((1, t),) if first_tile(t) else ((0, t - 1), (1, t))

        @block.tensor
        def _(pe):
            def scores(u):
                t, p = units[u]
                lo = P if first_tile(t) else 0
                if u >= 2:
                    pe.wait_ge(prob_ready, u - 1)
                for i in range(2):
                    d = slice(HD2 * i, HD2 * i + HD2)
                    out = s_ps[:, u % 2, i, lo:KW]
                    nc.tensor.matmul(out, s.qT[d, p, tile(t)], s.kT[d, p, t * P - P + lo:(t + 1) * P],
                                     start=True, stop=False)
                    last = nc.tensor.matmul(out, k.w["ident16"][:], k.w["window_mask"][:, lo:KW],
                                            start=False, stop=True)
                last.then_inc(s_ready, 1)

            def turn(u):
                t, p = units[u]
                pe.wait_ge(prob_ready, u + 1)
                if u >= 2:
                    pe.wait_ge(probT_ready, u - 1)
                for i in range(2):
                    for at, _ in blocks(t):
                        last = nc.tensor.transpose(p_ps[:, u % 2, i, tile(at)], prob[:, u % 2, i, tile(at)],
                                                   k.w["ident"][:])
                last.then_inc(p_turned, 1)

            def values(u):
                t, p = units[u]
                pe.wait_ge(probT_ready, u + 1)
                if p == 0 and t >= 1:
                    pe.wait_ge(o_scaled, t)
                for i in range(2):
                    h = 2 * p + i
                    for n, (at, kt) in enumerate(blocks(t)):
                        last = nc.tensor.matmul(o_ps[:, h], probT[:, u % 2, i, tile(at)],
                                                s.v[:, kt, h * HD2:(h + 1) * HD2],
                                                start=n == 0, stop=at == 1)
                last.then_inc(o_ready, 1)

            def turn_out(t):
                pe.wait_ge(o_scaled, t + 1)
                if t >= 1:
                    pe.wait_ge(oT_ready, t)
                for j in range(QT):
                    last = nc.tensor.transpose(t_ps[:, j], o[:, t % 2, tile(j)], k.w["ident"][:])
                last.then_inc(o_turned, 1)

            for u in range(U + 2):
                if u < U:
                    scores(u)
                if 1 <= u <= U:
                    turn(u - 1)
                if u >= 2:
                    values(u - 2)
                if u >= 2 + PAIRS and (u - 2) % PAIRS == 0:
                    turn_out((u - 2) // PAIRS - 1)
            turn_out(NT - 1)

        @block.scalar
        def _(act):
            for u, (t, p) in enumerate(units):
                lo = P if first_tile(t) else 0
                act.wait_ge(bias_ready, u + 1)
                if u >= 2:
                    act.wait_ge(p_turned, u - 1)
                if p == 0 and t >= 2:
                    act.wait_ge(inv_ready, t - 1)
                for i in range(2):
                    h = 2 * p + i
                    last = nc.scalar.activation(prob[:, u % 2, i, lo:KW], s_ps[:, u % 2, i, lo:KW], ACT.Exp,
                                                bias=bias[:, u % 4, i:i + 1], scale=s.rq[:, t, h:h + 1],
                                                accum_out=total[:, t % 2, h:h + 1])
                last.then_inc(prob_ready, 1)
                if p == 1 and t >= 1:
                    act.wait_ge(o_turned, t)
                    nc.scalar.activation(s.oT[:, :, tile(t - 1)], t_ps[:], ACT.Copy).then_inc(oT_ready, 1)
            act.wait_ge(o_turned, NT)
            nc.scalar.activation(s.oT[:, :, tile(NT - 1)], t_ps[:], ACT.Copy).then_inc(oT_ready, 1)

        @block.vector
        def _(dve):
            def maxima(u):
                t, p = units[u]
                lo = P if first_tile(t) else 0
                dve.wait_ge(s_ready, u + 1)
                if u >= 4:
                    dve.wait_ge(bias_ready, u - 3)
                nc.vector.tensor_reduce(mx[:, u % 4], s_ps[:, u % 2, :, lo:KW], AX, ALU.max).then_inc(mx_ready, 1)
                dve.wait_ge(mx_ready, u + 1)
                if u >= 4:
                    dve.wait_ge(prob_ready, u - 3)
                nc.vector.scalar_tensor_tensor(out=bias[:, u % 4], in0=mx[:, u % 4], scalar=-1.0,
                                               in1=s.rq[:, t, 2 * p:2 * p + 2], op0=ALU.mult,
                                               op1=ALU.mult).then_inc(bias_ready, 1)

            def normalise(t):
                dve.wait_ge(prob_ready, (t + 1) * PAIRS)
                if t >= 2:
                    dve.wait_ge(o_scaled, t - 1)
                nc.vector.reciprocal(inv[:, t % 2], total[:, t % 2]).then_inc(inv_ready, 1)
                dve.wait_ge(inv_ready, t + 1)
                dve.wait_ge(o_ready, (t + 1) * PAIRS)
                if t >= 2:
                    dve.wait_ge(o_turned, t - 1)
                nc.vector.tensor_tensor(o[:, t % 2].rearrange("p (h d) -> p h d", d=HD2), o_ps[:],
                                        inv[:, t % 2].unsqueeze(2).to_broadcast([P, HEADS2, HD2]),
                                        ALU.mult).then_inc(o_scaled, 1)

            for u in range(U + 1):
                if u < U:
                    maxima(u)
                if u >= 1:
                    t, _ = units[u - 1]
                    lo = P if first_tile(t) else 0
                    dve.wait_ge(p_turned, u)
                    if u >= 3:
                        dve.wait_ge(o_ready, u - 2)
                    nc.vector.tensor_copy(probT[:, (u - 1) % 2, :, lo:KW], p_ps[:, (u - 1) % 2, :, lo:KW]
                                          ).then_inc(probT_ready, 1)
                if u % PAIRS == 0 and u >= PAIRS:
                    normalise(u // PAIRS - 1)


def local_out_stage(nc, k, s, depth):
    with ExitStack() as ctx:
        o_ps = ctx.enter_context(nc.psum_tensor(f"wo_ps{depth}", [P, NCH, CH], F32))
        out_ready = nc.alloc_semaphore(f"wo_ready{depth}")
        added = nc.alloc_semaphore(f"wo_added{depth}")
        block = ctx.enter_context(nc.Block())

        @block.tensor
        def _(pe):
            for c in range(NCH):
                for j in range(QT):
                    last = nc.tensor.matmul(o_ps[:, c], k.w["L1_wo"][:, depth, j], s.oT[:, j, chunk(c)],
                                            start=j == 0, stop=j == QT - 1)
                last.then_inc(out_ready, 1)

        @block.vector
        def _(dve):
            for c in range(NCH):
                dve.wait_ge(out_ready, c + 1)
                nc.vector.tensor_tensor(k.h[:, chunk(c)], k.h[:, chunk(c)], o_ps[:, c], ALU.add).then_inc(added, 1)


def hidden_stage(nc, k, s, depth):
    tag = f"_hd{depth}"
    tiles = [(m, min(P, HID - m * P)) for m in range(-(-HID // P))]
    M = len(tiles)
    units = [(c, m) for c in range(NCH) for m in range(M)]
    U = len(units)
    w1, w2, b1, b2 = k.w["L1_w1"], k.w["L1_w2"], k.w["L1_b1"], k.w["L1_b2"]
    with ExitStack() as ctx:
        sb = lambda name, shape: ctx.enter_context(nc.sbuf_tensor(name + tag, shape, F32))
        gelu, hid = sb("gelu", [P, 2, CH]), sb("hid", [P, 3, CH])
        a_ps = ctx.enter_context(nc.psum_tensor("a_ps" + tag, [P, 2, CH], F32))
        g_ps = ctx.enter_context(nc.psum_tensor("g_ps" + tag, [P, 2, CH], F32))
        o_ps = ctx.enter_context(nc.psum_tensor("o_ps" + tag, [P, 2, CH], F32))
        sem = lambda name: nc.alloc_semaphore(name + tag)
        g_ready, a_ready, gelu_ready, hid_ready, down_done, h_ready, x_ready = (
            sem("g"), sem("a"), sem("gelu"), sem("hid"), sem("down"), sem("h"), sem("x"))
        block = ctx.enter_context(nc.Block())

        @block.tensor
        def _(pe):
            def up(u):
                c, m = units[u]
                n = tiles[m][1]
                if u >= 2:
                    pe.wait_ge(gelu_ready, u - 1)
                    pe.wait_ge(hid_ready, u - 1)
                nc.tensor.matmul(g_ps[0:n, u % 2], w1[:, depth, HID + m * P:HID + m * P + n], s.normed[:, chunk(c)],
                                 start=True, stop=True).then_inc(g_ready, 1)
                nc.tensor.matmul(a_ps[0:n, u % 2], w1[:, depth, m * P:m * P + n], s.normed[:, chunk(c)],
                                 start=True, stop=True).then_inc(a_ready, 1)

            def down(u):
                c, m = units[u]
                n = tiles[m][1]
                pe.wait_ge(hid_ready, u + 1)
                if m == 0 and c >= 2:
                    pe.wait_ge(h_ready, c - 1)
                nc.tensor.matmul(o_ps[:, c % 2], w2[0:n, depth, m], hid[0:n, u % 3],
                                 start=m == 0, stop=m == M - 1).then_inc(down_done, 1)

            for u in range(U + 2):
                if u < U:
                    up(u)
                if u >= 2:
                    down(u - 2)

        @block.scalar
        def _(act):
            for u, (c, m) in enumerate(units):
                n = tiles[m][1]
                act.wait_ge(g_ready, u + 1)
                if u >= 2:
                    act.wait_ge(hid_ready, u - 1)
                nc.scalar.activation(gelu[0:n, u % 2], g_ps[0:n, u % 2], ACT.Gelu,
                                     bias=b1[0:n, depth, 1, m:m + 1]).then_inc(gelu_ready, 1)

        @block.vector
        def _(dve):
            def add(c):
                b = batch_of(c)
                dve.wait_ge(down_done, (c + 1) * M)
                nc.vector.scalar_tensor_tensor(out=k.h[:, chunk(c)], in0=o_ps[:, c % 2], scalar=b2[:, depth:depth + 1],
                                               in1=k.h[:, chunk(c)], op0=ALU.add, op1=ALU.add).then_inc(h_ready, 1)
                if depth == DEPTH - 1:
                    dve.wait_ge(h_ready, c + 1)
                    nc.vector.scalar_tensor_tensor(out=k.x[:, chunk(c)], in0=k.h[:, chunk(c)],
                                                   scalar=k.mod[:, 1, GATE_B, b:b + 1], in1=k.x[:, chunk(c)],
                                                   op0=ALU.mult, op1=ALU.add).then_inc(x_ready, 1)

            for u, (c, m) in enumerate(units):
                n = tiles[m][1]
                dve.wait_ge(a_ready, u + 1)
                dve.wait_ge(gelu_ready, u + 1)
                if u >= 3:
                    dve.wait_ge(down_done, u - 2)
                nc.vector.scalar_tensor_tensor(out=hid[0:n, u % 3], in0=a_ps[0:n, u % 2],
                                               scalar=b1[0:n, depth, 0, m:m + 1], in1=gelu[0:n, u % 2],
                                               op0=ALU.add, op1=ALU.mult).then_inc(hid_ready, 1)
                if m == 1 and c >= 1:
                    add(c - 1)
            add(NCH - 1)


def local_block(nc, k):
    for depth in range(DEPTH):
        with ExitStack() as ctx:
            sb = lambda name, shape: ctx.enter_context(nc.sbuf_tensor(f"{name}_lb{depth}", shape, F32))
            s = Kit()
            s.shifted, s.qT = sb("shifted", [P, T]), sb("qT", [P, QT, T])
            s.oT = s.qT
            with (nc.sbuf_tensor(f"kT{depth}", [P, QT, T], F32) as s.kT,
                  nc.sbuf_tensor(f"v{depth}", [P, NT, INNER], F32) as s.v,
                  nc.sbuf_tensor(f"rq{depth}", [P, NT, HEADS2], F32) as s.rq):
                shift_stage(nc, k, depth, 0, s.shifted)
                local_qkv_stage(nc, k, s, depth)
                local_attention_stage(nc, k, s, depth)
            local_out_stage(nc, k, s, depth)
            shift_stage(nc, k, depth, 1, s.shifted)
            s.normed = sb("normed", [P, T])
            layernorm_stage(nc, k, f"l{depth}", s.shifted, s.normed,
                            lambda b: (k.w["L1_ln"][:, 0, depth:depth + 1], k.w["L1_ln"][:, 1, depth:depth + 1]))
            hidden_stage(nc, k, s, depth)

HEADS3 = 16
HD3 = P // HEADS3
NH3 = NB * HEADS3
QTS = SEQ // P
Q_PART = (0, 0, 1, 1, 0, 2)
K_PART = (0, 1, 0, 1, 2, 0)
SLOTS = len(Q_PART)
ROWS = SLOTS * HD3
M_PARTS = 2
RING = 4
AHEAD = 2
V1 = HD3 + 1


def causal_project_stage(nc, k, s):
    with ExitStack() as ctx:
        rest = ctx.enter_context(nc.sbuf_tensor("rest_cp", [P, 2, 2, CH], F32))
        part = ctx.enter_context(nc.sbuf_tensor("part_cp", [P, 2, PARTS, T], BF16))
        qk_ps = ctx.enter_context(nc.psum_tensor("qk_ps_cp", [P, 4, CH], F32))
        v_ps = ctx.enter_context(nc.psum_tensor("v_ps_cp", [P, 2, CH], F32))
        sem = lambda name: nc.alloc_semaphore(name + "_cp")
        qk_ready, part0, rest_ready, part1, part2, v_ready, v_stored, ones_ready, stored = (
            sem("qk"), sem("part0"), sem("rest"), sem("part1"), sem("part2"), sem("v"), sem("v_stored"), sem("ones"),
            sem("stored"))
        block = ctx.enter_context(nc.Block())
        units = [(c, i) for c in range(NCH) for i in range(2)]

        @block.tensor
        def _(pe):
            for u, (c, i) in enumerate(units):
                if u >= 4:
                    pe.wait_ge(rest_ready, u - 3)
                nc.tensor.matmul(qk_ps[:, u % 4], k.w["L2_W"][:, i], k.h[:, chunk(c)],
                                 start=True, stop=True).then_inc(qk_ready, 1)
            for t in range(NT):
                if t >= 2:
                    pe.wait_ge(v_stored, t - 1)
                nc.tensor.matmul(v_ps[:, t % 2, 0:P], k.h[:, tile(t)], k.w["L2_W"][:, 2],
                                 start=True, stop=True).then_inc(v_ready, 1)

        @block.scalar
        def _(act):
            for u, (c, i) in enumerate(units):
                act.wait_ge(qk_ready, u + 1)
                nc.scalar.activation(part[:, i, 0, chunk(c)], qk_ps[:, u % 4], ACT.Copy).then_inc(part0, 1)
            act.wait_ge(ones_ready, 1)
            for t in range(NT):
                b, kt = divmod(t, QTS)
                act.wait_ge(v_ready, t + 1)
                nc.scalar.activation(s.v1[:, b * HEADS3:(b + 1) * HEADS3, kt, 0:HD3],
                                     v_ps[:, t % 2, 0:P].rearrange("p (h d) -> p h d", d=HD3),
                                     ACT.Copy).then_inc(v_stored, 1)

        @block.vector
        def _(dve):
            nc.vector.memset(s.v1[:], 1.0).then_inc(ones_ready, 1)
            for u, (c, i) in enumerate(units):
                dve.wait_ge(part0, u + 1)
                if u >= 2:
                    dve.wait_ge(part2, u - 1)
                nc.vector.tensor_tensor(rest[:, u % 2, 0], qk_ps[:, u % 4], part[:, i, 0, chunk(c)],
                                        ALU.subtract).then_inc(rest_ready, 1)
                dve.wait_ge(rest_ready, u + 1)
                nc.vector.tensor_copy(part[:, i, 1, chunk(c)], rest[:, u % 2, 0]).then_inc(part1, 1)

        @block.gpsimd
        def _(pool):
            for u, (c, i) in enumerate(units):
                pool.wait_ge(part1, u + 1)
                nc.gpsimd.tensor_tensor(part[:, i, 2, chunk(c)], rest[:, u % 2, 0], part[:, i, 1, chunk(c)],
                                        ALU.subtract).then_inc(part2, 1)

        @block.sync
        def _(sp):
            for r in range(RING):
                sp.dma_start(s.ks[ROWS:ROWS + M_PARTS, r], k.dram["ones_rows"]).then_inc(stored, 16)
            sp.wait_ge(part2, len(units))
            for i, (order, dst) in enumerate(((Q_PART, s.q_dram), (K_PART, s.k_dram))):
                for slot, n in enumerate(order):
                    sp.dma_start(dst[slot].rearrange("(b p) n -> p b n", b=NB),
                                 part[:, i, n].rearrange("p (b n) -> p b n", b=NB)).then_inc(stored, 16)
            sp.wait_ge(stored, 16 * (RING + 2 * SLOTS))


def causal_attention_stage(nc, k, s):
    a_units = [(qt, kc) for qt in range(QTS) for kc in range(2) if kc * 4 <= qt]
    b_units = [(j, kt) for j in range(2) for kt in range(4 * j + 4)]
    A, B = len(a_units), len(b_units)
    scale = 1.0 / HD3 ** 0.5
    PT = 3
    with ExitStack() as ctx:
        sb = lambda name, shape, dt=F32: ctx.enter_context(nc.sbuf_tensor(name + "_ca", shape, dt))
        prob, mx = sb("prob", [P, PT, CH]), sb("mx", [P, 2, 2, QTS])
        m16, ms, mrow = sb("m16", [P, 2, QTS], BF16), sb("ms", [P, 2, M_PARTS, QTS]), sb("mrow", [M_PARTS * QTS, RING, P], BF16)
        vh, inv, zero = sb("vh", [P, RING, QTS, V1]), sb("inv", [P, 2, QTS, 1]), sb("zero", [P, P], BF16)
        a_ps = ctx.enter_context(nc.psum_tensor("a_ps_ca", [P, 2, CH], F32))
        b_ps = ctx.enter_context(nc.psum_tensor("b_ps_ca", [P, 2, CH], F32))
        o_ps = ctx.enter_context(nc.psum_tensor("o_ps_ca", [P, 2, CH], F32))
        t_ps = ctx.enter_context(nc.psum_tensor("t_ps_ca", [P, CH], F32))
        sem = lambda name: nc.alloc_semaphore(name + "_ca")
        loaded = [sem(f"loaded{r}") for r in range(RING)]
        m_loaded = [sem(f"m_loaded{r}") for r in range(RING)]
        zero_ready, a_ready, max_done, m_step, split_ready, m_turned, mrow_ready = (
            sem("zero"), sem("a"), sem("max"), sem("m_step"), sem("split"), sem("m_turned"), sem("mrow"))
        b_ready, exp_done, pv_done, v_ready, inv_ready, y_done = (
            sem("b"), sem("exp"), sem("pv"), sem("v"), sem("inv"), sem("y"))
        C_MAX = C_EXP = C_Y = C_TURN = 2
        C_PV, C_SPLIT, C_MROW = PT, 2, 1
        block = ctx.enter_context(nc.Block())
        width = lambda qt, kc: min(4, qt + 1 - 4 * kc) * P
        LOOPS = NH3 // RING - 1
        head = lambda it, r: it * RING + r
        behind = lambda it: isinstance(it, int) and it == LOOPS

        def whole(engine, body, before=None):
            if before is not None:
                before()
            with engine.Fori(0, LOOPS, 1) as it:
                for r in range(RING):
                    body(it, r, False)
            for r in range(RING):
                body(LOOPS, r, r >= RING - AHEAD)

        def of(it, r, off):
            return (it + (r + off) // RING, (r + off) % RING)

        @block.sync
        def _(sp):
            def load(it, r):
                src = lambda dram: dram[:, bass.ds(head(it, r) * HD3, HD3)]
                sp.dma_start(s.qs[0:ROWS, r], src(s.q_dram)).then_inc(loaded[r], 16)
                sp.dma_start(s.ks[0:ROWS, r], src(s.k_dram)).then_inc(loaded[r], 16)

            def maximum_rows(it, r):
                sp.wait_ge(mrow_ready, head(it, r) + 1 + C_MROW)
                sp.dma_start(s.qs[ROWS:ROWS + M_PARTS, r], mrow[:, r]).then_inc(m_loaded[r], 16)

            def before():
                for r in range(AHEAD + 1):
                    load(0, r)
                maximum_rows(0, 0)

            def body(it, r, last):
                if not (behind(it) and r >= 1):
                    sp.wait_ge(b_ready, head(it, r) * B)
                    load(*of(it, r, AHEAD + 1))
                if not (behind(it) and r == RING - 1):
                    maximum_rows(*of(it, r, 1))

            whole(sp, body, before)

        @block.tensor
        def _(pe):
            def scores(it, r, i):
                qt, kc = a_units[i]
                w = width(qt, kc)
                if i == 0:
                    pe.wait_ge(loaded[r], it * 32 + 32)
                pe.wait_ge(max_done, head(it, r) * A + (i - 2 + 1 + C_MAX))
                diagonal = qt // 4 == kc
                last = nc.tensor.matmul(a_ps[:, i % 2, 0:w], s.qs[0:ROWS, r, tile(qt)],
                                        s.ks[0:ROWS, r, kc * CH:kc * CH + w], start=True, stop=not diagonal)
                if diagonal:
                    last = nc.tensor.matmul(a_ps[:, i % 2, w - P:w], k.w["ident16"][:], k.w["causal_mask"][:, 0],
                                            start=False, stop=True)
                last.then_inc(a_ready, 1)

            def turn_maxima(it, r):
                pe.wait_ge(split_ready, head(it, r) + 1 + C_SPLIT)
                pe.wait_ge(mrow_ready, head(it, r) + C_MROW)
                nc.tensor.transpose(t_ps[0:M_PARTS * QTS, 0:P], ms[:, r % 2].rearrange("p m t -> p (m t)"),
                                    k.w["ident"][:]).then_inc(m_turned, 1)

            def scores_t(it, r, i):
                j, kt = b_units[i]
                lo = max(0, kt - 4 * j) * P
                if i == 0:
                    pe.wait_ge(m_loaded[r], it * 16 + 16)
                pe.wait_ge(exp_done, head(it, r) * B + (i - 2 + 1 + C_EXP))
                diagonal = kt >= 4 * j
                last = nc.tensor.matmul(b_ps[:, i % 2, lo:CH], s.ks[0:ROWS + M_PARTS, r, tile(kt)],
                                        s.qs[0:ROWS + M_PARTS, r, j * CH + lo:(j + 1) * CH],
                                        start=True, stop=not diagonal)
                if diagonal:
                    last = nc.tensor.matmul(b_ps[:, i % 2, lo:lo + P], k.w["ident16"][:], k.w["causal_mask"][:, 1],
                                            start=False, stop=True)
                last.then_inc(b_ready, 1)

            def values(it, r, i):
                j, kt = b_units[i]
                if i == 0:
                    pe.wait_ge(y_done, head(it, r) + (1 - 2 + C_Y))
                    nc.tensor.matmul(o_ps[:, r % 2, 0:QTS * V1], zero[:], k.w["ident16"][:, 0:QTS * V1],
                                     start=True, stop=True, skip_group_check=True)
                    pe.wait_ge(v_ready, head(it, r) + 1)
                pe.wait_ge(exp_done, head(it, r) * B + (i + 1 + C_EXP))
                for q in range(max(0, kt - 4 * j), 4):
                    qt = 4 * j + q
                    last = nc.tensor.matmul(o_ps[:, r % 2, qt * V1:(qt + 1) * V1], prob[:, i % PT, tile(q)],
                                            vh[:, r, kt], start=False, stop=True, skip_group_check=True)
                last.then_inc(pv_done, 1)

            def before():
                pe.sem_inc(m_turned, C_TURN)
                pe.wait_ge(zero_ready, 1)
                for r in range(AHEAD):
                    for i in range(A):
                        scores(0, r, i)
                    if r == 1:
                        turn_maxima(0, 0)

            def body(it, r, last):
                for i in range(B + 2):
                    if i < A and not last:
                        scores(*of(it, r, AHEAD), i)
                    if i < B:
                        scores_t(it, r, i)
                    if i == 3 and not (behind(it) and r == RING - 1):
                        turn_maxima(*of(it, r, 1))
                    if i >= 2:
                        values(it, r, i - 2)

            whole(pe, body, before)

        @block.scalar
        def _(act):
            def maxima_row(it, r):
                act.wait_ge(m_turned, head(it, r) + (1 + C_TURN))
                act.wait_ge(m_loaded[r], it * 16)
                nc.scalar.activation(mrow[:, r], t_ps[0:M_PARTS * QTS, 0:P], ACT.Copy).then_inc(mrow_ready, 1)

            def before():
                act.sem_inc(exp_done, C_EXP)
                act.sem_inc(mrow_ready, C_MROW)
                maxima_row(0, 0)

            def body(it, r, last):
                for i, (j, kt) in enumerate(b_units):
                    lo = max(0, kt - 4 * j) * P
                    act.wait_ge(b_ready, head(it, r) * B + (i + 1))
                    act.wait_ge(pv_done, head(it, r) * B + (i - PT + 1 + C_PV))
                    nc.scalar.activation(prob[:, i % PT, lo:CH], b_ps[:, i % 2, lo:CH], ACT.Exp,
                                         scale=scale).then_inc(exp_done, 1)
                    if i == 4 and not (behind(it) and r == RING - 1):
                        maxima_row(*of(it, r, 1))

            whole(act, body, before)

        @block.gpsimd
        def _(pool):
            def take(it, r):
                nc.gpsimd.tensor_copy(vh[:, r], s.v1[:, bass.ds(head(it, r), 1)].rearrange("p o t d -> p (o t) d")
                                      ).then_inc(v_ready, 1)

            def before():
                for r in range(AHEAD):
                    take(0, r)

            def body(it, r, last):
                if not last:
                    pool.wait_ge(y_done, head(it, r) + (1 - 2 + C_Y))
                    pool.wait_ge(zero_ready, 1)
                    take(*of(it, r, AHEAD))

            whole(pool, body, before)

        @block.vector
        def _(dve):
            def maximum(it, r, i):
                qt, kc = a_units[i]
                if i == 0:
                    dve.wait_ge(split_ready, head(it, r) + (1 - 2 + C_SPLIT))
                dve.wait_ge(a_ready, head(it, r) * A + (i + 1))
                nc.vector.tensor_reduce(mx[:, r % 2, kc, qt:qt + 1], a_ps[:, i % 2, 0:width(qt, kc)], AX,
                                        ALU.max).then_inc(max_done, 1)

            def split(it, r):
                n = head(it, r) * 3
                m = mx[:, r % 2, 0]
                dve.wait_ge(max_done, head(it, r) * A + (A + C_MAX))
                nc.vector.tensor_tensor(m[:, 4:], m[:, 4:], mx[:, r % 2, 1, 4:], ALU.max).then_inc(m_step, 1)
                dve.wait_ge(m_step, n + 1)
                nc.vector.tensor_scalar(m16[:, r % 2], m, -1.0, None, ALU.mult).then_inc(m_step, 1)
                dve.wait_ge(m_step, n + 2)
                dve.wait_ge(m_turned, head(it, r) + (1 - 2 + C_TURN))
                nc.vector.tensor_copy(ms[:, r % 2, 0], m16[:, r % 2]).then_inc(m_step, 1)
                dve.wait_ge(m_step, n + 3)
                nc.vector.scalar_tensor_tensor(out=ms[:, r % 2, 1], in0=m, scalar=-1.0, in1=m16[:, r % 2],
                                               op0=ALU.mult, op1=ALU.subtract).then_inc(split_ready, 1)

            def normalise(it, r):
                o = o_ps[:, r % 2, 0:QTS * V1].rearrange("p (t d) -> p t d", d=V1)
                dve.wait_ge(y_done, head(it, r) + (1 - 2 + C_Y))
                dve.wait_ge(pv_done, head(it, r) * B + (B + C_PV))
                nc.vector.reciprocal(inv[:, r % 2], o[:, :, HD3:]).then_inc(inv_ready, 1)
                dve.wait_ge(inv_ready, head(it, r) + 1)
                quads = HEADS3 // RING
                b, h = it // quads, it % quads * RING + r
                y = s.y[:, bass.ds(b, 1), :, bass.ds(h, 1)].rearrange("p o t u d -> p (o t u) d")
                nc.vector.tensor_tensor(y,
                                        o[:, :, 0:HD3], inv[:, r % 2].to_broadcast([P, QTS, HD3]),
                                        ALU.mult).then_inc(y_done, 1)

            def before():
                nc.vector.memset(zero[:], 0.0).then_inc(zero_ready, 1)
                dve.sem_inc(max_done, C_MAX)
                dve.sem_inc(split_ready, C_SPLIT)
                dve.sem_inc(y_done, C_Y)
                dve.sem_inc(pv_done, C_PV)
                for r in range(AHEAD):
                    for i in range(A):
                        maximum(0, r, i)
                    split(0, r)

            def body(it, r, last):
                if not last:
                    for i in range(A):
                        maximum(*of(it, r, AHEAD), i)
                    split(*of(it, r, AHEAD))
                normalise(it, r)

            whole(dve, body, before)


def causal_out_stage(nc, k, s):
    with ExitStack() as ctx:
        yT = ctx.enter_context(nc.sbuf_tensor("yT_co", [P, T], F32))
        t_ps = ctx.enter_context(nc.psum_tensor("t_ps_co", [P, NCH, CH], F32))
        o_ps = ctx.enter_context(nc.psum_tensor("o_ps_co", [P, NCH, CH], F32))
        turned, yT_ready, out_ready, added = (
            nc.alloc_semaphore(n + "_co") for n in ("turned", "yT", "out", "added"))
        block = ctx.enter_context(nc.Block())

        @block.tensor
        def _(pe):
            for c in range(NCH + 1):
                if c < NCH:
                    for j in range(CH // P):
                        b, qt = divmod(c * (CH // P) + j, QTS)
                        last = nc.tensor.transpose(t_ps[:, c, tile(j)], s.y[:, b, qt].rearrange("p h d -> p (h d)"),
                                                   k.w["ident"][:])
                    last.then_inc(turned, 1)
                if c >= 1:
                    pe.wait_ge(yT_ready, c)
                    nc.tensor.matmul(o_ps[:, c - 1], k.w["L2_W"][:, 3], yT[:, chunk(c - 1)],
                                     start=True, stop=True).then_inc(out_ready, 1)

        @block.scalar
        def _(act):
            for c in range(NCH):
                act.wait_ge(turned, c + 1)
                nc.scalar.activation(yT[:, chunk(c)], t_ps[:, c], ACT.Copy).then_inc(yT_ready, 1)

        @block.vector
        def _(dve):
            for c in range(NCH):
                b = batch_of(c)
                dve.wait_ge(out_ready, c + 1)
                nc.vector.scalar_tensor_tensor(out=k.x[:, chunk(c)], in0=o_ps[:, c],
                                               scalar=k.mod[:, 2, GATE_A, b:b + 1], in1=k.x[:, chunk(c)],
                                               op0=ALU.mult, op1=ALU.add).then_inc(added, 1)


def causal_attention_block(nc, k):
    with ExitStack() as ctx:
        s = Kit()
        s.y = ctx.enter_context(nc.sbuf_tensor("y3", [P, NB, QTS, HEADS3, HD3], F32))
        s.q_dram = nc.dram_tensor("q_parts", [SLOTS, NB * P, SEQ], BF16).ap()
        s.k_dram = nc.dram_tensor("k_parts", [SLOTS, NB * P, SEQ], BF16).ap()
        with (nc.sbuf_tensor("qs", [ROWS + M_PARTS, RING, SEQ], BF16) as s.qs,
              nc.sbuf_tensor("ks", [ROWS + M_PARTS, RING, SEQ], BF16) as s.ks,
              nc.sbuf_tensor("v1_ca", [P, NH3, QTS, V1], F32) as s.v1):
            causal_project_stage(nc, k, s)
            causal_attention_stage(nc, k, s)
        causal_out_stage(nc, k, s)



EPS_SUM = 1e-7
EPS_NORM = 1e-12


def linear_attention_block(nc, k):
    TPR = SEQ // P
    with ExitStack() as ctx:
        sb = lambda name, shape: ctx.enter_context(nc.sbuf_tensor(name + "_li", shape, F32))
        w, bias, mean = sb("w", [P, 3 * P]), sb("bias", [P, 3 * P]), sb("mean", [P, 4])
        qkv, q2, k2 = sb("qkv", [P, 2, 3 * P]), sb("q2", [P, NT, P]), sb("k2", [P, NT, P])
        v, q4 = sb("v", [P, NT, P]), sb("q4", [P, P])
        sums = sb("sums", [P, 3, NT])
        f = sb("f", [P, 6, NT])
        qT, kv, kn, kf, y, o = (sb("qT", [P, T]), sb("kv", [P, NB, P]), sb("kn", [P, NB]), sb("kf", [P, NB]),
                                sb("y", [P, 2, CH]), sb("o", [P, 2, CH]))
        gb = sb("gate_bias", [P, NB])
        sem = lambda name: nc.alloc_semaphore(name + "_li")

        with ExitStack() as first:
            ps = first.enter_context(nc.psum_tensor("qkv_ps_li", [P, 2, CH], F32))
            centered, qkv_ready, biased, q_squared, k_squared, summed = (
                sem("centered"), sem("qkv"), sem("biased"), sem("q_squared"), sem("k_squared"), sem("summed"))
            block = first.enter_context(nc.Block())

            @block.tensor
            def _(pe):
                pe.wait_ge(centered, 5)
                for t in range(NT):
                    if t >= 2:
                        pe.wait_ge(biased, t - 1)
                    nc.tensor.matmul(ps[:, t % 2, 0:3 * P], k.h[:, tile(t)], w[:], start=True, stop=True).then_inc(qkv_ready, 1)

            @block.vector
            def _(dve):
                blocks = lambda ap: ap.rearrange("p (i n) -> p i n", n=P)
                for j, src in enumerate((k.w["L3_Wqkv"], k.w["L3_bqkv"])):
                    nc.vector.tensor_reduce(mean[:, 2 * j:2 * j + 2], blocks(src[:, 0:2 * P]), AX, ALU.add).then_inc(centered, 1)
                dve.wait_ge(centered, 2)
                nc.vector.tensor_scalar(mean[:], mean[:], 1.0 / P, None, ALU.mult).then_inc(centered, 1)
                dve.wait_ge(centered, 3)
                for j, (src, dst) in enumerate(((k.w["L3_Wqkv"], w), (k.w["L3_bqkv"], bias))):
                    nc.vector.tensor_copy(dst[:, 2 * P:], src[:, 2 * P:])
                    nc.vector.tensor_tensor(blocks(dst[:, 0:2 * P]), blocks(src[:, 0:2 * P]),
                                            mean[:, 2 * j:2 * j + 2].unsqueeze(2).to_broadcast([P, 2, P]),
                                            ALU.subtract).then_inc(centered, 1)
                dve.wait_ge(centered, 5)
                for t in range(NT):
                    dve.wait_ge(qkv_ready, t + 1)
                    if t >= 2:
                        dve.wait_ge(k_squared, t - 1)
                    nc.vector.tensor_tensor(qkv[:, t % 2], ps[:, t % 2, 0:3 * P], bias[:], ALU.add).then_inc(biased, 1)

            @block.scalar
            def _(act):
                for t in range(NT):
                    act.wait_ge(biased, t + 1)
                    if t >= 1:
                        act.wait_ge(summed, t)
                    nc.scalar.activation(q2[:, t], qkv[:, t % 2, 0:P], ACT.Square,
                                         accum_out=sums[:, 0, t:t + 1]).then_inc(q_squared, 1)
                    nc.scalar.activation(v[:, t], qkv[:, t % 2, 2 * P:3 * P], ACT.Copy)
                    nc.scalar.activation(k2[:, t], qkv[:, t % 2, P:2 * P], ACT.Square,
                                         accum_out=sums[:, 1, t:t + 1]).then_inc(k_squared, 1)
                    act.wait_ge(q_squared, t + 1)
                    nc.scalar.activation(q4[:], q2[:, t], ACT.Square, accum_out=sums[:, 2, t:t + 1]).then_inc(summed, 1)

        with ExitStack() as second:
            kv_ps = second.enter_context(nc.psum_tensor("kv_ps_li", [P, NB, CH], F32))
            kn_ps = second.enter_context(nc.psum_tensor("kn_ps_li", [P, NB, CH], F32))
            t_ps = second.enter_context(nc.psum_tensor("t_ps_li", [P, 2, CH], F32))
            step, root, k_scaled, q_scaled, k4_ready, kv_ready, q_turned, kn_root, kv_step, qT_ready = (
                sem("step"), sem("root"), sem("k_scaled"), sem("q_scaled"), sem("k4"), sem("kv"), sem("q_turned"),
                sem("kn_root"), sem("kv_step"), sem("qT"))
            k4 = second.enter_context(nc.sbuf_tensor("k4_li", [P, 2, P], F32))
            block = second.enter_context(nc.Block())

            @block.scalar
            def _(act):
                act.wait_ge(step, 1)
                nc.scalar.activation(f[:, 2], sums[:, 2], ACT.Sqrt).then_inc(root, 1)
                for t in range(NT):
                    act.wait_ge(k_scaled, t + 1)
                    if t >= 2:
                        act.wait_ge(kv_ready, t - 1)
                    nc.scalar.activation(k4[:, t % 2], k2[:, t], ACT.Square).then_inc(k4_ready, 1)
                    if t % 4 == 3:
                        c = t // 4
                        act.wait_ge(q_turned, c + 1)
                        nc.scalar.activation(qT[:, chunk(c)], t_ps[:, c % 2], ACT.Copy).then_inc(qT_ready, 1)
                act.wait_ge(kv_step, 1)
                nc.scalar.activation(kn[:], kn[:], ACT.Sqrt).then_inc(kn_root, 1)

            @block.vector
            def _(dve):
                nc.vector.tensor_scalar(f[:, 0:2], sums[:, 0:2], EPS_SUM, None, ALU.add).then_inc(step, 1)
                dve.wait_ge(step, 1)
                nc.vector.reciprocal(f[:, 0:2], f[:, 0:2]).then_inc(step, 1)
                dve.wait_ge(step, 2)
                for t in range(NT):
                    nc.vector.tensor_scalar(k2[:, t], k2[:, t], f[:, 1, t:t + 1], None, ALU.mult).then_inc(k_scaled, 1)
                dve.wait_ge(root, 1)
                nc.vector.tensor_tensor(f[:, 3], f[:, 2], f[:, 0], ALU.mult).then_inc(step, 1)
                dve.wait_ge(step, 3)
                nc.vector.tensor_scalar(f[:, 3], f[:, 3], EPS_NORM, float(SEQ) ** 0.5, ALU.max, ALU.mult).then_inc(step, 1)
                dve.wait_ge(step, 4)
                nc.vector.reciprocal(f[:, 4], f[:, 3]).then_inc(step, 1)
                dve.wait_ge(step, 5)
                nc.vector.tensor_tensor(f[:, 5], f[:, 4], f[:, 0], ALU.mult).then_inc(step, 1)
                dve.wait_ge(step, 6)
                for t in range(NT):
                    nc.vector.tensor_scalar(q2[:, t], q2[:, t], f[:, 5, t:t + 1], None, ALU.mult).then_inc(q_scaled, 1)
                dve.wait_ge(kv_ready, NT)
                for b in range(NB):
                    last = nc.vector.tensor_copy(kn[:, b:b + 1], kn_ps[:, b, 0:1])
                last.then_inc(kv_step, 1)
                dve.wait_ge(kn_root, 1)
                nc.vector.tensor_scalar(kn[:], kn[:], EPS_NORM, None, ALU.max).then_inc(kv_step, 1)
                dve.wait_ge(kv_step, 2)
                nc.vector.reciprocal(kf[:], kn[:]).then_inc(kv_step, 1)
                dve.wait_ge(kv_step, 3)
                for b in range(NB):
                    nc.vector.tensor_scalar(kv[:, b], kv_ps[:, b, 0:P], kf[:, b:b + 1], None, ALU.mult).then_inc(kv_step, 1)
                nc.vector.tensor_scalar(gb[:], k.mod[:, 3, GATE_A], k.w["L3_bln"][:], None, ALU.mult).then_inc(kv_step, 1)

            @block.tensor
            def _(pe):
                for t in range(NT):
                    b, first_t, last_t = t // TPR, t % TPR == 0, t % TPR == TPR - 1
                    pe.wait_ge(k_scaled, t + 1)
                    nc.tensor.matmul(kv_ps[:, b, 0:P], k2[:, t], v[:, t], start=first_t, stop=last_t)
                    pe.wait_ge(k4_ready, t + 1)
                    nc.tensor.matmul(kn_ps[:, b, 0:1], k4[:, t % 2], k.w["ones"][:, 0:1],
                                     start=first_t, stop=last_t).then_inc(kv_ready, 1)
                    pe.wait_ge(q_scaled, t + 1)
                    if t % 4 == 0 and t >= 8:
                        pe.wait_ge(qT_ready, t // 4 - 1)
                    last = nc.tensor.transpose(t_ps[:, t // 4 % 2, tile(t % 4)], q2[:, t], k.w["ident"][:])
                    if t % 4 == 3:
                        last.then_inc(q_turned, 1)

        y_ps = ctx.enter_context(nc.psum_tensor("y_ps_li", [P, 2, CH], F32))
        o_ps = ctx.enter_context(nc.psum_tensor("o_ps_li", [P, 2, CH], F32))
        y_ready, y_biased, o_ready, gated, added = sem("y"), sem("y_biased"), sem("o"), sem("gated"), sem("added")
        block = ctx.enter_context(nc.Block())

        @block.tensor
        def _(pe):
            for c in range(NCH + 1):
                if c < NCH:
                    if c >= 2:
                        pe.wait_ge(y_biased, c - 1)
                    nc.tensor.matmul(y_ps[:, c % 2], w[:, 2 * P:], k.h[:, chunk(c)], start=True, stop=False)
                    nc.tensor.matmul(y_ps[:, c % 2], kv[:, batch_of(c)], qT[:, chunk(c)],
                                     start=False, stop=True).then_inc(y_ready, 1)
                if c >= 1:
                    pe.wait_ge(y_biased, c)
                    if c >= 3:
                        pe.wait_ge(gated, c - 2)
                    nc.tensor.matmul(o_ps[:, (c - 1) % 2], k.w["L3_Wln"][:], y[:, (c - 1) % 2],
                                     start=True, stop=True).then_inc(o_ready, 1)

        def project(act, c):
            b = batch_of(c)
            act.wait_ge(o_ready, c + 1)
            if c >= 2:
                act.wait_ge(added, c - 1)
            nc.scalar.activation(o[:, c % 2], o_ps[:, c % 2], ACT.Identity, bias=gb[:, b:b + 1],
                                 scale=k.mod[:, 3, GATE_A, b:b + 1]).then_inc(gated, 1)

        @block.scalar
        def _(act):
            for c in range(NCH):
                act.wait_ge(y_ready, c + 1)
                if c >= 2:
                    act.wait_ge(o_ready, c - 1)
                nc.scalar.activation(y[:, c % 2], y_ps[:, c % 2], ACT.Identity, bias=k.w["L3_bv"][:, 0:1]).then_inc(y_biased, 1)
                if c >= 1:
                    project(act, c - 1)
            project(act, NCH - 1)

        @block.vector
        def _(dve):
            for c in range(NCH):
                dve.wait_ge(gated, c + 1)
                nc.vector.tensor_tensor(k.x[:, chunk(c)], k.x[:, chunk(c)], o[:, c % 2], ALU.add).then_inc(added, 1)

def store_stage(nc, k, out):
    with ExitStack() as ctx:
        stored = nc.alloc_semaphore("stored")
        block = ctx.enter_context(nc.Block())

        @block.sync
        def _(sp):
            sp.dma_start(out, k.x[:]).then_inc(stored, 16)
            sp.wait_ge(stored, 16)


FIRST = ("mean_w", "eps", "ident", "ones", "iota8", "pick")


def transformer(nc, dram, out, only=None):
    with ExitStack() as ctx:
        k = Kit()
        k.dram = dram
        k.x = ctx.enter_context(nc.sbuf_tensor("x", [P, T], F32))
        k.h = ctx.enter_context(nc.sbuf_tensor("h", [P, T], F32))
        k.mod = ctx.enter_context(nc.sbuf_tensor("mod", [P, 4, 6, NB], F32))
        k.first_loaded = nc.alloc_semaphore("first_loaded")
        k.w = {}
        for name in FIRST:
            d = dram[name]
            k.w[name] = ctx.enter_context(nc.sbuf_tensor(f"{name}_sb", list(d.shape), d.dtype))
        modulation_stage(nc, k)
        for stages in (HALF_LAYERS if only is None else only):
            stages(nc, k)
        store_stage(nc, k, out)


HALF_LAYERS = [
    half_layer(0, 0, ("L0_W_in", "L0_heads", "L0_conv", "upto", "after", "L0_D", "L0_norm_w", "L0_W_out"), mamba_block),
    half_layer(0, 1, ("L0_router", "L0_out_bias"),
               lambda nc, k: experts_block(nc, k, 0, 2, ACT.Silu, True, True, TOP_EPS)),
    half_layer(1, 0, ("L1_Wq", "L1_Wkv", "L1_Wo", "head_sum", "head_pick"), pair_attention_stage),
    half_layer(1, 1, ("ident16", "window_mask", "rotary", "L1_wqkv", "L1_qk_scale", "L1_wo", "L1_ln", "L1_w1",
                      "L1_w2", "L1_b1", "L1_b2"), local_block),
    half_layer(2, 0, ("L2_W", "ident16", "causal_mask"), causal_attention_block),
    half_layer(2, 1, (), lambda nc, k: experts_block(nc, k, 2, 4, ACT.Silu, True, False)),
    half_layer(3, 0, ("L3_Wqkv", "L3_bqkv", "L3_bv", "L3_Wln", "L3_bln"), linear_attention_block),
    half_layer(3, 1, ("L3_router", "L3_out_bias"),
               lambda nc, k: experts_block(nc, k, 3, 4, ACT.Gelu, False, True)),
]




def rotary_tables():
    f32 = np.float32
    half = np.arange(0, HD2, 2, dtype=f32)
    t = np.arange(SEQ, dtype=f32)
    freqs = np.tile(t[:, None] * (f32(1.0) / f32(10000.0) ** (half / f32(HD2)))[None], (1, 2))
    base = (half + f32(0.4 * HD2)) / f32(1.4 * HD2)
    scale = np.tile(base[None] ** ((t - SEQ // 2) / f32(WINDOW // 2))[:, None], (1, 2))
    cos, sin = np.cos(freqs), np.sin(freqs) * np.repeat(f32([-1, 1]), HALF)[None]
    tables = np.stack([cos * scale, sin * scale, cos / scale, sin / scale]).astype(f32)
    return np.ascontiguousarray(tables.reshape(4, SEQ // P, P, HD2).transpose(2, 0, 1, 3))


def window_mask():
    i = P + np.arange(P)[:, None]
    j = np.arange(2 * P)[None, :]
    out = (i < j) | (i > j + WINDOW) | (j < i // WINDOW * WINDOW - WINDOW)
    return np.where(out, NEG, 0.0).astype(HOST16)


def constants():
    i = np.arange(P)
    heads = (2 * np.arange(8)[None, :, None] + i[:, None, None] // HD1 == np.arange(LANE)).astype(np.float32)
    return {
        "mean_w": np.full((P, P), 1.0 / P, np.float32),
        "ones": np.ones((P, P), np.float32),
        "eps": np.full((P, 1), EPS, np.float32),
        "ident": np.eye(P, dtype=np.float32),
        "upto": (i[:, None] <= i[None, :]).astype(np.float32),
        "head_sum": heads,
        "head_pick": np.tile(heads.transpose(2, 1, 0), (P // LANE, 1, 1)),
        "ident16": np.eye(P).astype(HOST16),
        "window_mask": window_mask(),
        "rotary": rotary_tables(),
        "causal_mask": np.stack([np.where(i[None] > i[:, None], NEG, 0.0), np.where(i[:, None] > i[None], NEG, 0.0)],
                                axis=1).astype(HOST16),
        "ones_rows": np.ones((M_PARTS, SEQ), HOST16),
        "iota8": np.tile(np.arange(E, dtype=np.float32)[None], (P, 1)),
        "pick": np.ascontiguousarray(np.broadcast_to(
            (i[:PARTS * PART, None] % PART == np.arange(E)[None, :])[:, :, None],
            (PARTS * PART, E, P))).astype(HOST16),
        "after": (i[:, None] > i[None, :]).astype(np.float32),
    }


def rows(a, n=P):
    return np.ascontiguousarray(np.swapaxes(a.reshape(-1, n, *a.shape[1:]), 0, 1))


def across(ws):
    e, r, n = ws.shape
    return ws.reshape(e, r // P, P, n).transpose(0, 2, 1, 3).reshape(e, P, -1)


def by_column(b):
    return b.reshape(b.shape[0], -1, P).transpose(0, 2, 1)


def out_bias(b):
    a = np.zeros((PARTS, PART, P), np.float32)
    a[:, :E] = b
    return a.reshape(PARTS * PART, P)


def laid_out(v):
    v = {name: np.asarray(a) for name, a in v.items()}
    a = constants()
    a["xT"] = np.ascontiguousarray(v["L0_attn_u"].reshape(T, P).T)
    a["cT"] = np.ascontiguousarray(np.concatenate([v[f"L{i}_c"] for i in range(4)]).T)
    a["wmod"] = np.ascontiguousarray(np.stack([v[f"L{i}_wmod"] for i in range(4)], axis=1))
    a["L0_W_in"] = v["L0_attn_W_in"]
    a["L0_heads"] = np.tile(np.concatenate([v["L0_attn_dt_bias"], v["L0_attn_A_log"]])[None], (P, 1))
    a["L0_conv"] = rows(np.concatenate([v["L0_attn_conv_w"], v["L0_attn_conv_b"][:, None]], axis=1))
    a["L0_D"] = rows(np.repeat(v["L0_attn_D"], HD0))
    a["L0_norm_w"] = rows(v["L0_attn_norm_w"])
    a["L0_W_out"] = rows(v["L0_attn_W_out"])
    a["L0_router"] = v["L0_ffn_W_router"]
    a["L0_experts"] = np.concatenate([v["L0_ffn_W_gate"], v["L0_ffn_W_up"], across(v["L0_ffn_W_out"]),
                                      by_column(v["L0_ffn_b_gate"]), by_column(v["L0_ffn_b_up"])], axis=2)
    a["L0_out_bias"] = out_bias(v["L0_ffn_b_out"])
    a["L1_Wq"], a["L1_Wkv"], a["L1_Wo"] = v["L1_attn_Wq"], v["L1_attn_Wkv"], rows(v["L1_attn_Wo"])
    a["L1_wqkv"] = v["L1_ffn_wqkv"].transpose(1, 0, 2)
    crossed = lambda q: np.roll(q, HALF, axis=1)
    q, kk = v["L1_ffn_q_scale"], v["L1_ffn_k_scale"]
    a["L1_qk_scale"] = np.tile(np.stack([q, crossed(q), kk, crossed(kk)], axis=1)[None], (P, 1, 1, 1))
    a["L1_wo"] = v["L1_ffn_wo"].reshape(DEPTH, QT, P, P).transpose(2, 0, 1, 3)
    a["L1_ln"] = np.stack([v["L1_ffn_ln_g"], v["L1_ffn_ln_b"]]).transpose(2, 0, 1)
    a["L1_w1"] = v["L1_ffn_w1"].transpose(1, 0, 2)
    hid_tiles = -(-HID // P)
    a["L1_w2"] = np.pad(v["L1_ffn_w2"], ((0, 0), (0, hid_tiles * P - HID), (0, 0))
                        ).reshape(DEPTH, hid_tiles, P, P).transpose(2, 0, 1, 3)
    a["L1_b1"] = np.pad(v["L1_ffn_b1"].reshape(DEPTH, 2, HID), ((0, 0), (0, 0), (0, hid_tiles * P - HID))
                        ).reshape(DEPTH, 2, hid_tiles, P).transpose(3, 0, 1, 2)
    a["L1_b2"] = v["L1_ffn_b2"].T
    a["L2_W"] = np.stack([v["L2_attn_W_" + n].T for n in "QKVO"], axis=1)
    a["L2_experts"] = np.concatenate([v["L2_ffn_Wg"], v["L2_ffn_Wu"], across(v["L2_ffn_Wd"])], axis=2)
    a["L3_Wqkv"], a["L3_Wln"] = v["L3_attn_Wqkv"], v["L3_attn_Wln"]
    a["L3_bqkv"] = np.tile(v["L3_attn_bqkv"][None], (P, 1))
    a["L3_bv"], a["L3_bln"] = v["L3_attn_bqkv"][2 * P:, None], v["L3_attn_bln"][:, None]
    a["L3_router"] = np.ascontiguousarray(v["L3_ffn_router_w"].T)
    a["L3_experts"] = np.concatenate([v["L3_ffn_w1"].transpose(0, 2, 1), across(v["L3_ffn_w2"].transpose(0, 2, 1)),
                                      by_column(v["L3_ffn_b1"])], axis=2)
    a["L3_out_bias"] = out_bias(v["L3_ffn_b2"])
    return {name: np.ascontiguousarray(x) for name, x in a.items()}


def kernel(**inputs):
    import concourse.bacc as bacc
    from concourse.bass_utils import run_bass_kernel_spmd

    nc = bacc.Bacc("TRN2", target_bir_lowering=False, num_devices=1)
    arrays = laid_out(inputs)
    dram = {name: nc.dram_tensor("in_" + name, a.shape, mybir.dt.from_np(a.dtype), kind="ExternalInput").ap()
            for name, a in arrays.items()}
    out = nc.dram_tensor("out_xT", [P, T], F32, kind="ExternalOutput").ap()
    transformer(nc, dram, out)
    r = run_bass_kernel_spmd(nc, [{"in_" + name: a for name, a in arrays.items()}], core_ids=[0])
    return np.ascontiguousarray(np.asarray(r.results[0]["out_xT"]).T).reshape(NB, SEQ, P)
```

```python
from contextlib import ExitStack

import numpy as np

import concourse.bass as bass
from concourse import mybir

ALU = mybir.AluOpType
ACT = mybir.ActivationFunctionType
F32 = mybir.dt.float32
BF16 = mybir.dt.bfloat16
U32 = mybir.dt.uint32
HOST16 = mybir.dt.np(BF16)
AX = mybir.AxisListType.X

P = 128
NB = 2
SEQ = 1024
T = NB * SEQ
CH = 512
NCH = T // CH
NT = T // P
EPS = 1e-5
NEG = -1e30

SHIFT_A, SCALE_A, GATE_A, SHIFT_B, SCALE_B, GATE_B = range(6)



class Kit:
    pass


def chunk(c):
    return slice(c * CH, (c + 1) * CH)


def tile(t):
    return slice(t * P, (t + 1) * P)


def batch_of(c):
    return c * CH // SEQ


def modulation_stage(nc, k):
    with ExitStack() as ctx:
        c_sb = ctx.enter_context(nc.sbuf_tensor("c_sb", [P, 4 * NB], F32))
        w_sb = ctx.enter_context(nc.sbuf_tensor("wmod_sb", [P, 4, 6 * P], F32))
        sign = ctx.enter_context(nc.sbuf_tensor("gate_sign", [P, 4, 6, NB], F32))
        size = ctx.enter_context(nc.sbuf_tensor("gate_size", [P, 4, 6, NB], F32))
        ps = ctx.enter_context(nc.psum_tensor("mod_ps", [P, 4, 6, NB], F32))
        c_loaded = nc.alloc_semaphore("c_loaded")
        wmod_loaded = nc.alloc_semaphore("wmod_loaded")
        silu_ready = nc.alloc_semaphore("silu_c_ready")
        mod_ps_ready = nc.alloc_semaphore("mod_ps_ready")
        mod_steps = nc.alloc_semaphore("mod_steps")
        block = ctx.enter_context(nc.Block())

        @block.sync
        def _(sp):
            sp.dma_start(c_sb[:], k.dram["cT"]).then_inc(c_loaded, 16)
            sp.dma_start(w_sb[:], k.dram["wmod"]).then_inc(wmod_loaded, 16)
            sp.dma_start(k.x[:], k.dram["xT"]).then_inc(k.first_loaded, 16)
            for name in FIRST:
                sp.dma_start(k.w[name][:], k.dram[name]).then_inc(k.first_loaded, 16)
            sp.wait_ge(k.first_loaded, 16 * (1 + len(FIRST)))

        @block.scalar
        def _(act):
            act.wait_ge(c_loaded, 16)
            nc.scalar.activation(c_sb[:], c_sb[:], ACT.Silu).then_inc(silu_ready, 1)

        @block.tensor
        def _(pe):
            pe.wait_ge(wmod_loaded, 16)
            pe.wait_ge(silu_ready, 1)
            for layer in range(4):
                for j in range(6):
                    last = nc.tensor.matmul(ps[:, layer, j, :], w_sb[:, layer, tile(j)],
                                            c_sb[:, NB * layer:NB * layer + NB], start=True, stop=True)
            last.then_inc(mod_ps_ready, 1)

        @block.vector
        def _(dve):
            dve.wait_ge(mod_ps_ready, 1)
            nc.vector.tensor_copy(k.mod[:], ps[:]).then_inc(mod_steps, 1)
            dve.wait_ge(mod_steps, 1)
            nc.vector.tensor_scalar(sign[:], k.mod[:], 0.0, 2.0, ALU.is_ge, ALU.mult).then_inc(mod_steps, 1)
            nc.vector.scalar_tensor_tensor(out=size[:], in0=k.mod[:], scalar=-1.0, in1=k.mod[:], op0=ALU.mult,
                                           op1=ALU.max).then_inc(mod_steps, 1)
            dve.wait_ge(mod_steps, 3)
            nc.vector.tensor_scalar(size[:], size[:], 0.25, None, ALU.max).then_inc(mod_steps, 1)
            for j in (SCALE_A, SCALE_B):
                nc.vector.tensor_scalar(k.mod[:, :, j], k.mod[:, :, j], 1.0, None, ALU.add).then_inc(mod_steps, 1)
            dve.wait_ge(mod_steps, 6)
            for j in (GATE_A, GATE_B):
                nc.vector.scalar_tensor_tensor(out=k.mod[:, :, j], in0=sign[:, :, j], scalar=-1.0,
                                               in1=size[:, :, j], op0=ALU.add, op1=ALU.mult).then_inc(mod_steps, 1)
            dve.wait_ge(mod_steps, 8)


def adaln_stage(nc, k, layer, scale_at, shift_at, weights):
    layernorm_stage(nc, k, f"{layer}{scale_at}", k.x, k.h,
                    lambda b: (k.mod[:, layer, scale_at, b:b + 1], k.mod[:, layer, shift_at, b:b + 1]), weights)


def layernorm_stage(nc, k, name, src, dst, affine, weights=()):
    tag = f"_ln{name}"
    with ExitStack() as ctx:
        xc = ctx.enter_context(nc.sbuf_tensor("xc" + tag, [P, T], F32))
        sq = ctx.enter_context(nc.sbuf_tensor("sq" + tag, [P, 2, CH], F32))
        std = ctx.enter_context(nc.sbuf_tensor("std" + tag, [P, 2, CH], F32))
        rstd = ctx.enter_context(nc.sbuf_tensor("rstd" + tag, [P, 2, CH], F32))
        mean_ps = ctx.enter_context(nc.psum_tensor("mean_ps" + tag, [P, 2, CH], F32))
        var_ps = ctx.enter_context(nc.psum_tensor("var_ps" + tag, [P, 2, CH], F32))
        sem = lambda name: nc.alloc_semaphore(name + tag)
        mean_ready, centered, squared, var_ready = sem("mean"), sem("centered"), sem("squared"), sem("var")
        std_ready, rstd_ready, normed, h_ready, loaded = sem("std"), sem("rstd"), sem("normed"), sem("h"), sem("loaded")
        block = ctx.enter_context(nc.Block())

        @block.sync
        def _(sp):
            for w in weights:
                sp.dma_start(k.w[w][:], k.dram[w]).then_inc(loaded, 16)
            if weights:
                sp.wait_ge(loaded, 16 * len(weights))

        @block.tensor
        def _(pe):
            for c in range(NCH + 1):
                if c < NCH:
                    if c >= 2:
                        pe.wait_ge(centered, c - 1)
                    nc.tensor.matmul(mean_ps[:, c % 2], k.w["mean_w"][:], src[:, chunk(c)],
                                     start=True, stop=True).then_inc(mean_ready, 1)
                if c >= 1:
                    pe.wait_ge(squared, c)
                    if c >= 3:
                        pe.wait_ge(std_ready, c - 2)
                    nc.tensor.matmul(var_ps[:, (c - 1) % 2], k.w["mean_w"][:], sq[:, (c - 1) % 2],
                                     start=True, stop=True).then_inc(var_ready, 1)

        @block.scalar
        def _(act):
            for c in range(NCH + 1):
                if c < NCH:
                    act.wait_ge(centered, c + 1)
                    if c >= 2:
                        act.wait_ge(var_ready, c - 1)
                    nc.scalar.activation(sq[:, c % 2], xc[:, chunk(c)], ACT.Square).then_inc(squared, 1)
                if c >= 1:
                    act.wait_ge(var_ready, c)
                    if c >= 3:
                        act.wait_ge(rstd_ready, c - 2)
                    nc.scalar.activation(std[:, (c - 1) % 2], var_ps[:, (c - 1) % 2], ACT.Sqrt,
                                         bias=k.w["eps"][:, 0:1]).then_inc(std_ready, 1)

        @block.vector
        def _(dve):
            for c in range(NCH + 1):
                if c < NCH:
                    dve.wait_ge(mean_ready, c + 1)
                    nc.vector.tensor_tensor(xc[:, chunk(c)], src[:, chunk(c)], mean_ps[:, c % 2],
                                            ALU.subtract).then_inc(centered, 1)
                if c >= 1:
                    e, b = c - 1, batch_of(c - 1)
                    dve.wait_ge(std_ready, e + 1)
                    if e >= 2:
                        dve.wait_ge(normed, e - 1)
                    nc.vector.reciprocal(rstd[:, e % 2], std[:, e % 2]).then_inc(rstd_ready, 1)
                    dve.wait_ge(rstd_ready, e + 1)
                    nc.vector.tensor_tensor(dst[:, chunk(e)], xc[:, chunk(e)], rstd[:, e % 2],
                                            ALU.mult).then_inc(normed, 1)
                    dve.wait_ge(normed, e + 1)
                    nc.vector.tensor_scalar(dst[:, chunk(e)], dst[:, chunk(e)], *affine(b), ALU.mult, ALU.add).then_inc(h_ready, 1)


def half_layer(layer, half, weights, body):
    def stages(nc, k):
        with nc.cleanup_on_exit(), ExitStack() as ctx:
            for name in weights:
                d = k.dram[name]
                k.w[name] = ctx.enter_context(nc.sbuf_tensor(f"{name}_{layer}{half}", list(d.shape), d.dtype))
            at = (SCALE_A, SHIFT_A) if half == 0 else (SCALE_B, SHIFT_B)
            adaln_stage(nc, k, layer, *at, weights)
            body(nc, k)
    return stages


D_CONV = 4
HEADS0 = 4
HD0 = 64
NG = SEQ // P


def mamba_project_stage(nc, k, s):
    with ExitStack() as ctx:
        raw = ctx.enter_context(nc.sbuf_tensor("raw_xbc", [P, 2, NB, SEQ + D_CONV - 1], F32))
        conv = ctx.enter_context(nc.sbuf_tensor("conv_acc", [P, 2, NB, SEQ], F32))
        ps = ctx.enter_context(nc.psum_tensor("proj_ps", [P, 4, CH], F32))
        dt_ps = ctx.enter_context(nc.psum_tensor("dt_ps", [P, NT, HEADS0], F32))
        tmp = ctx.enter_context(nc.sbuf_tensor("dt_tmp", [P, 8, NT * HEADS0], F32))
        sem = lambda name: nc.alloc_semaphore(name + "_mp")
        proj_ready, evacuated, dt_ready, pads_ready = sem("proj"), sem("evacuated"), sem("dt_ps"), sem("pads")
        conv_step, conv_ready, silu_ready, dt_step, dt_act = (
            sem("conv_step"), sem("conv"), sem("silu"), sem("dt_step"), sem("dt_act"))
        win, cw = k.w["L0_W_in"], k.w["L0_conv"]
        block = ctx.enter_context(nc.Block())
        bank = lambda m, c: (m * NCH + c) % 4

        @block.tensor
        def _(pe):
            for t in range(NT):
                last = nc.tensor.matmul(dt_ps[:, t], k.h[:, tile(t)], win[:, 6 * P:6 * P + HEADS0],
                                        start=True, stop=True)
            last.then_inc(dt_ready, 1)
            for i, m in enumerate((2, 3, 4, 5, 0, 1)):
                for c in range(NCH):
                    n = i * NCH + c
                    if n >= 4:
                        pe.wait_ge(evacuated, n - 3)
                    nc.tensor.matmul(ps[:, n % 4], win[:, tile(m)], k.h[:, chunk(c)],
                                     start=True, stop=True).then_inc(proj_ready, 1)

        @block.scalar
        def _(act):
            act.wait_ge(pads_ready, 1)
            for i in range(6):
                if 2 <= i < 4:
                    act.wait_ge(conv_ready, i - 1)
                for c in range(NCH):
                    n = i * NCH + c
                    act.wait_ge(proj_ready, n + 1)
                    if i < 4:
                        b, at = batch_of(c), c * CH % SEQ
                        out, func = raw[:, i % 2, b, D_CONV - 1 + at:D_CONV - 1 + at + CH], ACT.Copy
                    else:
                        out, func = s.zg[:, i - 4, chunk(c)], ACT.Silu
                    nc.scalar.activation(out, ps[:, n % 4], func).then_inc(evacuated, 1)
            for i in range(4):
                act.wait_ge(conv_ready, i + 1)
                nc.scalar.activation(s.xbc[:, i].rearrange("p (b n) -> p b n", b=NB), s.conv_out[:, i],
                                     ACT.Silu).then_inc(silu_ready, 1)
            act.wait_ge(dt_step, 3)
            nc.scalar.activation(tmp[:, 2], tmp[:, 1], ACT.Exp, scale=-1.0).then_inc(dt_act, 1)
            nc.scalar.activation(s.decay_rate[:], k.w["L0_heads"][:, HEADS0:2 * HEADS0], ACT.Exp).then_inc(dt_act, 1)
            act.wait_ge(dt_act, 1)
            nc.scalar.activation(tmp[:, 3], tmp[:, 2], ACT.Ln, bias=1.0).then_inc(dt_act, 1)

        @block.vector
        def _(dve):
            nc.vector.memset(raw[:, :, :, 0:D_CONV - 1], 0.0).then_inc(pads_ready, 1)
            dve.wait_ge(dt_ready, 1)
            steps = [0]
            flat = dt_ps[:].rearrange("p t h -> p (t h)")
            bias = k.w["L0_heads"][:, 0:HEADS0].unsqueeze(1).to_broadcast([P, NT, HEADS0])
            nc.vector.tensor_tensor(tmp[:, 0].rearrange("p (t h) -> p t h", h=HEADS0), dt_ps[:], bias,
                                    ALU.add).then_inc(dt_step, 1)
            dve.wait_ge(dt_step, 1)
            nc.vector.scalar_tensor_tensor(out=tmp[:, 1], in0=tmp[:, 0], scalar=-1.0, in1=tmp[:, 0], op0=ALU.mult,
                                           op1=ALU.max).then_inc(dt_step, 1)
            dve.wait_ge(dt_step, 2)
            nc.vector.tensor_scalar(tmp[:, 0], tmp[:, 0], 0.0, None, ALU.max).then_inc(dt_step, 1)
            for i in range(4):
                if i >= 1:
                    dve.wait_ge(conv_ready, i)
                dve.wait_ge(evacuated, NCH * (i + 1))
                tap = lambda j: raw[:, i % 2, :, j:j + SEQ]
                nc.vector.tensor_scalar(conv[:, 0], tap(0), cw[:, i, 0:1], cw[:, i, D_CONV:D_CONV + 1],
                                        ALU.mult, ALU.add).then_inc(conv_step, 1)
                for j in range(1, D_CONV):
                    dve.wait_ge(conv_step, (D_CONV - 1) * i + j)
                    out = conv[:, j % 2] if j < D_CONV - 1 else s.conv_out[:, i]
                    nc.vector.scalar_tensor_tensor(out=out, in0=tap(j), scalar=cw[:, i, j:j + 1],
                                                   in1=conv[:, (j - 1) % 2], op0=ALU.mult,
                                                   op1=ALU.add).then_inc(
                                                       conv_ready if j == D_CONV - 1 else conv_step, 1)
            e, poly, small = tmp[:, 2], tmp[:, 4], tmp[:, 5]
            dve.wait_ge(dt_act, 1)
            n = 3
            nc.vector.tensor_scalar(poly, e, 1.0 / 7, -1.0 / 6, ALU.mult, ALU.add).then_inc(dt_step, 1)
            for coefficient in (1.0 / 5, -1.0 / 4, 1.0 / 3, -1.0 / 2, 1.0):
                n += 1
                dve.wait_ge(dt_step, n)
                nc.vector.tensor_tensor(poly, poly, e, ALU.mult).then_inc(dt_step, 1)
                n += 1
                dve.wait_ge(dt_step, n)
                nc.vector.tensor_scalar(poly, poly, coefficient, None, ALU.add).then_inc(dt_step, 1)
            n += 1
            dve.wait_ge(dt_step, n)
            nc.vector.tensor_tensor(poly, poly, e, ALU.mult).then_inc(dt_step, 1)
            nc.vector.tensor_scalar(small, e, 1.0 / 16, None, ALU.is_lt).then_inc(dt_step, 1)
            dve.wait_ge(dt_act, 3)
            n += 2
            dve.wait_ge(dt_step, n)
            nc.vector.tensor_tensor(poly, poly, tmp[:, 3], ALU.subtract).then_inc(dt_step, 1)
            dve.wait_ge(dt_step, n + 1)
            nc.vector.tensor_tensor(poly, poly, small, ALU.mult).then_inc(dt_step, 1)
            dve.wait_ge(dt_step, n + 2)
            nc.vector.tensor_tensor(poly, poly, tmp[:, 3], ALU.add).then_inc(dt_step, 1)
            dve.wait_ge(dt_step, n + 3)
            nc.vector.tensor_tensor(s.dt[:].rearrange("p t h -> p (t h)"), tmp[:, 0], poly,
                                    ALU.add).then_inc(dt_step, 1)
            dve.wait_ge(dt_step, n + 4)
            rate = s.decay_rate[:].unsqueeze(1).to_broadcast([P, NT, HEADS0])
            nc.vector.scalar_tensor_tensor(out=s.a[:], in0=s.dt[:], scalar=-1.0, in1=rate,
                                           op0=ALU.mult, op1=ALU.mult).then_inc(dt_step, 1)


def mamba_scan_stage(nc, k, s):
    HP = HEADS0 * HD0
    with ExitStack() as ctx:
        sb = lambda name, shape: ctx.enter_context(nc.sbuf_tensor(name, shape, F32))
        x_tok, b_tok = sb("x_dt_tok", [P, 2, HEADS0, HD0]), sb("b_tok", [P, 2, P])
        al, e1, e2 = sb("a_upto_l", [P, 2, HEADS0, P]), sb("e_between", [P, 2, HEADS0, P]), sb("e_upto", [P, 2, HEADS0, P])
        g, m = sb("cb_masked", [P, 2, P]), sb("m_masked", [P, 2, HEADS0, P])
        ce, xd = sb("c_decayed", [P, 2, HEADS0, P]), sb("x_decayed", [P, 2, HEADS0, HD0])
        state, kept = sb("state", [P, 2, HEADS0, HD0]), sb("state_kept", [P, HEADS0, HD0])
        t_ps = ctx.enter_context(nc.psum_tensor("turn_ps", [P, 2, 4, P], F32))
        seg_ps = ctx.enter_context(nc.psum_tensor("seg_ps", [P, 2, CH], F32))
        cum_ps = ctx.enter_context(nc.psum_tensor("cum_ps", [P, CH], F32))
        y_ps = ctx.enter_context(nc.psum_tensor("y_ps", [P, 2, CH], F32))
        ds_ps = ctx.enter_context(nc.psum_tensor("ds_ps", [P, HEADS0, HD0], F32))
        sem = lambda name: nc.alloc_semaphore(name + "_ms")
        turned, x_tok_ready, b_tok_ready, al_ready = sem("turned"), sem("x_tok"), sem("b_tok"), sem("al")
        seg_ready, cum_ready, e1_ready, e2_ready = sem("seg"), sem("cum"), sem("e1"), sem("e2")
        g_ready, m_ready, ce_ready, xd_ready = sem("g"), sem("m"), sem("ce"), sem("xd")
        y_ready, ds_ready, state_ready, kept_ready, y_taken = sem("y"), sem("ds"), sem("state"), sem("kept"), sem("y_taken")
        B, C = s.xbc[:, 2], s.xbc[:, 3]
        upto, after = k.w["upto"], k.w["after"]
        N = NT
        block = ctx.enter_context(nc.Block())

        @block.gpsimd
        def _(pool):
            def decays_in(n):
                if n >= 2:
                    pool.wait_ge(cum_ready, n - 1)
                nc.gpsimd.tensor_tensor(
                    al[:, n % 2], upto[:].unsqueeze(1).to_broadcast([P, HEADS0, P]),
                    s.a[:, n].unsqueeze(2).to_broadcast([P, HEADS0, P]), ALU.mult).then_inc(al_ready, 1)

            decays_in(0)
            for n in range(N):
                if n + 1 < N:
                    decays_in(n + 1)
                pool.wait_ge(e1_ready, n + 1)
                pool.wait_ge(x_tok_ready, n + 1)
                if n >= 2:
                    pool.wait_ge(ds_ready, n - 1)
                nc.gpsimd.tensor_tensor(xd[:, n % 2], x_tok[:, n % 2],
                                        e1[:, n % 2, :, P - 1:P].to_broadcast([P, HEADS0, HD0]),
                                        ALU.mult).then_inc(xd_ready, 1)
                if n % NG:
                    pool.wait_ge(e2_ready, n + 1)
                    if n >= 2:
                        pool.wait_ge(y_ready, n - 1)
                    nc.gpsimd.tensor_tensor(ce[:, n % 2], e2[:, n % 2],
                                            C[:, tile(n)].unsqueeze(1).to_broadcast([P, HEADS0, P]),
                                            ALU.mult).then_inc(ce_ready, 1)

        @block.tensor
        def _(pe):
            def turn(n):
                if n >= 2:
                    pe.wait_ge(g_ready, n - 1)
                for j in range(3):
                    nc.tensor.transpose(t_ps[:, n % 2, j], s.xbc[:, j, tile(n)], k.w["ident"][:])
                nc.tensor.matmul(t_ps[:, n % 2, 3], B[:, tile(n)], C[:, tile(n)],
                                 start=True, stop=True).then_inc(turned, 1)

            def decays(n):
                pe.wait_ge(al_ready, n + 1)
                if n >= 2:
                    pe.wait_ge(e1_ready, n - 1)
                nc.tensor.matmul(seg_ps[:, n % 2], after[:], al[:, n % 2].rearrange("p h l -> p (h l)"),
                                 start=True, stop=True).then_inc(seg_ready, 1)
                if n >= 1:
                    pe.wait_ge(e2_ready, n)
                nc.tensor.matmul(cum_ps[:], k.w["ones"][:], al[:, n % 2].rearrange("p h l -> p (h l)"),
                                 start=True, stop=True).then_inc(cum_ready, 1)

            turn(0)
            decays(0)
            for n in range(N):
                if n + 1 < N:
                    turn(n + 1)
                    decays(n + 1)
                pe.wait_ge(xd_ready, n + 1)
                pe.wait_ge(b_tok_ready, n + 1)
                if n >= 1:
                    pe.wait_ge(state_ready, n)
                nc.tensor.matmul(ds_ps[:].rearrange("p h d -> p (h d)"), b_tok[:, n % 2],
                                 xd[:, n % 2].rearrange("p h d -> p (h d)"), start=True, stop=True).then_inc(ds_ready, 1)
                pe.wait_ge(m_ready, n + 1)
                first = n % NG == 0
                if not first:
                    pe.wait_ge(ce_ready, n - n // NG)
                if n >= 2:
                    pe.wait_ge(y_taken, n - 1)
                for h in range(HEADS0):
                    out = y_ps[HD0 * (h % 2):HD0 * (h % 2) + HD0, n % 2, (h // 2) * P:(h // 2) * P + P]
                    last = nc.tensor.matmul(out, x_tok[:, n % 2, h], m[:, n % 2, h], start=True, stop=first)
                    if not first:
                        last = nc.tensor.matmul(out, state[:, (n - 1) % 2, h], ce[:, n % 2, h],
                                                start=False, stop=True)
                last.then_inc(y_ready, 1)

        @block.scalar
        def _(act):
            for n in range(N):
                act.wait_ge(seg_ready, n + 1)
                if n >= 2:
                    act.wait_ge(m_ready, n - 1)
                    act.wait_ge(xd_ready, n - 1)
                nc.scalar.activation(e1[:, n % 2].rearrange("p h l -> p (h l)"), seg_ps[:, n % 2],
                                     ACT.Exp).then_inc(e1_ready, 1)
                act.wait_ge(cum_ready, n + 1)
                if n >= 2:
                    act.wait_ge(kept_ready, n - 1)
                    if n >= 3:
                        act.wait_ge(ce_ready, (n - 1) - (n - 2) // NG - 1)
                nc.scalar.activation(e2[:, n % 2].rearrange("p h l -> p (h l)"), cum_ps[:],
                                     ACT.Exp).then_inc(e2_ready, 1)

        @block.vector
        def _(dve):
            for n in range(N):
                dve.wait_ge(turned, n + 1)
                if n >= 2:
                    dve.wait_ge(y_ready, n - 1)
                    dve.wait_ge(xd_ready, n - 1)
                nc.vector.tensor_tensor(x_tok[:, n % 2], t_ps[:, n % 2, 0:2].rearrange("p j (h d) -> p (j h) d", d=HD0),
                                        s.dt[:, n].unsqueeze(2).to_broadcast([P, HEADS0, HD0]),
                                        ALU.mult).then_inc(x_tok_ready, 1)
                if n >= 2:
                    dve.wait_ge(ds_ready, n - 1)
                nc.vector.tensor_copy(b_tok[:, n % 2], t_ps[:, n % 2, 2]).then_inc(b_tok_ready, 1)
                if n >= 2:
                    dve.wait_ge(m_ready, n - 1)
                nc.vector.tensor_tensor(g[:, n % 2], t_ps[:, n % 2, 3], upto[:], ALU.mult).then_inc(g_ready, 1)
                dve.wait_ge(g_ready, n + 1)
                dve.wait_ge(e1_ready, n + 1)
                nc.vector.tensor_tensor(m[:, n % 2], e1[:, n % 2],
                                        g[:, n % 2].unsqueeze(1).to_broadcast([P, HEADS0, P]),
                                        ALU.mult).then_inc(m_ready, 1)
                dve.wait_ge(e2_ready, n + 1)
                if n % NG == 0:
                    if n >= 1:
                        dve.wait_ge(state_ready, n)
                    nc.vector.memset(kept[:], 0.0).then_inc(kept_ready, 1)
                else:
                    dve.wait_ge(state_ready, n)
                    nc.vector.tensor_tensor(kept[:], state[:, (n - 1) % 2],
                                            e2[:, n % 2, :, P - 1:P].to_broadcast([P, HEADS0, HD0]),
                                            ALU.mult).then_inc(kept_ready, 1)
                dve.wait_ge(kept_ready, n + 1)
                dve.wait_ge(ds_ready, n + 1)
                if n >= 1:
                    dve.wait_ge(y_ready, n)
                nc.vector.tensor_tensor(state[:, n % 2], kept[:], ds_ps[:], ALU.add).then_inc(state_ready, 1)
                dve.wait_ge(y_ready, n + 1)
                for j in range(2):
                    last = nc.vector.scalar_tensor_tensor(
                        out=s.y[:, j, tile(n)], in0=s.xbc[:, j, tile(n)], scalar=k.w["L0_D"][:, j:j + 1],
                        in1=y_ps[:, n % 2, j * P:(j + 1) * P], op0=ALU.mult, op1=ALU.add)
                last.then_inc(y_taken, 1)


def mamba_out_stage(nc, k, s):
    with ExitStack() as ctx:
        sb = lambda name, shape: ctx.enter_context(nc.sbuf_tensor(name, shape, F32))
        yz, sq = sb("y_gated", [P, 2, 2, CH]), sb("y_squared", [P, 2, 2, CH])
        rms, rinv, w, tmp = sb("rms", [P, 2, CH]), sb("rms_inv", [P, 2, CH]), sb("w_out_n", [P, 2, P]), sb("out_n", [P, 2, CH])
        o_ps = ctx.enter_context(nc.psum_tensor("o_ps", [P, 2, CH], F32))
        s_ps = ctx.enter_context(nc.psum_tensor("s_ps", [P, 2, CH], F32))
        sem = lambda name: nc.alloc_semaphore(name + "_mo")
        w_ready, gated, squared, sum_ready, out_ready = sem("w"), sem("gated"), sem("squared"), sem("sum"), sem("out")
        rms_ready, rinv_ready, scaled, added = sem("rms"), sem("rinv"), sem("scaled"), sem("added")
        block = ctx.enter_context(nc.Block())

        @block.tensor
        def _(pe):
            pe.wait_ge(w_ready, 2)
            for c in range(NCH):
                pe.wait_ge(gated, c + 1)
                if c >= 2:
                    pe.wait_ge(scaled, c - 1)
                for j in range(2):
                    last = nc.tensor.matmul(o_ps[:, c % 2], w[:, j], yz[:, c % 2, j], start=j == 0, stop=j == 1)
                last.then_inc(out_ready, 1)
                pe.wait_ge(squared, c + 1)
                if c >= 2:
                    pe.wait_ge(rms_ready, c - 1)
                for j in range(2):
                    last = nc.tensor.matmul(s_ps[:, c % 2], k.w["mean_w"][:], sq[:, c % 2, j], start=j == 0, stop=j == 1)
                last.then_inc(sum_ready, 1)

        @block.scalar
        def _(act):
            for c in range(NCH):
                act.wait_ge(gated, c + 1)
                if c >= 2:
                    act.wait_ge(sum_ready, c - 1)
                nc.scalar.activation(sq[:, c % 2], yz[:, c % 2], ACT.Square).then_inc(squared, 1)
                act.wait_ge(sum_ready, c + 1)
                if c >= 2:
                    act.wait_ge(rinv_ready, c - 1)
                nc.scalar.activation(rms[:, c % 2], s_ps[:, c % 2], ACT.Sqrt, bias=k.w["eps"][:, 0:1],
                                     scale=0.5).then_inc(rms_ready, 1)

        @block.vector
        def _(dve):
            for j in range(2):
                nc.vector.tensor_scalar(w[:, j], k.w["L0_W_out"][:, j], k.w["L0_norm_w"][:, j:j + 1], None,
                                        ALU.mult).then_inc(w_ready, 1)

            def gate(c):
                if c >= 2:
                    dve.wait_ge(out_ready, c - 1)
                    dve.wait_ge(squared, c - 1)
                nc.vector.tensor_tensor(yz[:, c % 2], s.y[:, :, chunk(c)], s.zg[:, :, chunk(c)],
                                        ALU.mult).then_inc(gated, 1)

            gate(0)
            for c in range(NCH):
                if c + 1 < NCH:
                    gate(c + 1)
                b = batch_of(c)
                dve.wait_ge(rms_ready, c + 1)
                if c >= 2:
                    dve.wait_ge(scaled, c - 1)
                nc.vector.reciprocal(rinv[:, c % 2], rms[:, c % 2]).then_inc(rinv_ready, 1)
                dve.wait_ge(rinv_ready, c + 1)
                dve.wait_ge(out_ready, c + 1)
                if c >= 2:
                    dve.wait_ge(added, c - 1)
                nc.vector.tensor_tensor(tmp[:, c % 2], o_ps[:, c % 2], rinv[:, c % 2], ALU.mult).then_inc(scaled, 1)
                dve.wait_ge(scaled, c + 1)
                nc.vector.scalar_tensor_tensor(out=k.x[:, chunk(c)], in0=tmp[:, c % 2],
                                               scalar=k.mod[:, 0, GATE_A, b:b + 1], in1=k.x[:, chunk(c)],
                                               op0=ALU.mult, op1=ALU.add).then_inc(added, 1)


def mamba_block(nc, k):
    with ExitStack() as ctx:
        sb = lambda name, shape: ctx.enter_context(nc.sbuf_tensor(name, shape, F32))
        s = Kit()
        s.zg, s.xbc, s.y = sb("z_gate", [P, 2, T]), sb("xbc", [P, 4, T]), sb("y0", [P, 2, T])
        s.dt, s.a, s.decay_rate = sb("dt", [P, NT, HEADS0]), sb("a_dt", [P, NT, HEADS0]), sb("decay_rate", [P, HEADS0])
        with nc.sbuf_tensor("conv_out", [P, 4, NB, SEQ], F32) as s.conv_out:
            mamba_project_stage(nc, k, s)
        mamba_scan_stage(nc, k, s)
        mamba_out_stage(nc, k, s)

E = 8
PARTS = 3
PART = 32
TOP_EPS = 1e-8


def routing_stage(nc, k, r, router, top_sum_eps):
    tag = "_rt" + router
    TE = NT * E
    steps = 2 + 2 * NT + 3 + 2 + 3 + (1 if top_sum_eps else 0) + 2 + 3 * PARTS - 1
    with ExitStack() as ctx:
        sb = lambda name, shape, dt=F32: ctx.enter_context(nc.sbuf_tensor(name + tag, shape, dt))
        lg, top, top_at, at = sb("lg", [P, NT, E]), sb("top", [P, NT, E]), sb("top_at", [P, NT, E], U32), sb("at", [P, NT, E])
        ex, total, den = sb("ex", [P, NT, E]), sb("total", [P, NT, 1]), sb("den", [P, NT, 1])
        hit, rest = sb("hit", [P, 2, NT, E]), sb("rest", [P, 2, NT, E])
        part = sb("part", [P, PARTS, NT, E], BF16)
        spread = sb("spread", [P, NT, PARTS, PART])
        parts16 = sb("parts16", [PARTS * PART, T], BF16)
        lg_ps = ctx.enter_context(nc.psum_tensor("lg_ps" + tag, [P, CH], F32))
        t_ps = ctx.enter_context(nc.psum_tensor("t_ps" + tag, [P, 2, CH], F32))
        w_ps = ctx.enter_context(nc.psum_tensor("w_ps" + tag, [P, 4, CH], F32))
        sem = lambda name: nc.alloc_semaphore(name + tag)
        logits_ready, dve_step, act_step, turned = sem("logits"), sem("dve_step"), sem("act_step"), sem("turned")
        parts_ready, parts16_ready, wide_ready, wide_read_a, wide_read_v = (
            sem("parts"), sem("parts16"), sem("wide"), sem("wide_read_a"), sem("wide_read_v"))
        block = ctx.enter_context(nc.Block())

        @block.sync
        def _(sp):
            for s in range(2):
                sp.dma_start(r.slot[:, s], r.weights[s]).then_inc(r.slot_loaded[s], 16)

        @block.tensor
        def _(pe):
            for t in range(NT):
                last = nc.tensor.matmul(lg_ps[:, t * E:(t + 1) * E], k.h[:, tile(t)], k.w[router][:],
                                        start=True, stop=True)
            last.then_inc(logits_ready, 1)
            pe.wait_ge(dve_step, steps)
            for c in range(NCH):
                if c >= 2:
                    pe.wait_ge(parts_ready, c - 1)
                for j in range(CH // P):
                    last = nc.tensor.transpose(t_ps[0:PARTS * PART, c % 2, tile(j)],
                                               spread[:, c * CH // P + j].rearrange("p i e -> p (i e)"),
                                               k.w["ident"][:])
                last.then_inc(turned, 1)
            for e in range(E):
                for c in range(NCH):
                    n = e * NCH + c
                    if e == 0:
                        pe.wait_ge(parts16_ready, c + 1)
                    if n >= 4:
                        pe.wait_ge(wide_read_v if n % 2 else wide_read_a, n // 2 - 1)
                    nc.tensor.matmul(w_ps[:, n % 4], k.w["pick"][:, e], parts16[:, chunk(c)],
                                     start=True, stop=True).then_inc(wide_ready, 1)

        @block.scalar
        def _(act):
            act.wait_ge(dve_step, 2 + 2 * NT + 1)
            nc.scalar.activation(ex[:], ex[:], ACT.Exp).then_inc(act_step, 1)
            for c in range(NCH):
                act.wait_ge(turned, c + 1)
                nc.scalar.activation(r.parts[:, chunk(c)], t_ps[0:PARTS * PART, c % 2], ACT.Copy).then_inc(parts_ready, 1)
            for n in range(0, E * NCH, 2):
                act.wait_ge(wide_ready, n + 1)
                nc.scalar.activation(r.wide[:, n // NCH, chunk(n % NCH)], w_ps[:, n % 4],
                                     ACT.Copy).then_inc(wide_read_a, 1)

        count = [0]

        @block.vector
        def _(dve):
            def step(instruction):
                count[0] += 1
                instruction.then_inc(dve_step, 1)
                dve.wait_ge(dve_step, count[0])

            dve.wait_ge(logits_ready, 1)
            step(nc.vector.memset(spread[:], 0.0))
            step(nc.vector.tensor_copy(lg[:].rearrange("p t e -> p (t e)"), lg_ps[:, 0:TE]))
            for t in range(NT):
                nc.vector.max(top[:, t], lg[:, t]).then_inc(dve_step, 1)
            count[0] += NT
            dve.wait_ge(dve_step, count[0])
            for t in range(NT):
                nc.vector.max_index(top_at[:, t], top[:, t], lg[:, t]).then_inc(dve_step, 1)
            count[0] += NT
            dve.wait_ge(dve_step, count[0])
            greatest = top[:, :, 0:1].to_broadcast([P, NT, E])
            step(nc.vector.tensor_tensor(ex[:], lg[:], greatest, ALU.subtract))
            dve.wait_ge(act_step, 1)
            step(nc.vector.tensor_reduce(total[:, :, 0], ex[:], AX, ALU.add))
            step(nc.vector.tensor_copy(at[:], top_at[:]))
            for i in range(2):
                step(nc.vector.tensor_tensor(hit[:, i], k.w["iota8"][:].unsqueeze(1).to_broadcast([P, NT, E]),
                                             at[:, :, i:i + 1].to_broadcast([P, NT, E]), ALU.is_equal))
            step(nc.vector.tensor_tensor(hit[:, 0], hit[:, 0], hit[:, 1], ALU.add))
            step(nc.vector.tensor_tensor(hit[:, 0], hit[:, 0], ex[:], ALU.mult))
            step(nc.vector.tensor_reduce(den[:, :, 0], hit[:, 0], AX, ALU.add))
            if top_sum_eps:
                step(nc.vector.scalar_tensor_tensor(out=den[:], in0=total[:], scalar=top_sum_eps, in1=den[:],
                                                    op0=ALU.mult, op1=ALU.add))
            step(nc.vector.reciprocal(den[:], den[:]))
            step(nc.vector.tensor_tensor(rest[:, 0], hit[:, 0], den[:].to_broadcast([P, NT, E]), ALU.mult))
            for i in range(PARTS):
                step(nc.vector.tensor_copy(part[:, i], rest[:, i % 2]))
                step(nc.vector.tensor_copy(spread[:, :, i, 0:E], part[:, i]))
                if i + 1 < PARTS:
                    step(nc.vector.tensor_tensor(rest[:, (i + 1) % 2], rest[:, i % 2], part[:, i], ALU.subtract))
            for c in range(NCH):
                dve.wait_ge(parts_ready, c + 1)
                nc.vector.tensor_copy(parts16[:, chunk(c)], r.parts[:, chunk(c)]).then_inc(parts16_ready, 1)
            for n in range(1, E * NCH, 2):
                dve.wait_ge(wide_ready, n + 1)
                nc.vector.tensor_copy(r.wide[:, n // NCH, chunk(n % NCH)], w_ps[:, n % 4]).then_inc(wide_read_v, 1)

        assert count[0] == steps


CREDIT = 2


def experts_stage(nc, k, r, layer, tiles, func, gated, routed):
    tag = f"_ex{layer}"
    M, LAG, HB = tiles, 2, 4
    wide_cols = M * P
    UNITS = NCH * M
    PAIR = 2 * UNITS
    G0, U0 = 0, wide_cols
    D0 = (2 if gated else 1) * wide_cols
    BG, BU = D0 + M * P, D0 + M * P + M
    with ExitStack() as ctx:
        sb = lambda name, shape: ctx.enter_context(nc.sbuf_tensor(name + tag, shape, F32))
        act_out, mid, hid = sb("act_out", [P, 2, CH]), sb("mid", [P, 2, CH]), sb("hid", [P, HB, CH])
        zero = sb("zero", [P, P])
        acc = ctx.enter_context(nc.psum_tensor("acc" + tag, [P, NCH, CH], F32))
        g_ps = ctx.enter_context(nc.psum_tensor("g_ps" + tag, [P, 2, CH], F32))
        u_ps = ctx.enter_context(nc.psum_tensor("u_ps" + tag, [P, 2, CH], F32))
        sem = lambda name: nc.alloc_semaphore(name + tag)
        zero_ready, g_ready, u_ready, act_ready, mid_ready, hid_ready, down_done, added = (
            sem("zero"), sem("g"), sem("u"), sem("act"), sem("mid"), sem("hid"), sem("down"), sem("added"))
        block = ctx.enter_context(nc.Block())
        units = [(s, c, m) for s in range(2) for c in range(NCH) for m in range(M)]

        @block.sync
        def _(sp):
            with sp.Fori(0, E // 2 - 1, 1) as it:
                for s in range(2):
                    sp.wait_ge(down_done, it * PAIR + (s + 1) * UNITS + CREDIT)
                    sp.dma_start(r.slot[:, s], r.weights[bass.ds(it * 2 + (2 + s), 1)].rearrange("o p n -> p (o n)")
                                 ).then_inc(r.slot_loaded[s], 16)

        @block.tensor
        def _(pe):
            def up(it, u):
                s, c, m = units[u]
                if u % UNITS == 0:
                    pe.wait_ge(r.slot_loaded[s], it * 16 + 16)
                pe.wait_ge(act_ready, it * PAIR + (u + 1))
                nc.tensor.matmul(g_ps[:, u % 2], r.slot[:, s, G0 + m * P:G0 + (m + 1) * P], k.h[:, chunk(c)],
                                 start=True, stop=True).then_inc(g_ready, 1)
                if gated:
                    pe.wait_ge(mid_ready if routed else hid_ready, it * PAIR + (u + 1))
                    nc.tensor.matmul(u_ps[:, u % 2], r.slot[:, s, U0 + m * P:U0 + (m + 1) * P], k.h[:, chunk(c)],
                                     start=True, stop=True).then_inc(u_ready, 1)

            def down(it, u):
                s, c, m = units[u]
                pe.wait_ge(hid_ready, it * PAIR + (u + 1 + CREDIT))
                nc.tensor.matmul(acc[:, c], r.slot[:, s, D0 + m * P:D0 + (m + 1) * P], hid[:, u % HB],
                                 start=False, stop=True, skip_group_check=True).then_inc(down_done, 1)

            pe.sem_inc(down_done, CREDIT)
            if not routed:
                pe.wait_ge(zero_ready, 1)
            for c in range(NCH):
                if routed:
                    nc.tensor.matmul(acc[:, c], k.w[r.out_bias][:], r.parts[:, chunk(c)], start=True, stop=True)
                else:
                    nc.tensor.matmul(acc[:, c], zero[:], k.h[:, chunk(c)], start=True, stop=True)
            with pe.Fori(0, E // 2, 1) as it:
                for u in range(PAIR + LAG):
                    if u < PAIR:
                        up(it, u)
                    if u >= LAG:
                        down(it, u - LAG)

        @block.scalar
        def _(act):
            act.sem_inc(act_ready, CREDIT)
            with act.Fori(0, E // 2, 1) as it:
                for u, (s, c, m) in enumerate(units):
                    act.wait_ge(g_ready, it * PAIR + (u + 1))
                    act.wait_ge(mid_ready if gated and routed else hid_ready, it * PAIR + (u + 1))
                    bias = r.slot[:, s, BG + m:BG + m + 1] if routed else 0.0
                    nc.scalar.activation(act_out[:, u % 2], g_ps[:, u % 2], func, bias=bias).then_inc(act_ready, 1)

        @block.vector
        def _(dve):
            if not routed:
                nc.vector.memset(zero[:], 0.0).then_inc(zero_ready, 1)
            dve.sem_inc(hid_ready, CREDIT)
            dve.sem_inc(mid_ready, CREDIT)
            with dve.Fori(0, E // 2, 1) as it:
                for u, (s, c, m) in enumerate(units):
                    if gated:
                        dve.wait_ge(u_ready, it * PAIR + (u + 1))
                    if gated and routed:
                        dve.wait_ge(act_ready, it * PAIR + (u + 1 + CREDIT))
                        dve.wait_ge(hid_ready, it * PAIR + (u + 1))
                        nc.vector.scalar_tensor_tensor(
                            out=mid[:, u % 2], in0=u_ps[:, u % 2], scalar=r.slot[:, s, BU + m:BU + m + 1],
                            in1=act_out[:, u % 2], op0=ALU.add, op1=ALU.mult).then_inc(mid_ready, 1)
                        dve.wait_ge(mid_ready, it * PAIR + (u + 1 + CREDIT))
                    else:
                        dve.wait_ge(act_ready, it * PAIR + (u + 1 + CREDIT))
                    if u >= HB:
                        dve.wait_ge(down_done, it * PAIR + (u - HB + 1 + CREDIT))
                    else:
                        dve.wait_ge(down_done, it * PAIR + CREDIT)
                    if routed:
                        nc.vector.tensor_tensor(
                            hid[:, u % HB], (mid if gated else act_out)[:, u % 2],
                            r.wide[:, bass.ds(it * 2 + s, 1), chunk(c)].rearrange("p o n -> p (o n)"),
                            ALU.mult).then_inc(hid_ready, 1)
                    else:
                        nc.vector.tensor_tensor(hid[:, u % HB], u_ps[:, u % 2], act_out[:, u % 2],
                                                ALU.mult).then_inc(hid_ready, 1)
            dve.wait_ge(down_done, E * UNITS + CREDIT)
            for c in range(NCH):
                b = batch_of(c)
                last = nc.vector.scalar_tensor_tensor(
                    out=k.x[:, chunk(c)], in0=acc[:, c], scalar=k.mod[:, layer, GATE_B, b:b + 1],
                    in1=k.x[:, chunk(c)], op0=ALU.mult, op1=ALU.add)
            last.then_inc(added, 1)


def experts_block(nc, k, layer, tiles, func, gated, routed, top_sum_eps=None):
    cols = tiles * P * (3 if gated else 2) + (tiles * (2 if gated else 1) if routed else 0)
    with ExitStack() as ctx:
        r = Kit()
        r.weights = k.dram[f"L{layer}_experts"]
        r.slot = ctx.enter_context(nc.sbuf_tensor(f"slot{layer}", [P, 2, cols], F32))
        r.slot_loaded = [nc.alloc_semaphore(f"slot{layer}_{s}") for s in range(2)]
        r.out_bias = f"L{layer}_out_bias"
        if routed:
            r.parts = ctx.enter_context(nc.sbuf_tensor(f"parts{layer}", [PARTS * PART, T], F32))
            r.wide = ctx.enter_context(nc.sbuf_tensor(f"wide{layer}", [P, E, T], F32))
            routing_stage(nc, k, r, f"L{layer}_router", top_sum_eps)
        else:
            with nc.Block() as block:
                @block.sync
                def _(sp):
                    for s in range(2):
                        sp.dma_start(r.slot[:, s], r.weights[s]).then_inc(r.slot_loaded[s], 16)
        experts_stage(nc, k, r, layer, tiles, func, gated, routed)

HEADS1 = 16
HD1 = 64
LANE = 32


def pair_attention_stage(nc, k):
    NJ = SEQ // CH
    M = HEADS1 * HD1 // P
    units = [(j, t) for j in range(NJ) for t in range(M)]
    U = len(units)
    scale = 1.0 / HD1 ** 0.5
    wq, wkv, wo = k.w["L1_Wq"], k.w["L1_Wkv"], k.w["L1_Wo"]
    row = lambda i, j: slice(i * SEQ + j * CH, i * SEQ + (j + 1) * CH)
    lanes = lambda i, j: slice(LANE * (2 * i + j), LANE * (2 * i + j) + LANE)
    with ExitStack() as ctx:
        sb = lambda name, shape: ctx.enter_context(nc.sbuf_tensor(name + "_pa", shape, F32))
        hd = sb("h_diff", [P, SEQ])
        kd, prod = sb("k_diff", [P, 2, CH]), sb("qk_prod", [P, 2, 2, CH])
        mx, e0, e1, w0 = sb("mx", [P, CH]), sb("e0", [P, CH]), sb("e1", [P, CH]), sb("w0", [P, CH])
        vd, wv, vec = sb("v_diff", [P, 2, CH]), sb("w_v", [P, 2, 2, CH]), sb("vec", [P, 2, 2, CH])
        sem = lambda name: nc.alloc_semaphore(name + "_pa")
        hd_ready, kd_ps_ready, q_ready, kd_ready, prod_ready, dots_done = (
            sem("hd"), sem("kd_ps"), sem("q"), sem("kd"), sem("prod"), sem("dots"))
        soft_step, e_ready = sem("soft_step"), sem("e")
        vd_ps_ready, v1_ready, wide_ready, vd_ready, wv_ready, vec_ready, out_ready, added = (
            sem("vd_ps"), sem("v1"), sem("wide"), sem("vd"), sem("wv"), sem("vec"), sem("out"), sem("added"))

        with ExitStack() as first:
            q_ps = first.enter_context(nc.psum_tensor("q_ps_pa", [P, 2, 2, CH], F32))
            kd_ps = first.enter_context(nc.psum_tensor("kd_ps_pa", [P, 2, CH], F32))
            d_ps = first.enter_context(nc.psum_tensor("d_ps_pa", [P, CH], F32))
            block = first.enter_context(nc.Block())

            @block.tensor
            def _(pe):
                def project(u):
                    j, t = units[u]
                    if u >= 2:
                        pe.wait_ge(kd_ready, u - 1)
                    nc.tensor.matmul(kd_ps[:, u % 2], wkv[:, tile(t)], hd[:, j * CH:(j + 1) * CH],
                                     start=True, stop=True).then_inc(kd_ps_ready, 1)
                    if u >= 2:
                        pe.wait_ge(prod_ready, 2 * (u - 1))
                    for i in range(NB):
                        nc.tensor.matmul(q_ps[:, u % 2, i], wq[:, tile(t)], k.h[:, row(i, j)],
                                         start=True, stop=True).then_inc(q_ready, 1)

                def dots(u):
                    j, t = units[u]
                    for i in range(NB):
                        pe.wait_ge(prod_ready, 2 * u + i + 1)
                        nc.tensor.matmul(d_ps[lanes(i, j)], k.w["head_sum"][:, t], prod[:, u % 2, i],
                                         start=t == 0, stop=t == M - 1,
                                         tile_position=(0, lanes(i, j).start)).then_inc(dots_done, 1)

                pe.wait_ge(hd_ready, 1)
                for u in range(U + 1):
                    if u < U:
                        project(u)
                    if u >= 1:
                        dots(u - 1)

            @block.scalar
            def _(act):
                for u in range(U):
                    act.wait_ge(kd_ps_ready, u + 1)
                    if u >= 2:
                        act.wait_ge(prod_ready, 2 * (u - 1))
                    nc.scalar.activation(kd[:, u % 2], kd_ps[:, u % 2], ACT.Copy).then_inc(kd_ready, 1)
                act.wait_ge(soft_step, 2)
                nc.scalar.activation(e0[:], e0[:], ACT.Exp, scale=scale).then_inc(e_ready, 1)
                nc.scalar.activation(e1[:], mx[:], ACT.Exp, scale=-scale).then_inc(e_ready, 1)

            @block.vector
            def _(dve):
                nc.vector.tensor_tensor(hd[:], k.h[:, 0:SEQ], k.h[:, SEQ:T], ALU.subtract).then_inc(hd_ready, 1)
                for u in range(U):
                    dve.wait_ge(kd_ready, u + 1)
                    for i in range(NB):
                        dve.wait_ge(q_ready, 2 * u + i + 1)
                        if u >= 2:
                            dve.wait_ge(dots_done, 2 * (u - 2) + i + 1)
                        nc.vector.tensor_tensor(prod[:, u % 2, i], q_ps[:, u % 2, i], kd[:, u % 2],
                                                ALU.mult).then_inc(prod_ready, 1)
                dve.wait_ge(dots_done, 2 * U)
                nc.vector.tensor_scalar(mx[:], d_ps[:], 0.0, None, ALU.max).then_inc(soft_step, 1)
                dve.wait_ge(soft_step, 1)
                nc.vector.tensor_tensor(e0[:], d_ps[:], mx[:], ALU.subtract).then_inc(soft_step, 1)
                dve.wait_ge(e_ready, 2)
                nc.vector.tensor_tensor(e1[:], e0[:], e1[:], ALU.add).then_inc(soft_step, 1)
                dve.wait_ge(soft_step, 3)
                nc.vector.reciprocal(e1[:], e1[:]).then_inc(soft_step, 1)
                dve.wait_ge(soft_step, 4)
                nc.vector.tensor_tensor(w0[:], e0[:], e1[:], ALU.mult).then_inc(soft_step, 1)

        vd_ps = ctx.enter_context(nc.psum_tensor("vd_ps_pa", [P, CH], F32))
        v1_ps = ctx.enter_context(nc.psum_tensor("v1_ps_pa", [P, 2, CH], F32))
        wide_ps = ctx.enter_context(nc.psum_tensor("wide_ps_pa", [P, 2, CH], F32))
        o_ps = ctx.enter_context(nc.psum_tensor("o_ps_pa", [P, 2, CH], F32))
        block = ctx.enter_context(nc.Block())
        VK = M * P

        @block.tensor
        def _(pe):
            def project(u):
                j, t = units[u]
                w = wkv[:, VK + t * P:VK + (t + 1) * P]
                if u >= 1:
                    pe.wait_ge(vd_ready, u)
                nc.tensor.matmul(vd_ps[:], w, hd[:, j * CH:(j + 1) * CH],
                                 start=True, stop=True).then_inc(vd_ps_ready, 1)
                for i in range(NB):
                    if u >= 1:
                        pe.wait_ge(wv_ready, 2 * (u - 1) + i + 1)
                    q = lanes(i, j)
                    nc.tensor.matmul(wide_ps[:, i], k.w["head_pick"][q, t], w0[q], start=True, stop=True,
                                     tile_position=(q.start, 0)).then_inc(wide_ready, 1)
                if u >= 2:
                    pe.wait_ge(vec_ready, 2 * (u - 1))
                nc.tensor.matmul(v1_ps[:, u % 2], w, k.h[:, row(1, j)],
                                 start=True, stop=True).then_inc(v1_ready, 1)

            def out(u):
                j, t = units[u]
                for i in range(NB):
                    pe.wait_ge(vec_ready, 2 * u + i + 1)
                    if j and t == 0:
                        pe.wait_ge(added, 2 * (j - 1) + i + 1)
                    nc.tensor.matmul(o_ps[:, i], wo[:, t], vec[:, u % 2, i],
                                     start=t == 0, stop=t == M - 1).then_inc(out_ready, 1)

            for u in range(U + 1):
                if u < U:
                    project(u)
                if u >= 1:
                    out(u - 1)

        @block.scalar
        def _(act):
            for u in range(U):
                act.wait_ge(vd_ps_ready, u + 1)
                if u >= 2:
                    act.wait_ge(wv_ready, 2 * (u - 1))
                nc.scalar.activation(vd[:, u % 2], vd_ps[:], ACT.Copy).then_inc(vd_ready, 1)

        @block.vector
        def _(dve):
            def add(j):
                for i in range(NB):
                    dve.wait_ge(out_ready, 2 * (j + 1) * M - 1 + i)
                    nc.vector.scalar_tensor_tensor(out=k.x[:, row(i, j)], in0=o_ps[:, i],
                                                   scalar=k.mod[:, 1, GATE_A, i:i + 1], in1=k.x[:, row(i, j)],
                                                   op0=ALU.mult, op1=ALU.add).then_inc(added, 1)

            for u in range(U):
                dve.wait_ge(vd_ready, u + 1)
                for i in range(NB):
                    dve.wait_ge(wide_ready, 2 * u + i + 1)
                    if u >= 2:
                        dve.wait_ge(vec_ready, 2 * (u - 2) + i + 1)
                    nc.vector.tensor_tensor(wv[:, u % 2, i], wide_ps[:, i], vd[:, u % 2],
                                            ALU.mult).then_inc(wv_ready, 1)
                dve.wait_ge(v1_ready, u + 1)
                for i in range(NB):
                    dve.wait_ge(wv_ready, 2 * u + i + 1)
                    if u >= 2:
                        dve.wait_ge(out_ready, 2 * (u - 2) + i + 1)
                    nc.vector.tensor_tensor(vec[:, u % 2, i], wv[:, u % 2, i], v1_ps[:, u % 2],
                                            ALU.add).then_inc(vec_ready, 1)
                if u == M:
                    add(0)
            add(1)


DEPTH = 2
HEADS2 = 8
HD2 = 64
HALF = HD2 // 2
INNER = HEADS2 * HD2
WINDOW = 64
HID = P * 4 * 2 // 3
QK_SCALE = 8.0
NORM_EPS = 1e-12
QT = INNER // P


def shift_stage(nc, k, depth, half, dst):
    with ExitStack() as ctx:
        shifted = nc.alloc_semaphore(f"shifted{depth}{half}")
        block = ctx.enter_context(nc.Block())
        late = slice(P // 2, P)

        @block.scalar
        def _(act):
            nc.scalar.activation(dst[0:P // 2], k.h[0:P // 2], ACT.Copy).then_inc(shifted, 1)

        @block.vector
        def _(dve):
            for b in range(NB):
                nc.vector.memset(dst[late, b * SEQ:b * SEQ + 1], 0.0).then_inc(shifted, 1)
                nc.vector.tensor_copy(dst[late, b * SEQ + 1:(b + 1) * SEQ],
                                      k.h[late, b * SEQ:(b + 1) * SEQ - 1]).then_inc(shifted, 1)


def local_qkv_stage(nc, k, s, depth):
    tag = f"_lq{depth}"
    w = k.w["L1_wqkv"]
    heads = lambda ap: ap.rearrange("p (h d) -> p h d", d=HD2)
    with ExitStack() as ctx:
        sb = lambda name, shape: ctx.enter_context(nc.sbuf_tensor(name + tag, shape, F32))
        table = sb("table", [P, 4, SEQ // P, HD2])
        sq, ss, norm, rk = sb("sq", [P, 2 * INNER]), sb("ss", [P, 2, 2 * HEADS2]), sb("norm", [P, 2, 2 * HEADS2]), sb("rk", [P, 2, 2 * HEADS2])
        straight, crossed = sb("straight", [P, 2, 2, INNER]), sb("crossed", [P, 2, 2, INNER])
        turned = straight
        qkv_ps = ctx.enter_context(nc.psum_tensor("qkv_ps" + tag, [P, 2, 3, CH], F32))
        t_ps = ctx.enter_context(nc.psum_tensor("t_ps" + tag, [P, 2, QT, P], F32))
        sem = lambda name: nc.alloc_semaphore(name + tag)
        tables_ready, qkv_ready, v_read, squared, summed, normed, clipped, rk_ready = (
            sem("tables"), sem("qkv"), sem("v_read"), sem("squared"), sem("summed"), sem("normed"), sem("clipped"), sem("rk"))
        mults, sums_q, sums_k, k_scaled, t_ready, t_read = (
            sem("mults"), sem("sums_q"), sem("sums_k"), sem("k_scaled"), sem("t"), sem("t_read"))
        block = ctx.enter_context(nc.Block())

        @block.tensor
        def _(pe):
            def project(t):
                if t >= 2:
                    pe.wait_ge(v_read, t - 1)
                    pe.wait_ge(squared, t - 1)
                    pe.wait_ge(mults, 4 * (t - 1))
                for j in range(3):
                    last = nc.tensor.matmul(qkv_ps[:, t % 2, j], s.shifted[:, tile(t)],
                                            w[:, depth, j * INNER:(j + 1) * INNER], start=True, stop=True)
                last.then_inc(qkv_ready, 1)

            def turn(t):
                for i in range(2):
                    pe.wait_ge(k_scaled if i else sums_q, t + 1)
                    if t:
                        pe.wait_ge(t_read, 2 * (t - 1) + i + 1)
                    for j in range(QT):
                        last = nc.tensor.transpose(t_ps[:, i, j], turned[:, t % 2, i, tile(j)], k.w["ident"][:])
                    last.then_inc(t_ready, 1)

            for t in range(NT + 1):
                if t < NT:
                    project(t)
                if t >= 1:
                    turn(t - 1)

        @block.scalar
        def _(act):
            def store(t):
                for i, dst in enumerate((s.qT, s.kT)):
                    act.wait_ge(t_ready, 2 * t + i + 1)
                    nc.scalar.activation(dst[:, :, tile(t)], t_ps[:, i], ACT.Copy).then_inc(t_read, 1)

            for t in range(NT + 1):
                if t < NT:
                    act.wait_ge(qkv_ready, t + 1)
                    if t >= 1:
                        act.wait_ge(summed, t)
                    nc.scalar.activation(sq[:].rearrange("p (j n) -> p j n", j=2), qkv_ps[:, t % 2, 0:2],
                                         ACT.Square).then_inc(squared, 1)
                    nc.scalar.activation(s.v[:, t], qkv_ps[:, t % 2, 2], ACT.Copy).then_inc(v_read, 1)
                    act.wait_ge(summed, t + 1)
                    if t >= 2:
                        act.wait_ge(clipped, t - 1)
                    nc.scalar.activation(norm[:, t % 2], ss[:, t % 2], ACT.Sqrt).then_inc(normed, 1)
                if t >= 1:
                    store(t - 1)

        @block.vector
        def _(dve):
            for j in range(4):
                nc.vector.tensor_tensor(table[:, j], k.w["rotary"][:, j],
                                        k.w["L1_qk_scale"][:, depth, j].unsqueeze(1).to_broadcast([P, SEQ // P, HD2]),
                                        ALU.mult).then_inc(tables_ready, 1)
            dve.wait_ge(tables_ready, 4)
            for t in range(NT):
                dve.wait_ge(squared, t + 1)
                if t >= 2:
                    dve.wait_ge(normed, t - 1)
                nc.vector.tensor_reduce(ss[:, t % 2], heads(sq[:]), AX, ALU.add).then_inc(summed, 1)
                if t >= 2:
                    dve.wait_ge(t_ready, 2 * (t - 1))
                dve.wait_ge(qkv_ready, t + 1)
                dve.wait_ge(v_read, t + 1)
                for i in range(2):
                    ps = heads(qkv_ps[:, t % 2, i])
                    cos = table[:, 2 * i, t % (SEQ // P)].unsqueeze(1).to_broadcast([P, HEADS2, HD2])
                    sin = table[:, 2 * i + 1, t % (SEQ // P)]
                    nc.vector.tensor_tensor(heads(straight[:, t % 2, i]), ps, cos, ALU.mult).then_inc(mults, 1)
                    for half in range(2):
                        here, there = slice(half * HALF, (half + 1) * HALF), slice((1 - half) * HALF, (2 - half) * HALF)
                        last = nc.vector.tensor_tensor(
                            heads(crossed[:, t % 2, i])[:, :, here], ps[:, :, there],
                            sin[:, here].unsqueeze(1).to_broadcast([P, HEADS2, HALF]), ALU.mult)
                    last.then_inc(mults, 1)
                dve.wait_ge(normed, t + 1)
                nc.vector.tensor_scalar(norm[:, t % 2], norm[:, t % 2], NORM_EPS, None, ALU.max).then_inc(clipped, 1)
                dve.wait_ge(clipped, t + 1)
                if t >= 2:
                    dve.wait_ge(k_scaled, t - 1)
                nc.vector.reciprocal(rk[:, t % 2], norm[:, t % 2]).then_inc(rk_ready, 1)
                dve.wait_ge(rk_ready, t + 1)
                nc.vector.tensor_scalar(s.rq[:, t], rk[:, t % 2, 0:HEADS2], QK_SCALE, None, ALU.mult)

        @block.gpsimd
        def _(pool):
            for t in range(NT):
                for i, done in enumerate((sums_q, sums_k)):
                    pool.wait_ge(mults, 4 * t + 2 * i + 2)
                    nc.gpsimd.tensor_tensor(turned[:, t % 2, i], straight[:, t % 2, i], crossed[:, t % 2, i],
                                            ALU.add).then_inc(done, 1)
                pool.wait_ge(rk_ready, t + 1)
                pool.wait_ge(sums_k, t + 1)
                nc.gpsimd.tensor_tensor(heads(turned[:, t % 2, 1]), heads(turned[:, t % 2, 1]),
                                        rk[:, t % 2, HEADS2:].unsqueeze(2).to_broadcast([P, HEADS2, HD2]),
                                        ALU.mult).then_inc(k_scaled, 1)


def local_attention_stage(nc, k, s, depth):
    tag = f"_la{depth}"
    PAIRS = HEADS2 // 2
    units = [(t, p) for t in range(NT) for p in range(PAIRS)]
    U = len(units)
    first_tile = lambda t: t % (SEQ // P) == 0
    KW = 2 * P
    with ExitStack() as ctx:
        sb = lambda name, shape, dt=F32: ctx.enter_context(nc.sbuf_tensor(name + tag, shape, dt))
        mx, bias, total = sb("mx", [P, 4, 2]), sb("bias", [P, 4, 2]), sb("total", [P, 2, HEADS2])
        prob, probT = sb("prob", [P, 2, 2, KW]), sb("probT", [P, 2, 2, KW])
        inv, o = sb("inv", [P, 2, HEADS2]), sb("o", [P, 2, INNER])
        s_ps = ctx.enter_context(nc.psum_tensor("s_ps" + tag, [P, 2, 2, CH], F32))
        p_ps = ctx.enter_context(nc.psum_tensor("p_ps" + tag, [P, 2, 2, KW], F32))
        o_ps = ctx.enter_context(nc.psum_tensor("o_ps" + tag, [P, HEADS2, HD2], F32))
        t_ps = ctx.enter_context(nc.psum_tensor("ot_ps" + tag, [P, QT, P], F32))
        sem = lambda name: nc.alloc_semaphore(name + tag)
        s_ready, mx_ready, bias_ready, prob_ready, p_turned, probT_ready, o_ready = (
            sem("s"), sem("mx"), sem("bias"), sem("prob"), sem("p_turned"), sem("probT"), sem("o"))
        inv_ready, o_scaled, o_turned, oT_ready = sem("inv"), sem("o_scaled"), sem("o_turned"), sem("oT")
        block = ctx.enter_context(nc.Block())

        def blocks(t):
            return ((1, t),) if first_tile(t) else ((0, t - 1), (1, t))

        @block.tensor
        def _(pe):
            def scores(u):
                t, p = units[u]
                lo = P if first_tile(t) else 0
                if u >= 2:
                    pe.wait_ge(prob_ready, u - 1)
                for i in range(2):
                    d = slice(HD2 * i, HD2 * i + HD2)
                    out = s_ps[:, u % 2, i, lo:KW]
                    nc.tensor.matmul(out, s.qT[d, p, tile(t)], s.kT[d, p, t * P - P + lo:(t + 1) * P],
                                     start=True, stop=False)
                    last = nc.tensor.matmul(out, k.w["ident16"][:], k.w["window_mask"][:, lo:KW],
                                            start=False, stop=True)
                last.then_inc(s_ready, 1)

            def turn(u):
                t, p = units[u]
                pe.wait_ge(prob_ready, u + 1)
                if u >= 2:
                    pe.wait_ge(probT_ready, u - 1)
                for i in range(2):
                    for at, _ in blocks(t):
                        last = nc.tensor.transpose(p_ps[:, u % 2, i, tile(at)], prob[:, u % 2, i, tile(at)],
                                                   k.w["ident"][:])
                last.then_inc(p_turned, 1)

            def values(u):
                t, p = units[u]
                pe.wait_ge(probT_ready, u + 1)
                if p == 0 and t >= 1:
                    pe.wait_ge(o_scaled, t)
                for i in range(2):
                    h = 2 * p + i
                    for n, (at, kt) in enumerate(blocks(t)):
                        last = nc.tensor.matmul(o_ps[:, h], probT[:, u % 2, i, tile(at)],
                                                s.v[:, kt, h * HD2:(h + 1) * HD2],
                                                start=n == 0, stop=at == 1)
                last.then_inc(o_ready, 1)

            def turn_out(t):
                pe.wait_ge(o_scaled, t + 1)
                if t >= 1:
                    pe.wait_ge(oT_ready, t)
                for j in range(QT):
                    last = nc.tensor.transpose(t_ps[:, j], o[:, t % 2, tile(j)], k.w["ident"][:])
                last.then_inc(o_turned, 1)

            for u in range(U + 2):
                if u < U:
                    scores(u)
                if 1 <= u <= U:
                    turn(u - 1)
                if u >= 2:
                    values(u - 2)
                if u >= 2 + PAIRS and (u - 2) % PAIRS == 0:
                    turn_out((u - 2) // PAIRS - 1)
            turn_out(NT - 1)

        @block.scalar
        def _(act):
            for u, (t, p) in enumerate(units):
                lo = P if first_tile(t) else 0
                act.wait_ge(bias_ready, u + 1)
                if u >= 2:
                    act.wait_ge(p_turned, u - 1)
                if p == 0 and t >= 2:
                    act.wait_ge(inv_ready, t - 1)
                for i in range(2):
                    h = 2 * p + i
                    last = nc.scalar.activation(prob[:, u % 2, i, lo:KW], s_ps[:, u % 2, i, lo:KW], ACT.Exp,
                                                bias=bias[:, u % 4, i:i + 1], scale=s.rq[:, t, h:h + 1],
                                                accum_out=total[:, t % 2, h:h + 1])
                last.then_inc(prob_ready, 1)
                if p == 1 and t >= 1:
                    act.wait_ge(o_turned, t)
                    nc.scalar.activation(s.oT[:, :, tile(t - 1)], t_ps[:], ACT.Copy).then_inc(oT_ready, 1)
            act.wait_ge(o_turned, NT)
            nc.scalar.activation(s.oT[:, :, tile(NT - 1)], t_ps[:], ACT.Copy).then_inc(oT_ready, 1)

        @block.vector
        def _(dve):
            def maxima(u):
                t, p = units[u]
                lo = P if first_tile(t) else 0
                dve.wait_ge(s_ready, u + 1)
                if u >= 4:
                    dve.wait_ge(bias_ready, u - 3)
                nc.vector.tensor_reduce(mx[:, u % 4], s_ps[:, u % 2, :, lo:KW], AX, ALU.max).then_inc(mx_ready, 1)
                dve.wait_ge(mx_ready, u + 1)
                if u >= 4:
                    dve.wait_ge(prob_ready, u - 3)
                nc.vector.scalar_tensor_tensor(out=bias[:, u % 4], in0=mx[:, u % 4], scalar=-1.0,
                                               in1=s.rq[:, t, 2 * p:2 * p + 2], op0=ALU.mult,
                                               op1=ALU.mult).then_inc(bias_ready, 1)

            def normalise(t):
                dve.wait_ge(prob_ready, (t + 1) * PAIRS)
                if t >= 2:
                    dve.wait_ge(o_scaled, t - 1)
                nc.vector.reciprocal(inv[:, t % 2], total[:, t % 2]).then_inc(inv_ready, 1)
                dve.wait_ge(inv_ready, t + 1)
                dve.wait_ge(o_ready, (t + 1) * PAIRS)
                if t >= 2:
                    dve.wait_ge(o_turned, t - 1)
                nc.vector.tensor_tensor(o[:, t % 2].rearrange("p (h d) -> p h d", d=HD2), o_ps[:],
                                        inv[:, t % 2].unsqueeze(2).to_broadcast([P, HEADS2, HD2]),
                                        ALU.mult).then_inc(o_scaled, 1)

            for u in range(U + 1):
                if u < U:
                    maxima(u)
                if u >= 1:
                    t, _ = units[u - 1]
                    lo = P if first_tile(t) else 0
                    dve.wait_ge(p_turned, u)
                    if u >= 3:
                        dve.wait_ge(o_ready, u - 2)
                    nc.vector.tensor_copy(probT[:, (u - 1) % 2, :, lo:KW], p_ps[:, (u - 1) % 2, :, lo:KW]
                                          ).then_inc(probT_ready, 1)
                if u % PAIRS == 0 and u >= PAIRS:
                    normalise(u // PAIRS - 1)


def local_out_stage(nc, k, s, depth):
    with ExitStack() as ctx:
        o_ps = ctx.enter_context(nc.psum_tensor(f"wo_ps{depth}", [P, NCH, CH], F32))
        out_ready = nc.alloc_semaphore(f"wo_ready{depth}")
        added = nc.alloc_semaphore(f"wo_added{depth}")
        block = ctx.enter_context(nc.Block())

        @block.tensor
        def _(pe):
            for c in range(NCH):
                for j in range(QT):
                    last = nc.tensor.matmul(o_ps[:, c], k.w["L1_wo"][:, depth, j], s.oT[:, j, chunk(c)],
                                            start=j == 0, stop=j == QT - 1)
                last.then_inc(out_ready, 1)

        @block.vector
        def _(dve):
            for c in range(NCH):
                dve.wait_ge(out_ready, c + 1)
                nc.vector.tensor_tensor(k.h[:, chunk(c)], k.h[:, chunk(c)], o_ps[:, c], ALU.add).then_inc(added, 1)


def hidden_stage(nc, k, s, depth):
    tag = f"_hd{depth}"
    tiles = [(m, min(P, HID - m * P)) for m in range(-(-HID // P))]
    M = len(tiles)
    units = [(c, m) for c in range(NCH) for m in range(M)]
    U = len(units)
    w1, w2, b1, b2 = k.w["L1_w1"], k.w["L1_w2"], k.w["L1_b1"], k.w["L1_b2"]
    with ExitStack() as ctx:
        sb = lambda name, shape: ctx.enter_context(nc.sbuf_tensor(name + tag, shape, F32))
        gelu, hid = sb("gelu", [P, 2, CH]), sb("hid", [P, 3, CH])
        a_ps = ctx.enter_context(nc.psum_tensor("a_ps" + tag, [P, 2, CH], F32))
        g_ps = ctx.enter_context(nc.psum_tensor("g_ps" + tag, [P, 2, CH], F32))
        o_ps = ctx.enter_context(nc.psum_tensor("o_ps" + tag, [P, 2, CH], F32))
        sem = lambda name: nc.alloc_semaphore(name + tag)
        g_ready, a_ready, gelu_ready, hid_ready, down_done, h_ready, x_ready = (
            sem("g"), sem("a"), sem("gelu"), sem("hid"), sem("down"), sem("h"), sem("x"))
        block = ctx.enter_context(nc.Block())

        @block.tensor
        def _(pe):
            def up(u):
                c, m = units[u]
                n = tiles[m][1]
                if u >= 2:
                    pe.wait_ge(gelu_ready, u - 1)
                    pe.wait_ge(hid_ready, u - 1)
                nc.tensor.matmul(g_ps[0:n, u % 2], w1[:, depth, HID + m * P:HID + m * P + n], s.normed[:, chunk(c)],
                                 start=True, stop=True).then_inc(g_ready, 1)
                nc.tensor.matmul(a_ps[0:n, u % 2], w1[:, depth, m * P:m * P + n], s.normed[:, chunk(c)],
                                 start=True, stop=True).then_inc(a_ready, 1)

            def down(u):
                c, m = units[u]
                n = tiles[m][1]
                pe.wait_ge(hid_ready, u + 1)
                if m == 0 and c >= 2:
                    pe.wait_ge(h_ready, c - 1)
                nc.tensor.matmul(o_ps[:, c % 2], w2[0:n, depth, m], hid[0:n, u % 3],
                                 start=m == 0, stop=m == M - 1).then_inc(down_done, 1)

            for u in range(U + 2):
                if u < U:
                    up(u)
                if u >= 2:
                    down(u - 2)

        @block.scalar
        def _(act):
            for u, (c, m) in enumerate(units):
                n = tiles[m][1]
                act.wait_ge(g_ready, u + 1)
                if u >= 2:
                    act.wait_ge(hid_ready, u - 1)
                nc.scalar.activation(gelu[0:n, u % 2], g_ps[0:n, u % 2], ACT.Gelu,
                                     bias=b1[0:n, depth, 1, m:m + 1]).then_inc(gelu_ready, 1)

        @block.vector
        def _(dve):
            def add(c):
                b = batch_of(c)
                dve.wait_ge(down_done, (c + 1) * M)
                nc.vector.scalar_tensor_tensor(out=k.h[:, chunk(c)], in0=o_ps[:, c % 2], scalar=b2[:, depth:depth + 1],
                                               in1=k.h[:, chunk(c)], op0=ALU.add, op1=ALU.add).then_inc(h_ready, 1)
                if depth == DEPTH - 1:
                    dve.wait_ge(h_ready, c + 1)
                    nc.vector.scalar_tensor_tensor(out=k.x[:, chunk(c)], in0=k.h[:, chunk(c)],
                                                   scalar=k.mod[:, 1, GATE_B, b:b + 1], in1=k.x[:, chunk(c)],
                                                   op0=ALU.mult, op1=ALU.add).then_inc(x_ready, 1)

            for u, (c, m) in enumerate(units):
                n = tiles[m][1]
                dve.wait_ge(a_ready, u + 1)
                dve.wait_ge(gelu_ready, u + 1)
                if u >= 3:
                    dve.wait_ge(down_done, u - 2)
                nc.vector.scalar_tensor_tensor(out=hid[0:n, u % 3], in0=a_ps[0:n, u % 2],
                                               scalar=b1[0:n, depth, 0, m:m + 1], in1=gelu[0:n, u % 2],
                                               op0=ALU.add, op1=ALU.mult).then_inc(hid_ready, 1)
                if m == 1 and c >= 1:
                    add(c - 1)
            add(NCH - 1)


def local_block(nc, k):
    for depth in range(DEPTH):
        with ExitStack() as ctx:
            sb = lambda name, shape: ctx.enter_context(nc.sbuf_tensor(f"{name}_lb{depth}", shape, F32))
            s = Kit()
            s.shifted, s.qT = sb("shifted", [P, T]), sb("qT", [P, QT, T])
            s.oT = s.qT
            with (nc.sbuf_tensor(f"kT{depth}", [P, QT, T], F32) as s.kT,
                  nc.sbuf_tensor(f"v{depth}", [P, NT, INNER], F32) as s.v,
                  nc.sbuf_tensor(f"rq{depth}", [P, NT, HEADS2], F32) as s.rq):
                shift_stage(nc, k, depth, 0, s.shifted)
                local_qkv_stage(nc, k, s, depth)
                local_attention_stage(nc, k, s, depth)
            local_out_stage(nc, k, s, depth)
            shift_stage(nc, k, depth, 1, s.shifted)
            s.normed = sb("normed", [P, T])
            layernorm_stage(nc, k, f"l{depth}", s.shifted, s.normed,
                            lambda b: (k.w["L1_ln"][:, 0, depth:depth + 1], k.w["L1_ln"][:, 1, depth:depth + 1]))
            hidden_stage(nc, k, s, depth)

HEADS3 = 16
HD3 = P // HEADS3
NH3 = NB * HEADS3
QTS = SEQ // P
Q_PART = (0, 0, 1, 1, 0, 2)
K_PART = (0, 1, 0, 1, 2, 0)
SLOTS = len(Q_PART)
ROWS = SLOTS * HD3
FULL = 3 * P // 4
M_PARTS = 2
QUAD = 4
NQ = NH3 // QUAD
RING = 2 * QUAD
QUARTER = P // QUAD
V1 = QUARTER


def causal_project_stage(nc, k, s):
    with ExitStack() as ctx:
        rest = ctx.enter_context(nc.sbuf_tensor("rest_cp", [P, 2, 2, CH], F32))
        part = ctx.enter_context(nc.sbuf_tensor("part_cp", [P, 2, PARTS, T], BF16))
        qk_ps = ctx.enter_context(nc.psum_tensor("qk_ps_cp", [P, 4, CH], F32))
        v_ps = ctx.enter_context(nc.psum_tensor("v_ps_cp", [P, 2, CH], F32))
        sem = lambda name: nc.alloc_semaphore(name + "_cp")
        qk_ready, part0, rest_ready, part1, part2, v_ready, v_stored, ones_ready, stored = (
            sem("qk"), sem("part0"), sem("rest"), sem("part1"), sem("part2"), sem("v"), sem("v_stored"), sem("ones"),
            sem("stored"))
        block = ctx.enter_context(nc.Block())
        units = [(c, i) for c in range(NCH) for i in range(2)]

        @block.tensor
        def _(pe):
            for u, (c, i) in enumerate(units):
                if u >= 4:
                    pe.wait_ge(rest_ready, u - 3)
                nc.tensor.matmul(qk_ps[:, u % 4], k.w["L2_W"][:, i], k.h[:, chunk(c)],
                                 start=True, stop=True).then_inc(qk_ready, 1)
            for t in range(NT):
                if t >= 2:
                    pe.wait_ge(v_stored, t - 1)
                nc.tensor.matmul(v_ps[:, t % 2, 0:P], k.h[:, tile(t)], k.w["L2_W"][:, 2],
                                 start=True, stop=True).then_inc(v_ready, 1)

        @block.scalar
        def _(act):
            for u, (c, i) in enumerate(units):
                act.wait_ge(qk_ready, u + 1)
                nc.scalar.activation(part[:, i, 0, chunk(c)], qk_ps[:, u % 4], ACT.Copy).then_inc(part0, 1)
            act.wait_ge(ones_ready, 1)
            for t in range(NT):
                b, kt = divmod(t, QTS)
                act.wait_ge(v_ready, t + 1)
                nc.scalar.activation(s.v1[:, b * HEADS3:(b + 1) * HEADS3, kt, 0:HD3],
                                     v_ps[:, t % 2, 0:P].rearrange("p (h d) -> p h d", d=HD3),
                                     ACT.Copy).then_inc(v_stored, 1)

        @block.vector
        def _(dve):
            nc.vector.memset(s.v1[:], 1.0).then_inc(ones_ready, 1)
            for u, (c, i) in enumerate(units):
                dve.wait_ge(part0, u + 1)
                if u >= 2:
                    dve.wait_ge(part2, u - 1)
                nc.vector.tensor_tensor(rest[:, u % 2, 0], qk_ps[:, u % 4], part[:, i, 0, chunk(c)],
                                        ALU.subtract).then_inc(rest_ready, 1)
                dve.wait_ge(rest_ready, u + 1)
                nc.vector.tensor_copy(part[:, i, 1, chunk(c)], rest[:, u % 2, 0]).then_inc(part1, 1)

        @block.gpsimd
        def _(pool):
            for u, (c, i) in enumerate(units):
                pool.wait_ge(part1, u + 1)
                nc.gpsimd.tensor_tensor(part[:, i, 2, chunk(c)], rest[:, u % 2, 0], part[:, i, 1, chunk(c)],
                                        ALU.subtract).then_inc(part2, 1)

        @block.sync
        def _(sp):
            for r in range(RING):
                sp.dma_start(s.ks[ROWS:FULL + M_PARTS, r], k.dram["zero_one_rows"]).then_inc(stored, 16)
                sp.dma_start(s.qs[ROWS:FULL, r], k.dram["zero_one_rows"][0:FULL - ROWS]).then_inc(stored, 16)
            sp.wait_ge(part2, len(units))
            for i, (order, dst) in enumerate(((Q_PART, s.q_dram), (K_PART, s.k_dram))):
                for slot, n in enumerate(order):
                    for b in range(NB):
                        sp.dma_start(dst[b * NQ // NB:(b + 1) * NQ // NB, slot],
                                     part[:, i, n, b * SEQ:(b + 1) * SEQ]).then_inc(stored, 16)
            sp.wait_ge(stored, 16 * 2 * (RING + SLOTS * NB))


def causal_attention_stage(nc, k, s):
    a_tiles = [(g, qt, kc) for g in range(QUAD) for qt in range(QTS) for kc in range(2) if kc * 4 <= qt]
    groups = [(j, kt) for j in range(2) for kt in range(4 * j + 4)]
    A, G = len(a_tiles), len(groups)
    B = G * QUAD
    FIRST_A, LAST_A = 2, G - 2
    PER_GROUP = -(-A // (LAST_A - FIRST_A))
    scale = 1.0 / HD3 ** 0.5
    A_BANKS = B_BANKS = 3
    M_ROWS = M_PARTS * QUAD * QTS
    with ExitStack() as ctx:
        sb = lambda name, shape, dt=F32: ctx.enter_context(nc.sbuf_tensor(name + "_ca", shape, dt))
        prob, mx = sb("prob", [P, 2, QUAD, CH]), sb("mx", [P, 2, 2, QUAD, QTS])
        m16, ms = sb("m16", [P, 2, QUAD, QTS], BF16), sb("ms", [P, 2, M_PARTS, QUAD, QTS])
        mrow = sb("mrow", [2 * M_ROWS, P], BF16)
        vh, out = sb("vh", [P, 2, QUAD, QTS, V1]), sb("out", [P, 2, 2, CH])
        a_ps = ctx.enter_context(nc.psum_tensor("a_ps_ca", [P, A_BANKS, CH], F32))
        b_ps = ctx.enter_context(nc.psum_tensor("b_ps_ca", [P, B_BANKS, CH], F32))
        o_ps = ctx.enter_context(nc.psum_tensor("o_ps_ca", [P, 2, CH], F32))
        t_ps = a_ps[:, 0]
        sem = lambda name: nc.alloc_semaphore(name + "_ca")
        loaded = [sem(f"loaded{q}") for q in range(2)]
        m_loaded = [sem(f"m_loaded{q}") for q in range(2)]
        stored = [sem(f"stored{q}") for q in range(2)]
        max_done = [sem(f"max_done{q}") for q in range(2)]
        ms_cleared, a_ready, m_step, split_ready, m_turned, mrow_ready = (
            sem("ms_cleared"), sem("a"), sem("m_step"), sem("split"), sem("m_turned"), sem("mrow"))
        b_ready, exp_done, pv_done, v_ready, out_ready = sem("b"), sem("exp"), sem("pv"), sem("v"), sem("out")
        C_PV = C_OUT = C_TURN = C_SPLIT = 2
        C_EXP, C_MROW = B_BANKS, 1
        block = ctx.enter_context(nc.Block())
        width = lambda qt, kc: min(4, qt + 1 - 4 * kc) * P
        low = lambda j, kt: max(0, kt - 4 * j) * P
        LOOPS = NQ // 2 - 1
        quad = lambda it, q: it * 2 + q
        of = lambda q: slice(q * M_ROWS, (q + 1) * M_ROWS)
        heads = lambda q: slice(q * QUAD, (q + 1) * QUAD)
        after = lambda it, q: (it + (q + 1) // 2, (q + 1) % 2)

        def whole(engine, body):
            with engine.Fori(0, LOOPS, 1) as it:
                for q in range(2):
                    body(it, q, False)
            for q in range(2):
                body(LOOPS, q, q == 1)

        @block.sync
        def _(sp):
            def load(it, q):
                src = lambda dram: dram[bass.ds(quad(it, q), 1)].rearrange("o s (d g) n -> (o s d) (g n)", g=QUAD)
                sp.dma_start(s.qs[0:ROWS, heads(q)], src(s.q_dram)).then_inc(loaded[q], 16)
                sp.dma_start(s.ks[0:ROWS, heads(q)], src(s.k_dram)).then_inc(loaded[q], 16)

            def maximum_rows(it, q):
                sp.wait_ge(mrow_ready, quad(it, q) + 1 + C_MROW)
                sp.dma_start(s.qs[FULL:FULL + M_PARTS, heads(q)], mrow[of(q)]).then_inc(m_loaded[q], 16)

            load(0, 0)
            maximum_rows(0, 0)

            def body(it, q, last):
                if not last:
                    sp.wait_ge(b_ready, quad(it, q) * B + 1)
                    load(*after(it, q))
                    maximum_rows(*after(it, q))
                sp.wait_ge(out_ready, quad(it, q) * 2 + (2 + C_OUT))
                sp.dma_start(s.o_dram[bass.ds(quad(it, q), 1)].rearrange("o p n -> p (o n)"),
                             out[:, q].rearrange("p j n -> p (j n)")).then_inc(stored[q], 16)

            whole(sp, body)
            for q in range(2):
                sp.wait_ge(stored[q], 16 * NQ // 2)

        @block.tensor
        def _(pe):
            def scores(it, q, i):
                g, qt, kc = a_tiles[i]
                w, r = width(qt, kc), q * QUAD + g
                if i == 0:
                    pe.wait_ge(loaded[q], it * 32 + 32)
                    pe.wait_ge(mrow_ready, quad(it, q) + C_MROW)
                if i >= A_BANKS:
                    pe.wait_ge(max_done[q], it * A + (i - A_BANKS + 1))
                diagonal = qt // 4 == kc
                last = nc.tensor.matmul(a_ps[:, i % A_BANKS, 0:w], s.qs[0:FULL, r, tile(qt)],
                                        s.ks[0:FULL, r, kc * CH:kc * CH + w], start=True, stop=not diagonal)
                if diagonal:
                    last = nc.tensor.matmul(a_ps[:, i % A_BANKS, w - P:w], k.w["ident16"][:], k.w["causal_mask"][:, 0],
                                            start=False, stop=True)
                last.then_inc(a_ready, 1)

            def turn_maxima(it, q):
                pe.wait_ge(split_ready, quad(it, q) + 1 + C_SPLIT)
                nc.tensor.transpose(t_ps[:, 0:P], ms[:].rearrange("p q m g t -> p (q m g t)"),
                                    k.w["ident"][:]).then_inc(m_turned, 1)

            def scores_t(it, q, u, g):
                (j, kt), r, i = groups[u], q * QUAD + g, u * QUAD + g
                lo = low(j, kt)
                if i == 0:
                    pe.wait_ge(m_loaded[q], it * 16 + 16)
                pe.wait_ge(exp_done, quad(it, q) * B + (i - B_BANKS + 1 + C_EXP))
                diagonal = kt >= 4 * j
                last = nc.tensor.matmul(b_ps[:, i % B_BANKS, lo:CH], s.ks[0:FULL + M_PARTS, r, tile(kt)],
                                        s.qs[0:FULL + M_PARTS, r, j * CH + lo:(j + 1) * CH],
                                        start=True, stop=not diagonal)
                if diagonal:
                    last = nc.tensor.matmul(b_ps[:, i % B_BANKS, lo:lo + P], k.w["ident16"][:],
                                            k.w["causal_mask"][:, 1], start=False, stop=True)
                last.then_inc(b_ready, 1)

            def values(it, q, u):
                j, kt = groups[u]
                lo = low(j, kt)
                if u == 0:
                    pe.wait_ge(v_ready, quad(it, q) + 1)
                if kt == 0:
                    pe.wait_ge(out_ready, quad(it, q) * 2 + (j - 2 + 1 + C_OUT))
                pe.wait_ge(exp_done, quad(it, q) * B + ((u + 1) * QUAD + C_EXP))
                for g in range(QUAD):
                    last = nc.tensor.matmul(o_ps[g * QUARTER:(g + 1) * QUARTER, j, lo:CH], vh[:, q, g, kt],
                                            prob[:, u % 2, g, lo:CH], start=kt == 0, stop=kt == 4 * j + 3,
                                            tile_position=(0, g * QUARTER), skip_group_check=True)
                last.then_inc(pv_done, 1)

            pe.sem_inc(m_turned, C_TURN)
            pe.sem_inc(pv_done, C_PV)
            for i in range(A):
                scores(0, 0, i)
            pe.wait_ge(ms_cleared, 1)
            turn_maxima(0, 0)

            def body(it, q, last):
                i = 0
                for u in range(G):
                    for g in range(QUAD):
                        scores_t(it, q, u, g)
                        if u >= FIRST_A and not last:
                            to = min(A, (u - FIRST_A) * PER_GROUP + (g + 1) * PER_GROUP // QUAD)
                            while i < to:
                                scores(*after(it, q), i)
                                i += 1
                    if u == LAST_A and not last:
                        turn_maxima(*after(it, q))
                    if u >= 1:
                        values(it, q, u - 1)
                values(it, q, G - 1)

            whole(pe, body)

        @block.scalar
        def _(act):
            def maxima_row(it, q):
                act.wait_ge(m_turned, quad(it, q) + (1 + C_TURN))
                act.wait_ge(m_loaded[q], it * 16)
                nc.scalar.activation(mrow[of(q)], t_ps[of(q), 0:P], ACT.Copy).then_inc(mrow_ready, 1)

            def take_out(it, q, j):
                act.wait_ge(stored[q], it * 16)
                act.wait_ge(pv_done, quad(it, q) * G + (4 * (j + 1) + 4 * j + C_PV))
                nc.scalar.activation(out[:, q, j], o_ps[:, j], ACT.Copy).then_inc(out_ready, 1)

            act.sem_inc(exp_done, C_EXP)
            act.sem_inc(mrow_ready, C_MROW)
            act.sem_inc(out_ready, C_OUT)
            act.wait_ge(m_turned, 1 + C_TURN)
            nc.scalar.activation(mrow[of(0)], t_ps[of(0), 0:P], ACT.Copy).then_inc(mrow_ready, 1)

            def body(it, q, last):
                for u, (j, kt) in enumerate(groups):
                    lo = low(j, kt)
                    for g in range(QUAD):
                        i = u * QUAD + g
                        act.wait_ge(b_ready, quad(it, q) * B + (i + 1))
                        if g == 0:
                            act.wait_ge(pv_done, quad(it, q) * G + (u - 2 + 1 + C_PV))
                        nc.scalar.activation(prob[:, u % 2, g, lo:CH], b_ps[:, i % B_BANKS, lo:CH], ACT.Exp,
                                             scale=scale).then_inc(exp_done, 1)
                    if u == 5:
                        take_out(it, q, 0)
                    if u == LAST_A and not last:
                        maxima_row(*after(it, q))
                take_out(it, q, 1)

            whole(act, body)

        @block.gpsimd
        def _(pool):
            def take(it, q):
                nc.gpsimd.tensor_copy(vh[:, q].rearrange("p g t d -> p (g t) d"),
                                      s.v1[:, bass.ds(quad(it, q) * QUAD, QUAD)].rearrange("p g t d -> p (g t) d")
                                      ).then_inc(v_ready, 1)

            take(0, 0)

            def body(it, q, last):
                if not last:
                    pool.wait_ge(out_ready, quad(it, q) * 2 + C_OUT)
                    take(*after(it, q))

            whole(pool, body)

        @block.vector
        def _(dve):
            def maximum(it, q, i):
                g, qt, kc = a_tiles[i]
                if i == 0:
                    dve.wait_ge(split_ready, quad(it, q) + (1 - 2 + C_SPLIT))
                dve.wait_ge(a_ready, quad(it, q) * A + (i + 1))
                nc.vector.tensor_reduce(mx[:, q, kc, g, qt:qt + 1], a_ps[:, i % A_BANKS, 0:width(qt, kc)], AX,
                                        ALU.max).then_inc(max_done[q], 1)

            def split(it, q):
                n = quad(it, q) * 3
                if q == 1:
                    dve.wait_ge(ms_cleared, 1)
                m = mx[:, q, 0]
                dve.wait_ge(max_done[q], it * A + A)
                nc.vector.tensor_tensor(m[:, :, 4:], m[:, :, 4:], mx[:, q, 1, :, 4:], ALU.max).then_inc(m_step, 1)
                dve.wait_ge(m_step, n + 1)
                nc.vector.tensor_scalar(m16[:, q], m, -1.0, None, ALU.mult).then_inc(m_step, 1)
                dve.wait_ge(m_step, n + 2)
                dve.wait_ge(m_turned, quad(it, q) + (1 - 2 + C_TURN))
                nc.vector.tensor_copy(ms[:, q, 0], m16[:, q]).then_inc(m_step, 1)
                dve.wait_ge(m_step, n + 3)
                nc.vector.scalar_tensor_tensor(out=ms[:, q, 1], in0=m, scalar=-1.0, in1=m16[:, q],
                                               op0=ALU.mult, op1=ALU.subtract).then_inc(split_ready, 1)

            dve.sem_inc(split_ready, C_SPLIT)
            nc.vector.memset(ms[:, 1], 0.0).then_inc(ms_cleared, 1)
            for i in range(A):
                maximum(0, 0, i)
            split(0, 0)

            def body(it, q, last):
                if not last:
                    for i in range(A):
                        maximum(*after(it, q), i)
                    split(*after(it, q))

            whole(dve, body)


def causal_out_stage(nc, k, s):
    with ExitStack() as ctx:
        ys = ctx.enter_context(nc.sbuf_tensor("ys_co", [P, 2, T], F32))
        o_ps = ctx.enter_context(nc.psum_tensor("o_ps_co", [P, NCH, CH], F32))
        loaded = [nc.alloc_semaphore(f"loaded{b}_co") for b in range(NB)]
        inv_ready, y_ready, out_ready, added = (
            nc.alloc_semaphore(n + "_co") for n in ("inv", "y", "out", "added"))
        block = ctx.enter_context(nc.Block())
        rows_of = s.o_dram.rearrange("(b q) (g e) n -> b q g e n", b=NB, e=QUARTER)

        @block.sync
        def _(sp):
            for b in range(NB):
                for i in range(2):
                    sp.dma_start(ys[:, i, b * SEQ:(b + 1) * SEQ],
                                 rows_of[b, :, :, i * HD3:(i + 1) * HD3]).then_inc(loaded[b], 16)

        @block.tensor
        def _(pe):
            for c in range(NCH):
                pe.wait_ge(y_ready, c + 1)
                nc.tensor.matmul(o_ps[:, c], k.w["L2_W"][:, 3], ys[:, 0, chunk(c)],
                                 start=True, stop=True).then_inc(out_ready, 1)

        @block.vector
        def _(dve):
            for c in range(NCH):
                if c % 2 == 0:
                    dve.wait_ge(loaded[batch_of(c)], 32)
                nc.vector.reciprocal(ys[:, 1, chunk(c)], ys[:, 1, chunk(c)]).then_inc(inv_ready, 1)
                dve.wait_ge(inv_ready, c + 1)
                nc.vector.tensor_tensor(ys[:, 0, chunk(c)], ys[:, 0, chunk(c)], ys[:, 1, chunk(c)],
                                        ALU.mult).then_inc(y_ready, 1)
            for c in range(NCH):
                b = batch_of(c)
                dve.wait_ge(out_ready, c + 1)
                nc.vector.scalar_tensor_tensor(out=k.x[:, chunk(c)], in0=o_ps[:, c],
                                               scalar=k.mod[:, 2, GATE_A, b:b + 1], in1=k.x[:, chunk(c)],
                                               op0=ALU.mult, op1=ALU.add).then_inc(added, 1)


def causal_attention_block(nc, k):
    with ExitStack() as ctx:
        s = Kit()
        s.q_dram = nc.dram_tensor("q_parts", [NQ, SLOTS, QUAD * HD3, SEQ], BF16).ap()
        s.k_dram = nc.dram_tensor("k_parts", [NQ, SLOTS, QUAD * HD3, SEQ], BF16).ap()
        s.o_dram = nc.dram_tensor("o_and_sums", [NQ, P, SEQ], F32).ap()
        with (nc.sbuf_tensor("qs", [FULL + M_PARTS, RING, SEQ], BF16) as s.qs,
              nc.sbuf_tensor("ks", [FULL + M_PARTS, RING, SEQ], BF16) as s.ks,
              nc.sbuf_tensor("v1_ca", [P, NH3, QTS, V1], F32) as s.v1):
            causal_project_stage(nc, k, s)
            causal_attention_stage(nc, k, s)
        causal_out_stage(nc, k, s)

EPS_SUM = 1e-7
EPS_NORM = 1e-12


def linear_attention_block(nc, k):
    TPR = SEQ // P
    with ExitStack() as ctx:
        sb = lambda name, shape: ctx.enter_context(nc.sbuf_tensor(name + "_li", shape, F32))
        w, bias, mean = sb("w", [P, 3 * P]), sb("bias", [P, 3 * P]), sb("mean", [P, 4])
        qkv, q2, k2 = sb("qkv", [P, 2, 3 * P]), sb("q2", [P, NT, P]), sb("k2", [P, NT, P])
        v, q4 = sb("v", [P, NT, P]), sb("q4", [P, P])
        sums = sb("sums", [P, 3, NT])
        f = sb("f", [P, 6, NT])
        qT, kv, kn, kf, y, o = (sb("qT", [P, T]), sb("kv", [P, NB, P]), sb("kn", [P, NB]), sb("kf", [P, NB]),
                                sb("y", [P, 2, CH]), sb("o", [P, 2, CH]))
        gb = sb("gate_bias", [P, NB])
        sem = lambda name: nc.alloc_semaphore(name + "_li")

        with ExitStack() as first:
            ps = first.enter_context(nc.psum_tensor("qkv_ps_li", [P, 2, CH], F32))
            centered, qkv_ready, biased, q_squared, k_squared, summed = (
                sem("centered"), sem("qkv"), sem("biased"), sem("q_squared"), sem("k_squared"), sem("summed"))
            block = first.enter_context(nc.Block())

            @block.tensor
            def _(pe):
                pe.wait_ge(centered, 5)
                for t in range(NT):
                    if t >= 2:
                        pe.wait_ge(biased, t - 1)
                    nc.tensor.matmul(ps[:, t % 2, 0:3 * P], k.h[:, tile(t)], w[:], start=True, stop=True).then_inc(qkv_ready, 1)

            @block.vector
            def _(dve):
                blocks = lambda ap: ap.rearrange("p (i n) -> p i n", n=P)
                for j, src in enumerate((k.w["L3_Wqkv"], k.w["L3_bqkv"])):
                    nc.vector.tensor_reduce(mean[:, 2 * j:2 * j + 2], blocks(src[:, 0:2 * P]), AX, ALU.add).then_inc(centered, 1)
                dve.wait_ge(centered, 2)
                nc.vector.tensor_scalar(mean[:], mean[:], 1.0 / P, None, ALU.mult).then_inc(centered, 1)
                dve.wait_ge(centered, 3)
                for j, (src, dst) in enumerate(((k.w["L3_Wqkv"], w), (k.w["L3_bqkv"], bias))):
                    nc.vector.tensor_copy(dst[:, 2 * P:], src[:, 2 * P:])
                    nc.vector.tensor_tensor(blocks(dst[:, 0:2 * P]), blocks(src[:, 0:2 * P]),
                                            mean[:, 2 * j:2 * j + 2].unsqueeze(2).to_broadcast([P, 2, P]),
                                            ALU.subtract).then_inc(centered, 1)
                dve.wait_ge(centered, 5)
                for t in range(NT):
                    dve.wait_ge(qkv_ready, t + 1)
                    if t >= 2:
                        dve.wait_ge(k_squared, t - 1)
                    nc.vector.tensor_tensor(qkv[:, t % 2], ps[:, t % 2, 0:3 * P], bias[:], ALU.add).then_inc(biased, 1)

            @block.scalar
            def _(act):
                for t in range(NT):
                    act.wait_ge(biased, t + 1)
                    if t >= 1:
                        act.wait_ge(summed, t)
                    nc.scalar.activation(q2[:, t], qkv[:, t % 2, 0:P], ACT.Square,
                                         accum_out=sums[:, 0, t:t + 1]).then_inc(q_squared, 1)
                    nc.scalar.activation(v[:, t], qkv[:, t % 2, 2 * P:3 * P], ACT.Copy)
                    nc.scalar.activation(k2[:, t], qkv[:, t % 2, P:2 * P], ACT.Square,
                                         accum_out=sums[:, 1, t:t + 1]).then_inc(k_squared, 1)
                    act.wait_ge(q_squared, t + 1)
                    nc.scalar.activation(q4[:], q2[:, t], ACT.Square, accum_out=sums[:, 2, t:t + 1]).then_inc(summed, 1)

        with ExitStack() as second:
            kv_ps = second.enter_context(nc.psum_tensor("kv_ps_li", [P, NB, CH], F32))
            kn_ps = second.enter_context(nc.psum_tensor("kn_ps_li", [P, NB, CH], F32))
            t_ps = second.enter_context(nc.psum_tensor("t_ps_li", [P, 2, CH], F32))
            step, root, k_scaled, q_scaled, k4_ready, kv_ready, q_turned, kn_root, kv_step, qT_ready = (
                sem("step"), sem("root"), sem("k_scaled"), sem("q_scaled"), sem("k4"), sem("kv"), sem("q_turned"),
                sem("kn_root"), sem("kv_step"), sem("qT"))
            k4 = second.enter_context(nc.sbuf_tensor("k4_li", [P, 2, P], F32))
            block = second.enter_context(nc.Block())

            @block.scalar
            def _(act):
                act.wait_ge(step, 1)
                nc.scalar.activation(f[:, 2], sums[:, 2], ACT.Sqrt).then_inc(root, 1)
                for t in range(NT):
                    act.wait_ge(k_scaled, t + 1)
                    if t >= 2:
                        act.wait_ge(kv_ready, t - 1)
                    nc.scalar.activation(k4[:, t % 2], k2[:, t], ACT.Square).then_inc(k4_ready, 1)
                    if t % 4 == 3:
                        c = t // 4
                        act.wait_ge(q_turned, c + 1)
                        nc.scalar.activation(qT[:, chunk(c)], t_ps[:, c % 2], ACT.Copy).then_inc(qT_ready, 1)
                act.wait_ge(kv_step, 1)
                nc.scalar.activation(kn[:], kn[:], ACT.Sqrt).then_inc(kn_root, 1)

            @block.vector
            def _(dve):
                nc.vector.tensor_scalar(f[:, 0:2], sums[:, 0:2], EPS_SUM, None, ALU.add).then_inc(step, 1)
                dve.wait_ge(step, 1)
                nc.vector.reciprocal(f[:, 0:2], f[:, 0:2]).then_inc(step, 1)
                dve.wait_ge(step, 2)
                for t in range(NT):
                    nc.vector.tensor_scalar(k2[:, t], k2[:, t], f[:, 1, t:t + 1], None, ALU.mult).then_inc(k_scaled, 1)
                dve.wait_ge(root, 1)
                nc.vector.tensor_tensor(f[:, 3], f[:, 2], f[:, 0], ALU.mult).then_inc(step, 1)
                dve.wait_ge(step, 3)
                nc.vector.tensor_scalar(f[:, 3], f[:, 3], EPS_NORM, float(SEQ) ** 0.5, ALU.max, ALU.mult).then_inc(step, 1)
                dve.wait_ge(step, 4)
                nc.vector.reciprocal(f[:, 4], f[:, 3]).then_inc(step, 1)
                dve.wait_ge(step, 5)
                nc.vector.tensor_tensor(f[:, 5], f[:, 4], f[:, 0], ALU.mult).then_inc(step, 1)
                dve.wait_ge(step, 6)
                for t in range(NT):
                    nc.vector.tensor_scalar(q2[:, t], q2[:, t], f[:, 5, t:t + 1], None, ALU.mult).then_inc(q_scaled, 1)
                dve.wait_ge(kv_ready, NT)
                for b in range(NB):
                    last = nc.vector.tensor_copy(kn[:, b:b + 1], kn_ps[:, b, 0:1])
                last.then_inc(kv_step, 1)
                dve.wait_ge(kn_root, 1)
                nc.vector.tensor_scalar(kn[:], kn[:], EPS_NORM, None, ALU.max).then_inc(kv_step, 1)
                dve.wait_ge(kv_step, 2)
                nc.vector.reciprocal(kf[:], kn[:]).then_inc(kv_step, 1)
                dve.wait_ge(kv_step, 3)
                for b in range(NB):
                    nc.vector.tensor_scalar(kv[:, b], kv_ps[:, b, 0:P], kf[:, b:b + 1], None, ALU.mult).then_inc(kv_step, 1)
                nc.vector.tensor_scalar(gb[:], k.mod[:, 3, GATE_A], k.w["L3_bln"][:], None, ALU.mult).then_inc(kv_step, 1)

            @block.tensor
            def _(pe):
                for t in range(NT):
                    b, first_t, last_t = t // TPR, t % TPR == 0, t % TPR == TPR - 1
                    pe.wait_ge(k_scaled, t + 1)
                    nc.tensor.matmul(kv_ps[:, b, 0:P], k2[:, t], v[:, t], start=first_t, stop=last_t)
                    pe.wait_ge(k4_ready, t + 1)
                    nc.tensor.matmul(kn_ps[:, b, 0:1], k4[:, t % 2], k.w["ones"][:, 0:1],
                                     start=first_t, stop=last_t).then_inc(kv_ready, 1)
                    pe.wait_ge(q_scaled, t + 1)
                    if t % 4 == 0 and t >= 8:
                        pe.wait_ge(qT_ready, t // 4 - 1)
                    last = nc.tensor.transpose(t_ps[:, t // 4 % 2, tile(t % 4)], q2[:, t], k.w["ident"][:])
                    if t % 4 == 3:
                        last.then_inc(q_turned, 1)

        y_ps = ctx.enter_context(nc.psum_tensor("y_ps_li", [P, 2, CH], F32))
        o_ps = ctx.enter_context(nc.psum_tensor("o_ps_li", [P, 2, CH], F32))
        y_ready, y_biased, o_ready, gated, added = sem("y"), sem("y_biased"), sem("o"), sem("gated"), sem("added")
        block = ctx.enter_context(nc.Block())

        @block.tensor
        def _(pe):
            for c in range(NCH + 1):
                if c < NCH:
                    if c >= 2:
                        pe.wait_ge(y_biased, c - 1)
                    nc.tensor.matmul(y_ps[:, c % 2], w[:, 2 * P:], k.h[:, chunk(c)], start=True, stop=False)
                    nc.tensor.matmul(y_ps[:, c % 2], kv[:, batch_of(c)], qT[:, chunk(c)],
                                     start=False, stop=True).then_inc(y_ready, 1)
                if c >= 1:
                    pe.wait_ge(y_biased, c)
                    if c >= 3:
                        pe.wait_ge(gated, c - 2)
                    nc.tensor.matmul(o_ps[:, (c - 1) % 2], k.w["L3_Wln"][:], y[:, (c - 1) % 2],
                                     start=True, stop=True).then_inc(o_ready, 1)

        def project(act, c):
            b = batch_of(c)
            act.wait_ge(o_ready, c + 1)
            if c >= 2:
                act.wait_ge(added, c - 1)
            nc.scalar.activation(o[:, c % 2], o_ps[:, c % 2], ACT.Identity, bias=gb[:, b:b + 1],
                                 scale=k.mod[:, 3, GATE_A, b:b + 1]).then_inc(gated, 1)

        @block.scalar
        def _(act):
            for c in range(NCH):
                act.wait_ge(y_ready, c + 1)
                if c >= 2:
                    act.wait_ge(o_ready, c - 1)
                nc.scalar.activation(y[:, c % 2], y_ps[:, c % 2], ACT.Identity, bias=k.w["L3_bv"][:, 0:1]).then_inc(y_biased, 1)
                if c >= 1:
                    project(act, c - 1)
            project(act, NCH - 1)

        @block.vector
        def _(dve):
            for c in range(NCH):
                dve.wait_ge(gated, c + 1)
                nc.vector.tensor_tensor(k.x[:, chunk(c)], k.x[:, chunk(c)], o[:, c % 2], ALU.add).then_inc(added, 1)

def store_stage(nc, k, out):
    with ExitStack() as ctx:
        stored = nc.alloc_semaphore("stored")
        block = ctx.enter_context(nc.Block())

        @block.sync
        def _(sp):
            sp.dma_start(out, k.x[:]).then_inc(stored, 16)
            sp.wait_ge(stored, 16)


FIRST = ("mean_w", "eps", "ident", "ones", "iota8", "pick")


def transformer(nc, dram, out, only=None):
    with ExitStack() as ctx:
        k = Kit()
        k.dram = dram
        k.x = ctx.enter_context(nc.sbuf_tensor("x", [P, T], F32))
        k.h = ctx.enter_context(nc.sbuf_tensor("h", [P, T], F32))
        k.mod = ctx.enter_context(nc.sbuf_tensor("mod", [P, 4, 6, NB], F32))
        k.first_loaded = nc.alloc_semaphore("first_loaded")
        k.w = {}
        for name in FIRST:
            d = dram[name]
            k.w[name] = ctx.enter_context(nc.sbuf_tensor(f"{name}_sb", list(d.shape), d.dtype))
        modulation_stage(nc, k)
        for stages in (HALF_LAYERS if only is None else only):
            stages(nc, k)
        store_stage(nc, k, out)


HALF_LAYERS = [
    half_layer(0, 0, ("L0_W_in", "L0_heads", "L0_conv", "upto", "after", "L0_D", "L0_norm_w", "L0_W_out"), mamba_block),
    half_layer(0, 1, ("L0_router", "L0_out_bias"),
               lambda nc, k: experts_block(nc, k, 0, 2, ACT.Silu, True, True, TOP_EPS)),
    half_layer(1, 0, ("L1_Wq", "L1_Wkv", "L1_Wo", "head_sum", "head_pick"), pair_attention_stage),
    half_layer(1, 1, ("ident16", "window_mask", "rotary", "L1_wqkv", "L1_qk_scale", "L1_wo", "L1_ln", "L1_w1",
                      "L1_w2", "L1_b1", "L1_b2"), local_block),
    half_layer(2, 0, ("L2_W", "ident16", "causal_mask"), causal_attention_block),
    half_layer(2, 1, (), lambda nc, k: experts_block(nc, k, 2, 4, ACT.Silu, True, False)),
    half_layer(3, 0, ("L3_Wqkv", "L3_bqkv", "L3_bv", "L3_Wln", "L3_bln"), linear_attention_block),
    half_layer(3, 1, ("L3_router", "L3_out_bias"),
               lambda nc, k: experts_block(nc, k, 3, 4, ACT.Gelu, False, True)),
]




def rotary_tables():
    f32 = np.float32
    half = np.arange(0, HD2, 2, dtype=f32)
    t = np.arange(SEQ, dtype=f32)
    freqs = np.tile(t[:, None] * (f32(1.0) / f32(10000.0) ** (half / f32(HD2)))[None], (1, 2))
    base = (half + f32(0.4 * HD2)) / f32(1.4 * HD2)
    scale = np.tile(base[None] ** ((t - SEQ // 2) / f32(WINDOW // 2))[:, None], (1, 2))
    cos, sin = np.cos(freqs), np.sin(freqs) * np.repeat(f32([-1, 1]), HALF)[None]
    tables = np.stack([cos * scale, sin * scale, cos / scale, sin / scale]).astype(f32)
    return np.ascontiguousarray(tables.reshape(4, SEQ // P, P, HD2).transpose(2, 0, 1, 3))


def window_mask():
    i = P + np.arange(P)[:, None]
    j = np.arange(2 * P)[None, :]
    out = (i < j) | (i > j + WINDOW) | (j < i // WINDOW * WINDOW - WINDOW)
    return np.where(out, NEG, 0.0).astype(HOST16)


def constants():
    i = np.arange(P)
    heads = (2 * np.arange(8)[None, :, None] + i[:, None, None] // HD1 == np.arange(LANE)).astype(np.float32)
    return {
        "mean_w": np.full((P, P), 1.0 / P, np.float32),
        "ones": np.ones((P, P), np.float32),
        "eps": np.full((P, 1), EPS, np.float32),
        "ident": np.eye(P, dtype=np.float32),
        "upto": (i[:, None] <= i[None, :]).astype(np.float32),
        "head_sum": heads,
        "head_pick": np.tile(heads.transpose(2, 1, 0), (P // LANE, 1, 1)),
        "ident16": np.eye(P).astype(HOST16),
        "window_mask": window_mask(),
        "rotary": rotary_tables(),
        "causal_mask": np.stack([np.where(i[None] > i[:, None], NEG, 0.0), np.where(i[:, None] > i[None], NEG, 0.0)],
                                axis=1).astype(HOST16),
        "zero_one_rows": (np.arange(ROWS, FULL + M_PARTS)[:, None] >= FULL).repeat(SEQ, axis=1).astype(HOST16),
        "iota8": np.tile(np.arange(E, dtype=np.float32)[None], (P, 1)),
        "pick": np.ascontiguousarray(np.broadcast_to(
            (i[:PARTS * PART, None] % PART == np.arange(E)[None, :])[:, :, None],
            (PARTS * PART, E, P))).astype(HOST16),
        "after": (i[:, None] > i[None, :]).astype(np.float32),
    }


def rows(a, n=P):
    return np.ascontiguousarray(np.swapaxes(a.reshape(-1, n, *a.shape[1:]), 0, 1))


def across(ws):
    e, r, n = ws.shape
    return ws.reshape(e, r // P, P, n).transpose(0, 2, 1, 3).reshape(e, P, -1)


def by_column(b):
    return b.reshape(b.shape[0], -1, P).transpose(0, 2, 1)


def out_bias(b):
    a = np.zeros((PARTS, PART, P), np.float32)
    a[:, :E] = b
    return a.reshape(PARTS * PART, P)


def laid_out(v):
    v = {name: np.asarray(a) for name, a in v.items()}
    a = constants()
    a["xT"] = np.ascontiguousarray(v["L0_attn_u"].reshape(T, P).T)
    a["cT"] = np.ascontiguousarray(np.concatenate([v[f"L{i}_c"] for i in range(4)]).T)
    a["wmod"] = np.ascontiguousarray(np.stack([v[f"L{i}_wmod"] for i in range(4)], axis=1))
    a["L0_W_in"] = v["L0_attn_W_in"]
    a["L0_heads"] = np.tile(np.concatenate([v["L0_attn_dt_bias"], v["L0_attn_A_log"]])[None], (P, 1))
    a["L0_conv"] = rows(np.concatenate([v["L0_attn_conv_w"], v["L0_attn_conv_b"][:, None]], axis=1))
    a["L0_D"] = rows(np.repeat(v["L0_attn_D"], HD0))
    a["L0_norm_w"] = rows(v["L0_attn_norm_w"])
    a["L0_W_out"] = rows(v["L0_attn_W_out"])
    a["L0_router"] = v["L0_ffn_W_router"]
    a["L0_experts"] = np.concatenate([v["L0_ffn_W_gate"], v["L0_ffn_W_up"], across(v["L0_ffn_W_out"]),
                                      by_column(v["L0_ffn_b_gate"]), by_column(v["L0_ffn_b_up"])], axis=2)
    a["L0_out_bias"] = out_bias(v["L0_ffn_b_out"])
    a["L1_Wq"], a["L1_Wkv"], a["L1_Wo"] = v["L1_attn_Wq"], v["L1_attn_Wkv"], rows(v["L1_attn_Wo"])
    a["L1_wqkv"] = v["L1_ffn_wqkv"].transpose(1, 0, 2)
    crossed = lambda q: np.roll(q, HALF, axis=1)
    q, kk = v["L1_ffn_q_scale"], v["L1_ffn_k_scale"]
    a["L1_qk_scale"] = np.tile(np.stack([q, crossed(q), kk, crossed(kk)], axis=1)[None], (P, 1, 1, 1))
    a["L1_wo"] = v["L1_ffn_wo"].reshape(DEPTH, QT, P, P).transpose(2, 0, 1, 3)
    a["L1_ln"] = np.stack([v["L1_ffn_ln_g"], v["L1_ffn_ln_b"]]).transpose(2, 0, 1)
    a["L1_w1"] = v["L1_ffn_w1"].transpose(1, 0, 2)
    hid_tiles = -(-HID // P)
    a["L1_w2"] = np.pad(v["L1_ffn_w2"], ((0, 0), (0, hid_tiles * P - HID), (0, 0))
                        ).reshape(DEPTH, hid_tiles, P, P).transpose(2, 0, 1, 3)
    a["L1_b1"] = np.pad(v["L1_ffn_b1"].reshape(DEPTH, 2, HID), ((0, 0), (0, 0), (0, hid_tiles * P - HID))
                        ).reshape(DEPTH, 2, hid_tiles, P).transpose(3, 0, 1, 2)
    a["L1_b2"] = v["L1_ffn_b2"].T
    by_quad = lambda w: w.reshape(P, -1, QUAD, HD3).swapaxes(2, 3).reshape(P, P)
    a["L2_W"] = np.stack([by_quad(v["L2_attn_W_Q"].T), by_quad(v["L2_attn_W_K"].T), v["L2_attn_W_V"].T, v["L2_attn_W_O"].T], axis=1)
    a["L2_experts"] = np.concatenate([v["L2_ffn_Wg"], v["L2_ffn_Wu"], across(v["L2_ffn_Wd"])], axis=2)
    a["L3_Wqkv"], a["L3_Wln"] = v["L3_attn_Wqkv"], v["L3_attn_Wln"]
    a["L3_bqkv"] = np.tile(v["L3_attn_bqkv"][None], (P, 1))
    a["L3_bv"], a["L3_bln"] = v["L3_attn_bqkv"][2 * P:, None], v["L3_attn_bln"][:, None]
    a["L3_router"] = np.ascontiguousarray(v["L3_ffn_router_w"].T)
    a["L3_experts"] = np.concatenate([v["L3_ffn_w1"].transpose(0, 2, 1), across(v["L3_ffn_w2"].transpose(0, 2, 1)),
                                      by_column(v["L3_ffn_b1"])], axis=2)
    a["L3_out_bias"] = out_bias(v["L3_ffn_b2"])
    return {name: np.ascontiguousarray(x) for name, x in a.items()}


def kernel(**inputs):
    import concourse.bacc as bacc
    from concourse.bass_utils import run_bass_kernel_spmd

    nc = bacc.Bacc("TRN2", target_bir_lowering=False, num_devices=1)
    arrays = laid_out(inputs)
    dram = {name: nc.dram_tensor("in_" + name, a.shape, mybir.dt.from_np(a.dtype), kind="ExternalInput").ap()
            for name, a in arrays.items()}
    out = nc.dram_tensor("out_xT", [P, T], F32, kind="ExternalOutput").ap()
    transformer(nc, dram, out)
    r = run_bass_kernel_spmd(nc, [{"in_" + name: a for name, a in arrays.items()}], core_ids=[0])
    return np.ascontiguousarray(np.asarray(r.results[0]["out_xT"]).T).reshape(NB, SEQ, P)
```

```python
from contextlib import ExitStack

import numpy as np

import concourse.bass as bass
from concourse import mybir

ALU = mybir.AluOpType
ACT = mybir.ActivationFunctionType
F32 = mybir.dt.float32
BF16 = mybir.dt.bfloat16
F16 = mybir.dt.float16
U32 = mybir.dt.uint32
HOST16 = mybir.dt.np(BF16)
AX = mybir.AxisListType.X

P = 128
NB = 2
SEQ = 1024
T = NB * SEQ
CH = 512
NCH = T // CH
NT = T // P
EPS = 1e-5
NEG = -1e30

SHIFT_A, SCALE_A, GATE_A, SHIFT_B, SCALE_B, GATE_B = range(6)



class Kit:
    pass


def chunk(c):
    return slice(c * CH, (c + 1) * CH)


def tile(t):
    return slice(t * P, (t + 1) * P)


def batch_of(c):
    return c * CH // SEQ


def modulation_stage(nc, k):
    with ExitStack() as ctx:
        c_sb = ctx.enter_context(nc.sbuf_tensor("c_sb", [P, 4 * NB], F32))
        w_sb = ctx.enter_context(nc.sbuf_tensor("wmod_sb", [P, 4, 6 * P], F32))
        sign = ctx.enter_context(nc.sbuf_tensor("gate_sign", [P, 4, 6, NB], F32))
        size = ctx.enter_context(nc.sbuf_tensor("gate_size", [P, 4, 6, NB], F32))
        ps = ctx.enter_context(nc.psum_tensor("mod_ps", [P, 4, 6, NB], F32))
        c_loaded = nc.alloc_semaphore("c_loaded")
        wmod_loaded = nc.alloc_semaphore("wmod_loaded")
        silu_ready = nc.alloc_semaphore("silu_c_ready")
        mod_ps_ready = nc.alloc_semaphore("mod_ps_ready")
        mod_steps = nc.alloc_semaphore("mod_steps")
        block = ctx.enter_context(nc.Block())

        @block.sync
        def _(sp):
            sp.dma_start(c_sb[:], k.dram["cT"]).then_inc(c_loaded, 16)
            sp.dma_start(w_sb[:], k.dram["wmod"]).then_inc(wmod_loaded, 16)
            sp.dma_start(k.x[:], k.dram["xT"]).then_inc(k.first_loaded, 16)
            for name in FIRST:
                sp.dma_start(k.w[name][:], k.dram[name]).then_inc(k.first_loaded, 16)
            sp.wait_ge(k.first_loaded, 16 * (1 + len(FIRST)))

        @block.scalar
        def _(act):
            act.wait_ge(c_loaded, 16)
            nc.scalar.activation(c_sb[:], c_sb[:], ACT.Silu).then_inc(silu_ready, 1)

        @block.tensor
        def _(pe):
            pe.wait_ge(wmod_loaded, 16)
            pe.wait_ge(silu_ready, 1)
            for layer in range(4):
                for j in range(6):
                    last = nc.tensor.matmul(ps[:, layer, j, :], w_sb[:, layer, tile(j)],
                                            c_sb[:, NB * layer:NB * layer + NB], start=True, stop=True)
            last.then_inc(mod_ps_ready, 1)

        @block.vector
        def _(dve):
            dve.wait_ge(mod_ps_ready, 1)
            nc.vector.tensor_copy(k.mod[:], ps[:]).then_inc(mod_steps, 1)
            dve.wait_ge(mod_steps, 1)
            nc.vector.tensor_scalar(sign[:], k.mod[:], 0.0, 2.0, ALU.is_ge, ALU.mult).then_inc(mod_steps, 1)
            nc.vector.scalar_tensor_tensor(out=size[:], in0=k.mod[:], scalar=-1.0, in1=k.mod[:], op0=ALU.mult,
                                           op1=ALU.max).then_inc(mod_steps, 1)
            dve.wait_ge(mod_steps, 3)
            nc.vector.tensor_scalar(size[:], size[:], 0.25, None, ALU.max).then_inc(mod_steps, 1)
            for j in (SCALE_A, SCALE_B):
                nc.vector.tensor_scalar(k.mod[:, :, j], k.mod[:, :, j], 1.0, None, ALU.add).then_inc(mod_steps, 1)
            dve.wait_ge(mod_steps, 6)
            for j in (GATE_A, GATE_B):
                nc.vector.scalar_tensor_tensor(out=k.mod[:, :, j], in0=sign[:, :, j], scalar=-1.0,
                                               in1=size[:, :, j], op0=ALU.add, op1=ALU.mult).then_inc(mod_steps, 1)
            dve.wait_ge(mod_steps, 8)


def adaln_stage(nc, k, layer, scale_at, shift_at, weights):
    layernorm_stage(nc, k, f"{layer}{scale_at}", k.x, k.h,
                    lambda b: (k.mod[:, layer, scale_at, b:b + 1], k.mod[:, layer, shift_at, b:b + 1]), weights)


def layernorm_stage(nc, k, name, src, dst, affine, weights=()):
    tag = f"_ln{name}"
    TPC = CH // P
    with ExitStack() as ctx:
        xc = ctx.enter_context(nc.sbuf_tensor("xc" + tag, [P, T], F32))
        sq = ctx.enter_context(nc.sbuf_tensor("sq" + tag, [P, NCH, CH], F32))
        std = ctx.enter_context(nc.sbuf_tensor("std" + tag, [P, NCH, TPC], F32))
        rstd = ctx.enter_context(nc.sbuf_tensor("rstd" + tag, [P, NCH, TPC], F32))
        diag = ctx.enter_context(nc.sbuf_tensor("diag" + tag, [P, 2, TPC, P], F32))
        mean_ps = ctx.enter_context(nc.psum_tensor("mean_ps" + tag, [P, NCH, CH], F32))
        var_ps = ctx.enter_context(nc.psum_tensor("var_ps" + tag, [P, 2, CH], F32))
        rstd_ps = ctx.enter_context(nc.psum_tensor("rstd_ps" + tag, [P, 2, CH], F32))
        sem = lambda name: nc.alloc_semaphore(name + tag)
        mean_ready, centered, squared, var_ready = sem("mean"), sem("centered"), sem("squared"), sem("var")
        std_ready, rstd_ready, diag_ready, spread, scaled, h_ready, loaded = (
            sem("std"), sem("rstd"), sem("diag"), sem("spread"), sem("scaled"), sem("h"), sem("loaded"))
        block = ctx.enter_context(nc.Block())

        @block.sync
        def _(sp):
            for w in weights:
                sp.dma_start(k.w[w][:], k.dram[w]).then_inc(loaded, 16)
            if weights:
                sp.wait_ge(loaded, 16 * len(weights))

        @block.tensor
        def _(pe):
            def mean(c):
                nc.tensor.matmul(mean_ps[:, c], k.w["mean_w"][:], src[:, chunk(c)],
                                 start=True, stop=True).then_inc(mean_ready, 1)

            def variance(c):
                pe.wait_ge(squared, c + 1)
                if c >= 2:
                    pe.wait_ge(std_ready, c - 1)
                for j in range(TPC):
                    last = nc.tensor.matmul(var_ps[:, c % 2, j:j + 1], sq[:, c, tile(j)], k.w["mean_w"][:, 0:1],
                                            start=True, stop=True)
                last.then_inc(var_ready, 1)

            def spread_rstd(c):
                pe.wait_ge(diag_ready, c + 1)
                if c >= 2:
                    pe.wait_ge(scaled, c - 1)
                nc.tensor.matmul(rstd_ps[:, c % 2], k.w["ones"][:], diag[:, c % 2].rearrange("p j t -> p (j t)"),
                                 start=True, stop=True).then_inc(spread, 1)

            for c in range(NCH):
                mean(c)
            for c in range(NCH + 1):
                if c < NCH:
                    variance(c)
                if c >= 1:
                    spread_rstd(c - 1)

        @block.scalar
        def _(act):
            for c in range(NCH + 2):
                if c < NCH:
                    act.wait_ge(centered, c + 1)
                    nc.scalar.activation(sq[:, c], xc[:, chunk(c)], ACT.Square).then_inc(squared, 1)
                if 1 <= c <= NCH:
                    act.wait_ge(var_ready, c)
                    nc.scalar.activation(std[:, c - 1], var_ps[:, (c - 1) % 2, 0:TPC], ACT.Sqrt,
                                         bias=k.w["eps"][:, 0:1]).then_inc(std_ready, 1)
                if c >= 2:
                    e = c - 2
                    act.wait_ge(scaled, e + 1)
                    nc.scalar.activation(dst[:, chunk(e)], xc[:, chunk(e)], ACT.Identity,
                                         bias=affine(batch_of(e))[1]).then_inc(h_ready, 1)

        @block.vector
        def _(dve):
            for c in range(NCH + 2):
                if c < NCH:
                    dve.wait_ge(mean_ready, c + 1)
                    nc.vector.tensor_tensor(xc[:, chunk(c)], src[:, chunk(c)], mean_ps[:, c],
                                            ALU.subtract).then_inc(centered, 1)
                if 1 <= c <= NCH:
                    e = c - 1
                    dve.wait_ge(std_ready, e + 1)
                    nc.vector.reciprocal(rstd[:, e], std[:, e]).then_inc(rstd_ready, 1)
                    dve.wait_ge(rstd_ready, e + 1)
                    if e >= 2:
                        dve.wait_ge(spread, e - 1)
                    nc.vector.tensor_tensor(diag[:, e % 2], k.w["ident"][:].unsqueeze(1).to_broadcast([P, TPC, P]),
                                            rstd[:, e].unsqueeze(2).to_broadcast([P, TPC, P]),
                                            ALU.mult).then_inc(diag_ready, 1)
                if c >= 2:
                    e = c - 2
                    dve.wait_ge(spread, e + 1)
                    dve.wait_ge(squared, e + 1)
                    nc.vector.scalar_tensor_tensor(out=xc[:, chunk(e)], in0=xc[:, chunk(e)],
                                                   scalar=affine(batch_of(e))[0], in1=rstd_ps[:, e % 2],
                                                   op0=ALU.mult, op1=ALU.mult).then_inc(scaled, 1)


def half_layer(layer, half, weights, body):
    def stages(nc, k):
        with nc.cleanup_on_exit(), ExitStack() as ctx:
            for name in weights:
                d = k.dram[name]
                k.w[name] = ctx.enter_context(nc.sbuf_tensor(f"{name}_{layer}{half}", list(d.shape), d.dtype))
            at = (SCALE_A, SHIFT_A) if half == 0 else (SCALE_B, SHIFT_B)
            adaln_stage(nc, k, layer, *at, weights)
            body(nc, k)
    return stages


D_CONV = 4
HEADS0 = 4
HD0 = 64
NG = SEQ // P


def mamba_project_stage(nc, k, s):
    with ExitStack() as ctx:
        raw = ctx.enter_context(nc.sbuf_tensor("raw_xbc", [P, 2, NB, SEQ + D_CONV - 1], F32))
        conv = ctx.enter_context(nc.sbuf_tensor("conv_acc", [P, 2, NB, SEQ], F32))
        ps = ctx.enter_context(nc.psum_tensor("proj_ps", [P, 4, CH], F32))
        dt_ps = ctx.enter_context(nc.psum_tensor("dt_ps", [P, NT, HEADS0], F32))
        tmp = ctx.enter_context(nc.sbuf_tensor("dt_tmp", [P, 8, NT * HEADS0], F32))
        sem = lambda name: nc.alloc_semaphore(name + "_mp")
        proj_ready, evacuated, dt_ready, pads_ready = sem("proj"), sem("evacuated"), sem("dt_ps"), sem("pads")
        conv_step, conv_ready, silu_ready, dt_step, dt_act = (
            sem("conv_step"), sem("conv"), sem("silu"), sem("dt_step"), sem("dt_act"))
        win, cw = k.w["L0_W_in"], k.w["L0_conv"]
        block = ctx.enter_context(nc.Block())
        bank = lambda m, c: (m * NCH + c) % 4

        @block.tensor
        def _(pe):
            for i, m in enumerate((2, 3, 4, 5, 0, 1)):
                if i == 2:
                    for t in range(NT):
                        last = nc.tensor.matmul(dt_ps[:, t], k.h[:, tile(t)], win[:, 6 * P:6 * P + HEADS0],
                                                start=True, stop=True)
                    last.then_inc(dt_ready, 1)
                for c in range(NCH):
                    n = i * NCH + c
                    if n >= 4:
                        pe.wait_ge(evacuated, n - 3)
                    nc.tensor.matmul(ps[:, n % 4], win[:, tile(m)], k.h[:, chunk(c)],
                                     start=True, stop=True).then_inc(proj_ready, 1)

        @block.scalar
        def _(act):
            act.wait_ge(pads_ready, 1)
            for i in range(6):
                if 2 <= i < 4:
                    act.wait_ge(conv_ready, i - 1)
                for c in range(NCH):
                    n = i * NCH + c
                    act.wait_ge(proj_ready, n + 1)
                    if i < 4:
                        b, at = batch_of(c), c * CH % SEQ
                        out, func = raw[:, i % 2, b, D_CONV - 1 + at:D_CONV - 1 + at + CH], ACT.Copy
                    else:
                        out, func = s.zg[:, i - 4, chunk(c)], ACT.Silu
                    nc.scalar.activation(out, ps[:, n % 4], func).then_inc(evacuated, 1)
            for i in range(4):
                act.wait_ge(conv_ready, i + 1)
                nc.scalar.activation(s.xbc[:, i].rearrange("p (b n) -> p b n", b=NB), s.conv_out[:, i],
                                     ACT.Silu).then_inc(silu_ready, 1)
            act.wait_ge(dt_step, 3)
            nc.scalar.activation(tmp[:, 2], tmp[:, 1], ACT.Exp, scale=-1.0).then_inc(dt_act, 1)
            nc.scalar.activation(s.decay_rate[:], k.w["L0_heads"][:, HEADS0:2 * HEADS0], ACT.Exp).then_inc(dt_act, 1)
            act.wait_ge(dt_act, 1)
            nc.scalar.activation(tmp[:, 3], tmp[:, 2], ACT.Ln, bias=1.0).then_inc(dt_act, 1)

        @block.vector
        def _(dve):
            nc.vector.memset(raw[:, :, :, 0:D_CONV - 1], 0.0).then_inc(pads_ready, 1)
            for i in range(4):
                if i == 2:
                    dve.wait_ge(dt_ready, 1)
                    flat = dt_ps[:].rearrange("p t h -> p (t h)")
                    bias = k.w["L0_heads"][:, 0:HEADS0].unsqueeze(1).to_broadcast([P, NT, HEADS0])
                    nc.vector.tensor_tensor(tmp[:, 0].rearrange("p (t h) -> p t h", h=HEADS0), dt_ps[:], bias,
                                            ALU.add).then_inc(dt_step, 1)
                    dve.wait_ge(dt_step, 1)
                    nc.vector.scalar_tensor_tensor(out=tmp[:, 1], in0=tmp[:, 0], scalar=-1.0, in1=tmp[:, 0], op0=ALU.mult,
                                                   op1=ALU.max).then_inc(dt_step, 1)
                    dve.wait_ge(dt_step, 2)
                    nc.vector.tensor_scalar(tmp[:, 0], tmp[:, 0], 0.0, None, ALU.max).then_inc(dt_step, 1)
                if i >= 1:
                    dve.wait_ge(conv_ready, i)
                dve.wait_ge(evacuated, NCH * (i + 1))
                tap = lambda j: raw[:, i % 2, :, j:j + SEQ]
                nc.vector.tensor_scalar(conv[:, 0], tap(0), cw[:, i, 0:1], cw[:, i, D_CONV:D_CONV + 1],
                                        ALU.mult, ALU.add).then_inc(conv_step, 1)
                for j in range(1, D_CONV):
                    dve.wait_ge(conv_step, (D_CONV - 1) * i + j)
                    out = conv[:, j % 2] if j < D_CONV - 1 else s.conv_out[:, i]
                    nc.vector.scalar_tensor_tensor(out=out, in0=tap(j), scalar=cw[:, i, j:j + 1],
                                                   in1=conv[:, (j - 1) % 2], op0=ALU.mult,
                                                   op1=ALU.add).then_inc(
                                                       conv_ready if j == D_CONV - 1 else conv_step, 1)
            e, poly, small = tmp[:, 2], tmp[:, 4], tmp[:, 5]
            dve.wait_ge(dt_act, 1)
            n = 3
            nc.vector.tensor_scalar(poly, e, 1.0 / 7, -1.0 / 6, ALU.mult, ALU.add).then_inc(dt_step, 1)
            for coefficient in (1.0 / 5, -1.0 / 4, 1.0 / 3, -1.0 / 2, 1.0):
                n += 1
                dve.wait_ge(dt_step, n)
                nc.vector.tensor_tensor(poly, poly, e, ALU.mult).then_inc(dt_step, 1)
                n += 1
                dve.wait_ge(dt_step, n)
                nc.vector.tensor_scalar(poly, poly, coefficient, None, ALU.add).then_inc(dt_step, 1)
            n += 1
            dve.wait_ge(dt_step, n)
            nc.vector.tensor_tensor(poly, poly, e, ALU.mult).then_inc(dt_step, 1)
            nc.vector.tensor_scalar(small, e, 1.0 / 16, None, ALU.is_lt).then_inc(dt_step, 1)
            dve.wait_ge(dt_act, 3)
            n += 2
            dve.wait_ge(dt_step, n)
            nc.vector.tensor_tensor(poly, poly, tmp[:, 3], ALU.subtract).then_inc(dt_step, 1)
            dve.wait_ge(dt_step, n + 1)
            nc.vector.tensor_tensor(poly, poly, small, ALU.mult).then_inc(dt_step, 1)
            dve.wait_ge(dt_step, n + 2)
            nc.vector.tensor_tensor(poly, poly, tmp[:, 3], ALU.add).then_inc(dt_step, 1)
            dve.wait_ge(dt_step, n + 3)
            nc.vector.tensor_tensor(s.dt[:].rearrange("p t h -> p (t h)"), tmp[:, 0], poly,
                                    ALU.add).then_inc(dt_step, 1)
            dve.wait_ge(dt_step, n + 4)
            rate = s.decay_rate[:].unsqueeze(1).to_broadcast([P, NT, HEADS0])
            nc.vector.scalar_tensor_tensor(out=s.a[:], in0=s.dt[:], scalar=-1.0, in1=rate,
                                           op0=ALU.mult, op1=ALU.mult).then_inc(dt_step, 1)


def mamba_scan_stage(nc, k, s):
    HP = HEADS0 * HD0
    with ExitStack() as ctx:
        sb = lambda name, shape: ctx.enter_context(nc.sbuf_tensor(name, shape, F32))
        x_tok, b_tok = sb("x_dt_tok", [P, 2, HEADS0, HD0]), sb("b_tok", [P, 2, P])
        al, e1, e2 = sb("a_upto_l", [P, 2, HEADS0, P]), sb("e_between", [P, 2, HEADS0, P]), sb("e_upto", [P, 2, HEADS0, P])
        g, m = sb("cb_masked", [P, 2, P]), sb("m_masked", [P, 2, HEADS0, P])
        ce, xd = sb("c_decayed", [P, 2, HEADS0, P]), sb("x_decayed", [P, 2, HEADS0, HD0])
        state, kept = sb("state", [P, 2, HEADS0, HD0]), sb("state_kept", [P, HEADS0, HD0])
        t_ps = ctx.enter_context(nc.psum_tensor("turn_ps", [P, 2, 4, P], F32))
        seg_ps = ctx.enter_context(nc.psum_tensor("seg_ps", [P, 2, CH], F32))
        cum_ps = ctx.enter_context(nc.psum_tensor("cum_ps", [P, CH], F32))
        y_ps = ctx.enter_context(nc.psum_tensor("y_ps", [P, 2, CH], F32))
        ds_ps = ctx.enter_context(nc.psum_tensor("ds_ps", [P, HEADS0, HD0], F32))
        sem = lambda name: nc.alloc_semaphore(name + "_ms")
        turned, x_tok_ready, b_tok_ready, al_ready = sem("turned"), sem("x_tok"), sem("b_tok"), sem("al")
        seg_ready, cum_ready, e1_ready, e2_ready = sem("seg"), sem("cum"), sem("e1"), sem("e2")
        g_ready, m_ready, ce_ready, xd_ready = sem("g"), sem("m"), sem("ce"), sem("xd")
        y_ready, ds_ready, state_ready, kept_ready, y_taken = sem("y"), sem("ds"), sem("state"), sem("kept"), sem("y_taken")
        B, C = s.xbc[:, 2], s.xbc[:, 3]
        upto, after = k.w["upto"], k.w["after"]
        N = NT
        block = ctx.enter_context(nc.Block())

        @block.gpsimd
        def _(pool):
            def decays_in(n):
                if n >= 2:
                    pool.wait_ge(cum_ready, n - 1)
                nc.gpsimd.tensor_tensor(
                    al[:, n % 2], upto[:].unsqueeze(1).to_broadcast([P, HEADS0, P]),
                    s.a[:, n].unsqueeze(2).to_broadcast([P, HEADS0, P]), ALU.mult).then_inc(al_ready, 1)

            decays_in(0)
            for n in range(N):
                if n + 1 < N:
                    decays_in(n + 1)
                pool.wait_ge(e1_ready, n + 1)
                pool.wait_ge(x_tok_ready, n + 1)
                if n >= 2:
                    pool.wait_ge(ds_ready, n - 1)
                nc.gpsimd.tensor_tensor(xd[:, n % 2], x_tok[:, n % 2],
                                        e1[:, n % 2, :, P - 1:P].to_broadcast([P, HEADS0, HD0]),
                                        ALU.mult).then_inc(xd_ready, 1)
                if n % NG:
                    pool.wait_ge(e2_ready, n + 1)
                    if n >= 2:
                        pool.wait_ge(y_ready, n - 1)
                    nc.gpsimd.tensor_tensor(ce[:, n % 2], e2[:, n % 2],
                                            C[:, tile(n)].unsqueeze(1).to_broadcast([P, HEADS0, P]),
                                            ALU.mult).then_inc(ce_ready, 1)

        @block.tensor
        def _(pe):
            def turn(n):
                if n >= 2:
                    pe.wait_ge(g_ready, n - 1)
                for j in range(3):
                    nc.tensor.transpose(t_ps[:, n % 2, j], s.xbc[:, j, tile(n)], k.w["ident"][:])
                nc.tensor.matmul(t_ps[:, n % 2, 3], B[:, tile(n)], C[:, tile(n)],
                                 start=True, stop=True).then_inc(turned, 1)

            def decays(n):
                pe.wait_ge(al_ready, n + 1)
                if n >= 2:
                    pe.wait_ge(e1_ready, n - 1)
                nc.tensor.matmul(seg_ps[:, n % 2], after[:], al[:, n % 2].rearrange("p h l -> p (h l)"),
                                 start=True, stop=True).then_inc(seg_ready, 1)
                if n >= 1:
                    pe.wait_ge(e2_ready, n)
                nc.tensor.matmul(cum_ps[:], k.w["ones"][:], al[:, n % 2].rearrange("p h l -> p (h l)"),
                                 start=True, stop=True).then_inc(cum_ready, 1)

            turn(0)
            decays(0)
            for n in range(N):
                if n + 1 < N:
                    turn(n + 1)
                    decays(n + 1)
                pe.wait_ge(xd_ready, n + 1)
                pe.wait_ge(b_tok_ready, n + 1)
                if n >= 1:
                    pe.wait_ge(state_ready, n)
                nc.tensor.matmul(ds_ps[:].rearrange("p h d -> p (h d)"), b_tok[:, n % 2],
                                 xd[:, n % 2].rearrange("p h d -> p (h d)"), start=True, stop=True).then_inc(ds_ready, 1)
                pe.wait_ge(m_ready, n + 1)
                first = n % NG == 0
                if not first:
                    pe.wait_ge(ce_ready, n - n // NG)
                if n >= 2:
                    pe.wait_ge(y_taken, n - 1)
                for h in range(HEADS0):
                    out = y_ps[HD0 * (h % 2):HD0 * (h % 2) + HD0, n % 2, (h // 2) * P:(h // 2) * P + P]
                    last = nc.tensor.matmul(out, x_tok[:, n % 2, h], m[:, n % 2, h], start=True, stop=first)
                    if not first:
                        last = nc.tensor.matmul(out, state[:, (n - 1) % 2, h], ce[:, n % 2, h],
                                                start=False, stop=True)
                last.then_inc(y_ready, 1)

        @block.scalar
        def _(act):
            for n in range(N):
                act.wait_ge(seg_ready, n + 1)
                if n >= 2:
                    act.wait_ge(m_ready, n - 1)
                    act.wait_ge(xd_ready, n - 1)
                nc.scalar.activation(e1[:, n % 2].rearrange("p h l -> p (h l)"), seg_ps[:, n % 2],
                                     ACT.Exp).then_inc(e1_ready, 1)
                act.wait_ge(cum_ready, n + 1)
                if n >= 2:
                    act.wait_ge(kept_ready, n - 1)
                    if n >= 3:
                        act.wait_ge(ce_ready, (n - 1) - (n - 2) // NG - 1)
                nc.scalar.activation(e2[:, n % 2].rearrange("p h l -> p (h l)"), cum_ps[:],
                                     ACT.Exp).then_inc(e2_ready, 1)

        @block.vector
        def _(dve):
            for n in range(N):
                dve.wait_ge(turned, n + 1)
                if n >= 2:
                    dve.wait_ge(y_ready, n - 1)
                    dve.wait_ge(xd_ready, n - 1)
                nc.vector.tensor_tensor(x_tok[:, n % 2], t_ps[:, n % 2, 0:2].rearrange("p j (h d) -> p (j h) d", d=HD0),
                                        s.dt[:, n].unsqueeze(2).to_broadcast([P, HEADS0, HD0]),
                                        ALU.mult).then_inc(x_tok_ready, 1)
                if n >= 2:
                    dve.wait_ge(ds_ready, n - 1)
                nc.vector.tensor_copy(b_tok[:, n % 2], t_ps[:, n % 2, 2]).then_inc(b_tok_ready, 1)
                if n >= 2:
                    dve.wait_ge(m_ready, n - 1)
                nc.vector.tensor_tensor(g[:, n % 2], t_ps[:, n % 2, 3], upto[:], ALU.mult).then_inc(g_ready, 1)
                dve.wait_ge(g_ready, n + 1)
                dve.wait_ge(e1_ready, n + 1)
                nc.vector.tensor_tensor(m[:, n % 2], e1[:, n % 2],
                                        g[:, n % 2].unsqueeze(1).to_broadcast([P, HEADS0, P]),
                                        ALU.mult).then_inc(m_ready, 1)
                dve.wait_ge(e2_ready, n + 1)
                if n % NG == 0:
                    if n >= 1:
                        dve.wait_ge(state_ready, n)
                    nc.vector.memset(kept[:], 0.0).then_inc(kept_ready, 1)
                else:
                    dve.wait_ge(state_ready, n)
                    nc.vector.tensor_tensor(kept[:], state[:, (n - 1) % 2],
                                            e2[:, n % 2, :, P - 1:P].to_broadcast([P, HEADS0, HD0]),
                                            ALU.mult).then_inc(kept_ready, 1)
                dve.wait_ge(kept_ready, n + 1)
                dve.wait_ge(ds_ready, n + 1)
                if n >= 1:
                    dve.wait_ge(y_ready, n)
                nc.vector.tensor_tensor(state[:, n % 2], kept[:], ds_ps[:], ALU.add).then_inc(state_ready, 1)
                dve.wait_ge(y_ready, n + 1)
                for j in range(2):
                    last = nc.vector.scalar_tensor_tensor(
                        out=s.y[:, j, tile(n)], in0=s.xbc[:, j, tile(n)], scalar=k.w["L0_D"][:, j:j + 1],
                        in1=y_ps[:, n % 2, j * P:(j + 1) * P], op0=ALU.mult, op1=ALU.add)
                last.then_inc(y_taken, 1)


def mamba_out_stage(nc, k, s):
    with ExitStack() as ctx:
        sb = lambda name, shape: ctx.enter_context(nc.sbuf_tensor(name, shape, F32))
        yz, sq = sb("y_gated", [P, 2, 2, CH]), sb("y_squared", [P, 2, 2, CH])
        rms, rinv, w, tmp = sb("rms", [P, 2, CH]), sb("rms_inv", [P, 2, CH]), sb("w_out_n", [P, 2, P]), sb("out_n", [P, 2, CH])
        o_ps = ctx.enter_context(nc.psum_tensor("o_ps", [P, 2, CH], F32))
        s_ps = ctx.enter_context(nc.psum_tensor("s_ps", [P, 2, CH], F32))
        sem = lambda name: nc.alloc_semaphore(name + "_mo")
        w_ready, gated, squared, sum_ready, out_ready = sem("w"), sem("gated"), sem("squared"), sem("sum"), sem("out")
        rms_ready, rinv_ready, scaled, added = sem("rms"), sem("rinv"), sem("scaled"), sem("added")
        block = ctx.enter_context(nc.Block())

        @block.tensor
        def _(pe):
            pe.wait_ge(w_ready, 2)
            for c in range(NCH):
                pe.wait_ge(gated, c + 1)
                if c >= 2:
                    pe.wait_ge(scaled, c - 1)
                for j in range(2):
                    last = nc.tensor.matmul(o_ps[:, c % 2], w[:, j], yz[:, c % 2, j], start=j == 0, stop=j == 1)
                last.then_inc(out_ready, 1)
                pe.wait_ge(squared, c + 1)
                if c >= 2:
                    pe.wait_ge(rms_ready, c - 1)
                for j in range(2):
                    last = nc.tensor.matmul(s_ps[:, c % 2], k.w["mean_w"][:], sq[:, c % 2, j], start=j == 0, stop=j == 1)
                last.then_inc(sum_ready, 1)

        @block.scalar
        def _(act):
            for c in range(NCH):
                act.wait_ge(gated, c + 1)
                if c >= 2:
                    act.wait_ge(sum_ready, c - 1)
                nc.scalar.activation(sq[:, c % 2], yz[:, c % 2], ACT.Square).then_inc(squared, 1)
                act.wait_ge(sum_ready, c + 1)
                if c >= 2:
                    act.wait_ge(rinv_ready, c - 1)
                nc.scalar.activation(rms[:, c % 2], s_ps[:, c % 2], ACT.Sqrt, bias=k.w["eps"][:, 0:1],
                                     scale=0.5).then_inc(rms_ready, 1)

        @block.vector
        def _(dve):
            for j in range(2):
                nc.vector.tensor_scalar(w[:, j], k.w["L0_W_out"][:, j], k.w["L0_norm_w"][:, j:j + 1], None,
                                        ALU.mult).then_inc(w_ready, 1)

            def gate(c):
                if c >= 2:
                    dve.wait_ge(out_ready, c - 1)
                    dve.wait_ge(squared, c - 1)
                nc.vector.tensor_tensor(yz[:, c % 2], s.y[:, :, chunk(c)], s.zg[:, :, chunk(c)],
                                        ALU.mult).then_inc(gated, 1)

            gate(0)
            for c in range(NCH):
                if c + 1 < NCH:
                    gate(c + 1)
                b = batch_of(c)
                dve.wait_ge(rms_ready, c + 1)
                if c >= 2:
                    dve.wait_ge(scaled, c - 1)
                nc.vector.reciprocal(rinv[:, c % 2], rms[:, c % 2]).then_inc(rinv_ready, 1)
                dve.wait_ge(rinv_ready, c + 1)
                dve.wait_ge(out_ready, c + 1)
                if c >= 2:
                    dve.wait_ge(added, c - 1)
                nc.vector.tensor_tensor(tmp[:, c % 2], o_ps[:, c % 2], rinv[:, c % 2], ALU.mult).then_inc(scaled, 1)
                dve.wait_ge(scaled, c + 1)
                nc.vector.scalar_tensor_tensor(out=k.x[:, chunk(c)], in0=tmp[:, c % 2],
                                               scalar=k.mod[:, 0, GATE_A, b:b + 1], in1=k.x[:, chunk(c)],
                                               op0=ALU.mult, op1=ALU.add).then_inc(added, 1)


def mamba_block(nc, k):
    with ExitStack() as ctx:
        sb = lambda name, shape: ctx.enter_context(nc.sbuf_tensor(name, shape, F32))
        s = Kit()
        s.zg, s.xbc, s.y = sb("z_gate", [P, 2, T]), sb("xbc", [P, 4, T]), sb("y0", [P, 2, T])
        s.dt, s.a, s.decay_rate = sb("dt", [P, NT, HEADS0]), sb("a_dt", [P, NT, HEADS0]), sb("decay_rate", [P, HEADS0])
        with nc.sbuf_tensor("conv_out", [P, 4, NB, SEQ], F32) as s.conv_out:
            mamba_project_stage(nc, k, s)
        mamba_scan_stage(nc, k, s)
        mamba_out_stage(nc, k, s)


E = 8
PARTS = 3
PART = 32
TOP_EPS = 1e-8


PASSES = ((0, 0), (0, 1), (1, 0))


def first_parts(nc, k, r):
    for c in range(NCH):
        nc.scalar.activation(r.h16[:, 0, chunk(c)], k.h[:, chunk(c)], ACT.Copy).then_inc(r.h_first, 1)


def second_parts(nc, k, r, dve):
    for c in range(NCH):
        dve.wait_ge(r.h_first, c + 1)
        nc.vector.tensor_tensor(r.h16[:, 1, chunk(c)], k.h[:, chunk(c)], r.h16[:, 0, chunk(c)],
                                ALU.subtract).then_inc(r.h_split, 1)


def split_weights(nc, r, pool, s, nth):
    pool.wait_ge(r.slot_loaded[s], nth * 16)
    w = r.slot[:, s, 0:r.up_cols]
    nc.gpsimd.tensor_tensor(r.w16[:, s, 0].rearrange("p (m c) -> p m c", c=P), w.rearrange("p (m c) -> p m c", c=P),
                            r.zero[:].unsqueeze(1).to_broadcast([P, r.up_cols // P, P]),
                            ALU.add).then_inc(r.w_first[s], 1)
    pool.wait_ge(r.w_first[s], nth)
    nc.gpsimd.tensor_tensor(r.w16[:, s, 1], w, r.w16[:, s, 0], ALU.subtract).then_inc(r.w_split[s], 1)


def split_first_weights(nc, r, pool):
    nc.gpsimd.memset(r.zero[:], 0.0).then_inc(r.zero_ready, 1)
    pool.wait_ge(r.zero_ready, 1)
    for s in range(2):
        split_weights(nc, r, pool, s, 1)


def routing_stage(nc, k, r, router, top_sum_eps):
    tag = "_rt" + router
    TE = NT * E
    steps = 2 + 2 * NT + 3 + 2 + 3 + (1 if top_sum_eps else 0) + 2 + 3 * PARTS - 1
    with ExitStack() as ctx:
        sb = lambda name, shape, dt=F32: ctx.enter_context(nc.sbuf_tensor(name + tag, shape, dt))
        lg, top, top_at, at = sb("lg", [P, NT, E]), sb("top", [P, NT, E]), sb("top_at", [P, NT, E], U32), sb("at", [P, NT, E])
        ex, total, den = sb("ex", [P, NT, E]), sb("total", [P, NT, 1]), sb("den", [P, NT, 1])
        hit, rest = sb("hit", [P, 2, NT, E]), sb("rest", [P, 2, NT, E])
        part = sb("part", [P, PARTS, NT, E], BF16)
        spread = sb("spread", [P, NT, PARTS, PART])
        parts16 = sb("parts16", [PARTS * PART, T], BF16)
        lg_ps = ctx.enter_context(nc.psum_tensor("lg_ps" + tag, [P, CH], F32))
        t_ps = ctx.enter_context(nc.psum_tensor("t_ps" + tag, [P, 2, CH], F32))
        w_ps = ctx.enter_context(nc.psum_tensor("w_ps" + tag, [P, 4, CH], F32))
        sem = lambda name: nc.alloc_semaphore(name + tag)
        logits_ready, dve_step, act_step, turned = sem("logits"), sem("dve_step"), sem("act_step"), sem("turned")
        parts_ready, parts16_ready, wide_ready, wide_read_a, wide_read_v = (
            sem("parts"), sem("parts16"), sem("wide"), sem("wide_read_a"), sem("wide_read_v"))
        block = ctx.enter_context(nc.Block())

        @block.sync
        def _(sp):
            for s in range(2):
                sp.dma_start(r.slot[:, s], r.weights[s]).then_inc(r.slot_loaded[s], 16)

        @block.tensor
        def _(pe):
            for t in range(NT):
                last = nc.tensor.matmul(lg_ps[:, t * E:(t + 1) * E], k.h[:, tile(t)], k.w[router][:],
                                        start=True, stop=True)
            last.then_inc(logits_ready, 1)
            pe.wait_ge(dve_step, steps)
            for c in range(NCH):
                if c >= 2:
                    pe.wait_ge(parts_ready, c - 1)
                for j in range(CH // P):
                    last = nc.tensor.transpose(t_ps[0:PARTS * PART, c % 2, tile(j)],
                                               spread[:, c * CH // P + j].rearrange("p i e -> p (i e)"),
                                               k.w["ident"][:])
                last.then_inc(turned, 1)
            for e in range(E):
                for c in range(NCH):
                    n = e * NCH + c
                    if e == 0:
                        pe.wait_ge(parts16_ready, c + 1)
                    if n >= 4:
                        pe.wait_ge(wide_read_v if n % 2 else wide_read_a, n // 2 - 1)
                    nc.tensor.matmul(w_ps[:, n % 4], k.w["pick"][:, e], parts16[:, chunk(c)],
                                     start=True, stop=True).then_inc(wide_ready, 1)

        @block.gpsimd
        def _(pool):
            split_first_weights(nc, r, pool)

        @block.scalar
        def _(act):
            first_parts(nc, k, r)
            act.wait_ge(dve_step, 2 + 2 * NT + 1)
            nc.scalar.activation(ex[:], ex[:], ACT.Exp).then_inc(act_step, 1)
            for c in range(NCH):
                act.wait_ge(turned, c + 1)
                nc.scalar.activation(r.parts[:, chunk(c)], t_ps[0:PARTS * PART, c % 2], ACT.Copy).then_inc(parts_ready, 1)
            for n in range(0, E * NCH, 2):
                act.wait_ge(wide_ready, n + 1)
                nc.scalar.activation(r.wide[:, n // NCH, chunk(n % NCH)], w_ps[:, n % 4],
                                     ACT.Copy).then_inc(wide_read_a, 1)

        count = [0]

        @block.vector
        def _(dve):
            def step(instruction):
                count[0] += 1
                instruction.then_inc(dve_step, 1)
                dve.wait_ge(dve_step, count[0])

            step(nc.vector.memset(spread[:], 0.0))
            second_parts(nc, k, r, dve)
            dve.wait_ge(logits_ready, 1)
            step(nc.vector.tensor_copy(lg[:].rearrange("p t e -> p (t e)"), lg_ps[:, 0:TE]))
            for t in range(NT):
                nc.vector.max(top[:, t], lg[:, t]).then_inc(dve_step, 1)
            count[0] += NT
            dve.wait_ge(dve_step, count[0])
            for t in range(NT):
                nc.vector.max_index(top_at[:, t], top[:, t], lg[:, t]).then_inc(dve_step, 1)
            count[0] += NT
            dve.wait_ge(dve_step, count[0])
            greatest = top[:, :, 0:1].to_broadcast([P, NT, E])
            step(nc.vector.tensor_tensor(ex[:], lg[:], greatest, ALU.subtract))
            dve.wait_ge(act_step, 1)
            step(nc.vector.tensor_reduce(total[:, :, 0], ex[:], AX, ALU.add))
            step(nc.vector.tensor_copy(at[:], top_at[:]))
            for i in range(2):
                step(nc.vector.tensor_tensor(hit[:, i], k.w["iota8"][:].unsqueeze(1).to_broadcast([P, NT, E]),
                                             at[:, :, i:i + 1].to_broadcast([P, NT, E]), ALU.is_equal))
            step(nc.vector.tensor_tensor(hit[:, 0], hit[:, 0], hit[:, 1], ALU.add))
            step(nc.vector.tensor_tensor(hit[:, 0], hit[:, 0], ex[:], ALU.mult))
            step(nc.vector.tensor_reduce(den[:, :, 0], hit[:, 0], AX, ALU.add))
            if top_sum_eps:
                step(nc.vector.scalar_tensor_tensor(out=den[:], in0=total[:], scalar=top_sum_eps, in1=den[:],
                                                    op0=ALU.mult, op1=ALU.add))
            step(nc.vector.reciprocal(den[:], den[:]))
            step(nc.vector.tensor_tensor(rest[:, 0], hit[:, 0], den[:].to_broadcast([P, NT, E]), ALU.mult))
            for i in range(PARTS):
                step(nc.vector.tensor_copy(part[:, i], rest[:, i % 2]))
                step(nc.vector.tensor_copy(spread[:, :, i, 0:E], part[:, i]))
                if i + 1 < PARTS:
                    step(nc.vector.tensor_tensor(rest[:, (i + 1) % 2], rest[:, i % 2], part[:, i], ALU.subtract))
            for c in range(NCH):
                dve.wait_ge(parts_ready, c + 1)
                nc.vector.tensor_copy(parts16[:, chunk(c)], r.parts[:, chunk(c)]).then_inc(parts16_ready, 1)
            for n in range(1, E * NCH, 2):
                dve.wait_ge(wide_ready, n + 1)
                nc.vector.tensor_copy(r.wide[:, n // NCH, chunk(n % NCH)], w_ps[:, n % 4]).then_inc(wide_read_v, 1)

        assert count[0] == steps


CREDIT = 2


def experts_stage(nc, k, r, layer, tiles, func, gated, routed):
    tag = f"_ex{layer}"
    M, LAG, HB = tiles, 2, 4
    wide_cols = M * P
    UNITS = NCH * M
    PAIR = 2 * UNITS
    G0, U0 = 0, wide_cols
    D0 = (2 if gated else 1) * wide_cols
    BG, BU = D0 + M * P, D0 + M * P + M
    with ExitStack() as ctx:
        sb = lambda name, shape: ctx.enter_context(nc.sbuf_tensor(name + tag, shape, F32))
        act_out, mid, hid = sb("act_out", [P, 2, CH]), sb("mid", [P, 2, CH]), sb("hid", [P, HB, CH])
        acc = ctx.enter_context(nc.psum_tensor("acc" + tag, [P, NCH, CH], F32))
        g_ps = ctx.enter_context(nc.psum_tensor("g_ps" + tag, [P, 2, CH], F32))
        u_ps = ctx.enter_context(nc.psum_tensor("u_ps" + tag, [P, 2, CH], F32))
        sem = lambda name: nc.alloc_semaphore(name + tag)
        g_ready, u_ready, act_ready, mid_ready, hid_ready, down_done, added = (
            sem("g"), sem("u"), sem("act"), sem("mid"), sem("hid"), sem("down"), sem("added"))
        block = ctx.enter_context(nc.Block())
        units = [(s, c, m) for s in range(2) for c in range(NCH) for m in range(M)]

        @block.sync
        def _(sp):
            with sp.Fori(0, E // 2 - 1, 1) as it:
                for s in range(2):
                    sp.wait_ge(down_done, it * PAIR + (s + 1) * UNITS + CREDIT)
                    sp.dma_start(r.slot[:, s], r.weights[bass.ds(it * 2 + (2 + s), 1)].rearrange("o p n -> p (o n)")
                                 ).then_inc(r.slot_loaded[s], 16)

        @block.tensor
        def _(pe):
            def product(out, s, at, c):
                for n, (i, j) in enumerate(PASSES):
                    last = nc.tensor.matmul(out, r.w16[:, s, i, at:at + P], r.h16[:, j, chunk(c)],
                                            start=n == 0, stop=n == len(PASSES) - 1)
                return last

            def up(it, u):
                s, c, m = units[u]
                if u % UNITS == 0:
                    pe.wait_ge(r.w_split[s], it + 1)
                if m == 0:
                    pe.wait_ge(r.h_split, c + 1)
                pe.wait_ge(act_ready, it * PAIR + (u + 1))
                product(g_ps[:, u % 2], s, G0 + m * P, c).then_inc(g_ready, 1)
                if gated:
                    pe.wait_ge(mid_ready if routed else hid_ready, it * PAIR + (u + 1))
                    product(u_ps[:, u % 2], s, U0 + m * P, c).then_inc(u_ready, 1)

            def down(it, u):
                s, c, m = units[u]
                pe.wait_ge(hid_ready, it * PAIR + (u + 1 + CREDIT))
                nc.tensor.matmul(acc[:, c], r.slot[:, s, D0 + m * P:D0 + (m + 1) * P], hid[:, u % HB],
                                 start=False, stop=True, skip_group_check=True).then_inc(down_done, 1)

            pe.sem_inc(down_done, CREDIT)
            if not routed:
                pe.wait_ge(r.zero_ready, 1)
            for c in range(NCH):
                if routed:
                    nc.tensor.matmul(acc[:, c], k.w[r.out_bias][:], r.parts[:, chunk(c)], start=True, stop=True)
                else:
                    nc.tensor.matmul(acc[:, c], r.zero[:], k.h[:, chunk(c)], start=True, stop=True)
            with pe.Fori(0, E // 2, 1) as it:
                for u in range(PAIR + LAG):
                    if u < PAIR:
                        up(it, u)
                    if u >= LAG:
                        down(it, u - LAG)

        @block.scalar
        def _(act):
            act.sem_inc(act_ready, CREDIT)
            if not routed:
                first_parts(nc, k, r)
            with act.Fori(0, E // 2, 1) as it:
                for u, (s, c, m) in enumerate(units):
                    act.wait_ge(g_ready, it * PAIR + (u + 1))
                    act.wait_ge(mid_ready if gated and routed else hid_ready, it * PAIR + (u + 1))
                    bias = r.slot[:, s, BG + m:BG + m + 1] if routed else 0.0
                    nc.scalar.activation(act_out[:, u % 2], g_ps[:, u % 2], func, bias=bias).then_inc(act_ready, 1)

        @block.gpsimd
        def _(pool):
            if not routed:
                split_first_weights(nc, r, pool)
            with pool.Fori(0, E // 2 - 1, 1) as it:
                for s in range(2):
                    split_weights(nc, r, pool, s, it + 2)

        @block.vector
        def _(dve):
            if not routed:
                second_parts(nc, k, r, dve)
            dve.sem_inc(hid_ready, CREDIT)
            dve.sem_inc(mid_ready, CREDIT)
            with dve.Fori(0, E // 2, 1) as it:
                for u, (s, c, m) in enumerate(units):
                    if gated:
                        dve.wait_ge(u_ready, it * PAIR + (u + 1))
                    if gated and routed:
                        dve.wait_ge(act_ready, it * PAIR + (u + 1 + CREDIT))
                        dve.wait_ge(hid_ready, it * PAIR + (u + 1))
                        nc.vector.scalar_tensor_tensor(
                            out=mid[:, u % 2], in0=u_ps[:, u % 2], scalar=r.slot[:, s, BU + m:BU + m + 1],
                            in1=act_out[:, u % 2], op0=ALU.add, op1=ALU.mult).then_inc(mid_ready, 1)
                        dve.wait_ge(mid_ready, it * PAIR + (u + 1 + CREDIT))
                    else:
                        dve.wait_ge(act_ready, it * PAIR + (u + 1 + CREDIT))
                    if u >= HB:
                        dve.wait_ge(down_done, it * PAIR + (u - HB + 1 + CREDIT))
                    else:
                        dve.wait_ge(down_done, it * PAIR + CREDIT)
                    if routed:
                        nc.vector.tensor_tensor(
                            hid[:, u % HB], (mid if gated else act_out)[:, u % 2],
                            r.wide[:, bass.ds(it * 2 + s, 1), chunk(c)].rearrange("p o n -> p (o n)"),
                            ALU.mult).then_inc(hid_ready, 1)
                    else:
                        nc.vector.tensor_tensor(hid[:, u % HB], u_ps[:, u % 2], act_out[:, u % 2],
                                                ALU.mult).then_inc(hid_ready, 1)
            dve.wait_ge(down_done, E * UNITS + CREDIT)
            for c in range(NCH):
                b = batch_of(c)
                last = nc.vector.scalar_tensor_tensor(
                    out=k.x[:, chunk(c)], in0=acc[:, c], scalar=k.mod[:, layer, GATE_B, b:b + 1],
                    in1=k.x[:, chunk(c)], op0=ALU.mult, op1=ALU.add)
            last.then_inc(added, 1)


def experts_block(nc, k, layer, tiles, func, gated, routed, top_sum_eps=None):
    cols = tiles * P * (3 if gated else 2) + (tiles * (2 if gated else 1) if routed else 0)
    with ExitStack() as ctx:
        r = Kit()
        r.weights = k.dram[f"L{layer}_experts"]
        r.slot = ctx.enter_context(nc.sbuf_tensor(f"slot{layer}", [P, 2, cols], F32))
        r.slot_loaded = [nc.alloc_semaphore(f"slot{layer}_{s}") for s in range(2)]
        r.out_bias = f"L{layer}_out_bias"
        r.up_cols = tiles * P * (2 if gated else 1)
        r.zero = ctx.enter_context(nc.sbuf_tensor(f"zero{layer}", [P, P], F32))
        r.h16 = ctx.enter_context(nc.sbuf_tensor(f"h16_{layer}", [P, 2, T], F16))
        r.w16 = ctx.enter_context(nc.sbuf_tensor(f"w16_{layer}", [P, 2, 2, r.up_cols], F16))
        r.zero_ready, r.h_first, r.h_split = (
            nc.alloc_semaphore(f"{n}{layer}") for n in ("zero_ready", "h_first", "h_split"))
        r.w_first, r.w_split = ([nc.alloc_semaphore(f"{n}{layer}_{s}") for s in range(2)] for n in ("w_first", "w_split"))
        if routed:
            r.parts = ctx.enter_context(nc.sbuf_tensor(f"parts{layer}", [PARTS * PART, T], F32))
            r.wide = ctx.enter_context(nc.sbuf_tensor(f"wide{layer}", [P, E, T], F32))
            routing_stage(nc, k, r, f"L{layer}_router", top_sum_eps)
        else:
            with nc.Block() as block:
                @block.sync
                def _(sp):
                    for s in range(2):
                        sp.dma_start(r.slot[:, s], r.weights[s]).then_inc(r.slot_loaded[s], 16)
        experts_stage(nc, k, r, layer, tiles, func, gated, routed)


HEADS1 = 16
HD1 = 64
LANE = 32


def pair_attention_stage(nc, k):
    NJ = SEQ // CH
    M = HEADS1 * HD1 // P
    units = [(j, t) for j in range(NJ) for t in range(M)]
    U = len(units)
    scale = 1.0 / HD1 ** 0.5
    wq, wkv, wo = k.w["L1_Wq"], k.w["L1_Wkv"], k.w["L1_Wo"]
    row = lambda i, j: slice(i * SEQ + j * CH, i * SEQ + (j + 1) * CH)
    lanes = lambda i, j: slice(LANE * (2 * i + j), LANE * (2 * i + j) + LANE)
    with ExitStack() as ctx:
        sb = lambda name, shape: ctx.enter_context(nc.sbuf_tensor(name + "_pa", shape, F32))
        hd = sb("h_diff", [P, SEQ])
        sb16 = lambda name, cols: ctx.enter_context(nc.sbuf_tensor(name + "16_pa", [P, 2, cols], F16))
        h16, hd16, wq16, wkv16 = sb16("h", T), sb16("h_diff", SEQ), sb16("wq", M * P), sb16("wkv", 2 * M * P)
        kd, prod = sb("k_diff", [P, 2, CH]), sb("qk_prod", [P, 2, 2, CH])
        mx, e0, e1, w0 = sb("mx", [P, CH]), sb("e0", [P, CH]), sb("e1", [P, CH]), sb("w0", [P, CH])
        w16 = ctx.enter_context(nc.sbuf_tensor("w16_pa", [P, PARTS, CH], BF16))
        vd, wv, vec = sb("v_diff", [P, 2, CH]), sb("w_v", [P, 2, 2, CH]), sb("vec", [P, 2, 2, CH])
        sem = lambda name: nc.alloc_semaphore(name + "_pa")
        hd_ready, kd_ps_ready, q_ready, kd_ready, prod_ready, dots_done = (
            sem("hd"), sem("kd_ps"), sem("q"), sem("kd"), sem("prod"), sem("dots"))
        soft_step, e_ready = sem("soft_step"), sem("e")
        hd_first, h_first, hd_split, h_split, w_first, w_split = (
            sem("hd_first"), sem("h_first"), sem("hd_split"), sem("h_split"), sem("w_first"), sem("w_split"))

        def product(out, w16, t, x16, cols):
            for n, (i, part) in enumerate(PASSES):
                last = nc.tensor.matmul(out, w16[:, i, tile(t)], x16[:, part, cols],
                                        start=n == 0, stop=n == len(PASSES) - 1)
            return last
        vd_ps_ready, v1_ready, wide_ready, vd_ready, wv_ready, vec_ready, out_ready, added = (
            sem("vd_ps"), sem("v1"), sem("wide"), sem("vd"), sem("wv"), sem("vec"), sem("out"), sem("added"))

        with ExitStack() as first:
            q_ps = first.enter_context(nc.psum_tensor("q_ps_pa", [P, 2, 2, CH], F32))
            kd_ps = first.enter_context(nc.psum_tensor("kd_ps_pa", [P, 2, CH], F32))
            d_ps = first.enter_context(nc.psum_tensor("d_ps_pa", [P, CH], F32))
            block = first.enter_context(nc.Block())

            @block.tensor
            def _(pe):
                def project(u):
                    j, t = units[u]
                    if u >= 2:
                        pe.wait_ge(kd_ready, u - 1)
                    pe.wait_ge(w_split, min(t + 1, M) * 2)
                    pe.wait_ge(hd_split, j + 1)
                    product(kd_ps[:, u % 2], wkv16, t, hd16, slice(j * CH, (j + 1) * CH)).then_inc(kd_ps_ready, 1)
                    if u >= 2:
                        pe.wait_ge(prod_ready, 2 * (u - 1))
                    for i in range(NB):
                        pe.wait_ge(h_split, NB * j + i + 1)
                        product(q_ps[:, u % 2, i], wq16, t, h16, row(i, j)).then_inc(q_ready, 1)

                def dots(u):
                    j, t = units[u]
                    for i in range(NB):
                        pe.wait_ge(prod_ready, 2 * u + i + 1)
                        nc.tensor.matmul(d_ps[lanes(i, j)], k.w["head_sum"][:, t], prod[:, u % 2, i],
                                         start=t == 0, stop=t == M - 1,
                                         tile_position=(0, lanes(i, j).start)).then_inc(dots_done, 1)

                for u in range(U + 1):
                    if u < U:
                        project(u)
                    if u >= 1:
                        dots(u - 1)

            @block.gpsimd
            def _(pool):
                parts = [pair for t in range(M) for pair in ((wkv16, wkv, tile(t)), (wq16, wq, tile(t)))]
                parts += [(wkv16, wkv, tile(M + t)) for t in range(M)]
                for n, (w16, w, cols) in enumerate(parts):
                    nc.gpsimd.tensor_copy(w16[:, 0, cols], w[:, cols]).then_inc(w_first, 1)
                    pool.wait_ge(w_first, n + 1)
                    nc.gpsimd.tensor_tensor(w16[:, 1, cols], w[:, cols], w16[:, 0, cols],
                                            ALU.subtract).then_inc(w_split, 1)

            @block.scalar
            def _(act):
                def first_parts(j):
                    cols = slice(j * CH, (j + 1) * CH)
                    act.wait_ge(hd_ready, 1)
                    nc.scalar.activation(hd16[:, 0, cols], hd[:, cols], ACT.Copy).then_inc(hd_first, 1)
                    for i in range(NB):
                        nc.scalar.activation(h16[:, 0, row(i, j)], k.h[:, row(i, j)], ACT.Copy).then_inc(h_first, 1)

                first_parts(0)
                for u in range(U):
                    if u == M // 2:
                        first_parts(1)
                    act.wait_ge(kd_ps_ready, u + 1)
                    if u >= 2:
                        act.wait_ge(prod_ready, 2 * (u - 1))
                    nc.scalar.activation(kd[:, u % 2], kd_ps[:, u % 2], ACT.Copy).then_inc(kd_ready, 1)
                act.wait_ge(soft_step, 2)
                nc.scalar.activation(e0[:], e0[:], ACT.Exp, scale=scale).then_inc(e_ready, 1)
                nc.scalar.activation(e1[:], mx[:], ACT.Exp, scale=-scale).then_inc(e_ready, 1)

            @block.vector
            def _(dve):
                nc.vector.tensor_tensor(hd[:], k.h[:, 0:SEQ], k.h[:, SEQ:T], ALU.subtract).then_inc(hd_ready, 1)

                def second_parts(j):
                    cols = slice(j * CH, (j + 1) * CH)
                    dve.wait_ge(hd_ready, 1)
                    dve.wait_ge(hd_first, j + 1)
                    nc.vector.tensor_tensor(hd16[:, 1, cols], hd[:, cols], hd16[:, 0, cols],
                                            ALU.subtract).then_inc(hd_split, 1)
                    for i in range(NB):
                        dve.wait_ge(h_first, NB * j + i + 1)
                        nc.vector.tensor_tensor(h16[:, 1, row(i, j)], k.h[:, row(i, j)], h16[:, 0, row(i, j)],
                                                ALU.subtract).then_inc(h_split, 1)

                second_parts(0)
                for u in range(U):
                    if u == M // 2 + 1:
                        second_parts(1)
                    dve.wait_ge(kd_ready, u + 1)
                    for i in range(NB):
                        dve.wait_ge(q_ready, 2 * u + i + 1)
                        if u >= 2:
                            dve.wait_ge(dots_done, 2 * (u - 2) + i + 1)
                        nc.vector.tensor_tensor(prod[:, u % 2, i], q_ps[:, u % 2, i], kd[:, u % 2],
                                                ALU.mult).then_inc(prod_ready, 1)
                dve.wait_ge(dots_done, 2 * U)
                nc.vector.tensor_scalar(mx[:], d_ps[:], 0.0, None, ALU.max).then_inc(soft_step, 1)
                dve.wait_ge(soft_step, 1)
                nc.vector.tensor_tensor(e0[:], d_ps[:], mx[:], ALU.subtract).then_inc(soft_step, 1)
                dve.wait_ge(e_ready, 2)
                nc.vector.tensor_tensor(e1[:], e0[:], e1[:], ALU.add).then_inc(soft_step, 1)
                dve.wait_ge(soft_step, 3)
                nc.vector.reciprocal(e1[:], e1[:]).then_inc(soft_step, 1)
                dve.wait_ge(soft_step, 4)
                nc.vector.tensor_tensor(w0[:], e0[:], e1[:], ALU.mult).then_inc(soft_step, 1)
                n = 5
                for part in range(PARTS):
                    dve.wait_ge(soft_step, n)
                    nc.vector.tensor_copy(w16[:, part], w0[:]).then_inc(soft_step, 1)
                    n += 1
                    if part < PARTS - 1:
                        dve.wait_ge(soft_step, n)
                        nc.vector.tensor_tensor(w0[:], w0[:], w16[:, part], ALU.subtract).then_inc(soft_step, 1)
                        n += 1

        vd_ps = ctx.enter_context(nc.psum_tensor("vd_ps_pa", [P, CH], F32))
        v1_ps = ctx.enter_context(nc.psum_tensor("v1_ps_pa", [P, 2, CH], F32))
        wide_ps = ctx.enter_context(nc.psum_tensor("wide_ps_pa", [P, 2, CH], F32))
        o_ps = ctx.enter_context(nc.psum_tensor("o_ps_pa", [P, 2, CH], F32))
        block = ctx.enter_context(nc.Block())

        @block.tensor
        def _(pe):
            def project(u):
                j, t = units[u]
                if u >= 1:
                    pe.wait_ge(vd_ready, u)
                product(vd_ps[:], wkv16, M + t, hd16, slice(j * CH, (j + 1) * CH)).then_inc(vd_ps_ready, 1)
                for i in range(NB):
                    if u >= 1:
                        pe.wait_ge(wv_ready, 2 * (u - 1) + i + 1)
                    for part in range(PARTS):
                        last = nc.tensor.matmul(wide_ps[:, i], k.w["head_pick"][:, 2 * i + j, t], w16[:, part],
                                                start=part == 0, stop=part == PARTS - 1)
                    last.then_inc(wide_ready, 1)
                if u >= 2:
                    pe.wait_ge(vec_ready, 2 * (u - 1))
                product(v1_ps[:, u % 2], wkv16, M + t, h16, row(1, j)).then_inc(v1_ready, 1)

            def out(u):
                j, t = units[u]
                for i in range(NB):
                    pe.wait_ge(vec_ready, 2 * u + i + 1)
                    if j and t == 0:
                        pe.wait_ge(added, 2 * (j - 1) + i + 1)
                    nc.tensor.matmul(o_ps[:, i], wo[:, t], vec[:, u % 2, i],
                                     start=t == 0, stop=t == M - 1).then_inc(out_ready, 1)

            for u in range(U + 1):
                if u < U:
                    project(u)
                if u >= 1:
                    out(u - 1)

        @block.scalar
        def _(act):
            for u in range(U):
                act.wait_ge(vd_ps_ready, u + 1)
                if u >= 2:
                    act.wait_ge(wv_ready, 2 * (u - 1))
                nc.scalar.activation(vd[:, u % 2], vd_ps[:], ACT.Copy).then_inc(vd_ready, 1)

        @block.vector
        def _(dve):
            def add(j):
                for i in range(NB):
                    dve.wait_ge(out_ready, 2 * (j + 1) * M - 1 + i)
                    nc.vector.scalar_tensor_tensor(out=k.x[:, row(i, j)], in0=o_ps[:, i],
                                                   scalar=k.mod[:, 1, GATE_A, i:i + 1], in1=k.x[:, row(i, j)],
                                                   op0=ALU.mult, op1=ALU.add).then_inc(added, 1)

            for u in range(U):
                dve.wait_ge(vd_ready, u + 1)
                for i in range(NB):
                    dve.wait_ge(wide_ready, 2 * u + i + 1)
                    if u >= 2:
                        dve.wait_ge(vec_ready, 2 * (u - 2) + i + 1)
                    nc.vector.tensor_tensor(wv[:, u % 2, i], wide_ps[:, i], vd[:, u % 2],
                                            ALU.mult).then_inc(wv_ready, 1)
                dve.wait_ge(v1_ready, u + 1)
                for i in range(NB):
                    dve.wait_ge(wv_ready, 2 * u + i + 1)
                    if u >= 2:
                        dve.wait_ge(out_ready, 2 * (u - 2) + i + 1)
                    nc.vector.tensor_tensor(vec[:, u % 2, i], wv[:, u % 2, i], v1_ps[:, u % 2],
                                            ALU.add).then_inc(vec_ready, 1)
                if u == M:
                    add(0)
            add(1)


DEPTH = 2
HEADS2 = 8
HD2 = 64
HALF = HD2 // 2
INNER = HEADS2 * HD2
WINDOW = 64
HID = P * 4 * 2 // 3
QK_SCALE = 8.0
NORM_EPS = 1e-12
QT = INNER // P


def shift_stage(nc, k, depth, half, dst):
    with ExitStack() as ctx:
        shifted = nc.alloc_semaphore(f"shifted{depth}{half}")
        block = ctx.enter_context(nc.Block())
        late = slice(P // 2, P)

        @block.scalar
        def _(act):
            nc.scalar.activation(dst[0:P // 2], k.h[0:P // 2], ACT.Copy).then_inc(shifted, 1)

        @block.vector
        def _(dve):
            for b in range(NB):
                nc.vector.memset(dst[late, b * SEQ:b * SEQ + 1], 0.0).then_inc(shifted, 1)
                nc.vector.tensor_copy(dst[late, b * SEQ + 1:(b + 1) * SEQ],
                                      k.h[late, b * SEQ:(b + 1) * SEQ - 1]).then_inc(shifted, 1)


def local_qkv_stage(nc, k, s, depth):
    tag = f"_lq{depth}"
    TURN = 2
    w = k.w["L1_wqkv"]
    heads = lambda ap: ap.rearrange("p (h d) -> p h d", d=HD2)
    with ExitStack() as ctx:
        sb = lambda name, shape: ctx.enter_context(nc.sbuf_tensor(name + tag, shape, F32))
        table = sb("table", [P, 4, SEQ // P, HD2])
        sq, ss, norm, rk = sb("sq", [P, 2 * INNER]), sb("ss", [P, 2, 2 * HEADS2]), sb("norm", [P, 2, 2 * HEADS2]), sb("rk", [P, 2, 2 * HEADS2])
        straight, crossed = sb("straight", [P, 2, 2, INNER]), sb("crossed", [P, 2, 2, INNER])
        turned = straight
        qkv_ps = ctx.enter_context(nc.psum_tensor("qkv_ps" + tag, [P, 2, 3, CH], F32))
        t_ps = ctx.enter_context(nc.psum_tensor("t_ps" + tag, [P, 2, QT, P], F32))
        sem = lambda name: nc.alloc_semaphore(name + tag)
        tables_ready, qkv_ready, v_read, squared, summed, normed, clipped, rk_ready = (
            sem("tables"), sem("qkv"), sem("v_read"), sem("squared"), sem("summed"), sem("normed"), sem("clipped"), sem("rk"))
        mults, sums_q, sums_k, k_scaled, t_ready, t_read = (
            sem("mults"), sem("sums_q"), sem("sums_k"), sem("k_scaled"), sem("t"), sem("t_read"))
        block = ctx.enter_context(nc.Block())

        @block.tensor
        def _(pe):
            def project(t):
                if t >= 2:
                    pe.wait_ge(v_read, t - 1)
                    pe.wait_ge(squared, t - 1)
                    pe.wait_ge(mults, 4 * (t - 1))
                for j in range(3):
                    last = nc.tensor.matmul(qkv_ps[:, t % 2, j], s.shifted[:, tile(t)],
                                            w[:, depth, j * INNER:(j + 1) * INNER], start=True, stop=True)
                last.then_inc(qkv_ready, 1)

            def turn(t):
                for i in range(2):
                    pe.wait_ge(k_scaled if i else sums_q, t + 1)
                    if t:
                        pe.wait_ge(t_read, 2 * (t - 1) + i + 1)
                    for j in range(QT):
                        last = nc.tensor.transpose(t_ps[:, i, j], turned[:, t % 2, i, tile(j)], k.w["ident"][:])
                    last.then_inc(t_ready, 1)

            for t in range(NT + TURN):
                if t < NT:
                    project(t)
                if t >= TURN:
                    turn(t - TURN)

        @block.scalar
        def _(act):
            def store(t):
                for i, dst in enumerate((s.qT, s.kT)):
                    act.wait_ge(t_ready, 2 * t + i + 1)
                    nc.scalar.activation(dst[:, :, tile(t)], t_ps[:, i], ACT.Copy).then_inc(t_read, 1)

            for t in range(NT + TURN):
                if t < NT:
                    act.wait_ge(qkv_ready, t + 1)
                    if t >= 1:
                        act.wait_ge(summed, t)
                    nc.scalar.activation(sq[:].rearrange("p (j n) -> p j n", j=2), qkv_ps[:, t % 2, 0:2],
                                         ACT.Square).then_inc(squared, 1)
                    nc.scalar.activation(s.v[:, t], qkv_ps[:, t % 2, 2], ACT.Copy).then_inc(v_read, 1)
                    act.wait_ge(summed, t + 1)
                    if t >= 2:
                        act.wait_ge(clipped, t - 1)
                    nc.scalar.activation(norm[:, t % 2], ss[:, t % 2], ACT.Sqrt).then_inc(normed, 1)
                if t >= TURN:
                    store(t - TURN)

        @block.vector
        def _(dve):
            for j in range(4):
                nc.vector.tensor_tensor(table[:, j], k.w["rotary"][:, j],
                                        k.w["L1_qk_scale"][:, depth, j].unsqueeze(1).to_broadcast([P, SEQ // P, HD2]),
                                        ALU.mult).then_inc(tables_ready, 1)
            dve.wait_ge(tables_ready, 4)
            for t in range(NT):
                dve.wait_ge(squared, t + 1)
                if t >= 2:
                    dve.wait_ge(normed, t - 1)
                nc.vector.tensor_reduce(ss[:, t % 2], heads(sq[:]), AX, ALU.add).then_inc(summed, 1)
                if t >= 2:
                    dve.wait_ge(t_ready, 2 * (t - 1))
                dve.wait_ge(qkv_ready, t + 1)
                dve.wait_ge(v_read, t + 1)
                for i in range(2):
                    ps = heads(qkv_ps[:, t % 2, i])
                    cos = table[:, 2 * i, t % (SEQ // P)].unsqueeze(1).to_broadcast([P, HEADS2, HD2])
                    sin = table[:, 2 * i + 1, t % (SEQ // P)]
                    nc.vector.tensor_tensor(heads(straight[:, t % 2, i]), ps, cos, ALU.mult).then_inc(mults, 1)
                    for half in range(2):
                        here, there = slice(half * HALF, (half + 1) * HALF), slice((1 - half) * HALF, (2 - half) * HALF)
                        last = nc.vector.tensor_tensor(
                            heads(crossed[:, t % 2, i])[:, :, here], ps[:, :, there],
                            sin[:, here].unsqueeze(1).to_broadcast([P, HEADS2, HALF]), ALU.mult)
                    last.then_inc(mults, 1)
                dve.wait_ge(normed, t + 1)
                nc.vector.tensor_scalar(norm[:, t % 2], norm[:, t % 2], NORM_EPS, None, ALU.max).then_inc(clipped, 1)
                dve.wait_ge(clipped, t + 1)
                if t >= 2:
                    dve.wait_ge(k_scaled, t - 1)
                nc.vector.reciprocal(rk[:, t % 2], norm[:, t % 2]).then_inc(rk_ready, 1)
                dve.wait_ge(rk_ready, t + 1)
                nc.vector.tensor_scalar(s.rq[:, t], rk[:, t % 2, 0:HEADS2], QK_SCALE, None, ALU.mult)

        @block.gpsimd
        def _(pool):
            for t in range(NT):
                for i, done in enumerate((sums_q, sums_k)):
                    pool.wait_ge(mults, 4 * t + 2 * i + 2)
                    nc.gpsimd.tensor_tensor(turned[:, t % 2, i], straight[:, t % 2, i], crossed[:, t % 2, i],
                                            ALU.add).then_inc(done, 1)
                pool.wait_ge(rk_ready, t + 1)
                pool.wait_ge(sums_k, t + 1)
                nc.gpsimd.tensor_tensor(heads(turned[:, t % 2, 1]), heads(turned[:, t % 2, 1]),
                                        rk[:, t % 2, HEADS2:].unsqueeze(2).to_broadcast([P, HEADS2, HD2]),
                                        ALU.mult).then_inc(k_scaled, 1)


def local_attention_stage(nc, k, s, depth):
    tag = f"_la{depth}"
    PAIRS = HEADS2 // 2
    units = [(t, p) for t in range(NT) for p in range(PAIRS)]
    U = len(units)
    first_tile = lambda t: t % (SEQ // P) == 0
    KW = 2 * P
    R = 4
    INVERT, TURN, VALUES, TAKE_OUT = 1, 3, 4, 6
    start = lambda t: P if first_tile(t) else 0
    rows = lambda i: slice(i * HD2, (i + 1) * HD2)
    with ExitStack() as ctx:
        sb = lambda name, shape, dt=F32: ctx.enter_context(nc.sbuf_tensor(name + tag, shape, dt))
        mx, bias, total, inv = (sb(name, [P, R, 2]) for name in ("mx", "bias", "total", "inv"))
        prob, probT = sb("prob", [P, R, 2, KW]), sb("probT", [P, 2, 2, KW])
        one_head = sb("one_head", [P, 2, 2, QT, P])
        s_ps = ctx.enter_context(nc.psum_tensor("s_ps" + tag, [P, R, 2, KW], F32))
        p_ps = ctx.enter_context(nc.psum_tensor("p_ps" + tag, [P, 2, 2, KW], F32))
        o_ps = ctx.enter_context(nc.psum_tensor("o_ps" + tag, [P, 2, PAIRS, P], F32))
        sem = lambda name: nc.alloc_semaphore(name + tag)
        s_ready, mx_ready, bias_ready, prob_ready, inv_ready, scaled = (
            sem("s"), sem("mx"), sem("bias"), sem("prob"), sem("inv"), sem("scaled"))
        p_turned, probT_ready, o_ready, oT_ready, zeros_ready = (
            sem("p_turned"), sem("probT"), sem("o"), sem("oT"), sem("zeros"))
        head_ready = [sem(f"head{i}") for i in range(2)]
        block = ctx.enter_context(nc.Block())

        def blocks(t):
            return ((1, t),) if first_tile(t) else ((0, t - 1), (1, t))

        @block.tensor
        def _(pe):
            def scores(u):
                t, p = units[u]
                lo = start(t)
                if u >= R:
                    pe.wait_ge(prob_ready, u - R + 1)
                if p == 0:
                    pe.wait_ge(zeros_ready, 2)
                    for i in range(2):
                        pe.wait_ge(head_ready[i], t + 1)
                for i in range(2):
                    nc.tensor.matmul(s_ps[:, u % R, i, lo:KW], one_head[:, t % 2, i, p],
                                     s.kT[:, p, t * P - P + lo:(t + 1) * P], start=i == 0, stop=False)
                nc.tensor.matmul(s_ps[:, u % R, :, lo:KW], k.w["ident16"][:], k.w["window_mask"][:, :, lo:KW],
                                 start=False, stop=True).then_inc(s_ready, 1)

            def turn(u):
                t, p = units[u]
                pe.wait_ge(scaled, u + 1)
                if u >= 2:
                    pe.wait_ge(probT_ready, u - 1)
                for i in range(2):
                    for at, _ in blocks(t):
                        last = nc.tensor.transpose(p_ps[:, u % 2, i, tile(at)], prob[:, u % R, i, tile(at)],
                                                   k.w["ident"][:])
                last.then_inc(p_turned, 1)

            def values(u):
                t, p = units[u]
                pe.wait_ge(probT_ready, u + 1)
                if p == 0 and t >= 2:
                    pe.wait_ge(oT_ready, t - 1)
                for n, (at, kt) in enumerate(blocks(t)):
                    for i in range(2):
                        h = 2 * p + i
                        last = nc.tensor.matmul(o_ps[rows(i), t % 2, p], s.v[:, kt, h * HD2:(h + 1) * HD2],
                                                probT[:, u % 2, i, tile(at)], start=n == 0, stop=at == 1,
                                                tile_position=(0, i * HD2))
                last.then_inc(o_ready, 1)

            for u in range(U + VALUES):
                if u < U:
                    scores(u)
                if TURN <= u < U + TURN:
                    turn(u - TURN)
                if u >= VALUES:
                    values(u - VALUES)

        def take_queries(copy, i, t):
            copy(one_head[rows(i), t % 2, i], s.qT[rows(i), :, tile(t)]).then_inc(head_ready[i], 1)

        @block.scalar
        def _(act):
            def take_out(t):
                act.wait_ge(o_ready, (t + 1) * PAIRS)
                nc.scalar.activation(s.oT[:, :, tile(t)], o_ps[:, t % 2], ACT.Copy).then_inc(oT_ready, 1)

            copy = lambda out, src: nc.scalar.activation(out, src, ACT.Copy)
            take_queries(copy, 0, 0)
            for u in range(U + TAKE_OUT):
                if u < U:
                    t, p = units[u]
                    lo = start(t)
                    if p == 1 and t + 1 < NT:
                        if t >= 1:
                            act.wait_ge(s_ready, t * PAIRS)
                        take_queries(copy, 0, t + 1)
                    act.wait_ge(bias_ready, u + 1)
                    if u >= R:
                        act.wait_ge(p_turned, u - R + 1)
                        act.wait_ge(inv_ready, u - R + 1)
                    for i in range(2):
                        h = 2 * p + i
                        last = nc.scalar.activation(prob[:, u % R, i, lo:KW], s_ps[:, u % R, i, lo:KW], ACT.Exp,
                                                    bias=bias[:, u % R, i:i + 1], scale=s.rq[:, t, h:h + 1],
                                                    accum_out=total[:, u % R, i:i + 1])
                    last.then_inc(prob_ready, 1)
                if u >= TAKE_OUT and (u - TAKE_OUT) % PAIRS == 0 and (u - TAKE_OUT) // PAIRS < NT:
                    take_out((u - TAKE_OUT) // PAIRS)

        @block.gpsimd
        def _(pool):
            for i in range(2):
                nc.gpsimd.memset(one_head[rows(1 - i), :, i], 0.0).then_inc(zeros_ready, 1)
            for u, (t, p) in enumerate(units):
                lo = start(t)
                pool.wait_ge(inv_ready, u + 1)
                nc.gpsimd.tensor_tensor(prob[:, u % R, :, lo:KW], prob[:, u % R, :, lo:KW],
                                        inv[:, u % R].unsqueeze(2).to_broadcast([P, 2, KW - lo]),
                                        ALU.mult).then_inc(scaled, 1)

        @block.vector
        def _(dve):
            def maxima(u):
                t, p = units[u]
                dve.wait_ge(s_ready, u + 1)
                if u >= R:
                    dve.wait_ge(bias_ready, u - R + 1)
                nc.vector.tensor_reduce(mx[:, u % R], s_ps[:, u % R, :, start(t):KW], AX, ALU.max).then_inc(mx_ready, 1)
                dve.wait_ge(mx_ready, u + 1)
                if u >= R:
                    dve.wait_ge(prob_ready, u - R + 1)
                nc.vector.scalar_tensor_tensor(out=bias[:, u % R], in0=mx[:, u % R], scalar=-1.0,
                                               in1=s.rq[:, t, 2 * p:2 * p + 2], op0=ALU.mult,
                                               op1=ALU.mult).then_inc(bias_ready, 1)

            def invert(u):
                dve.wait_ge(prob_ready, u + 1)
                if u >= R:
                    dve.wait_ge(scaled, u - R + 1)
                nc.vector.reciprocal(inv[:, u % R], total[:, u % R]).then_inc(inv_ready, 1)

            def take_turned(u):
                lo = start(units[u][0])
                dve.wait_ge(p_turned, u + 1)
                if u >= 2:
                    dve.wait_ge(o_ready, u - 1)
                nc.vector.tensor_copy(probT[:, u % 2, :, lo:KW], p_ps[:, u % 2, :, lo:KW]).then_inc(probT_ready, 1)

            take_queries(nc.vector.tensor_copy, 1, 0)
            for u in range(U + TURN):
                if u < U:
                    t, p = units[u]
                    if p == 1 and t + 1 < NT:
                        if t >= 1:
                            dve.wait_ge(s_ready, t * PAIRS)
                        take_queries(nc.vector.tensor_copy, 1, t + 1)
                    maxima(u)
                if INVERT <= u < U + INVERT:
                    invert(u - INVERT)
                if u >= TURN:
                    take_turned(u - TURN)


def local_out_stage(nc, k, s, depth):
    with ExitStack() as ctx:
        o_ps = ctx.enter_context(nc.psum_tensor(f"wo_ps{depth}", [P, NCH, CH], F32))
        out_ready = nc.alloc_semaphore(f"wo_ready{depth}")
        added = nc.alloc_semaphore(f"wo_added{depth}")
        block = ctx.enter_context(nc.Block())

        @block.tensor
        def _(pe):
            for c in range(NCH):
                for j in range(QT):
                    last = nc.tensor.matmul(o_ps[:, c], k.w["L1_wo"][:, depth, j], s.oT[:, j, chunk(c)],
                                            start=j == 0, stop=j == QT - 1)
                last.then_inc(out_ready, 1)

        @block.vector
        def _(dve):
            for c in range(NCH):
                dve.wait_ge(out_ready, c + 1)
                nc.vector.tensor_tensor(k.h[:, chunk(c)], k.h[:, chunk(c)], o_ps[:, c], ALU.add).then_inc(added, 1)


def hidden_stage(nc, k, s, depth):
    tag = f"_hd{depth}"
    M = -(-HID // P)
    units = [(c, m) for c in range(NCH) for m in range(M)]
    U = len(units)
    w1, w2, b1, b2 = k.w["L1_w1"], k.w["L1_w2"], k.w["L1_b1"], k.w["L1_b2"]
    with ExitStack() as ctx:
        sb = lambda name, shape: ctx.enter_context(nc.sbuf_tensor(name + tag, shape, F32))
        gelu, hid = sb("gelu", [P, 2, CH]), sb("hid", [P, 3, CH])
        x16 = ctx.enter_context(nc.sbuf_tensor("x16" + tag, [P, 2, T], F16))
        w16 = ctx.enter_context(nc.sbuf_tensor("w16" + tag, [P, 2, 2, M * P], F16))
        a_ps = ctx.enter_context(nc.psum_tensor("a_ps" + tag, [P, 2, CH], F32))
        g_ps = ctx.enter_context(nc.psum_tensor("g_ps" + tag, [P, 2, CH], F32))
        o_ps = ctx.enter_context(nc.psum_tensor("o_ps" + tag, [P, 2, CH], F32))
        sem = lambda name: nc.alloc_semaphore(name + tag)
        g_ready, a_ready, gelu_ready, hid_ready, down_done, h_ready, x_ready = (
            sem("g"), sem("a"), sem("gelu"), sem("hid"), sem("down"), sem("h"), sem("x"))
        x_first, x_split, w_first, w_split = sem("x_first"), sem("x_split"), sem("w_first"), sem("w_split")
        block = ctx.enter_context(nc.Block())

        @block.tensor
        def _(pe):
            def up(u):
                c, m = units[u]
                if c == 0:
                    pe.wait_ge(w_split, 2 * (m + 1))
                if m == 0:
                    pe.wait_ge(x_split, c + 1)
                if u >= 2:
                    pe.wait_ge(gelu_ready, u - 1)
                    pe.wait_ge(hid_ready, u - 1)
                for out, half, done in ((g_ps, 1, g_ready), (a_ps, 0, a_ready)):
                    for n, (i, j) in enumerate(PASSES):
                        last = nc.tensor.matmul(out[:, u % 2], w16[:, i, half, tile(m)], x16[:, j, chunk(c)],
                                                start=n == 0, stop=n == len(PASSES) - 1)
                    last.then_inc(done, 1)

            def down(u):
                c, m = units[u]
                pe.wait_ge(hid_ready, u + 1)
                if m == 0 and c >= 2:
                    pe.wait_ge(h_ready, c - 1)
                nc.tensor.matmul(o_ps[:, c % 2], w2[:, depth, m], hid[:, u % 3],
                                 start=m == 0, stop=m == M - 1).then_inc(down_done, 1)

            for u in range(U + 2):
                if u < U:
                    up(u)
                if u >= 2:
                    down(u - 2)

        @block.gpsimd
        def _(pool):
            for n, (m, half) in enumerate((m, half) for m in range(M) for half in (1, 0)):
                w = w1[:, depth, half, tile(m)]
                nc.gpsimd.tensor_copy(w16[:, 0, half, tile(m)], w).then_inc(w_first, 1)
                pool.wait_ge(w_first, n + 1)
                nc.gpsimd.tensor_tensor(w16[:, 1, half, tile(m)], w, w16[:, 0, half, tile(m)],
                                        ALU.subtract).then_inc(w_split, 1)

        @block.scalar
        def _(act):
            def first_part(c):
                nc.scalar.activation(x16[:, 0, chunk(c)], s.normed[:, chunk(c)], ACT.Copy).then_inc(x_first, 1)

            first_part(0)
            for u, (c, m) in enumerate(units):
                if m == 0 and c + 1 < NCH:
                    first_part(c + 1)
                act.wait_ge(g_ready, u + 1)
                if u >= 2:
                    act.wait_ge(hid_ready, u - 1)
                nc.scalar.activation(gelu[:, u % 2], g_ps[:, u % 2], ACT.Gelu,
                                     bias=b1[:, depth, 1, m:m + 1]).then_inc(gelu_ready, 1)

        @block.vector
        def _(dve):
            def add(c):
                b = batch_of(c)
                dve.wait_ge(down_done, (c + 1) * M)
                nc.vector.scalar_tensor_tensor(out=k.h[:, chunk(c)], in0=o_ps[:, c % 2], scalar=b2[:, depth:depth + 1],
                                               in1=k.h[:, chunk(c)], op0=ALU.add, op1=ALU.add).then_inc(h_ready, 1)
                if depth == DEPTH - 1:
                    dve.wait_ge(h_ready, c + 1)
                    nc.vector.scalar_tensor_tensor(out=k.x[:, chunk(c)], in0=k.h[:, chunk(c)],
                                                   scalar=k.mod[:, 1, GATE_B, b:b + 1], in1=k.x[:, chunk(c)],
                                                   op0=ALU.mult, op1=ALU.add).then_inc(x_ready, 1)

            def second_part(c):
                dve.wait_ge(x_first, c + 1)
                nc.vector.tensor_tensor(x16[:, 1, chunk(c)], s.normed[:, chunk(c)], x16[:, 0, chunk(c)],
                                        ALU.subtract).then_inc(x_split, 1)

            second_part(0)
            for u, (c, m) in enumerate(units):
                if m == 0 and c + 1 < NCH:
                    second_part(c + 1)
                dve.wait_ge(a_ready, u + 1)
                dve.wait_ge(gelu_ready, u + 1)
                if u >= 3:
                    dve.wait_ge(down_done, u - 2)
                nc.vector.scalar_tensor_tensor(out=hid[:, u % 3], in0=a_ps[:, u % 2],
                                               scalar=b1[:, depth, 0, m:m + 1], in1=gelu[:, u % 2],
                                               op0=ALU.add, op1=ALU.mult).then_inc(hid_ready, 1)
                if m == 1 and c >= 1:
                    add(c - 1)
            add(NCH - 1)


def local_block(nc, k):
    for depth in range(DEPTH):
        with ExitStack() as ctx:
            sb = lambda name, shape: ctx.enter_context(nc.sbuf_tensor(f"{name}_lb{depth}", shape, F32))
            s = Kit()
            s.shifted, s.qT = sb("shifted", [P, T]), sb("qT", [P, QT, T])
            s.oT = s.qT
            with (nc.sbuf_tensor(f"kT{depth}", [P, QT, T], F32) as s.kT,
                  nc.sbuf_tensor(f"v{depth}", [P, NT, INNER], F32) as s.v,
                  nc.sbuf_tensor(f"rq{depth}", [P, NT, HEADS2], F32) as s.rq):
                shift_stage(nc, k, depth, 0, s.shifted)
                local_qkv_stage(nc, k, s, depth)
                local_attention_stage(nc, k, s, depth)
            local_out_stage(nc, k, s, depth)
            shift_stage(nc, k, depth, 1, s.shifted)
            s.normed = sb("normed", [P, T])
            layernorm_stage(nc, k, f"l{depth}", s.shifted, s.normed,
                            lambda b: (k.w["L1_ln"][:, 0, depth:depth + 1], k.w["L1_ln"][:, 1, depth:depth + 1]))
            hidden_stage(nc, k, s, depth)


HEADS3 = 16
HD3 = P // HEADS3
NH3 = NB * HEADS3
QTS = SEQ // P
Q_PART = (0, 0, 1, 1, 0, 2)
K_PART = (0, 1, 0, 1, 2, 0)
SLOTS = len(Q_PART)
ROWS = SLOTS * HD3
FULL = 3 * P // 4
M_PARTS = 2
QUAD = 4
NQ = NH3 // QUAD
RING = 2 * QUAD
QUARTER = P // QUAD
V1 = QUARTER


def causal_project_stage(nc, k, s):
    with ExitStack() as ctx:
        rest = ctx.enter_context(nc.sbuf_tensor("rest_cp", [P, 2, 2, CH], F32))
        part = ctx.enter_context(nc.sbuf_tensor("part_cp", [P, 2, PARTS, T], BF16))
        qk_ps = ctx.enter_context(nc.psum_tensor("qk_ps_cp", [P, 4, CH], F32))
        v_ps = ctx.enter_context(nc.psum_tensor("v_ps_cp", [P, 2, CH], F32))
        sem = lambda name: nc.alloc_semaphore(name + "_cp")
        qk_ready, part0, rest_ready, part1, part2, v_ready, v_stored, ones_ready, stored = (
            sem("qk"), sem("part0"), sem("rest"), sem("part1"), sem("part2"), sem("v"), sem("v_stored"), sem("ones"),
            sem("stored"))
        block = ctx.enter_context(nc.Block())
        units = [(c, i) for c in range(NCH) for i in range(2)]
        slots_of = lambda part: [(i, slot, dst) for i, (order, dst) in enumerate(((Q_PART, s.q_dram), (K_PART, s.k_dram)))
                                 for slot, n in enumerate(order) if n == part]

        @block.tensor
        def _(pe):
            for u, (c, i) in enumerate(units):
                if u >= 4:
                    pe.wait_ge(rest_ready, u - 3)
                nc.tensor.matmul(qk_ps[:, u % 4], k.w["L2_W"][:, i], k.h[:, chunk(c)],
                                 start=True, stop=True).then_inc(qk_ready, 1)
            for t in range(NT):
                if t >= 2:
                    pe.wait_ge(v_stored, t - 1)
                nc.tensor.matmul(v_ps[:, t % 2, 0:P], k.h[:, tile(t)], k.w["L2_W"][:, 2],
                                 start=True, stop=True).then_inc(v_ready, 1)

        @block.scalar
        def _(act):
            for u, (c, i) in enumerate(units):
                act.wait_ge(qk_ready, u + 1)
                nc.scalar.activation(part[:, i, 0, chunk(c)], qk_ps[:, u % 4], ACT.Copy).then_inc(part0, 1)
            for t in range(NT):
                b, kt = divmod(t, QTS)
                act.wait_ge(v_ready, t + 1)
                nc.scalar.activation(s.v1[:, b * HEADS3:(b + 1) * HEADS3, kt, 0:HD3],
                                     v_ps[:, t % 2, 0:P].rearrange("p (h d) -> p h d", d=HD3),
                                     ACT.Copy).then_inc(v_stored, 1)

        @block.vector
        def _(dve):
            for u, (c, i) in enumerate(units):
                dve.wait_ge(part0, u + 1)
                if u >= 2:
                    dve.wait_ge(part2, u - 1)
                nc.vector.tensor_tensor(rest[:, u % 2, 0], qk_ps[:, u % 4], part[:, i, 0, chunk(c)],
                                        ALU.subtract).then_inc(rest_ready, 1)
                dve.wait_ge(rest_ready, u + 1)
                nc.vector.tensor_copy(part[:, i, 1, chunk(c)], rest[:, u % 2, 0]).then_inc(part1, 1)

        @block.gpsimd
        def _(pool):
            nc.gpsimd.memset(s.v1[:, :, :, HD3:].rearrange("p h t d -> p (h t) d"), 1.0).then_inc(ones_ready, 1)
            for u, (c, i) in enumerate(units):
                pool.wait_ge(part1, u + 1)
                nc.gpsimd.tensor_tensor(part[:, i, 2, chunk(c)], rest[:, u % 2, 0], part[:, i, 1, chunk(c)],
                                        ALU.subtract).then_inc(part2, 1)

        @block.sync
        def _(sp):
            for r in range(RING):
                sp.dma_start(s.ks[ROWS:FULL + M_PARTS, r], k.dram["zero_one_rows"]).then_inc(stored, 16)
                sp.dma_start(s.qs[ROWS:FULL, r], k.dram["zero_one_rows"][0:FULL - ROWS]).then_inc(stored, 16)
            per_row = len(units) // NB
            for b in range(NB):
                for n, ready in enumerate((part0, part1, part2)):
                    sp.wait_ge(ready, (b + 1) * per_row)
                    for i, slot, dst in slots_of(n):
                        sp.dma_start(dst[b * NQ // NB:(b + 1) * NQ // NB, slot],
                                     part[:, i, n, b * SEQ:(b + 1) * SEQ]).then_inc(stored, 16)
            sp.wait_ge(stored, 16 * 2 * (RING + SLOTS * NB))


def load_sums(sp, s, b):
    rows_of = s.o_dram.rearrange("(b q) (g e) n -> b q g e n", b=NB, e=QUARTER)
    for i in range(2):
        sp.dma_start(s.ys[:, i, b * SEQ:(b + 1) * SEQ],
                     rows_of[b, :, :, i * HD3:(i + 1) * HD3]).then_inc(s.ys_loaded[b], 16)


def divide_by_sums(nc, dve, s, c):
    dve.wait_ge(s.ys_loaded[batch_of(c)], 32)
    nc.vector.reciprocal(s.ys[:, 1, chunk(c)], s.ys[:, 1, chunk(c)]).then_inc(s.inv_ready, 1)
    dve.wait_ge(s.inv_ready, c + 1)
    nc.vector.tensor_tensor(s.ys[:, 0, chunk(c)], s.ys[:, 0, chunk(c)], s.ys[:, 1, chunk(c)],
                            ALU.mult).then_inc(s.y_ready, 1)


def causal_attention_stage(nc, k, s):
    a_tiles = [(g, qt, kc) for g in range(QUAD) for qt in range(QTS) for kc in range(2) if kc * 4 <= qt]
    groups = [(j, kt) for j in range(2) for kt in range(4 * j + 4)]
    A, G = len(a_tiles), len(groups)
    B = G * QUAD
    FIRST_A, LAST_A = 2, G - 2
    PER_GROUP = -(-A // (LAST_A - FIRST_A))
    scale = 1.0 / HD3 ** 0.5
    A_BANKS = B_BANKS = 3
    M_ROWS = M_PARTS * QUAD * QTS
    with ExitStack() as ctx:
        sb = lambda name, shape, dt=F32: ctx.enter_context(nc.sbuf_tensor(name + "_ca", shape, dt))
        prob, mx = sb("prob", [P, 2, QUAD, CH]), sb("mx", [P, 2, 2, QUAD, QTS])
        m16, ms = sb("m16", [P, 2, QUAD, QTS], BF16), sb("ms", [P, 2, M_PARTS, QUAD, QTS])
        mrow = sb("mrow", [2 * M_ROWS, P], BF16)
        vh, out = sb("vh", [P, 2, QUAD, QTS, V1]), sb("out", [P, 2, 2, CH])
        a_ps = ctx.enter_context(nc.psum_tensor("a_ps_ca", [P, A_BANKS, CH], F32))
        b_ps = ctx.enter_context(nc.psum_tensor("b_ps_ca", [P, B_BANKS, CH], F32))
        o_ps = ctx.enter_context(nc.psum_tensor("o_ps_ca", [P, 2, CH], F32))
        t_ps = a_ps[:, 0]
        sem = lambda name: nc.alloc_semaphore(name + "_ca")
        loaded = [sem(f"loaded{r}") for r in range(RING)]
        m_loaded = [sem(f"m_loaded{q}") for q in range(2)]
        stored = [sem(f"stored{q}") for q in range(2)]
        max_done = [sem(f"max_done{q}") for q in range(2)]
        ms_cleared, a_ready, m_step, split_ready, m_turned, mrow_ready = (
            sem("ms_cleared"), sem("a"), sem("m_step"), sem("split"), sem("m_turned"), sem("mrow"))
        b_ready, exp_done, pv_done, v_ready, out_ready = sem("b"), sem("exp"), sem("pv"), sem("v"), sem("out")
        C_PV = C_OUT = C_TURN = C_SPLIT = 2
        C_EXP, C_MROW = B_BANKS, 1
        block = ctx.enter_context(nc.Block())
        width = lambda qt, kc: min(4, qt + 1 - 4 * kc) * P
        low = lambda j, kt: max(0, kt - 4 * j) * P
        LOOPS = NQ // 2 - 1
        quad = lambda it, q: it * 2 + q
        of = lambda q: slice(q * M_ROWS, (q + 1) * M_ROWS)
        heads = lambda q: slice(q * QUAD, (q + 1) * QUAD)
        after = lambda it, q: (it + (q + 1) // 2, (q + 1) % 2)

        def whole(engine, body, between=lambda: None):
            with engine.Fori(0, LOOPS, 1) as it:
                for q in range(2):
                    body(it, q, False)
            between()
            for q in range(2):
                body(LOOPS, q, q == 1)

        @block.sync
        def _(sp):
            def load(it, q):
                for g in range(QUAD):
                    r = q * QUAD + g
                    src = lambda dram: dram[bass.ds(quad(it, q), 1)].rearrange(
                        "o s (d g) n -> (o s d) g n", g=QUAD)[:, g]
                    sp.dma_start(s.qs[0:ROWS, r], src(s.q_dram)).then_inc(loaded[r], 16)
                    sp.dma_start(s.ks[0:ROWS, r], src(s.k_dram)).then_inc(loaded[r], 16)

            def maximum_rows(it, q):
                sp.wait_ge(mrow_ready, quad(it, q) + 1 + C_MROW)
                sp.dma_start(s.qs[FULL:FULL + M_PARTS, heads(q)], mrow[of(q)]).then_inc(m_loaded[q], 16)

            load(0, 0)
            maximum_rows(0, 0)

            def body(it, q, last):
                if not last:
                    sp.wait_ge(b_ready, quad(it, q) * B + 1)
                    load(*after(it, q))
                    maximum_rows(*after(it, q))
                sp.wait_ge(out_ready, quad(it, q) * 2 + (2 + C_OUT))
                sp.dma_start(s.o_dram[bass.ds(quad(it, q), 1)].rearrange("o p n -> p (o n)"),
                             out[:, q].rearrange("p j n -> p (j n)")).then_inc(stored[q], 16)

            def first_row():
                for q in range(2):
                    sp.wait_ge(stored[q], 16 * NQ // 2 // NB)
                load_sums(sp, s, 0)

            whole(sp, body, first_row)
            for q in range(2):
                sp.wait_ge(stored[q], 16 * NQ // 2)

        @block.tensor
        def _(pe):
            def scores(it, q, i):
                g, qt, kc = a_tiles[i]
                w, r = width(qt, kc), q * QUAD + g
                if (qt, kc) == (0, 0):
                    pe.wait_ge(loaded[r], it * 32 + 32)
                if i == 0:
                    pe.wait_ge(mrow_ready, quad(it, q) + C_MROW)
                if i >= A_BANKS:
                    pe.wait_ge(max_done[q], it * A + (i - A_BANKS + 1))
                diagonal = qt // 4 == kc
                last = nc.tensor.matmul(a_ps[:, i % A_BANKS, 0:w], s.qs[0:FULL, r, tile(qt)],
                                        s.ks[0:FULL, r, kc * CH:kc * CH + w], start=True, stop=not diagonal)
                if diagonal:
                    last = nc.tensor.matmul(a_ps[:, i % A_BANKS, w - P:w], k.w["ident16"][:], k.w["causal_mask"][:, 0],
                                            start=False, stop=True)
                last.then_inc(a_ready, 1)

            def turn_maxima(it, q):
                pe.wait_ge(split_ready, quad(it, q) + 1 + C_SPLIT)
                nc.tensor.transpose(t_ps[:, 0:P], ms[:].rearrange("p q m g t -> p (q m g t)"),
                                    k.w["ident"][:]).then_inc(m_turned, 1)

            def scores_t(it, q, u, g):
                (j, kt), r, i = groups[u], q * QUAD + g, u * QUAD + g
                lo = low(j, kt)
                if i == 0:
                    pe.wait_ge(m_loaded[q], it * 16 + 16)
                pe.wait_ge(exp_done, quad(it, q) * B + (i - B_BANKS + 1 + C_EXP))
                diagonal = kt >= 4 * j
                last = nc.tensor.matmul(b_ps[:, i % B_BANKS, lo:CH], s.ks[0:FULL + M_PARTS, r, tile(kt)],
                                        s.qs[0:FULL + M_PARTS, r, j * CH + lo:(j + 1) * CH],
                                        start=True, stop=not diagonal)
                if diagonal:
                    last = nc.tensor.matmul(b_ps[:, i % B_BANKS, lo:lo + P], k.w["ident16"][:],
                                            k.w["causal_mask"][:, 1], start=False, stop=True)
                last.then_inc(b_ready, 1)

            def values(it, q, u):
                j, kt = groups[u]
                lo = low(j, kt)
                if u == 0:
                    pe.wait_ge(v_ready, quad(it, q) + 1)
                if kt == 0:
                    pe.wait_ge(out_ready, quad(it, q) * 2 + (j - 2 + 1 + C_OUT))
                pe.wait_ge(exp_done, quad(it, q) * B + ((u + 1) * QUAD + C_EXP))
                for g in range(QUAD):
                    last = nc.tensor.matmul(o_ps[g * QUARTER:(g + 1) * QUARTER, j, lo:CH], vh[:, q, g, kt],
                                            prob[:, u % 2, g, lo:CH], start=kt == 0, stop=kt == 4 * j + 3,
                                            tile_position=(0, g * QUARTER), skip_group_check=True)
                last.then_inc(pv_done, 1)

            pe.sem_inc(m_turned, C_TURN)
            pe.sem_inc(pv_done, C_PV)
            for i in range(A):
                scores(0, 0, i)
            pe.wait_ge(ms_cleared, 1)
            turn_maxima(0, 0)

            def body(it, q, last):
                i = 0
                for u in range(G):
                    for g in range(QUAD):
                        scores_t(it, q, u, g)
                        if u >= FIRST_A and not last:
                            to = min(A, (u - FIRST_A) * PER_GROUP + (g + 1) * PER_GROUP // QUAD)
                            while i < to:
                                scores(*after(it, q), i)
                                i += 1
                    if u == LAST_A and not last:
                        turn_maxima(*after(it, q))
                    if u >= 1:
                        values(it, q, u - 1)
                values(it, q, G - 1)

            whole(pe, body)

        @block.scalar
        def _(act):
            def maxima_row(it, q):
                act.wait_ge(m_turned, quad(it, q) + (1 + C_TURN))
                act.wait_ge(m_loaded[q], it * 16)
                nc.scalar.activation(mrow[of(q)], t_ps[of(q), 0:P], ACT.Copy).then_inc(mrow_ready, 1)

            def take_out(it, q, j):
                act.wait_ge(stored[q], it * 16)
                act.wait_ge(pv_done, quad(it, q) * G + (4 * (j + 1) + 4 * j + C_PV))
                nc.scalar.activation(out[:, q, j], o_ps[:, j], ACT.Copy).then_inc(out_ready, 1)

            act.sem_inc(exp_done, C_EXP)
            act.sem_inc(mrow_ready, C_MROW)
            act.sem_inc(out_ready, C_OUT)
            act.wait_ge(m_turned, 1 + C_TURN)
            nc.scalar.activation(mrow[of(0)], t_ps[of(0), 0:P], ACT.Copy).then_inc(mrow_ready, 1)

            def body(it, q, last):
                for u, (j, kt) in enumerate(groups):
                    lo = low(j, kt)
                    for g in range(QUAD):
                        i = u * QUAD + g
                        act.wait_ge(b_ready, quad(it, q) * B + (i + 1))
                        if g == 0:
                            act.wait_ge(pv_done, quad(it, q) * G + (u - 2 + 1 + C_PV))
                        nc.scalar.activation(prob[:, u % 2, g, lo:CH], b_ps[:, i % B_BANKS, lo:CH], ACT.Exp,
                                             scale=scale).then_inc(exp_done, 1)
                    if u == 5:
                        take_out(it, q, 0)
                    if u == LAST_A and not last:
                        maxima_row(*after(it, q))
                take_out(it, q, 1)

            whole(act, body)

        @block.gpsimd
        def _(pool):
            def take(it, q):
                nc.gpsimd.tensor_copy(vh[:, q].rearrange("p g t d -> p (g t) d"),
                                      s.v1[:, bass.ds(quad(it, q) * QUAD, QUAD)].rearrange("p g t d -> p (g t) d")
                                      ).then_inc(v_ready, 1)

            take(0, 0)

            def body(it, q, last):
                if not last:
                    pool.wait_ge(out_ready, quad(it, q) * 2 + C_OUT)
                    take(*after(it, q))

            whole(pool, body)

        @block.vector
        def _(dve):
            def maximum(it, q, i):
                g, qt, kc = a_tiles[i]
                if i == 0:
                    dve.wait_ge(split_ready, quad(it, q) + (1 - 2 + C_SPLIT))
                dve.wait_ge(a_ready, quad(it, q) * A + (i + 1))
                nc.vector.tensor_reduce(mx[:, q, kc, g, qt:qt + 1], a_ps[:, i % A_BANKS, 0:width(qt, kc)], AX,
                                        ALU.max).then_inc(max_done[q], 1)

            def split(it, q):
                n = quad(it, q) * 3
                if q == 1:
                    dve.wait_ge(ms_cleared, 1)
                m = mx[:, q, 0]
                dve.wait_ge(max_done[q], it * A + A)
                nc.vector.tensor_tensor(m[:, :, 4:], m[:, :, 4:], mx[:, q, 1, :, 4:], ALU.max).then_inc(m_step, 1)
                dve.wait_ge(m_step, n + 1)
                nc.vector.tensor_scalar(m16[:, q], m, -1.0, None, ALU.mult).then_inc(m_step, 1)
                dve.wait_ge(m_step, n + 2)
                dve.wait_ge(m_turned, quad(it, q) + (1 - 2 + C_TURN))
                nc.vector.tensor_copy(ms[:, q, 0], m16[:, q]).then_inc(m_step, 1)
                dve.wait_ge(m_step, n + 3)
                nc.vector.scalar_tensor_tensor(out=ms[:, q, 1], in0=m, scalar=-1.0, in1=m16[:, q],
                                               op0=ALU.mult, op1=ALU.subtract).then_inc(split_ready, 1)

            dve.sem_inc(split_ready, C_SPLIT)
            nc.vector.memset(ms[:, 1], 0.0).then_inc(ms_cleared, 1)
            for i in range(A):
                maximum(0, 0, i)
            split(0, 0)

            def body(it, q, last):
                if not last:
                    for i in range(A):
                        maximum(*after(it, q), i)
                    split(*after(it, q))

            whole(dve, body)
            for c in range(NCH // NB):
                divide_by_sums(nc, dve, s, c)


def causal_out_stage(nc, k, s):
    with ExitStack() as ctx:
        o_ps = ctx.enter_context(nc.psum_tensor("o_ps_co", [P, NCH, CH], F32))
        out_ready, added = (nc.alloc_semaphore(n + "_co") for n in ("out", "added"))
        block = ctx.enter_context(nc.Block())

        @block.sync
        def _(sp):
            load_sums(sp, s, 1)

        @block.tensor
        def _(pe):
            for c in range(NCH):
                pe.wait_ge(s.y_ready, c + 1)
                nc.tensor.matmul(o_ps[:, c], k.w["L2_W"][:, 3], s.ys[:, 0, chunk(c)],
                                 start=True, stop=True).then_inc(out_ready, 1)

        @block.vector
        def _(dve):
            for c in range(NCH // NB, NCH):
                divide_by_sums(nc, dve, s, c)
            for c in range(NCH):
                b = batch_of(c)
                dve.wait_ge(out_ready, c + 1)
                nc.vector.scalar_tensor_tensor(out=k.x[:, chunk(c)], in0=o_ps[:, c],
                                               scalar=k.mod[:, 2, GATE_A, b:b + 1], in1=k.x[:, chunk(c)],
                                               op0=ALU.mult, op1=ALU.add).then_inc(added, 1)


def causal_attention_block(nc, k):
    with ExitStack() as ctx:
        s = Kit()
        s.q_dram = nc.dram_tensor("q_parts", [NQ, SLOTS, QUAD * HD3, SEQ], BF16).ap()
        s.k_dram = nc.dram_tensor("k_parts", [NQ, SLOTS, QUAD * HD3, SEQ], BF16).ap()
        s.ys = ctx.enter_context(nc.sbuf_tensor("ys_ca", [P, 2, T], F32))
        s.ys_loaded = [nc.alloc_semaphore(f"ys_loaded{b}") for b in range(NB)]
        s.inv_ready, s.y_ready = nc.alloc_semaphore("inv_ca"), nc.alloc_semaphore("y_ca")
        s.o_dram = nc.dram_tensor("o_and_sums", [NQ, P, SEQ], F32).ap()
        with (nc.sbuf_tensor("qs", [FULL + M_PARTS, RING, SEQ], BF16) as s.qs,
              nc.sbuf_tensor("ks", [FULL + M_PARTS, RING, SEQ], BF16) as s.ks,
              nc.sbuf_tensor("v1_ca", [P, NH3, QTS, V1], F32) as s.v1):
            causal_project_stage(nc, k, s)
            causal_attention_stage(nc, k, s)
        causal_out_stage(nc, k, s)


EPS_SUM = 1e-7
EPS_NORM = 1e-12


def linear_attention_block(nc, k):
    TPR = SEQ // P
    with ExitStack() as ctx:
        sb = lambda name, shape: ctx.enter_context(nc.sbuf_tensor(name + "_li", shape, F32))
        w, bias, mean = sb("w", [P, 3 * P]), sb("bias", [P, 3 * P]), sb("mean", [P, 4])
        qkv, q2, k2 = sb("qkv", [P, 2, 3 * P]), sb("q2", [P, NT, P]), sb("k2", [P, NT, P])
        v, q4 = sb("v", [P, NT, P]), sb("q4", [P, P])
        sums = sb("sums", [P, 3, NT])
        f = sb("f", [P, 6, NT])
        qT, kv, kn, kf, y, o = (sb("qT", [P, T]), sb("kv", [P, NB, P]), sb("kn", [P, NB]), sb("kf", [P, NB]),
                                sb("y", [P, 2, CH]), sb("o", [P, 2, CH]))
        gb = sb("gate_bias", [P, NB])
        sem = lambda name: nc.alloc_semaphore(name + "_li")

        with ExitStack() as first:
            ps = first.enter_context(nc.psum_tensor("qkv_ps_li", [P, 2, CH], F32))
            centered, qkv_ready, biased, q_squared, k_squared, summed = (
                sem("centered"), sem("qkv"), sem("biased"), sem("q_squared"), sem("k_squared"), sem("summed"))
            block = first.enter_context(nc.Block())

            @block.tensor
            def _(pe):
                pe.wait_ge(centered, 5)
                for t in range(NT):
                    if t >= 2:
                        pe.wait_ge(biased, t - 1)
                    nc.tensor.matmul(ps[:, t % 2, 0:3 * P], k.h[:, tile(t)], w[:], start=True, stop=True).then_inc(qkv_ready, 1)

            @block.vector
            def _(dve):
                blocks = lambda ap: ap.rearrange("p (i n) -> p i n", n=P)
                for j, src in enumerate((k.w["L3_Wqkv"], k.w["L3_bqkv"])):
                    nc.vector.tensor_reduce(mean[:, 2 * j:2 * j + 2], blocks(src[:, 0:2 * P]), AX, ALU.add).then_inc(centered, 1)
                dve.wait_ge(centered, 2)
                nc.vector.tensor_scalar(mean[:], mean[:], 1.0 / P, None, ALU.mult).then_inc(centered, 1)
                dve.wait_ge(centered, 3)
                for j, (src, dst) in enumerate(((k.w["L3_Wqkv"], w), (k.w["L3_bqkv"], bias))):
                    nc.vector.tensor_copy(dst[:, 2 * P:], src[:, 2 * P:])
                    nc.vector.tensor_tensor(blocks(dst[:, 0:2 * P]), blocks(src[:, 0:2 * P]),
                                            mean[:, 2 * j:2 * j + 2].unsqueeze(2).to_broadcast([P, 2, P]),
                                            ALU.subtract).then_inc(centered, 1)
                dve.wait_ge(centered, 5)
                for t in range(NT):
                    dve.wait_ge(qkv_ready, t + 1)
                    if t >= 2:
                        dve.wait_ge(k_squared, t - 1)
                    nc.vector.tensor_tensor(qkv[:, t % 2], ps[:, t % 2, 0:3 * P], bias[:], ALU.add).then_inc(biased, 1)

            @block.scalar
            def _(act):
                for t in range(NT):
                    act.wait_ge(biased, t + 1)
                    if t >= 1:
                        act.wait_ge(summed, t)
                    nc.scalar.activation(q2[:, t], qkv[:, t % 2, 0:P], ACT.Square,
                                         accum_out=sums[:, 0, t:t + 1]).then_inc(q_squared, 1)
                    nc.scalar.activation(v[:, t], qkv[:, t % 2, 2 * P:3 * P], ACT.Copy)
                    nc.scalar.activation(k2[:, t], qkv[:, t % 2, P:2 * P], ACT.Square,
                                         accum_out=sums[:, 1, t:t + 1]).then_inc(k_squared, 1)
                    act.wait_ge(q_squared, t + 1)
                    nc.scalar.activation(q4[:], q2[:, t], ACT.Square, accum_out=sums[:, 2, t:t + 1]).then_inc(summed, 1)

        with ExitStack() as second:
            kv_ps = second.enter_context(nc.psum_tensor("kv_ps_li", [P, NB, CH], F32))
            kn_ps = second.enter_context(nc.psum_tensor("kn_ps_li", [P, NB, CH], F32))
            t_ps = second.enter_context(nc.psum_tensor("t_ps_li", [P, 2, CH], F32))
            step, root, k_scaled, q_scaled, k4_ready, kv_ready, q_turned, kn_root, kv_step, qT_ready = (
                sem("step"), sem("root"), sem("k_scaled"), sem("q_scaled"), sem("k4"), sem("kv"), sem("q_turned"),
                sem("kn_root"), sem("kv_step"), sem("qT"))
            k4 = second.enter_context(nc.sbuf_tensor("k4_li", [P, 2, P], F32))
            block = second.enter_context(nc.Block())

            @block.scalar
            def _(act):
                act.wait_ge(step, 1)
                nc.scalar.activation(f[:, 2], sums[:, 2], ACT.Sqrt).then_inc(root, 1)
                for t in range(NT):
                    act.wait_ge(k_scaled, t + 1)
                    if t >= 2:
                        act.wait_ge(kv_ready, t - 1)
                    nc.scalar.activation(k4[:, t % 2], k2[:, t], ACT.Square).then_inc(k4_ready, 1)
                    if t % 4 == 3:
                        c = t // 4
                        act.wait_ge(q_turned, c + 1)
                        nc.scalar.activation(qT[:, chunk(c)], t_ps[:, c % 2], ACT.Copy).then_inc(qT_ready, 1)
                act.wait_ge(kv_step, 1)
                nc.scalar.activation(kn[:], kn[:], ACT.Sqrt).then_inc(kn_root, 1)

            @block.vector
            def _(dve):
                nc.vector.tensor_scalar(f[:, 0:2], sums[:, 0:2], EPS_SUM, None, ALU.add).then_inc(step, 1)
                dve.wait_ge(step, 1)
                nc.vector.reciprocal(f[:, 0:2], f[:, 0:2]).then_inc(step, 1)
                dve.wait_ge(step, 2)
                for t in range(NT):
                    nc.vector.tensor_scalar(k2[:, t], k2[:, t], f[:, 1, t:t + 1], None, ALU.mult).then_inc(k_scaled, 1)
                dve.wait_ge(root, 1)
                nc.vector.tensor_tensor(f[:, 3], f[:, 2], f[:, 0], ALU.mult).then_inc(step, 1)
                dve.wait_ge(step, 3)
                nc.vector.tensor_scalar(f[:, 3], f[:, 3], EPS_NORM, float(SEQ) ** 0.5, ALU.max, ALU.mult).then_inc(step, 1)
                dve.wait_ge(step, 4)
                nc.vector.reciprocal(f[:, 4], f[:, 3]).then_inc(step, 1)
                dve.wait_ge(step, 5)
                nc.vector.tensor_tensor(f[:, 5], f[:, 4], f[:, 0], ALU.mult).then_inc(step, 1)
                dve.wait_ge(step, 6)
                for t in range(NT):
                    nc.vector.tensor_scalar(q2[:, t], q2[:, t], f[:, 5, t:t + 1], None, ALU.mult).then_inc(q_scaled, 1)
                dve.wait_ge(kv_ready, NT)
                for b in range(NB):
                    last = nc.vector.tensor_copy(kn[:, b:b + 1], kn_ps[:, b, 0:1])
                last.then_inc(kv_step, 1)
                dve.wait_ge(kn_root, 1)
                nc.vector.tensor_scalar(kn[:], kn[:], EPS_NORM, None, ALU.max).then_inc(kv_step, 1)
                dve.wait_ge(kv_step, 2)
                nc.vector.reciprocal(kf[:], kn[:]).then_inc(kv_step, 1)
                dve.wait_ge(kv_step, 3)
                for b in range(NB):
                    nc.vector.tensor_scalar(kv[:, b], kv_ps[:, b, 0:P], kf[:, b:b + 1], None, ALU.mult).then_inc(kv_step, 1)
                nc.vector.tensor_scalar(gb[:], k.mod[:, 3, GATE_A], k.w["L3_bln"][:], None, ALU.mult).then_inc(kv_step, 1)

            @block.tensor
            def _(pe):
                for t in range(NT):
                    b, first_t, last_t = t // TPR, t % TPR == 0, t % TPR == TPR - 1
                    pe.wait_ge(k_scaled, t + 1)
                    nc.tensor.matmul(kv_ps[:, b, 0:P], k2[:, t], v[:, t], start=first_t, stop=last_t)
                    pe.wait_ge(k4_ready, t + 1)
                    nc.tensor.matmul(kn_ps[:, b, 0:1], k4[:, t % 2], k.w["ones"][:, 0:1],
                                     start=first_t, stop=last_t).then_inc(kv_ready, 1)
                    pe.wait_ge(q_scaled, t + 1)
                    if t % 4 == 0 and t >= 8:
                        pe.wait_ge(qT_ready, t // 4 - 1)
                    last = nc.tensor.transpose(t_ps[:, t // 4 % 2, tile(t % 4)], q2[:, t], k.w["ident"][:])
                    if t % 4 == 3:
                        last.then_inc(q_turned, 1)

        y_ps = ctx.enter_context(nc.psum_tensor("y_ps_li", [P, 2, CH], F32))
        o_ps = ctx.enter_context(nc.psum_tensor("o_ps_li", [P, 2, CH], F32))
        y_ready, y_biased, o_ready, gated, added = sem("y"), sem("y_biased"), sem("o"), sem("gated"), sem("added")
        block = ctx.enter_context(nc.Block())

        @block.tensor
        def _(pe):
            for c in range(NCH + 1):
                if c < NCH:
                    if c >= 2:
                        pe.wait_ge(y_biased, c - 1)
                    nc.tensor.matmul(y_ps[:, c % 2], w[:, 2 * P:], k.h[:, chunk(c)], start=True, stop=False)
                    nc.tensor.matmul(y_ps[:, c % 2], kv[:, batch_of(c)], qT[:, chunk(c)],
                                     start=False, stop=True).then_inc(y_ready, 1)
                if c >= 1:
                    pe.wait_ge(y_biased, c)
                    if c >= 3:
                        pe.wait_ge(gated, c - 2)
                    nc.tensor.matmul(o_ps[:, (c - 1) % 2], k.w["L3_Wln"][:], y[:, (c - 1) % 2],
                                     start=True, stop=True).then_inc(o_ready, 1)

        def project(act, c):
            b = batch_of(c)
            act.wait_ge(o_ready, c + 1)
            if c >= 2:
                act.wait_ge(added, c - 1)
            nc.scalar.activation(o[:, c % 2], o_ps[:, c % 2], ACT.Identity, bias=gb[:, b:b + 1],
                                 scale=k.mod[:, 3, GATE_A, b:b + 1]).then_inc(gated, 1)

        @block.scalar
        def _(act):
            for c in range(NCH):
                act.wait_ge(y_ready, c + 1)
                if c >= 2:
                    act.wait_ge(o_ready, c - 1)
                nc.scalar.activation(y[:, c % 2], y_ps[:, c % 2], ACT.Identity, bias=k.w["L3_bv"][:, 0:1]).then_inc(y_biased, 1)
                if c >= 1:
                    project(act, c - 1)
            project(act, NCH - 1)

        @block.vector
        def _(dve):
            for c in range(NCH):
                dve.wait_ge(gated, c + 1)
                nc.vector.tensor_tensor(k.x[:, chunk(c)], k.x[:, chunk(c)], o[:, c % 2], ALU.add).then_inc(added, 1)


def store_stage(nc, k, out):
    with ExitStack() as ctx:
        stored = nc.alloc_semaphore("stored")
        block = ctx.enter_context(nc.Block())

        @block.sync
        def _(sp):
            sp.dma_start(out, k.x[:]).then_inc(stored, 16)
            sp.wait_ge(stored, 16)


FIRST = ("mean_w", "eps", "ident", "ones", "iota8", "pick")


def transformer(nc, dram, out, only=None):
    with ExitStack() as ctx:
        k = Kit()
        k.dram = dram
        k.x = ctx.enter_context(nc.sbuf_tensor("x", [P, T], F32))
        k.h = ctx.enter_context(nc.sbuf_tensor("h", [P, T], F32))
        k.mod = ctx.enter_context(nc.sbuf_tensor("mod", [P, 4, 6, NB], F32))
        k.first_loaded = nc.alloc_semaphore("first_loaded")
        k.w = {}
        for name in FIRST:
            d = dram[name]
            k.w[name] = ctx.enter_context(nc.sbuf_tensor(f"{name}_sb", list(d.shape), d.dtype))
        modulation_stage(nc, k)
        for stages in (HALF_LAYERS if only is None else only):
            stages(nc, k)
        store_stage(nc, k, out)


HALF_LAYERS = [
    half_layer(0, 0, ("L0_W_in", "L0_heads", "L0_conv", "upto", "after", "L0_D", "L0_norm_w", "L0_W_out"), mamba_block),
    half_layer(0, 1, ("L0_router", "L0_out_bias"),
               lambda nc, k: experts_block(nc, k, 0, 2, ACT.Silu, True, True, TOP_EPS)),
    half_layer(1, 0, ("L1_Wq", "L1_Wkv", "L1_Wo", "head_sum", "head_pick"), pair_attention_stage),
    half_layer(1, 1, ("ident16", "window_mask", "rotary", "L1_wqkv", "L1_qk_scale", "L1_wo", "L1_ln", "L1_w1",
                      "L1_w2", "L1_b1", "L1_b2"), local_block),
    half_layer(2, 0, ("L2_W", "ident16", "causal_mask"), causal_attention_block),
    half_layer(2, 1, (), lambda nc, k: experts_block(nc, k, 2, 4, ACT.Silu, True, False)),
    half_layer(3, 0, ("L3_Wqkv", "L3_bqkv", "L3_bv", "L3_Wln", "L3_bln"), linear_attention_block),
    half_layer(3, 1, ("L3_router", "L3_out_bias"),
               lambda nc, k: experts_block(nc, k, 3, 4, ACT.Gelu, False, True)),
]


def rotary_tables():
    f32 = np.float32
    half = np.arange(0, HD2, 2, dtype=f32)
    t = np.arange(SEQ, dtype=f32)
    freqs = np.tile(t[:, None] * (f32(1.0) / f32(10000.0) ** (half / f32(HD2)))[None], (1, 2))
    base = (half + f32(0.4 * HD2)) / f32(1.4 * HD2)
    scale = np.tile(base[None] ** ((t - SEQ // 2) / f32(WINDOW // 2))[:, None], (1, 2))
    cos, sin = np.cos(freqs), np.sin(freqs) * np.repeat(f32([-1, 1]), HALF)[None]
    tables = np.stack([cos * scale, sin * scale, cos / scale, sin / scale]).astype(f32)
    return np.ascontiguousarray(tables.reshape(4, SEQ // P, P, HD2).transpose(2, 0, 1, 3))


def window_mask():
    i = P + np.arange(P)[:, None]
    j = np.arange(2 * P)[None, :]
    out = (i < j) | (i > j + WINDOW) | (j < i // WINDOW * WINDOW - WINDOW)
    return np.tile(np.where(out, NEG, 0.0)[:, None], (1, 2, 1)).astype(HOST16)


def constants():
    i = np.arange(P)
    heads = (2 * np.arange(8)[None, :, None] + i[:, None, None] // HD1 == np.arange(LANE)).astype(np.float32)
    return {
        "mean_w": np.full((P, P), 1.0 / P, np.float32),
        "ones": np.ones((P, P), np.float32),
        "eps": np.full((P, 1), EPS, np.float32),
        "ident": np.eye(P, dtype=np.float32),
        "upto": (i[:, None] <= i[None, :]).astype(np.float32),
        "head_sum": heads,
        "head_pick": (np.eye(P // LANE)[:, None, :, None, None] * heads.transpose(2, 1, 0)[None, :, None]
                      ).reshape(P, P // LANE, -1, P).astype(HOST16),
        "ident16": np.eye(P).astype(HOST16),
        "window_mask": window_mask(),
        "rotary": rotary_tables(),
        "causal_mask": np.stack([np.where(i[None] > i[:, None], NEG, 0.0), np.where(i[:, None] > i[None], NEG, 0.0)],
                                axis=1).astype(HOST16),
        "zero_one_rows": (np.arange(ROWS, FULL + M_PARTS)[:, None] >= FULL).repeat(SEQ, axis=1).astype(HOST16),
        "iota8": np.tile(np.arange(E, dtype=np.float32)[None], (P, 1)),
        "pick": np.ascontiguousarray(np.broadcast_to(
            (i[:PARTS * PART, None] % PART == np.arange(E)[None, :])[:, :, None],
            (PARTS * PART, E, P))).astype(HOST16),
        "after": (i[:, None] > i[None, :]).astype(np.float32),
    }


def rows(a, n=P):
    return np.ascontiguousarray(np.swapaxes(a.reshape(-1, n, *a.shape[1:]), 0, 1))


def across(ws):
    e, r, n = ws.shape
    return ws.reshape(e, r // P, P, n).transpose(0, 2, 1, 3).reshape(e, P, -1)


def by_column(b):
    return b.reshape(b.shape[0], -1, P).transpose(0, 2, 1)


def out_bias(b):
    a = np.zeros((PARTS, PART, P), np.float32)
    a[:, :E] = b
    return a.reshape(PARTS * PART, P)


def laid_out(v):
    v = {name: np.asarray(a) for name, a in v.items()}
    a = constants()
    a["xT"] = np.ascontiguousarray(v["L0_attn_u"].reshape(T, P).T)
    a["cT"] = np.ascontiguousarray(np.concatenate([v[f"L{i}_c"] for i in range(4)]).T)
    a["wmod"] = np.ascontiguousarray(np.stack([v[f"L{i}_wmod"] for i in range(4)], axis=1))
    a["L0_W_in"] = v["L0_attn_W_in"]
    a["L0_heads"] = np.tile(np.concatenate([v["L0_attn_dt_bias"], v["L0_attn_A_log"]])[None], (P, 1))
    a["L0_conv"] = rows(np.concatenate([v["L0_attn_conv_w"], v["L0_attn_conv_b"][:, None]], axis=1))
    a["L0_D"] = rows(np.repeat(v["L0_attn_D"], HD0))
    a["L0_norm_w"] = rows(v["L0_attn_norm_w"])
    a["L0_W_out"] = rows(v["L0_attn_W_out"])
    a["L0_router"] = v["L0_ffn_W_router"]
    a["L0_experts"] = np.concatenate([v["L0_ffn_W_gate"], v["L0_ffn_W_up"], across(v["L0_ffn_W_out"]),
                                      by_column(v["L0_ffn_b_gate"]), by_column(v["L0_ffn_b_up"])], axis=2)
    a["L0_out_bias"] = out_bias(v["L0_ffn_b_out"])
    a["L1_Wq"], a["L1_Wkv"], a["L1_Wo"] = v["L1_attn_Wq"], v["L1_attn_Wkv"], rows(v["L1_attn_Wo"])
    a["L1_wqkv"] = v["L1_ffn_wqkv"].transpose(1, 0, 2)
    crossed = lambda q: np.roll(q, HALF, axis=1)
    q, kk = v["L1_ffn_q_scale"], v["L1_ffn_k_scale"]
    a["L1_qk_scale"] = np.tile(np.stack([q, crossed(q), kk, crossed(kk)], axis=1)[None], (P, 1, 1, 1))
    a["L1_wo"] = v["L1_ffn_wo"].reshape(DEPTH, QT, P, P).transpose(2, 0, 1, 3)
    a["L1_ln"] = np.stack([v["L1_ffn_ln_g"], v["L1_ffn_ln_b"]]).transpose(2, 0, 1)
    hid_tiles = -(-HID // P)
    a["L1_w1"] = np.pad(v["L1_ffn_w1"].reshape(DEPTH, P, 2, HID), ((0, 0), (0, 0), (0, 0), (0, hid_tiles * P - HID))
                        ).transpose(1, 0, 2, 3)
    a["L1_w2"] = np.pad(v["L1_ffn_w2"], ((0, 0), (0, hid_tiles * P - HID), (0, 0))
                        ).reshape(DEPTH, hid_tiles, P, P).transpose(2, 0, 1, 3)
    a["L1_b1"] = np.pad(v["L1_ffn_b1"].reshape(DEPTH, 2, HID), ((0, 0), (0, 0), (0, hid_tiles * P - HID))
                        ).reshape(DEPTH, 2, hid_tiles, P).transpose(3, 0, 1, 2)
    a["L1_b2"] = v["L1_ffn_b2"].T
    by_quad = lambda w: w.reshape(P, -1, QUAD, HD3).swapaxes(2, 3).reshape(P, P)
    a["L2_W"] = np.stack([by_quad(v["L2_attn_W_Q"].T), by_quad(v["L2_attn_W_K"].T), v["L2_attn_W_V"].T, v["L2_attn_W_O"].T], axis=1)
    a["L2_experts"] = np.concatenate([v["L2_ffn_Wg"], v["L2_ffn_Wu"], across(v["L2_ffn_Wd"])], axis=2)
    a["L3_Wqkv"], a["L3_Wln"] = v["L3_attn_Wqkv"], v["L3_attn_Wln"]
    a["L3_bqkv"] = np.tile(v["L3_attn_bqkv"][None], (P, 1))
    a["L3_bv"], a["L3_bln"] = v["L3_attn_bqkv"][2 * P:, None], v["L3_attn_bln"][:, None]
    a["L3_router"] = np.ascontiguousarray(v["L3_ffn_router_w"].T)
    a["L3_experts"] = np.concatenate([v["L3_ffn_w1"].transpose(0, 2, 1), across(v["L3_ffn_w2"].transpose(0, 2, 1)),
                                      by_column(v["L3_ffn_b1"])], axis=2)
    a["L3_out_bias"] = out_bias(v["L3_ffn_b2"])
    return {name: np.ascontiguousarray(x) for name, x in a.items()}


def kernel(**inputs):
    import concourse.bacc as bacc
    from concourse.bass_utils import run_bass_kernel_spmd

    nc = bacc.Bacc("TRN2", target_bir_lowering=False, num_devices=1)
    arrays = laid_out(inputs)
    dram = {name: nc.dram_tensor("in_" + name, a.shape, mybir.dt.from_np(a.dtype), kind="ExternalInput").ap()
            for name, a in arrays.items()}
    out = nc.dram_tensor("out_xT", [P, T], F32, kind="ExternalOutput").ap()
    transformer(nc, dram, out)
    r = run_bass_kernel_spmd(nc, [{"in_" + name: a for name, a in arrays.items()}], core_ids=[0])
    return np.ascontiguousarray(np.asarray(r.results[0]["out_xT"]).T).reshape(NB, SEQ, P)
```
